# Optimizing a Trainium2 kernel written in Bass

```python
import numpy as np
import jax
import jax.numpy as jnp

def _softmax(x, axis=-1):
    return jax.nn.softmax(x, axis=axis)

def _gelu(x):
    return jax.nn.gelu(x, approximate=True)

def _silu(x):
    return jax.nn.silu(x)

def _sigmoid(x):
    return jax.nn.sigmoid(x)

def _layernorm(x, axis=-1, eps=1e-05):
    m = jnp.mean(x, axis=axis, keepdims=True)
    v = jnp.var(x, axis=axis, keepdims=True)
    return (x - m) / jnp.sqrt(v + eps)

def _scatter_add(tgt, idx, src, axis=0):
    return tgt.at[idx].add(src)

def _segment_sum(src, seg, n):
    return jax.ops.segment_sum(src, seg, n)
kernel_name = 'mk_hybrid_d2_jaxref_r4_a29296'

def setup_inputs(seed: int=0):
    np.random.seed(seed)
    _w = jnp.asarray

    def _L0_attn_a_setup():
        import jax, jax.numpy as jnp
        import numpy as np
        D_MODEL = 256
        NHEAD = 16
        HEAD_DIM = D_MODEL // NHEAD
        EPS = 1e-06

        def _l2_normalize(x, eps=EPS):
            return x / (jnp.linalg.norm(x, axis=-1, keepdims=True) + eps)
        key = jax.random.key(seed)
        ks = jax.random.split(key, 7)
        B, S = (4, 512)
        scale = 1.0 / np.sqrt(D_MODEL)
        return {'x': jax.random.normal(ks[0], (B, S, D_MODEL), dtype=jnp.float32), 'Wq': jax.random.normal(ks[1], (D_MODEL, D_MODEL), dtype=jnp.float32) * scale, 'Wk': jax.random.normal(ks[2], (D_MODEL, D_MODEL), dtype=jnp.float32) * scale, 'Wv': jax.random.normal(ks[3], (D_MODEL, D_MODEL), dtype=jnp.float32) * scale, 'Wo': jax.random.normal(ks[4], (D_MODEL, D_MODEL), dtype=jnp.float32) * scale, 'Wbeta': jax.random.normal(ks[5], (NHEAD, D_MODEL), dtype=jnp.float32) * scale, 'rms_weight': jnp.ones((D_MODEL,), dtype=jnp.float32)}
    _L0_attn_a_in = _L0_attn_a_setup()

    def _L0_attn_b_setup():
        import jax, jax.numpy as jnp
        import numpy as np
        NUM_HEADS = 16

        def _heads(t, B, N, H, hd):
            return t.reshape(B, N, H, hd).transpose(0, 2, 1, 3)
        key = jax.random.key(seed)
        ks = jax.random.split(key, 9)
        B, N, D = (2, 512, 256)
        w = 0.02
        return {'x': jax.random.normal(ks[0], (B, N, D), dtype=jnp.float32), 'wq': jax.random.normal(ks[1], (D, D), dtype=jnp.float32) * w, 'bq': jax.random.normal(ks[2], (D,), dtype=jnp.float32) * w, 'wk': jax.random.normal(ks[3], (D, D), dtype=jnp.float32) * w, 'bk': jax.random.normal(ks[4], (D,), dtype=jnp.float32) * w, 'wv': jax.random.normal(ks[5], (D, D), dtype=jnp.float32) * w, 'bv': jax.random.normal(ks[6], (D,), dtype=jnp.float32) * w, 'wo': jax.random.normal(ks[7], (D, D), dtype=jnp.float32) * w, 'bo': jax.random.normal(ks[8], (D,), dtype=jnp.float32) * w}
    _L0_attn_b_in = _L0_attn_b_setup()

    def _L0_ffn_setup():
        import jax, jax.numpy as jnp
        import numpy as np
        D_MODEL = 256
        EXPANSION = 4
        D_HIDDEN = D_MODEL * EXPANSION
        NUM_STAGES = int(np.log2(D_HIDDEN))

        def butterfly(y, weights, dim):
            lead = y.shape[:-1]
            for stage in range(weights.shape[0]):
                s = 2 ** stage
                nb = dim // (2 * s)
                yr = y.reshape(*lead, nb, 2, s)
                a = yr[..., 0, :]
                b = yr[..., 1, :]
                w = weights[stage].reshape(nb, s, 2, 2)
                na = w[..., 0, 0] * a + w[..., 0, 1] * b
                nb2 = w[..., 1, 0] * a + w[..., 1, 1] * b
                y = jnp.stack([na, nb2], axis=-2).reshape(*lead, dim)
            return y
        key = jax.random.key(seed)
        ks = jax.random.split(key, 6)
        B, S = (4, 512)
        x = jax.random.normal(ks[0], (B, S, D_MODEL), jnp.float32)
        W_exp = jax.random.normal(ks[1], (D_MODEL, D_HIDDEN), jnp.float32) * 0.02
        b_exp = jnp.zeros((D_HIDDEN,), jnp.float32)
        up_weights = jax.random.normal(ks[2], (NUM_STAGES, D_HIDDEN // 2, 2, 2), jnp.float32) * 0.02
        up_bias = jnp.zeros((D_HIDDEN,), jnp.float32)
        down_weights = jax.random.normal(ks[3], (NUM_STAGES, D_HIDDEN // 2, 2, 2), jnp.float32) * 0.02
        W_con = jax.random.normal(ks[4], (D_HIDDEN, D_MODEL), jnp.float32) * 0.02
        b_con = jnp.zeros((D_MODEL,), jnp.float32)
        down_bias = jnp.zeros((D_MODEL,), jnp.float32)
        return dict(x=x, W_exp=W_exp, b_exp=b_exp, up_weights=up_weights, up_bias=up_bias, down_weights=down_weights, W_con=W_con, b_con=b_con, down_bias=down_bias)
    _L0_ffn_in = _L0_ffn_setup()

    def _L1_attn_a_setup():
        import jax, jax.numpy as jnp
        import numpy as np
        import math
        B, L, D, N2 = (8, 1024, 256, 32)

        def s4d_kernel(log_dt, log_A_real, A_imag, C_real, C_imag, length):
            dt = jnp.exp(log_dt)[:, None]
            A = -jnp.exp(log_A_real) + 1j * A_imag
            dtA = A * dt
            C = (C_real + 1j * C_imag) * (jnp.exp(dtA) - 1.0) / A
            t = jnp.arange(length, dtype=jnp.float32)
            vand = jnp.exp(dtA[:, :, None] * t)
            K = 2.0 * jnp.einsum('dn,dnl->dl', C, vand).real
            return K
        key = jax.random.key(seed)
        ks = jax.random.split(key, 6)
        x = jax.random.normal(ks[0], (B, L, D), dtype=jnp.float32)
        log_dt = jax.random.uniform(ks[1], (D,), minval=math.log(0.001), maxval=math.log(0.1)).astype(jnp.float32)
        log_A_real = jnp.log(0.5 * jnp.ones((D, N2), jnp.float32))
        A_imag = math.pi * jnp.broadcast_to(jnp.arange(N2, dtype=jnp.float32), (D, N2))
        C_real = jax.random.normal(ks[2], (D, N2), dtype=jnp.float32)
        C_imag = jax.random.normal(ks[3], (D, N2), dtype=jnp.float32)
        W = jax.random.normal(ks[4], (D, D), dtype=jnp.float32) / jnp.sqrt(jnp.float32(D))
        b = jax.random.normal(ks[5], (D,), dtype=jnp.float32) * 0.01
        return dict(x=x, log_dt=log_dt, log_A_real=log_A_real, A_imag=A_imag, C_real=C_real, C_imag=C_imag, W=W, b=b)
    _L1_attn_a_in = _L1_attn_a_setup()

    def _L1_attn_b_setup():
        import jax, jax.numpy as jnp
        import numpy as np
        D_MODEL = 256
        EXPAND = 2
        D_INNER = EXPAND * D_MODEL
        HEADDIM = 64
        NHEADS = D_INNER // HEADDIM
        NGROUPS = 1
        D_STATE = 128
        D_CONV = 4
        CHUNK = 64
        BATCH = 2
        SEQLEN = 1024

        def _segsum(x):
            T = x.shape[-1]
            cs = jnp.cumsum(x, axis=-1)
            ss = cs[..., :, None] - cs[..., None, :]
            mask = jnp.tril(jnp.ones((T, T), dtype=bool))
            return jnp.where(mask, ss, -jnp.inf)

        def _ssd(X, A, Bm, Cm):
            b, l, h, p = X.shape
            c = l // CHUNK
            X = X.reshape(b, c, CHUNK, h, p)
            A = A.reshape(b, c, CHUNK, h).transpose(0, 3, 1, 2)
            Bm = Bm.reshape(b, c, CHUNK, -1)
            Cm = Cm.reshape(b, c, CHUNK, -1)
            A_cs = jnp.cumsum(A, axis=-1)
            Lmat = jnp.exp(_segsum(A))
            Y_diag = jnp.einsum('bcln,bcsn,bhcls,bcshp->bclhp', Cm, Bm, Lmat, X)
            decay_states = jnp.exp(A_cs[..., -1:] - A_cs)
            states = jnp.einsum('bcln,bhcl,bclhp->bchpn', Bm, decay_states, X)
            init = jnp.zeros_like(states[:, :1])
            states = jnp.concatenate([init, states], axis=1)
            A_last = jnp.pad(A_cs[..., -1], ((0, 0), (0, 0), (1, 0)))
            decay_chunk = jnp.exp(_segsum(A_last))
            new_states = jnp.einsum('bhzc,bchpn->bzhpn', decay_chunk, states)
            states, final_state = (new_states[:, :-1], new_states[:, -1])
            out_decay = jnp.exp(A_cs)
            Y_off = jnp.einsum('bcln,bchpn,bhcl->bclhp', Cm, states, out_decay)
            return ((Y_diag + Y_off).reshape(b, l, h, p), final_state)
        key = jax.random.key(seed)
        ks = jax.random.split(key, 8)
        d_in_proj = 2 * D_INNER + 2 * NGROUPS * D_STATE + NHEADS
        conv_dim = D_INNER + 2 * NGROUPS * D_STATE
        u = jax.random.normal(ks[0], (BATCH, SEQLEN, D_MODEL), jnp.float32)
        W_in = jax.random.normal(ks[1], (D_MODEL, d_in_proj), jnp.float32) * D_MODEL ** (-0.5)
        conv_w = jax.random.normal(ks[2], (conv_dim, D_CONV), jnp.float32) * D_CONV ** (-0.5)
        conv_b = jnp.zeros((conv_dim,), jnp.float32)
        dt = jnp.exp(jax.random.uniform(ks[3], (NHEADS,)) * (np.log(0.1) - np.log(0.001)) + np.log(0.001))
        dt = jnp.clip(dt, 0.0001)
        dt_bias = dt + jnp.log(-jnp.expm1(-dt))
        A_log = jnp.log(jax.random.uniform(ks[4], (NHEADS,), minval=1.0, maxval=16.0))
        norm_w = jnp.ones((D_INNER,), jnp.float32)
        W_out = jax.random.normal(ks[5], (D_INNER, D_MODEL), jnp.float32) * D_INNER ** (-0.5)
        return dict(u=u, W_in=W_in, conv_w=conv_w, conv_b=conv_b, dt_bias=dt_bias, A_log=A_log, norm_w=norm_w, W_out=W_out)
    _L1_attn_b_in = _L1_attn_b_setup()

    def _L1_ffn_setup():
        import jax, jax.numpy as jnp
        import numpy as np
        key = jax.random.key(seed)
        ks = jax.random.split(key, 5)
        B, S, D_in, D_out, E, R = (4, 256, 256, 256, 8, 16)
        x = jax.random.normal(ks[0], (B, S, D_in), dtype=jnp.float32)
        weight = jax.random.normal(ks[1], (D_out, D_in), dtype=jnp.float32) / np.sqrt(D_in)
        gate_w = jax.random.normal(ks[2], (E, D_in), dtype=jnp.float32) / np.sqrt(D_in)
        lora_U = jax.random.normal(ks[3], (E, R, D_in), dtype=jnp.float32) / np.sqrt(D_in)
        lora_V = jax.random.normal(ks[4], (E, D_out, R), dtype=jnp.float32) / np.sqrt(R)
        return {'x': x, 'weight': weight, 'gate_w': gate_w, 'lora_U': lora_U, 'lora_V': lora_V}
    _L1_ffn_in = _L1_ffn_setup()
    _d = {'L0_attn_a_x': _L0_attn_a_in['x'], 'L0_attn_a_Wq': _L0_attn_a_in['Wq'], 'L0_attn_a_Wk': _L0_attn_a_in['Wk'], 'L0_attn_a_Wv': _L0_attn_a_in['Wv'], 'L0_attn_a_Wo': _L0_attn_a_in['Wo'], 'L0_attn_a_Wbeta': _L0_attn_a_in['Wbeta'], 'L0_attn_a_rms_weight': _L0_attn_a_in['rms_weight'], 'L0_attn_b_wq': _L0_attn_b_in['wq'], 'L0_attn_b_bq': _L0_attn_b_in['bq'], 'L0_attn_b_wk': _L0_attn_b_in['wk'], 'L0_attn_b_bk': _L0_attn_b_in['bk'], 'L0_attn_b_wv': _L0_attn_b_in['wv'], 'L0_attn_b_bv': _L0_attn_b_in['bv'], 'L0_attn_b_wo': _L0_attn_b_in['wo'], 'L0_attn_b_bo': _L0_attn_b_in['bo'], 'L0_ffn_W_exp': _L0_ffn_in['W_exp'], 'L0_ffn_b_exp': _L0_ffn_in['b_exp'], 'L0_ffn_up_weights': _L0_ffn_in['up_weights'], 'L0_ffn_up_bias': _L0_ffn_in['up_bias'], 'L0_ffn_down_weights': _L0_ffn_in['down_weights'], 'L0_ffn_W_con': _L0_ffn_in['W_con'], 'L0_ffn_b_con': _L0_ffn_in['b_con'], 'L0_ffn_down_bias': _L0_ffn_in['down_bias'], 'L1_attn_a_log_dt': _L1_attn_a_in['log_dt'], 'L1_attn_a_log_A_real': _L1_attn_a_in['log_A_real'], 'L1_attn_a_A_imag': _L1_attn_a_in['A_imag'], 'L1_attn_a_C_real': _L1_attn_a_in['C_real'], 'L1_attn_a_C_imag': _L1_attn_a_in['C_imag'], 'L1_attn_a_W': _L1_attn_a_in['W'], 'L1_attn_a_b': _L1_attn_a_in['b'], 'L1_attn_b_W_in': _L1_attn_b_in['W_in'], 'L1_attn_b_conv_w': _L1_attn_b_in['conv_w'], 'L1_attn_b_conv_b': _L1_attn_b_in['conv_b'], 'L1_attn_b_dt_bias': _L1_attn_b_in['dt_bias'], 'L1_attn_b_A_log': _L1_attn_b_in['A_log'], 'L1_attn_b_norm_w': _L1_attn_b_in['norm_w'], 'L1_attn_b_W_out': _L1_attn_b_in['W_out'], 'L1_ffn_weight': _L1_ffn_in['weight'], 'L1_ffn_gate_w': _L1_ffn_in['gate_w'], 'L1_ffn_lora_U': _L1_ffn_in['lora_U'], 'L1_ffn_lora_V': _L1_ffn_in['lora_V']}
    _x0 = _d['L0_attn_a_x']
    _d['L0_attn_a_x'] = jax.random.normal(jax.random.fold_in(jax.random.key(seed), 1), (8, 512, 256), dtype=_x0.dtype)
    del _x0
    return _d

def reference(L0_attn_a_x, L0_attn_a_Wq, L0_attn_a_Wk, L0_attn_a_Wv, L0_attn_a_Wo, L0_attn_a_Wbeta, L0_attn_a_rms_weight, L0_attn_b_wq, L0_attn_b_bq, L0_attn_b_wk, L0_attn_b_bk, L0_attn_b_wv, L0_attn_b_bv, L0_attn_b_wo, L0_attn_b_bo, L0_ffn_W_exp, L0_ffn_b_exp, L0_ffn_up_weights, L0_ffn_up_bias, L0_ffn_down_weights, L0_ffn_W_con, L0_ffn_b_con, L0_ffn_down_bias, L1_attn_a_log_dt, L1_attn_a_log_A_real, L1_attn_a_A_imag, L1_attn_a_C_real, L1_attn_a_C_imag, L1_attn_a_W, L1_attn_a_b, L1_attn_b_W_in, L1_attn_b_conv_w, L1_attn_b_conv_b, L1_attn_b_dt_bias, L1_attn_b_A_log, L1_attn_b_norm_w, L1_attn_b_W_out, L1_ffn_weight, L1_ffn_gate_w, L1_ffn_lora_U, L1_ffn_lora_V):

    def _L0_attn_a_ref(x, Wq, Wk, Wv, Wo, Wbeta, rms_weight):
        import jax, jax.numpy as jnp
        import numpy as np
        D_MODEL = 256
        NHEAD = 16
        HEAD_DIM = D_MODEL // NHEAD
        EPS = 1e-06

        def _l2_normalize(x, eps=EPS):
            return x / (jnp.linalg.norm(x, axis=-1, keepdims=True) + eps)
        B, S, D = x.shape
        N, H = (NHEAD, HEAD_DIM)
        silu = jax.nn.silu
        q = _l2_normalize(silu(x @ Wq.T).reshape(B, S, N, H))
        k = _l2_normalize(silu(x @ Wk.T).reshape(B, S, N, H))
        v = silu(x @ Wv.T).reshape(B, S, N, H)
        beta = jax.nn.sigmoid(x @ Wbeta.T)

        def step(M, inp):
            q_t, k_t, v_t, b_t = inp
            out_t = jnp.einsum('bnh,bnhd->bnd', q_t, M)
            retrieved = jnp.einsum('bnhd,bnd->bnh', M, k_t)
            delta = v_t - retrieved
            M = M + b_t[..., None, None] * jnp.einsum('bnh,bnd->bnhd', k_t, delta)
            return (M, out_t)
        M0 = jnp.zeros((B, N, H, H), dtype=x.dtype)
        xs = (q.transpose(1, 0, 2, 3), k.transpose(1, 0, 2, 3), v.transpose(1, 0, 2, 3), beta.transpose(1, 0, 2))
        _, outs = jax.lax.scan(step, M0, xs)
        out = outs.transpose(1, 0, 2, 3).reshape(B, S, D)
        rms = jnp.sqrt(jnp.mean(out * out, axis=-1, keepdims=True) + EPS)
        out = out / rms * rms_weight
        return out @ Wo.T

    def _L0_attn_b_ref(x, wq, bq, wk, bk, wv, bv, wo, bo):
        import jax, jax.numpy as jnp
        import numpy as np
        NUM_HEADS = 16

        def _heads(t, B, N, H, hd):
            return t.reshape(B, N, H, hd).transpose(0, 2, 1, 3)
        B, N, D = x.shape
        H = NUM_HEADS
        hd = D // H
        q = _heads(x @ wq.T + bq, B, N, H, hd)
        k = _heads(x @ wk.T + bk, B, N, H, hd)
        v = _heads(x @ wv.T + bv, B, N, H, hd)
        q2 = jnp.sum(q * q, axis=-1)
        k2 = jnp.sum(k * k, axis=-1)
        qk = jnp.einsum('bhid,bhjd->bhij', q, k)
        d2 = jnp.maximum(q2[..., :, None] + k2[..., None, :] - 2.0 * qk, 1e-12)
        attn = jax.nn.softmax(-jnp.sqrt(d2), axis=-1)
        out = jnp.einsum('bhij,bhjd->bhid', attn, v)
        out = out.transpose(0, 2, 1, 3).reshape(B, N, D)
        return out @ wo.T + bo

    def _L0_ffn_ref(x, W_exp, b_exp, up_weights, up_bias, down_weights, W_con, b_con, down_bias):
        import jax, jax.numpy as jnp
        import numpy as np
        D_MODEL = 256
        EXPANSION = 4
        D_HIDDEN = D_MODEL * EXPANSION
        NUM_STAGES = int(np.log2(D_HIDDEN))

        def butterfly(y, weights, dim):
            lead = y.shape[:-1]
            for stage in range(weights.shape[0]):
                s = 2 ** stage
                nb = dim // (2 * s)
                yr = y.reshape(*lead, nb, 2, s)
                a = yr[..., 0, :]
                b = yr[..., 1, :]
                w = weights[stage].reshape(nb, s, 2, 2)
                na = w[..., 0, 0] * a + w[..., 0, 1] * b
                nb2 = w[..., 1, 0] * a + w[..., 1, 1] * b
                y = jnp.stack([na, nb2], axis=-2).reshape(*lead, dim)
            return y
        h = jnp.einsum('bsd,dh->bsh', x, W_exp) + b_exp
        h = butterfly(h, up_weights, D_HIDDEN)
        h = jax.nn.gelu(h + up_bias, approximate=False)
        h = butterfly(h, down_weights, D_HIDDEN)
        y = jnp.einsum('bsh,hd->bsd', h, W_con) + b_con
        return y + down_bias

    def _L1_attn_a_ref(x, log_dt, log_A_real, A_imag, C_real, C_imag, W, b):
        import jax, jax.numpy as jnp
        import numpy as np
        import math
        B, L, D, N2 = (8, 1024, 256, 32)

        def s4d_kernel(log_dt, log_A_real, A_imag, C_real, C_imag, length):
            dt = jnp.exp(log_dt)[:, None]
            A = -jnp.exp(log_A_real) + 1j * A_imag
            dtA = A * dt
            C = (C_real + 1j * C_imag) * (jnp.exp(dtA) - 1.0) / A
            t = jnp.arange(length, dtype=jnp.float32)
            vand = jnp.exp(dtA[:, :, None] * t)
            K = 2.0 * jnp.einsum('dn,dnl->dl', C, vand).real
            return K
        Bb, Ll, Dd = x.shape
        K = s4d_kernel(log_dt, log_A_real, A_imag, C_real, C_imag, Ll)
        n_fft = 2 * Ll
        x_t = jnp.transpose(x, (0, 2, 1))
        k_f = jnp.fft.rfft(K, n=n_fft)
        x_f = jnp.fft.rfft(x_t, n=n_fft)
        y = jnp.fft.irfft(x_f * k_f[None], n=n_fft)[:, :, :Ll]
        y = jnp.transpose(y, (0, 2, 1))
        y = jax.nn.gelu(y, approximate=False)
        return y @ W.T + b

    def _L1_attn_b_ref(u, W_in, conv_w, conv_b, dt_bias, A_log, norm_w, W_out):
        import jax, jax.numpy as jnp
        import numpy as np
        D_MODEL = 256
        EXPAND = 2
        D_INNER = EXPAND * D_MODEL
        HEADDIM = 64
        NHEADS = D_INNER // HEADDIM
        NGROUPS = 1
        D_STATE = 128
        D_CONV = 4
        CHUNK = 64
        BATCH = 2
        SEQLEN = 1024

        def _segsum(x):
            T = x.shape[-1]
            cs = jnp.cumsum(x, axis=-1)
            ss = cs[..., :, None] - cs[..., None, :]
            mask = jnp.tril(jnp.ones((T, T), dtype=bool))
            return jnp.where(mask, ss, -jnp.inf)

        def _ssd(X, A, Bm, Cm):
            b, l, h, p = X.shape
            c = l // CHUNK
            X = X.reshape(b, c, CHUNK, h, p)
            A = A.reshape(b, c, CHUNK, h).transpose(0, 3, 1, 2)
            Bm = Bm.reshape(b, c, CHUNK, -1)
            Cm = Cm.reshape(b, c, CHUNK, -1)
            A_cs = jnp.cumsum(A, axis=-1)
            Lmat = jnp.exp(_segsum(A))
            Y_diag = jnp.einsum('bcln,bcsn,bhcls,bcshp->bclhp', Cm, Bm, Lmat, X)
            decay_states = jnp.exp(A_cs[..., -1:] - A_cs)
            states = jnp.einsum('bcln,bhcl,bclhp->bchpn', Bm, decay_states, X)
            init = jnp.zeros_like(states[:, :1])
            states = jnp.concatenate([init, states], axis=1)
            A_last = jnp.pad(A_cs[..., -1], ((0, 0), (0, 0), (1, 0)))
            decay_chunk = jnp.exp(_segsum(A_last))
            new_states = jnp.einsum('bhzc,bchpn->bzhpn', decay_chunk, states)
            states, final_state = (new_states[:, :-1], new_states[:, -1])
            out_decay = jnp.exp(A_cs)
            Y_off = jnp.einsum('bcln,bchpn,bhcl->bclhp', Cm, states, out_decay)
            return ((Y_diag + Y_off).reshape(b, l, h, p), final_state)
        b, l, _ = u.shape
        zxbcdt = u @ W_in
        z, xBC, dt = jnp.split(zxbcdt, [D_INNER, 2 * D_INNER + 2 * NGROUPS * D_STATE], axis=-1)
        dt = jax.nn.softplus(dt + dt_bias)
        A = -jnp.exp(A_log)
        xpad = jnp.pad(xBC, ((0, 0), (D_CONV - 1, 0), (0, 0)))
        xBC = sum((xpad[:, j:j + l, :] * conv_w[:, j] for j in range(D_CONV))) + conv_b
        xBC = jax.nn.silu(xBC)
        x, Bm, Cm = jnp.split(xBC, [D_INNER, D_INNER + NGROUPS * D_STATE], axis=-1)
        x = x.reshape(b, l, NHEADS, HEADDIM)
        y, _ = _ssd(x * dt[..., None], A * dt, Bm, Cm)
        y = y.reshape(b, l, D_INNER)
        z = jax.nn.silu(z)
        mu = y.mean(-1, keepdims=True)
        var = ((y - mu) ** 2).mean(-1, keepdims=True)
        y = (y - mu) * jax.lax.rsqrt(var + 1e-05) * norm_w
        y = y * z
        return y @ W_out

    def _L1_ffn_ref(x, weight, gate_w, lora_U, lora_V):
        import jax, jax.numpy as jnp
        import numpy as np
        scaling = 1.0 / lora_U.shape[1]
        B, S, D_in = x.shape
        xt = x.reshape(-1, D_in)
        gate = jax.nn.softmax(xt @ gate_w.T, axis=-1)
        base = xt @ weight.T
        t = jnp.einsum('nh,erh->ner', xt, lora_U)
        lora = jnp.einsum('ne,eor,ner->no', gate, lora_V, t)
        out = base + scaling * lora
        return out.reshape(B, S, -1)
    x = L0_attn_a_x
    x = x + _L0_attn_a_ref(_layernorm(x, axis=-1), L0_attn_a_Wq, L0_attn_a_Wk, L0_attn_a_Wv, L0_attn_a_Wo, L0_attn_a_Wbeta, L0_attn_a_rms_weight)
    x = x + _L0_ffn_ref(_layernorm(x, axis=-1), L0_ffn_W_exp, L0_ffn_b_exp, L0_ffn_up_weights, L0_ffn_up_bias, L0_ffn_down_weights, L0_ffn_W_con, L0_ffn_b_con, L0_ffn_down_bias)
    x = x + _L0_attn_b_ref(_layernorm(x, axis=-1), L0_attn_b_wq, L0_attn_b_bq, L0_attn_b_wk, L0_attn_b_bk, L0_attn_b_wv, L0_attn_b_bv, L0_attn_b_wo, L0_attn_b_bo)
    x = x + _L0_ffn_ref(_layernorm(x, axis=-1), L0_ffn_W_exp, L0_ffn_b_exp, L0_ffn_up_weights, L0_ffn_up_bias, L0_ffn_down_weights, L0_ffn_W_con, L0_ffn_b_con, L0_ffn_down_bias)
    x = x + _L1_attn_a_ref(_layernorm(x, axis=-1), L1_attn_a_log_dt, L1_attn_a_log_A_real, L1_attn_a_A_imag, L1_attn_a_C_real, L1_attn_a_C_imag, L1_attn_a_W, L1_attn_a_b)
    x = x + _L1_ffn_ref(_layernorm(x, axis=-1), L1_ffn_weight, L1_ffn_gate_w, L1_ffn_lora_U, L1_ffn_lora_V)
    x = x + _L1_attn_b_ref(_layernorm(x, axis=-1), L1_attn_b_W_in, L1_attn_b_conv_w, L1_attn_b_conv_b, L1_attn_b_dt_bias, L1_attn_b_A_log, L1_attn_b_norm_w, L1_attn_b_W_out)
    x = x + _L1_ffn_ref(_layernorm(x, axis=-1), L1_ffn_weight, L1_ffn_gate_w, L1_ffn_lora_U, L1_ffn_lora_V)
    return x

_drawn_inputs = setup_inputs


def setup_inputs(seed=0):
    import zlib

    import numpy as np

    out = dict(_drawn_inputs(seed))
    spreads = {'L0_attn_a_rms_weight': (1.0, 0.2),
     'L0_ffn_b_exp': (0.0, 0.1),
     'L0_ffn_up_bias': (0.0, 0.1),
     'L0_ffn_b_con': (0.0, 0.1),
     'L0_ffn_down_bias': (0.0, 0.1),
     'L1_attn_a_log_A_real': (-0.6931471824645996, 0.2),
     'L1_attn_b_conv_b': (0.0, 0.1),
     'L1_attn_b_norm_w': (1.0, 0.2)}
    factors = {'L0_attn_b_wq': 28.729,
     'L0_attn_b_bq': 200.0,
     'L0_attn_b_wk': 26.03,
     'L0_attn_b_bk': 200.0,
     'L0_attn_b_bv': 8.0,
     'L0_attn_b_bo': 3.373,
     'L1_attn_a_b': 8.0,
     'L1_ffn_gate_w': 4.11,
     'L1_ffn_lora_U': 2.682,
     'L1_ffn_lora_V': 2.731}
    for name, (base, spread) in spreads.items():
        noise = np.random.default_rng([zlib.crc32(name.encode()), seed]).standard_normal(out[name].shape)
        drawn = base * np.exp(spread * noise) if base else spread * noise
        out[name] = jnp.asarray(drawn.astype(out[name].dtype))
    for name, factor in factors.items():
        out[name] = (out[name] * factor).astype(out[name].dtype)
    return out
```

```python
from contextlib import ExitStack

import concourse.bass as bass
from concourse import mybir

ALU = mybir.AluOpType
ACT = mybir.ActivationFunctionType
F32 = mybir.dt.float32
AX = mybir.AxisListType

P = 128
B, S, D = 8, 512, 256
TPB = S // P
NT = B * TPB
KD = D // P
HID = 1024
NSTAGE = 10
EPS_LN = 1e-5


class Core:

    def __init__(self, nc, ctx):
        self.nc, self.ctx, self.sems = nc, ctx, []
        sb = self.sbuf
        self.X = sb("X", [P, NT, D])
        self.bn = sb("bn", [P, NT, 6])
        self.mv = sb("mv", [P, NT, 2])
        self.rstd = sb("rstd", [P, NT])
        self.shift = sb("shift", [P, NT])
        self.ident = sb("ident", [P, P])
        self.eps = sb("eps", [P, 1])
        self.ones = sb("ones", [P, P])
        self.begun = self.sem("begun")
        self.passed = self.sem("passed")
        self.sems = []

    def apart(self, eng):
        eng.wait_ge(self.begun, 1)

    def behind(self, eng):
        eng.sem_inc(self.passed, 1)

    def sbuf(self, name, shape, ctx=None):
        return (ctx or self.ctx).enter_context(self.nc.sbuf_tensor(name, shape, F32))

    def psum(self, name, shape, ctx=None):
        return (ctx or self.ctx).enter_context(self.nc.psum_tensor(name, shape, F32))

    def sem(self, name, ctx=None):
        handle = self.nc.alloc_semaphore(name)
        self.sems.append(handle)
        return handle

    def clear_semaphores(self):
        self.nc.all_engine_barrier()
        self.nc.clear_and_free_semaphores(self.sems)
        self.nc.all_engine_barrier()
        self.sems = []


def spread(ap, shape, axis):
    return ap.unsqueeze(axis).broadcast_to(shape)


def start(nc, core, x, ident):
    with ExitStack() as ctx:
        x_in = [core.sem(f"st_x_in{b}") for b in range(2)]
        ident_in = core.sem("st_ident_in")
        const_done = core.sem("st_const_done")
        block = ctx.enter_context(nc.Block())

        @block.sync
        def _(sp):
            xt = x.rearrange("b (t p) d -> p (b t) d", p=P)
            for h in range(2):
                sp.dma_start(core.X[:, h * NT // 2:(h + 1) * NT // 2, :],
                             xt[:, h * NT // 2:(h + 1) * NT // 2, :]).then_inc(x_in[h], 16)
            sp.dma_start(core.ident[:], ident).then_inc(ident_in, 16)
            sp.wait_ge(ident_in, 16)

        @block.gpsimd
        def _(pool):
            nc.gpsimd.memset(core.ones[:], 1.0)
            nc.gpsimd.memset(core.eps[:], EPS_LN).then_inc(const_done, 1)
            pool.wait_ge(const_done, 1)
            pool.sem_inc(core.begun, 1)

        @block.vector
        def _(dve):
            for t in range(NT):
                if t % (NT // 2) == 0:
                    dve.wait_ge(x_in[t // (NT // 2)], 16)
                nc.vector.bn_stats(core.bn[:, t, :], core.X[:, t, :])


def row_scales(nc, core, tag):
    with ExitStack() as ctx:
        mv_done = core.sem(f"{tag}_mv_done")
        root_done = core.sem(f"{tag}_root_done")
        rstd_done = core.sem(f"{tag}_rstd_done")
        block = ctx.enter_context(nc.Block())

        @block.scalar
        def _(act):
            act.wait_ge(mv_done, 1)
            nc.scalar.activation(core.rstd[:], core.mv[:, :, 1], ACT.Sqrt,
                                 bias=core.eps[:]).then_inc(root_done, 1)

        @block.vector
        def _(dve):
            for t in range(NT):
                last = nc.vector.bn_aggr(core.mv[:, t, :], core.bn[:, t, :])
            last.then_inc(mv_done, 1)
            dve.wait_ge(root_done, 1)
            nc.vector.reciprocal(core.rstd[:], core.rstd[:]).then_inc(rstd_done, 1)
            dve.wait_ge(rstd_done, 1)
            nc.vector.scalar_tensor_tensor(core.shift[:], core.mv[:, :, 0], -1.0, core.rstd[:],
                                           ALU.mult, ALU.mult)


class Butterfly:

    def __init__(self, nc, core, sources):
        self.sources = sources
        self.up = core.sbuf("bf_up", [P, 3, HID])
        self.down = core.sbuf("bf_down", [P, HID // P, D])
        self.bias_h = core.sbuf("bf_bias_h", [P, HID // P])
        self.bias_y = core.sbuf("bf_bias_y", [P, D])
        self.loaded = core.sem("bf_loaded")
        self.stage_in = [core.sem(f"bf_stage_in{i}") for i in range(2)]
        self.stage_used = core.sem("bf_stage_used")
        self.zeroed = core.sem("bf_zeroed")
        self.step = core.sem("bf_step")

    def allocate_folding(self, core, ctx):
        self.down_t = core.sbuf("bf_down_t", [P, KD, HID], ctx)

    def allocate(self, core, ctx):
        self.w = core.sbuf("bf_w", [P, 2, 4, HID // 2], ctx)
        self.t = core.sbuf("bf_t", [P, 4, 3, HID // 2], ctx)

    def load(self, sp):
        w_exp, b_exp, w_con_t, up_w, down_w = self.sources
        sp.dma_start(self.up[:, 0:KD, :], w_exp.rearrange("(k p) h -> p k h", p=P)).then_inc(self.loaded, 16)
        sp.dma_start(self.down_t[:], w_con_t.rearrange("(k p) h -> p k h", p=P)).then_inc(self.loaded, 16)
        sp.wait_ge(self.zeroed, 1)
        sp.dma_start(self.up[0:1, KD, :], b_exp.unsqueeze(0)).then_inc(self.loaded, 16)
        for n in range(2 * NSTAGE):
            if n >= 2:
                sp.wait_ge(self.stage_used, n - 1)
            src = (up_w if n < NSTAGE else down_w)[n % NSTAGE]
            sp.dma_start(self.w[:, n % 2], src.unsqueeze(0).broadcast_to([P, 4, HID // 2])).then_inc(
                self.stage_in[n % 2], 16)

    def work(self, nc, eng):
        e = nc.gpsimd
        e.memset(self.up[:, KD, :], 0.0).then_inc(self.zeroed, 1)
        eng.wait_ge(self.loaded, 48)
        n_step = 0
        for n in range(2 * NSTAGE):
            up = n < NSTAGE
            y, rows = (self.up, 3) if up else (self.down_t, KD)
            s = 1 << (n if up else 2 * NSTAGE - 1 - n)
            nb = HID // (2 * s)
            eng.wait_ge(self.stage_in[n % 2], 16 * (n // 2 + 1))
            for r in range(rows):
                v = y[:, r, :].rearrange("p (n two s) -> p n two s", two=2, s=s)
                for i in range(4):
                    w = self.w[:, n % 2, i, :].rearrange("p (n s) -> p n s", s=s)
                    t = self.t[:, i, r, :].rearrange("p (n s) -> p n s", s=s)
                    e.tensor_tensor(t, v[:, :, i % 2, :], w, ALU.mult).then_inc(self.step, 1)
                    n_step += 1
            eng.wait_ge(self.step, n_step)
            for r in range(rows):
                v = y[:, r, :].rearrange("p (n two s) -> p n two s", two=2, s=s)
                for o in range(2):
                    t0 = self.t[:, 2 * o, r, :].rearrange("p (n s) -> p n s", s=s)
                    t1 = self.t[:, 2 * o + 1, r, :].rearrange("p (n s) -> p n s", s=s)
                    last = e.tensor_tensor(v[:, :, o, :], t0, t1, ALU.add).then_inc(self.step, 1)
                    n_step += 1
            eng.wait_ge(self.step, n_step)
            eng.sem_inc(self.stage_used, 1)


def ffn_prepare(nc, core, bf, up_bias, b_con, down_bias):
    with ExitStack() as ctx:
        bias_in = core.sbuf("fp_bias_in", [P, 2, D], ctx)
        psT = [core.psum(f"fp_psT{i}", [P, 512], ctx) for i in range(2)]
        psB = core.psum("fp_psB", [P, 512], ctx)
        loaded = core.sem("fp_loaded")
        ub_in = core.sem("fp_ub_in")
        tr_done = core.sem("fp_tr_done")
        ev_done = core.sem("fp_ev_done")
        row_done = core.sem("fp_row_done")
        block = ctx.enter_context(nc.Block())
        NH = HID // P

        @block.sync
        def _(sp):
            sp.dma_start(bf.bias_h[:], up_bias).then_inc(ub_in, 16)
            sp.dma_start(bias_in[:, 0, :], b_con.unsqueeze(0).broadcast_to([P, D])).then_inc(loaded, 16)
            sp.dma_start(bias_in[:, 1, :], down_bias.unsqueeze(0).broadcast_to([P, D])).then_inc(loaded, 16)

        @block.tensor
        def _(pe):
            for g in range(NH // 2):
                if g >= 2:
                    pe.wait_ge(ev_done, g - 1)
                for m in range(2):
                    for k in range(KD):
                        last = nc.tensor.transpose(
                            psT[g % 2][:, (m * KD + k) * P:(m * KD + k + 1) * P],
                            bf.down_t[:, k, (2 * g + m) * P:(2 * g + m + 1) * P], core.ident[:])
                last.then_inc(tr_done, 1)
            for m in range(NH):
                last = nc.tensor.matmul(psB[:, m:m + 1], bf.up[0:1, KD, m * P:(m + 1) * P],
                                        core.ones[0:1, 0:1], start=True, stop=True)
            last.then_inc(row_done, 1)

        @block.vector
        def _(dve):
            for g in range(NH // 2):
                dve.wait_ge(tr_done, g + 1)
                nc.vector.tensor_copy(bf.down[:, 2 * g:2 * g + 2, :],
                                      psT[g % 2][:].rearrange("p (m d) -> p m d", m=2)).then_inc(ev_done, 1)
            dve.wait_ge(row_done, 1)
            dve.wait_ge(ub_in, 16)
            nc.vector.tensor_tensor(bf.bias_h[:], bf.bias_h[:], psB[:, 0:NH], ALU.add)
            dve.wait_ge(loaded, 32)
            nc.vector.tensor_tensor(bf.bias_y[:], bias_in[:, 0, :], bias_in[:, 1, :], ALU.add)


def ffn_stage(nc, core, bf, tag):
    with ExitStack() as ctx:
        NH = HID // P
        xn = core.sbuf(f"{tag}_xn", [P, TPB, D], ctx)
        xnT = core.sbuf(f"{tag}_xnT", [P, 2, KD, S], ctx)
        h = core.sbuf(f"{tag}_h", [P, 2, NH, S], ctx)
        psT = [core.psum(f"{tag}_psT{i}", [P, 512], ctx) for i in range(2)]
        psH = [core.psum(f"{tag}_psH{i}", [P, 512], ctx) for i in range(2)]
        psY = [core.psum(f"{tag}_psY{i}", [P, 512], ctx) for i in range(2)]
        xn_done = core.sem(f"{tag}_xn_done")
        xb_done = core.sem(f"{tag}_xb_done")
        tr_done = core.sem(f"{tag}_tr_done")
        xnT_done = core.sem(f"{tag}_xnT_done")
        h_ps = core.sem(f"{tag}_h_ps")
        h_done = core.sem(f"{tag}_h_done")
        y_ps = core.sem(f"{tag}_y_ps")
        x_done = core.sem(f"{tag}_x_done")
        block = ctx.enter_context(nc.Block())

        @block.tensor
        def _(pe):
            with pe.Fori(0, B // 2) as b2:
                for u in range(2):
                    at = lambda per, c: b2 * (2 * per) + (u * per + c)
                    for k in range(KD):
                        pe.wait_ge(xnT_done, at(KD, 0))
                        for j in range(TPB):
                            if k == 0:
                                pe.wait_ge(xn_done, at(TPB, j + 1))
                            last = nc.tensor.transpose(psT[k][:, j * P:(j + 1) * P],
                                                       xn[:, j, k * P:(k + 1) * P], core.ident[:])
                        last.then_inc(tr_done, 1)
                    pe.wait_ge(xnT_done, at(KD, KD))
                    for m in range(NH):
                        if m >= 2:
                            pe.wait_ge(h_done, at(NH, m - 1))
                        for k in range(KD):
                            last = nc.tensor.matmul(psH[m % 2][:], bf.up[:, k, m * P:(m + 1) * P],
                                                    xnT[:, u, k, :], start=(k == 0), stop=(k == KD - 1))
                        last.then_inc(h_ps, 1)
                    pe.wait_ge(h_done, at(NH, NH))
                    for j in range(TPB):
                        pe.wait_ge(x_done, at(TPB, max(j - 1, 0)))
                        for m in range(NH):
                            last = nc.tensor.matmul(psY[j % 2][:, 0:D], h[:, u, m, j * P:(j + 1) * P],
                                                    bf.down[:, m, :], start=(m == 0), stop=(m == NH - 1))
                        last.then_inc(y_ps, 1)

        @block.scalar
        def _(act):
            with act.Fori(0, B // 2) as b2:
                for u in range(2):
                    at = lambda per, c: b2 * (2 * per) + (u * per + c)
                    act.wait_ge(tr_done, at(KD, 0))
                    core.apart(act)
                    for j in range(TPB):
                        t = at(TPB, j)
                        nc.scalar.activation(xn[:, j, :], core.X[:, t, :], ACT.Identity,
                                             bias=core.shift[:, bass.ds(t, 1)],
                                             scale=core.rstd[:, bass.ds(t, 1)]).then_inc(xn_done, 1)
                    for k in range(KD):
                        act.wait_ge(tr_done, at(KD, k + 1))
                        nc.scalar.activation(xnT[:, u, k, :], psT[k][:], ACT.Identity).then_inc(xnT_done, 1)
                    for m in range(NH):
                        act.wait_ge(h_ps, at(NH, m + 1))
                        nc.scalar.activation(h[:, u, m, :], psH[m % 2][:], ACT.Gelu,
                                             bias=bf.bias_h[:, m:m + 1]).then_inc(h_done, 1)

        @block.vector
        def _(dve):
            with dve.Fori(0, B // 2) as b2:
                for u in range(2):
                    for j in range(TPB):
                        at = lambda per, c: b2 * (2 * per) + (u * per + c)
                        t = at(TPB, j)
                        dve.wait_ge(xn_done, at(TPB, j + 1))
                        nc.vector.tensor_tensor(core.X[:, t, :], core.X[:, t, :], bf.bias_y[:], ALU.add).then_inc(xb_done, 1)
                        dve.wait_ge(y_ps, at(TPB, j + 1))
                        dve.wait_ge(xb_done, at(TPB, j + 1))
                        nc.vector.tensor_tensor(core.X[:, t, :], psY[j % 2][:, 0:D], core.X[:, t, :],
                                                ALU.add).then_inc(x_done, 1)
                        dve.wait_ge(x_done, at(TPB, j + 1))
                        core.apart(dve)
                        nc.vector.bn_stats(core.bn[:, t, :], core.X[:, t, :])


def finish(nc, core, out):
    with ExitStack() as ctx:
        stored = core.sem("fin_stored")
        block = ctx.enter_context(nc.Block())

        @block.sync
        def _(sp):
            ot = out.rearrange("b (t p) d -> p (b t) d", p=P)
            sp.dma_start(ot[:, 0:NT // 2, :], core.X[:, 0:NT // 2, :]).then_inc(stored, 16)
            sp.dma_start(ot[:, NT // 2:, :], core.X[:, NT // 2:, :]).then_inc(stored, 16)
            sp.wait_ge(stored, 32)
E_LORA, R_LORA = 8, 16


def at_batch(b2, u):
    return lambda per, c: b2 * (2 * per) + (u * per + c)


class MixtureWeights:

    def __init__(self, nc, core):
        ER = E_LORA * R_LORA
        self.tg = core.sbuf("mx_tg", [P, KD, ER + E_LORA])
        self.base = core.sbuf("mx_base", [P, KD, D])
        self.v = core.sbuf("mx_v", [P, D])
        self.loaded = core.sem("mx_loaded")

    def load(self, sp, weight_t, gate_t, u_t, v):
        ER = E_LORA * R_LORA
        sp.dma_start(self.tg[:, :, 0:ER], u_t.rearrange("(k p) n -> p k n", p=P)).then_inc(self.loaded, 16)
        sp.dma_start(self.tg[:, :, ER:], gate_t.rearrange("(k p) n -> p k n", p=P)).then_inc(self.loaded, 16)
        sp.dma_start(self.base[:], weight_t.rearrange("(k p) n -> p k n", p=P)).then_inc(self.loaded, 16)
        sp.dma_start(self.v[:], v).then_inc(self.loaded, 16)


def mixture_stage(nc, core, mx, tag):
    with ExitStack() as ctx:
        ER = E_LORA * R_LORA
        G = E_LORA
        xn = core.sbuf(f"{tag}_xn", [P, TPB, D], ctx)
        xnT = core.sbuf(f"{tag}_xnT", [P, 2, KD, S], ctx)
        gate = core.sbuf(f"{tag}_gate", [P, TPB, G], ctx)
        gmax = core.sbuf(f"{tag}_gmax", [P, TPB], ctx)
        gsum = core.sbuf(f"{tag}_gsum", [P, TPB], ctx)
        tg = core.sbuf(f"{tag}_tg", [P, TPB, ER], ctx)
        tgT = core.sbuf(f"{tag}_tgT", [P, TPB * P], ctx)
        psT = [core.psum(f"{tag}_psT{i}", [P, 512], ctx) for i in range(2)]
        psG = core.psum(f"{tag}_psG", [P, 2, 512], ctx)
        psB = core.psum(f"{tag}_psB", [P, TPB, 512], ctx)
        xn_done = core.sem(f"{tag}_xn_done")
        tr_done = core.sem(f"{tag}_tr_done")
        xnT_done = core.sem(f"{tag}_xnT_done")
        tg_ps = core.sem(f"{tag}_tg_ps")
        shifted = core.sem(f"{tag}_shifted")
        exp_done = core.sem(f"{tag}_exp_done")
        gate_step = core.sem(f"{tag}_gate_step")
        tg_done = core.sem(f"{tag}_tg_done")
        tgT_ps = core.sem(f"{tag}_tgT_ps")
        tgT_done = core.sem(f"{tag}_tgT_done")
        y_ps = core.sem(f"{tag}_y_ps")
        x_done = core.sem(f"{tag}_x_done")
        pair = [psG[:, g, 0:2 * (ER + G)].rearrange("p (t n) -> p t n", t=2) for g in range(2)]
        block = ctx.enter_context(nc.Block())

        @block.scalar
        def _(act):
            with act.Fori(0, B // 2) as b2:
                for u in range(2):
                    at = at_batch(b2, u)
                    act.wait_ge(tr_done, at(KD, 0))
                    core.apart(act)
                    for j in range(TPB):
                        t = at(TPB, j)
                        nc.scalar.activation(xn[:, j, :], core.X[:, t, :], ACT.Identity,
                                             bias=core.shift[:, bass.ds(t, 1)],
                                             scale=core.rstd[:, bass.ds(t, 1)]).then_inc(xn_done, 1)
                    for k in range(KD):
                        act.wait_ge(tr_done, at(KD, k + 1))
                        nc.scalar.activation(xnT[:, u, k, :], psT[k][:], ACT.Identity).then_inc(xnT_done, 1)
                    act.wait_ge(shifted, at(1, 1))
                    nc.scalar.activation(gate[:], gate[:], ACT.Exp).then_inc(exp_done, 1)
                    act.wait_ge(tgT_ps, at(1, 1))
                    nc.scalar.activation(tgT[:], psT[0][:], ACT.Identity).then_inc(tgT_done, 1)

        @block.tensor
        def _(pe):
            pe.wait_ge(mx.loaded, 64)
            with pe.Fori(0, B // 2) as b2:
                for u in range(2):
                    at = at_batch(b2, u)
                    pe.wait_ge(tgT_done, at(1, 0))
                    for k in range(KD):
                        for j in range(TPB):
                            if k == 0:
                                pe.wait_ge(xn_done, at(TPB, j + 1))
                            last = nc.tensor.transpose(psT[k][:, j * P:(j + 1) * P],
                                                       xn[:, j, k * P:(k + 1) * P], core.ident[:])
                        last.then_inc(tr_done, 1)
                    pe.wait_ge(xnT_done, at(KD, KD))
                    pe.wait_ge(tg_done, at(2, 0))
                    for j in range(TPB):
                        for k in range(KD):
                            last = nc.tensor.matmul(pair[j // 2][:, j % 2, :], xnT[:, u, k, j * P:(j + 1) * P],
                                                    mx.tg[:, k, :], start=(k == 0), stop=(k == KD - 1))
                    last.then_inc(tg_ps, 1)
                    for j in range(TPB):
                        pe.wait_ge(x_done, at(TPB, 0))
                        for k in range(KD):
                            nc.tensor.matmul(psB[:, j, 0:D], xnT[:, u, k, j * P:(j + 1) * P],
                                             mx.base[:, k, :], start=(k == 0), stop=False)
                    for j in range(TPB):
                        pe.wait_ge(tg_done, at(2, j // 2 + 1))
                        last = nc.tensor.transpose(psT[0][:, j * P:(j + 1) * P], tg[:, j, :], core.ident[:])
                    last.then_inc(tgT_ps, 1)
                    pe.wait_ge(tgT_done, at(1, 1))
                    for j in range(TPB):
                        nc.tensor.matmul(psB[:, j, 0:D], tgT[:, j * P:(j + 1) * P], mx.v[:],
                                         start=False, stop=True).then_inc(y_ps, 1)

        @block.vector
        def _(dve):
            with dve.Fori(0, B // 2) as b2:
                for u in range(2):
                    at = at_batch(b2, u)
                    dve.wait_ge(tg_ps, at(1, 1))
                    for g in range(2):
                        nc.vector.tensor_reduce(gmax[:, 2 * g:2 * g + 2], pair[g][:, :, ER:], AX.X,
                                                ALU.max).then_inc(gate_step, 1)
                    for g in range(2):
                        dve.wait_ge(gate_step, at(6, g + 1))
                        last = nc.vector.tensor_tensor(gate[:, 2 * g:2 * g + 2, :], pair[g][:, :, ER:],
                                                       spread(gmax[:, 2 * g:2 * g + 2], [P, 2, G], 2), ALU.subtract)
                    last.then_inc(shifted, 1)
                    dve.wait_ge(exp_done, at(1, 1))
                    nc.vector.tensor_reduce(gsum[:], gate[:], AX.X, ALU.add).then_inc(gate_step, 1)
                    dve.wait_ge(gate_step, at(6, 3))
                    nc.vector.reciprocal(gsum[:], gsum[:]).then_inc(gate_step, 1)
                    dve.wait_ge(gate_step, at(6, 4))
                    nc.vector.scalar_tensor_tensor(gate[:], gate[:], 1.0 / R_LORA,
                                                   spread(gsum[:], [P, TPB, G], 2),
                                                   ALU.mult, ALU.mult).then_inc(gate_step, 2)
                    dve.wait_ge(gate_step, at(6, 6))
                    for j in range(TPB):
                        last = nc.vector.tensor_tensor(
                            tg[:, j, :].rearrange("p (e r) -> p e r", e=G),
                            pair[j // 2][:, j % 2, 0:ER].rearrange("p (e r) -> p e r", e=G),
                            spread(gate[:, j, :], [P, G, R_LORA], 2), ALU.mult)
                        if j % 2:
                            last.then_inc(tg_done, 1)
                    for j in range(TPB):
                        t = at(TPB, j)
                        dve.wait_ge(y_ps, at(TPB, j + 1))
                        nc.vector.tensor_tensor(core.X[:, t, :], psB[:, j, 0:D], core.X[:, t, :],
                                                ALU.add).then_inc(x_done, 1)
                        dve.wait_ge(x_done, at(TPB, j + 1))
                        core.apart(dve)
                        nc.vector.bn_stats(core.bn[:, t, :], core.X[:, t, :])
NMODE = 32
CPT = P // NMODE
NMT = D // CPT
NF = S // P
ROUND = 1.5 * 2.0 ** 23
PI = 3.141592653589793


class LongConv:

    def __init__(self, nc, core, ctx):
        self.fwd = core.sbuf("lc_fwd", [P, TPB, 2 * S], ctx)
        self.inv = core.sbuf("lc_inv", [P, 2 * NF, S], ctx)
        self.w = core.sbuf("lc_w", [P, KD, D], ctx)
        self.b = core.sbuf("lc_b", [P, D], ctx)
        self.k_re = core.sbuf("lc_k_re", [P, NF, D], ctx)
        self.k_im = core.sbuf("lc_k_im", [P, NF, D], ctx)
        self.k_re2 = core.sbuf("lc_k_re2", [P, NF, D], ctx)
        self.loaded = core.sem("lc_loaded")

    def load(self, sp, fwd, inv, w_t, b):
        sp.dma_start(self.fwd[:], fwd.rearrange("(k p) n -> p k n", p=P)).then_inc(self.loaded, 16)
        sp.dma_start(self.inv[:], inv.rearrange("(k p) n -> p k n", p=P)).then_inc(self.loaded, 16)
        sp.dma_start(self.w[:], w_t.rearrange("(k p) n -> p k n", p=P)).then_inc(self.loaded, 16)
        sp.dma_start(self.b[:], b.unsqueeze(0).broadcast_to([P, D])).then_inc(self.loaded, 16)


def conv_kernel(nc, core, lc, modes, index, conv_in):
    with ExitStack() as ctx:
        GRP = 16
        NG = NMT // GRP
        par = core.sbuf("ck_par", [P, 5, NMT], ctx)
        idx = core.sbuf("ck_idx", [P, P + TPB], ctx)
        chan = core.sbuf("ck_chan", [P, CPT], ctx)
        v = core.sbuf("ck_v", [P, 16, NMT], ctx)
        f_ph = core.sbuf("ck_f_ph", [P, 4, NMT * TPB], ctx)
        f_re = core.sbuf("ck_f_re", [P, NMT, TPB], ctx)
        f_im = core.sbuf("ck_f_im", [P, NMT, TPB], ctx)
        fm = core.sbuf("ck_fm", [P, 2, NMT, TPB * CPT], ctx)
        ph = core.sbuf("ck_ph", [P, GRP, P], ctx)
        rnd = core.sbuf("ck_rnd", [P, GRP, P], ctx)
        mag = core.sbuf("ck_mag", [P, GRP, P], ctx)
        g_re = core.sbuf("ck_g_re", [P, GRP, P], ctx)
        g_im = core.sbuf("ck_g_im", [P, GRP, P], ctx)
        kT = core.sbuf("ck_kT", [P, TPB, D], ctx)
        half_pi = core.sbuf("ck_half_pi", [P, 1], ctx)
        psK = core.psum("ck_psK", [P, 2, 512], ctx)
        psF = core.psum("ck_psF", [P, 2, 512], ctx)
        loaded = core.sem("ck_loaded")
        vec = core.sem("ck_vec")
        act_n = core.sem("ck_act")
        pe_g = core.sem("ck_pe_g")
        kT_done = core.sem("ck_kT_done")
        f_ps = core.sem("ck_f_ps")
        f_out = core.sem("ck_f_out")
        block = ctx.enter_context(nc.Block())
        LDT, LAR, AIM, CRE, CIM = range(5)
        (DT, AR, DR, DI, MAG, SIN, COS, TURN, RN, FR, ABS, T0, T1, NRE, NIM, DEN) = range(16)

        @block.sync
        def _(sp):
            sp.dma_start(par[:], modes.rearrange("a p t -> p a t")).then_inc(loaded, 16)
            sp.dma_start(idx[:], index.unsqueeze(0).broadcast_to([P, P + TPB])).then_inc(loaded, 16)
            sp.dma_start(chan[:], conv_in).then_inc(loaded, 16)


        @block.vector
        def _(dve):
            n = [0]

            def step(ins):
                n[0] += 1
                ins.then_inc(vec, 1)
                dve.wait_ge(vec, n[0])

            tt = nc.vector.tensor_tensor
            step(nc.vector.memset(half_pi[:], PI / 2))
            dve.wait_ge(loaded, 48)
            dve.wait_ge(act_n, 2)
            step(nc.vector.scalar_tensor_tensor(v[:, DR, :], v[:, AR, :], -1.0, v[:, DT, :], ALU.mult, ALU.mult))
            step(tt(v[:, DI, :], par[:, AIM, :], v[:, DT, :], ALU.mult))
            step(nc.vector.tensor_scalar(v[:, TURN, :], v[:, DI, :], 1 / (2 * PI), None, ALU.mult))
            step(nc.vector.tensor_scalar(v[:, RN, :], v[:, TURN, :], ROUND, -ROUND, ALU.add, ALU.add))
            step(tt(v[:, FR, :], v[:, TURN, :], v[:, RN, :], ALU.subtract))
            dve.wait_ge(act_n, 6)
            step(tt(v[:, T0, :], v[:, MAG, :], v[:, COS, :], ALU.mult))
            step(nc.vector.tensor_scalar(v[:, T0, :], v[:, T0, :], -1.0, None, ALU.add))
            step(tt(v[:, T1, :], v[:, MAG, :], v[:, SIN, :], ALU.mult))

            def cmul(o_re, o_im, a_re, a_im, b_re, b_im, s0, s1):
                step(tt(s0, a_re, b_re, ALU.mult))
                step(tt(s1, a_im, b_im, ALU.mult))
                step(tt(o_re, s0, s1, ALU.subtract))
                step(tt(s0, a_re, b_im, ALU.mult))
                step(tt(s1, a_im, b_re, ALU.mult))
                step(tt(o_im, s0, s1, ALU.add))

            cmul(v[:, NRE, :], v[:, NIM, :], par[:, CRE, :], par[:, CIM, :], v[:, T0, :], v[:, T1, :],
                 v[:, RN, :], v[:, FR, :])
            step(nc.vector.tensor_scalar(v[:, AR, :], v[:, AR, :], -1.0, None, ALU.mult))
            step(nc.vector.tensor_scalar(v[:, ABS, :], par[:, AIM, :], -1.0, None, ALU.mult))
            step(tt(v[:, T0, :], v[:, AR, :], v[:, AR, :], ALU.mult))
            step(tt(v[:, T1, :], par[:, AIM, :], par[:, AIM, :], ALU.mult))
            step(tt(v[:, DEN, :], v[:, T0, :], v[:, T1, :], ALU.add))
            step(nc.vector.reciprocal(v[:, DEN, :], v[:, DEN, :]))
            cmul(v[:, T0, :], v[:, T1, :], v[:, NRE, :], v[:, NIM, :], v[:, AR, :], v[:, ABS, :],
                 v[:, RN, :], v[:, FR, :])
            for o, i in ((NRE, T0), (NIM, T1)):
                step(nc.vector.scalar_tensor_tensor(v[:, o, :], v[:, i, :], 2.0, v[:, DEN, :], ALU.mult, ALU.mult))
            f3 = [f_ph[:, q, :].rearrange("p (t i) -> p t i", i=TPB) for q in range(4)]
            ix = spread(idx[:, P:], [P, NMT, TPB], 1)
            step(tt(f3[0], spread(v[:, TURN, :], [P, NMT, TPB], 2), ix, ALU.mult))
            step(nc.vector.tensor_scalar(f_ph[:, 1, :], f_ph[:, 0, :], ROUND, -ROUND, ALU.add, ALU.add))
            step(tt(f_ph[:, 0, :], f_ph[:, 0, :], f_ph[:, 1, :], ALU.subtract))
            step(tt(f3[1], spread(v[:, DR, :], [P, NMT, TPB], 2), ix, ALU.mult))
            assert n[0] == 33, n
            dve.wait_ge(act_n, 10)
            step(tt(f_ph[:, 2, :], f_ph[:, 2, :], f_ph[:, 1, :], ALU.mult))
            step(tt(f_ph[:, 3, :], f_ph[:, 3, :], f_ph[:, 1, :], ALU.mult))
            s0 = ph[:, 0:2, :].rearrange("p a (t i) -> p (a t) i", i=TPB)
            s1 = rnd[:, 0:2, :].rearrange("p a (t i) -> p (a t) i", i=TPB)
            cmul(f_re[:], f_im[:], spread(v[:, NRE, :], [P, NMT, TPB], 2), spread(v[:, NIM, :], [P, NMT, TPB], 2),
                 f3[3], f3[2], s0, s1)
            step(nc.vector.tensor_scalar(f_im[:], f_im[:], -1.0, None, ALU.mult))
            for c in range(CPT):
                for q, f in ((0, f_re), (1, f_im)):
                    dst = fm[:, q].rearrange("p t (i c) -> p t i c", c=CPT)[:, :, :, c]
                    step(nc.vector.tensor_scalar(dst, f[:], chan[:, c:c + 1], None, ALU.mult))
            assert n[0] == 50, n
            jx = spread(idx[:, 0:P], [P, GRP, P], 1)
            for g in range(NG):
                t = slice(g * GRP, (g + 1) * GRP)
                step(tt(ph[:], spread(v[:, TURN, t], [P, GRP, P], 2), jx, ALU.mult))
                step(nc.vector.tensor_scalar(rnd[:], ph[:], ROUND, -ROUND, ALU.add, ALU.add))
                step(tt(ph[:], ph[:], rnd[:], ALU.subtract))
                step(tt(mag[:], spread(v[:, DR, t], [P, GRP, P], 2), jx, ALU.mult))
                if g:
                    dve.wait_ge(pe_g, g)
                dve.wait_ge(act_n, 10 + 4 * (g + 1))
                step(tt(g_im[:], g_im[:], mag[:], ALU.mult))
                step(tt(g_re[:], g_re[:], mag[:], ALU.mult))
            dve.wait_ge(pe_g, NG)
            for h in range(2):
                t = NMT // 2
                dst = kT[:, :, h * D // 2:(h + 1) * D // 2].rearrange("p i (t c) -> p i t c", c=CPT)
                src = psK[:, h, :].rearrange("p (t i c) -> p i t c", i=TPB, c=CPT)
                for i in range(TPB):
                    last = nc.vector.tensor_copy(dst[:, i], src[:, i])
            last.then_inc(kT_done, 1)
            for m in range(2 * NF):
                dst = (lc.k_re if m < NF else lc.k_im)[:, m % NF, :]
                dve.wait_ge(f_ps, m + 1)
                nc.vector.tensor_copy(dst, psF[:, m % 2, 0:D]).then_inc(f_out, 1)
            dve.wait_ge(f_out, 2 * NF)
            step(nc.vector.tensor_copy(lc.k_re2[:], lc.k_re[:]))
            step(nc.vector.tensor_copy(lc.k_re2[0:1, 0, :], lc.k_im[0:1, 0, :]))
            step(nc.vector.memset(lc.k_im[0:1, 0, :], 0.0))

        @block.scalar
        def _(act):
            a = nc.scalar.activation
            act.wait_ge(loaded, 48)
            a(v[:, DT, :], par[:, LDT, :], ACT.Exp).then_inc(act_n, 1)
            a(v[:, AR, :], par[:, LAR, :], ACT.Exp).then_inc(act_n, 1)
            act.wait_ge(vec, 6)
            a(v[:, MAG, :], v[:, DR, :], ACT.Exp).then_inc(act_n, 1)
            a(v[:, SIN, :], v[:, FR, :], ACT.Sin, scale=2 * PI).then_inc(act_n, 1)
            a(v[:, ABS, :], v[:, FR, :], ACT.Abs).then_inc(act_n, 1)
            act.wait_ge(act_n, 5)
            a(v[:, COS, :], v[:, ABS, :], ACT.Sin, scale=-2 * PI, bias=half_pi[:]).then_inc(act_n, 1)
            act.wait_ge(vec, 33)
            a(f_ph[:, 2, :], f_ph[:, 0, :], ACT.Sin, scale=2 * PI).then_inc(act_n, 1)
            a(f_ph[:, 3, :], f_ph[:, 0, :], ACT.Abs).then_inc(act_n, 1)
            act.wait_ge(act_n, 8)
            a(f_ph[:, 3, :], f_ph[:, 3, :], ACT.Sin, scale=-2 * PI, bias=half_pi[:]).then_inc(act_n, 1)
            a(f_ph[:, 1, :], f_ph[:, 1, :], ACT.Exp).then_inc(act_n, 1)
            for g in range(NG):
                act.wait_ge(vec, 50 + 6 * g + 4)
                if g:
                    act.wait_ge(pe_g, g)
                n = 10 + 4 * g
                a(g_im[:], ph[:], ACT.Sin, scale=2 * PI).then_inc(act_n, 1)
                a(g_re[:], ph[:], ACT.Abs).then_inc(act_n, 1)
                act.wait_ge(act_n, n + 2)
                a(g_re[:], g_re[:], ACT.Sin, scale=-2 * PI, bias=half_pi[:]).then_inc(act_n, 1)
                a(mag[:], mag[:], ACT.Exp).then_inc(act_n, 1)

        @block.tensor
        def _(pe):
            for g in range(NG):
                pe.wait_ge(vec, 50 + 6 * (g + 1))
                for t in range(GRP):
                    tt_ = g * GRP + t
                    h, o = tt_ // (NMT // 2), (tt_ % (NMT // 2)) * TPB * CPT
                    for q, gg in ((0, g_re), (1, g_im)):
                        last = nc.tensor.matmul(psK[:, h, o:o + TPB * CPT], gg[:, t, :], fm[:, q, tt_, :],
                                                start=(q == 0), stop=(q == 1))
                last.then_inc(pe_g, 1)
            pe.wait_ge(lc.loaded, 64)
            pe.wait_ge(kT_done, 1)
            for m in range(2 * NF):
                if m >= 2:
                    pe.wait_ge(f_out, m - 1)
                for k in range(TPB):
                    last = nc.tensor.matmul(psF[:, m % 2, 0:D], lc.fwd[:, k, m * P:(m + 1) * P], kT[:, k, :],
                                            start=(k == 0), stop=(k == TPB - 1))
                last.then_inc(f_ps, 1)


def conv_stage(nc, core, lc, tag):
    with ExitStack() as ctx:
        xn = core.sbuf(f"{tag}_xn", [P, TPB, 2, D], ctx)
        y = core.sbuf(f"{tag}_y", [P, 2 * NF, 2 * D], ctx)
        prod = core.sbuf(f"{tag}_prod", [P, 2, 4, 2 * D], ctx)
        g = core.sbuf(f"{tag}_g", [P, 2, 2 * D], ctx)
        gT = core.sbuf(f"{tag}_gT", [P, 2, 2 * KD, P], ctx)
        psF = core.psum(f"{tag}_psF", [P, 2, 2, 512], ctx)
        psY = core.psum(f"{tag}_psY", [P, 2, 512], ctx)
        psT = core.psum(f"{tag}_psT", [P, 512], ctx)
        psO = core.psum(f"{tag}_psO", [P, 512], ctx)
        xn_done = core.sem(f"{tag}_xn_done")
        f_ps = core.sem(f"{tag}_f_ps")
        prod_done = core.sem(f"{tag}_prod_done")
        y_done = core.sem(f"{tag}_y_done")
        c_ps = core.sem(f"{tag}_c_ps")
        g_done = core.sem(f"{tag}_g_done")
        gT_ps = core.sem(f"{tag}_gT_ps")
        gT_done = core.sem(f"{tag}_gT_done")
        o_ps = core.sem(f"{tag}_o_ps")
        xb_done = core.sem(f"{tag}_xb_done")
        x_done = core.sem(f"{tag}_x_done")
        block = ctx.enter_context(nc.Block())

        @block.scalar
        def _(act):
            with act.Fori(0, B // 2) as i:
                act.wait_ge(f_ps, i * NF)
                core.apart(act)
                for k in range(TPB):
                    for b in range(2):
                        t = i * (2 * TPB) + (b * TPB + k)
                        nc.scalar.activation(xn[:, k, b, :], core.X[:, t, :], ACT.Identity,
                                             bias=core.shift[:, bass.ds(t, 1)],
                                             scale=core.rstd[:, bass.ds(t, 1)]).then_inc(xn_done, 1)
                for l in range(TPB):
                    act.wait_ge(c_ps, i * TPB + (l + 1))
                    act.wait_ge(gT_ps, i * TPB + max(l - 1, 0))
                    nc.scalar.activation(g[:, l % 2, :], psY[:, l % 2, :], ACT.Gelu).then_inc(g_done, 1)
                    act.wait_ge(gT_ps, i * TPB + (l + 1))
                    nc.scalar.activation(gT[:, l % 2], psT[:].rearrange("p (a q) -> p a q", q=P),
                                         ACT.Identity).then_inc(gT_done, 1)

        @block.tensor
        def _(pe):
            with pe.Fori(0, B // 2) as i:
                for f in range(NF):
                    pe.wait_ge(prod_done, i * NF + max(f - 1, 0))
                    for c in range(2):
                        for k in range(TPB):
                            if f == 0 and c == 0:
                                pe.wait_ge(xn_done, i * (2 * TPB) + 2 * (k + 1))
                            m = c * NF + f
                            last = nc.tensor.matmul(psF[:, f % 2, c, :], lc.fwd[:, k, m * P:(m + 1) * P],
                                                    xn[:, k].rearrange("p b d -> p (b d)"),
                                                    start=(k == 0), stop=(k == TPB - 1))
                    last.then_inc(f_ps, 1)

                def project(l):
                    pe.wait_ge(g_done, i * TPB + (l + 1))
                    pe.wait_ge(gT_done, i * TPB + l)
                    for a in range(2 * KD):
                        last = nc.tensor.transpose(psT[:, a * P:(a + 1) * P], g[:, l % 2, a * P:(a + 1) * P],
                                                   core.ident[:])
                    last.then_inc(gT_ps, 1)
                    pe.wait_ge(gT_done, i * TPB + (l + 1))
                    pe.wait_ge(x_done, i * (2 * TPB) + 2 * l)
                    for b in range(2):
                        for k in range(KD):
                            last = nc.tensor.matmul(psO[:, b * D:(b + 1) * D], gT[:, l % 2, b * KD + k, :],
                                                    lc.w[:, k, :], start=(k == 0), stop=(k == KD - 1))
                    last.then_inc(o_ps, 1)

                for l in range(TPB):
                    pe.wait_ge(g_done, i * TPB + max(l - 1, 0))
                    for n, (f, c) in enumerate((f, c) for f in range(NF) for c in range(2)):
                        pe.wait_ge(y_done, i * NF + (f + 1))
                        last = nc.tensor.matmul(psY[:, l % 2, :], lc.inv[:, c * NF + f, l * P:(l + 1) * P],
                                                y[:, c * NF + f, :], start=(n == 0), stop=(n == 2 * NF - 1))
                    last.then_inc(c_ps, 1)
                    if l:
                        project(l - 1)
                project(TPB - 1)

        @block.gpsimd
        def _(pool):
            with pool.Fori(0, B // 2) as i:
                for f in range(NF):
                    pool.wait_ge(prod_done, i * NF + (f + 1))
                    if f == 0:
                        pool.wait_ge(c_ps, i * TPB)
                    p4 = prod[:, f % 2]
                    nc.gpsimd.tensor_tensor(y[:, f, :], p4[:, 0, :], p4[:, 1, :], ALU.subtract)
                    nc.gpsimd.tensor_tensor(y[:, NF + f, :], p4[:, 2, :], p4[:, 3, :], ALU.add).then_inc(y_done, 1)

        @block.vector
        def _(dve):
            with dve.Fori(0, B // 2) as i:
                for f in range(NF):
                    dve.wait_ge(y_done, i * NF + max(f - 1, 0))
                    dve.wait_ge(f_ps, i * NF + (f + 1))
                    for q, (c, kk) in enumerate(((0, lc.k_re), (1, lc.k_im), (0, lc.k_im), (1, lc.k_re2))):
                        last = nc.vector.tensor_tensor(
                            prod[:, f % 2, q, :].rearrange("p (b d) -> p b d", b=2),
                            psF[:, f % 2, c, :].rearrange("p (b d) -> p b d", b=2),
                            spread(kk[:, f, :], [P, 2, D], 1), ALU.mult)
                    last.then_inc(prod_done, 1)
                dve.wait_ge(xn_done, i * (2 * TPB) + 2 * TPB)
                for l in range(TPB):
                    for b in range(2):
                        t = i * (2 * TPB) + (b * TPB + l)
                        nc.vector.tensor_tensor(core.X[:, t, :], core.X[:, t, :], lc.b[:], ALU.add).then_inc(xb_done, 1)
                for l in range(TPB):
                    for b in range(2):
                        t = i * (2 * TPB) + (b * TPB + l)
                        n = 2 * l + b + 1
                        dve.wait_ge(xb_done, i * (2 * TPB) + n)
                        dve.wait_ge(o_ps, i * TPB + (l + 1))
                        nc.vector.tensor_tensor(core.X[:, t, :], psO[:, b * D:(b + 1) * D], core.X[:, t, :],
                                                ALU.add).then_inc(x_done, 1)
                        dve.wait_ge(x_done, i * (2 * TPB) + n)
                        core.apart(dve)
                        nc.vector.bn_stats(core.bn[:, t, :], core.X[:, t, :])


def conv_constants():
    import numpy as np

    l = np.arange(S)[:, None]
    f = np.arange(S)[None, :]
    turn = 2 * np.pi * ((l * f) % (2 * S)) / (2 * S)
    fwd = np.concatenate([np.cos(turn), -np.sin(turn)], 1)
    fwd[:, S] = (-1.0) ** np.arange(S)
    inv = fwd.T / S
    inv[0] /= 2
    inv[S] /= 2
    index = np.concatenate([np.arange(P), P * np.arange(TPB)])
    chan = np.arange(P)[:, None] // NMODE == np.arange(CPT)[None, :]
    return [np.ascontiguousarray(a.astype(np.float32)) for a in (fwd, inv, index, chan)]
NH = 16
HD = D // NH
PAD = 32
HPT = P // PAD
NG_H = NH // HPT


def distance_attention_stage(nc, core, tag, wq_p, wk_p, bq_p, bk_p, wv, bv, wo, bo, sel, sign):
    with ExitStack() as ctx:
        wqk = core.sbuf(f"{tag}_wqk", [P, 2, KD, NH * PAD], ctx)
        bqk = core.sbuf(f"{tag}_bqk", [P, 2, NG_H], ctx)
        wv_sb = core.sbuf(f"{tag}_wv", [P, KD, D], ctx)
        wo_sb = core.sbuf(f"{tag}_wo", [P, KD, D], ctx)
        bv_sb = core.sbuf(f"{tag}_bv", [P, D], ctx)
        bo_sb = core.sbuf(f"{tag}_bo", [P, D], ctx)
        sel_sb = core.sbuf(f"{tag}_sel", [P, 2, P], ctx)
        sign_sb = core.sbuf(f"{tag}_sign", [P, 2], ctx)
        xn = core.sbuf(f"{tag}_xn", [P, TPB, D], ctx)
        xnT = core.sbuf(f"{tag}_xnT", [P, KD, S], ctx)
        raw = core.sbuf(f"{tag}_raw", [P, 2, S], ctx)
        sq = core.sbuf(f"{tag}_sq", [P, 2, S], ctx)
        qk = core.sbuf(f"{tag}_qk", [P, 2, NG_H, S], ctx)
        va = core.sbuf(f"{tag}_va", [P, TPB, NH, PAD], ctx)
        dist = core.sbuf(f"{tag}_dist", [P, 2, HPT, TPB, S], ctx)
        fold = core.sbuf(f"{tag}_fold", [P, 2, S], ctx)
        least = core.sbuf(f"{tag}_least", [P, 2, S], ctx)
        mq = core.sbuf(f"{tag}_mq", [P, 2, HPT, TPB], ctx)
        mb = core.sbuf(f"{tag}_mb", [P, HPT, S], ctx)
        oT = core.sbuf(f"{tag}_oT", [P, NG_H, S], ctx)
        rec = core.sbuf(f"{tag}_rec", [P, NH], ctx)
        on = core.sbuf(f"{tag}_on", [P, D], ctx)
        onT = core.sbuf(f"{tag}_onT", [P, KD, P], ctx)
        psS = core.psum(f"{tag}_psS", [P, TPB, 512], ctx)
        psM = core.psum(f"{tag}_psM", [P, 512], ctx)
        psB = core.psum(f"{tag}_psB", [P, 512], ctx)
        psO = core.psum(f"{tag}_psO", [P, 512], ctx)
        psX = core.psum(f"{tag}_psX", [P, 512], ctx)
        sem = lambda n: core.sem(f"{tag}_{n}", ctx)
        loaded, va_set = sem("loaded"), sem("va_set")
        xn_done, tr_done, xnT_done = sem("xn_done"), sem("tr_done"), sem("xnT_done")
        pr_ps, raw_done, sum_ps, qk_done = sem("pr_ps"), sem("raw_done"), sem("sum_ps"), sem("qk_done")
        v_ps, v_done = sem("v_ps"), sem("v_done")
        s_ps, clamp_done, fold_done, least_done = sem("s_ps"), sem("clamp_done"), sem("fold_done"), sem("least_done")
        m_ps, mq_done, root_done, mroot_done = sem("m_ps"), sem("mq_done"), sem("root_done"), sem("mroot_done")
        b_ps, mb_done, sub_done, exp_done = sem("b_ps"), sem("mb_done"), sem("sub_done"), sem("exp_done")
        oT_done = sem("oT_done")
        q_ps, rec_done, on_done, onT_ps, onT_done = sem("q_ps"), sem("rec_done"), sem("on_done"), sem("onT_ps"), sem("onT_done")
        pv_n = sem("pv_n")
        y_ps, xb_done, x_done = sem("y_ps"), sem("xb_done"), sem("x_done")
        block = ctx.enter_context(nc.Block())
        NPR = 2 * NG_H

        @block.sync
        def _(sp):
            for n, w in enumerate((wq_p, wk_p)):
                sp.dma_start(wqk[:, n], w.rearrange("(k p) n -> p k n", p=P)).then_inc(loaded, 16)
            for n, b in enumerate((bq_p, bk_p)):
                sp.dma_start(bqk[:, n], b).then_inc(loaded, 16)
            sp.dma_start(wv_sb[:], wv.rearrange("(k p) n -> p k n", p=P)).then_inc(loaded, 16)
            sp.dma_start(wo_sb[:], wo.rearrange("(k p) n -> p k n", p=P)).then_inc(loaded, 16)
            sp.dma_start(bv_sb[:], bv.unsqueeze(0).broadcast_to([P, D])).then_inc(loaded, 16)
            sp.dma_start(bo_sb[:], bo.unsqueeze(0).broadcast_to([P, D])).then_inc(loaded, 16)
            sp.dma_start(sel_sb[:], sel).then_inc(loaded, 16)
            sp.dma_start(sign_sb[:], sign).then_inc(loaded, 16)

        @block.tensor
        def _(pe):
            pe.wait_ge(loaded, 160)
            with pe.Fori(0, B) as b:
                at = lambda per, c: b * per + c
                for k in range(KD):
                    bank = (psO, psX)[k]
                    pe.wait_ge(x_done, at(TPB, 0))
                    for j in range(TPB):
                        if k == 0:
                            pe.wait_ge(xn_done, at(TPB, j + 1))
                        last = nc.tensor.transpose(bank[:, j * P:(j + 1) * P], xn[:, j, k * P:(k + 1) * P],
                                                   core.ident[:])
                    last.then_inc(tr_done, 1)
                pe.wait_ge(xnT_done, at(KD, KD))
                for p in range(NPR + 1):
                    if p < NPR:
                        pe.wait_ge(raw_done, at(NPR, max(p - 1, 0)))
                        for k in range(KD):
                            last = nc.tensor.matmul(psS[:, p % 2, :],
                                                    wqk[:, p // NG_H, k, (p % NG_H) * P:(p % NG_H + 1) * P],
                                                    xnT[:, k, :], start=(k == 0), stop=(k == KD - 1))
                        last.then_inc(pr_ps, 1)
                    if p:
                        pe.wait_ge(raw_done, at(NPR, p))
                        pe.wait_ge(qk_done, at(NPR, max(p - 2, 0)))
                        nc.tensor.matmul(psS[:, 2 + (p - 1) % 2, :], sel_sb[:, (p - 1) // NG_H, :],
                                         sq[:, (p - 1) % 2, :], start=True, stop=True).then_inc(sum_ps, 1)
                pe.wait_ge(qk_done, at(NPR, NPR))
                for j in range(TPB):
                    for k in range(KD):
                        last = nc.tensor.matmul(psS[:, j, 0:D], xnT[:, k, j * P:(j + 1) * P], wv_sb[:, k, :],
                                                start=(k == 0), stop=(k == KD - 1))
                    last.then_inc(v_ps, 1)
                pe.wait_ge(v_done, at(TPB, TPB))

                def turn_least(h):
                    pe.wait_ge(least_done, at(NH, h + 1))
                    pe.wait_ge(mq_done, at(NH, h))
                    for q in range(TPB):
                        last = nc.tensor.transpose(psM[:, q * P:(q + 1) * P], least[:, h % 2, q * P:(q + 1) * P],
                                                   core.ident[:])
                    last.then_inc(m_ps, 1)

                for g in range(NG_H + 1):
                    if g < NG_H:
                        for i in range(HPT):
                            h = g * HPT + i
                            r = slice(i * PAD, (i + 1) * PAD)
                            for kb in range(TPB):
                                if h:
                                    pe.wait_ge(clamp_done, at(2 * NH, 2 * h - 1 + kb // 2))
                                last = nc.tensor.matmul(psS[:, kb, :], qk[r, 1, g, kb * P:(kb + 1) * P],
                                                        qk[r, 0, g, :], start=True, stop=True)
                                if kb % 2:
                                    last.then_inc(s_ps, 1)
                            if i:
                                turn_least(h - 1)
                        turn_least(g * HPT + HPT - 1)
                        pe.wait_ge(mroot_done, at(NG_H, g + 1))
                        for i in range(HPT):
                            h = g * HPT + i
                            pe.wait_ge(mb_done, at(NH, h))
                            for q in range(TPB):
                                last = nc.tensor.transpose(
                                    psB[:, q * P:(q + 1) * P],
                                    mq[:, g % 2, i, q:q + 1].broadcast_to([P, P]), core.ident[:])
                            last.then_inc(b_ps, 1)
                    if g:
                        pe.wait_ge(oT_done, at(NG_H, g - 1))
                        for i in range(HPT):
                            h = (g - 1) * HPT + i
                            pe.wait_ge(exp_done, at(NH, h + 1))
                            for kb in range(TPB):
                                last = nc.tensor.matmul(psO[i * PAD:(i + 1) * PAD, :], va[:, kb, h, :],
                                                        dist[:, (g - 1) % 2, i, kb, :],
                                                        start=(kb == 0), stop=(kb == TPB - 1))
                            last.then_inc(pv_n, 1)
                pe.wait_ge(oT_done, at(NG_H, NG_H))
                for j in range(TPB):
                    pe.wait_ge(on_done, at(TPB, j))
                    for g in range(NG_H):
                        last = nc.tensor.transpose(psM[:, g * P:(g + 1) * P], oT[:, g, j * P:(j + 1) * P],
                                                   core.ident[:])
                    last.then_inc(q_ps, 1)
                    pe.wait_ge(on_done, at(TPB, j + 1))
                    for k in range(KD):
                        last = nc.tensor.transpose(psB[:, k * P:(k + 1) * P], on[:, k * P:(k + 1) * P], core.ident[:])
                    last.then_inc(onT_ps, 1)
                    pe.wait_ge(onT_done, at(TPB, j + 1))
                    pe.wait_ge(x_done, at(TPB, j))
                    for k in range(KD):
                        last = nc.tensor.matmul(psX[:, 0:D], onT[:, k, :], wo_sb[:, k, :],
                                                start=(k == 0), stop=(k == KD - 1))
                    last.then_inc(y_ps, 1)

        @block.scalar
        def _(act):
            act.wait_ge(loaded, 160)
            with act.Fori(0, B) as b:
                at = lambda per, c: b * per + c
                act.wait_ge(tr_done, at(KD, 0))
                core.apart(act)
                for j in range(TPB):
                    t = at(TPB, j)
                    nc.scalar.activation(xn[:, j, :], core.X[:, t, :], ACT.Identity,
                                         bias=core.shift[:, bass.ds(t, 1)],
                                         scale=core.rstd[:, bass.ds(t, 1)]).then_inc(xn_done, 1)
                for k in range(KD):
                    act.wait_ge(tr_done, at(KD, k + 1))
                    nc.scalar.activation(xnT[:, k, :], (psO, psX)[k][:], ACT.Identity).then_inc(xnT_done, 1)
                for p in range(NPR):
                    act.wait_ge(pr_ps, at(NPR, p + 1))
                    act.wait_ge(qk_done, at(NPR, max(p - 1, 0)))
                    bias = bqk[:, p // NG_H, p % NG_H:p % NG_H + 1]
                    nc.scalar.activation(raw[:, p % 2, :], psS[:, p % 2, :], ACT.Identity, bias=bias)
                    nc.scalar.activation(sq[:, p % 2, :], psS[:, p % 2, :], ACT.Square, bias=bias).then_inc(raw_done, 1)
                for g in range(NG_H + 1):
                    if g < NG_H:
                        for i in range(HPT):
                            h = g * HPT + i
                            act.wait_ge(clamp_done, at(2 * NH, 2 * h + 2))
                            act.wait_ge(least_done, at(NH, h + 1))
                            nc.scalar.activation(dist[:, g % 2, i], dist[:, g % 2, i], ACT.Sqrt).then_inc(root_done, 1)
                        act.wait_ge(mq_done, at(NH, (g + 1) * HPT))
                        nc.scalar.activation(mq[:, g % 2], mq[:, g % 2], ACT.Sqrt).then_inc(mroot_done, 1)
                        for i in range(HPT):
                            h = g * HPT + i
                            act.wait_ge(b_ps, at(NH, h + 1))
                            act.wait_ge(sub_done, at(NH, g * HPT))
                            nc.scalar.activation(mb[:, i, :], psB[:], ACT.Identity).then_inc(mb_done, 1)
                    if g:
                        for i in range(HPT):
                            h = (g - 1) * HPT + i
                            act.wait_ge(sub_done, at(NH, h + 1))
                            nc.scalar.activation(dist[:, (g - 1) % 2, i], dist[:, (g - 1) % 2, i], ACT.Exp,
                                                 scale=-1.0).then_inc(exp_done, 1)
                        act.wait_ge(pv_n, at(NH, g * HPT))
                        nc.scalar.activation(oT[:, g - 1, :], psO[:], ACT.Identity).then_inc(oT_done, 1)
                for j in range(TPB):
                    act.wait_ge(onT_ps, at(TPB, j + 1))
                    nc.scalar.activation(onT[:], psB[:, 0:D].rearrange("p (k q) -> p k q", k=KD),
                                         ACT.Identity).then_inc(onT_done, 1)

        @block.gpsimd
        def _(pool):
            nc.gpsimd.memset(va[:], 0.0).then_inc(va_set, 1)
            pool.wait_ge(va_set, 1)
            nc.gpsimd.memset(va[:, :, :, HD:HD + 1], 1.0).then_inc(va_set, 1)
            with pool.Fori(0, B) as b:
                for h in range(NH):
                    g, i = h // HPT, h % HPT
                    pool.wait_ge(root_done, b * NH + (h + 1))
                    pool.wait_ge(mb_done, b * NH + (h + 1))
                    d = dist[:, g % 2, i]
                    nc.gpsimd.tensor_tensor(d, d, spread(mb[:, i, :], [P, TPB, S], 1),
                                            ALU.subtract).then_inc(sub_done, 1)

        @block.vector
        def _(dve):
            dve.wait_ge(loaded, 160)
            dve.wait_ge(va_set, 2)
            with dve.Fori(0, B) as b:
                at = lambda per, c: b * per + c
                for p in range(NPR):
                    dve.wait_ge(sum_ps, at(NPR, p + 1))
                    nc.vector.scalar_tensor_tensor(qk[:, p // NG_H, p % NG_H, :], raw[:, p % 2, :],
                                                   sign_sb[:, p // NG_H:p // NG_H + 1], psS[:, 2 + p % 2, :],
                                                   ALU.mult, ALU.add).then_inc(qk_done, 1)
                for j in range(TPB):
                    dve.wait_ge(v_ps, at(TPB, j + 1))
                    nc.vector.tensor_tensor(va[:, j, :, 0:HD], psS[:, j, 0:D].rearrange("p (h d) -> p h d", h=NH),
                                            bv_sb[:].rearrange("p (h d) -> p h d", h=NH), ALU.add).then_inc(v_done, 1)
                dve.wait_ge(xn_done, at(TPB, TPB))
                for j in range(TPB):
                    t = at(TPB, j)
                    nc.vector.tensor_tensor(core.X[:, t, :], core.X[:, t, :], bo_sb[:], ALU.add).then_inc(xb_done, 1)

                def reduce_least(h):
                    dve.wait_ge(m_ps, at(NH, h + 1))
                    nc.vector.tensor_reduce(mq[:, h // HPT % 2, h % HPT, :],
                                            psM[:].rearrange("p (q k) -> p q k", k=P), AX.X,
                                            ALU.min).then_inc(mq_done, 1)

                for h in range(NH):
                    g, i = h // HPT, h % HPT
                    d = dist[:, g % 2, i]
                    if g >= 2:
                        dve.wait_ge(pv_n, at(NH, h - 2 * HPT + 1))
                    for c in range(2):
                        dve.wait_ge(s_ps, at(2 * NH, 2 * h + c + 1))
                        nc.vector.tensor_scalar(d[:, 2 * c:2 * c + 2, :], psS[:, 2 * c:2 * c + 2, :], 1e-12, None,
                                                ALU.max).then_inc(clamp_done, 1)
                    dve.wait_ge(clamp_done, at(2 * NH, 2 * h + 2))
                    nc.vector.tensor_tensor(fold[:], d[:, 0:2, :], d[:, 2:4, :], ALU.min).then_inc(fold_done, 1)
                    if i:
                        reduce_least(h - 1)
                    dve.wait_ge(fold_done, at(NH, h + 1))
                    nc.vector.tensor_tensor(least[:, h % 2, :], fold[:, 0, :], fold[:, 1, :], ALU.min).then_inc(least_done, 1)
                    if i == HPT - 1:
                        reduce_least(h)
                for j in range(TPB):
                    t = at(TPB, j)
                    heads = psM[:].rearrange("p (h c) -> p h c", c=PAD)
                    dve.wait_ge(q_ps, at(TPB, j + 1))
                    nc.vector.reciprocal(rec[:], heads[:, :, HD]).then_inc(rec_done, 1)
                    dve.wait_ge(rec_done, at(TPB, j + 1))
                    nc.vector.tensor_tensor(on[:].rearrange("p (h d) -> p h d", h=NH), heads[:, :, 0:HD],
                                            spread(rec[:], [P, NH, HD], 2), ALU.mult).then_inc(on_done, 1)
                    dve.wait_ge(xb_done, at(TPB, j + 1))
                    dve.wait_ge(y_ps, at(TPB, j + 1))
                    nc.vector.tensor_tensor(core.X[:, t, :], psX[:, 0:D], core.X[:, t, :], ALU.add).then_inc(x_done, 1)
                    dve.wait_ge(x_done, at(TPB, j + 1))
                    core.apart(dve)
                    nc.vector.bn_stats(core.bn[:, t, :], core.X[:, t, :])


def attention_constants():
    import numpy as np

    row = np.arange(P) % PAD
    sel = np.zeros((P, 2, P), np.float32)
    for p in range(P):
        if row[p] < HD:
            sel[p, 0, p // PAD * PAD + HD] = 1
            sel[p, 1, p // PAD * PAD + HD + 1] = 1
    sign = np.stack([np.where(row < HD, -2.0, 1.0), np.ones(P)], 1).astype(np.float32)
    return sel, sign


def pad_heads(a, one_row=None):
    import numpy as np

    out = np.zeros((*a.shape[:-1], NH, PAD), a.dtype)
    out[..., :HD] = a.reshape(*a.shape[:-1], NH, HD)
    if one_row is not None:
        out[..., one_row] = 1
    return out.reshape(*a.shape[:-1], NH * PAD)
DI = 512
HM, PM = 8, 64
NST = 128
TAPS = 4
NCT = (DI + 2 * NST) // P
KI = DI // P


def state_space_stage(nc, core, tag, w_in, conv_w, conv_b, dt_bias, a_log, norm_w, w_out, upto):
    with ExitStack() as ctx:
        WIN = 2 * DI + 2 * NST + HM
        sbf = lambda n, s: core.sbuf(f"{tag}_{n}", s, ctx)
        win = sbf("win", [P, KD, WIN])
        wout = sbf("wout", [P, KI, D])
        cw = sbf("cw", [P, NCT, TAPS])
        cb = sbf("cb", [P, NCT])
        nw = sbf("nw", [P, KI])
        dtb = sbf("dtb", [P, HM])
        neg_a = sbf("neg_a", [P, HM])
        tri = sbf("tri", [P, P])
        xn = sbf("xn", [P, TPB, D])
        xnT = sbf("xnT", [P, KD, S])
        padded = sbf("padded", [P, 2, TAPS - 1 + S])
        acc = sbf("acc", [P, 2, S])
        xbc = sbf("xbc", [P, NCT, S])
        z = sbf("z", [P, TPB, DI])
        dtT = sbf("dtT", [P, S])
        dv = sbf("dv", [P, 12, TPB, HM])
        xdt = sbf("xdt", [P, 2, DI])
        xdec = sbf("xdec", [P, 2, DI])
        b_tok = sbf("b_tok", [P, 2, NST])
        gm = sbf("gm", [P, 2, P])
        lt = sbf("lt", [P, 2, HM, P])
        st = sbf("st", [P, DI])
        st2 = sbf("st2", [P, DI])
        yo = sbf("yo", [P, DI])
        y = sbf("y", [P, TPB, DI])
        ybn = sbf("ybn", [P, TPB, 6])
        ymv = sbf("ymv", [P, TPB, 2])
        yr = sbf("yr", [P, TPB])
        yT = sbf("yT", [P, 2, KI, P])
        psP = core.psum(f"{tag}_psP", [P, 2, 512], ctx)
        psX = core.psum(f"{tag}_psX", [P, 512], ctx)
        psG = core.psum(f"{tag}_psG", [P, 512], ctx)
        psC = core.psum(f"{tag}_psC", [P, 2, 512], ctx)
        psY = core.psum(f"{tag}_psY", [P, 512], ctx)
        psO = core.psum(f"{tag}_psO", [P, 512], ctx)
        sem = lambda n: core.sem(f"{tag}_{n}", ctx)
        loaded, prep = sem("loaded"), sem("prep")
        a_exp = sem("a_exp")
        xn_done, tr_done, xnT_done = sem("xn_done"), sem("tr_done"), sem("xnT_done")
        p_ps, p_done, tap, conv_done, silu_done = sem("p_ps"), sem("p_done"), sem("tap"), sem("conv_done"), sem("silu_done")
        dt_ps, dt_step, dt_act, cs_ps = sem("dt_ps"), sem("dt_step"), sem("dt_act"), sem("cs_ps")
        x_ps, g_ps, c_ps = sem("x_ps"), sem("g_ps"), sem("c_ps")
        xdt_done, xdec_done, g_done, l_done, lexp_done, m_done = (
            sem("xdt_done"), sem("xdec_done"), sem("g_done"), sem("l_done"), sem("lexp_done"), sem("m_done"))
        yo_ps, yd_ps, st_ps, yo_done, y_done, st_done, st_step = (
            sem("yo_ps"), sem("yd_ps"), sem("st_ps"), sem("yo_done"), sem("y_done"), sem("st_done"), sem("st_step"))
        ybn_done, ymv_done, yroot_done, yr_done, yn_done, yz_done = (
            sem("ybn_done"), sem("ymv_done"), sem("yroot_done"), sem("yr_done"), sem("yn_done"), sem("yz_done"))
        yT_ps, yT_done, o_ps, x_done = sem("yT_ps"), sem("yT_done"), sem("o_ps"), sem("x_done")
        block = ctx.enter_context(nc.Block())
        NP_ = NCT + TPB + 1
        (XD, AB, RL, DT, A, CS, NCS, TOT, DIF, EOUT, DEC, ETOT) = range(12)

        @block.sync
        def _(sp):
            for dst, src in ((win[:], w_in.rearrange("(k p) n -> p k n", p=P)),
                             (wout[:], w_out.rearrange("(k p) n -> p k n", p=P)),
                             (cw[:], conv_w), (cb[:], conv_b), (nw[:], norm_w),
                             (dtb[:], dt_bias.unsqueeze(0).broadcast_to([P, HM])),
                             (neg_a[:], a_log.unsqueeze(0).broadcast_to([P, HM])), (tri[:], upto)):
                sp.dma_start(dst, src).then_inc(loaded, 16)

        @block.tensor
        def _(pe):
            pe.wait_ge(loaded, 128)
            pe.wait_ge(prep, 1 + KI)
            with pe.Fori(0, B) as b:
                at = lambda per, c: b * per + c
                for k in range(KD):
                    pe.wait_ge(p_done, at(NP_, 0))
                    pe.wait_ge(st_done, at(TPB - 1, 0))
                    for j in range(TPB):
                        if k == 0:
                            pe.wait_ge(xn_done, at(TPB, j + 1))
                        last = nc.tensor.transpose(psP[:, k, j * P:(j + 1) * P], xn[:, j, k * P:(k + 1) * P],
                                                   core.ident[:])
                    last.then_inc(tr_done, 1)
                pe.wait_ge(xnT_done, at(KD, KD))
                for p in range(NP_):
                    if p >= 2:
                        pe.wait_ge(p_done, at(NP_, p - 1))
                    for k in range(KD):
                        if p < NCT:
                            lhsT, rhs = win[:, k, DI + p * P:DI + (p + 1) * P], xnT[:, k, :]
                            out = psP[:, p % 2, :]
                        elif p < NCT + TPB:
                            j = p - NCT
                            lhsT, rhs = xnT[:, k, j * P:(j + 1) * P], win[:, k, 0:DI]
                            out = psP[:, p % 2, :]
                        else:
                            lhsT, rhs = win[:, k, WIN - HM:WIN], xnT[:, k, :]
                            out = psP[0:HM, p % 2, :]
                        last = nc.tensor.matmul(out, lhsT, rhs, start=(k == 0), stop=(k == KD - 1))
                    last.then_inc(p_ps, 1)
                pe.wait_ge(p_done, at(NP_, NP_))
                pe.wait_ge(x_done, at(TPB, 0))
                core.behind(pe)
                for j in range(TPB):
                    last = nc.tensor.transpose(psG[:, j * HM:(j + 1) * HM], dtT[0:HM, j * P:(j + 1) * P],
                                               core.ident[0:HM, 0:HM])
                last.then_inc(dt_ps, 1)
                pe.wait_ge(dt_step, at(8, 4))
                nc.tensor.matmul(psG[:, 64:64 + TPB * HM], tri[:], dv[:, A].rearrange("p c h -> p (c h)"),
                                 start=True, stop=True)
                nc.tensor.matmul(psG[:, 128:128 + TPB * HM], core.ones[:], dv[:, A].rearrange("p c h -> p (c h)"),
                                 start=True, stop=True).then_inc(cs_ps, 1)
                pe.wait_ge(silu_done, at(NCT, NCT))
                pe.wait_ge(dt_step, at(8, 8))

                def chunk_inputs(c):
                    q = slice(c * P, (c + 1) * P)
                    pe.wait_ge(xdt_done, at(TPB, c))
                    for k in range(KI):
                        last = nc.tensor.transpose(psX[:, k * P:(k + 1) * P], xbc[:, k, q], core.ident[:])
                    last.then_inc(x_ps, 1)
                    pe.wait_ge(g_done, at(TPB, c))
                    nc.tensor.transpose(psG[:, 0:NST], xbc[:, KI, q], core.ident[:])
                    nc.tensor.matmul(psG[:, NST:2 * NST], xbc[:, KI, q], xbc[:, KI + 1, q],
                                     start=True, stop=True).then_inc(g_ps, 1)
                    pe.wait_ge(l_done, at(TPB, c))
                    for h in range(HM):
                        last = nc.tensor.transpose(psC[:, h // 4, (h % 4) * P:(h % 4 + 1) * P],
                                                   dv[:, CS, c, h:h + 1].broadcast_to([P, P]), core.ident[:])
                    last.then_inc(c_ps, 1)

                chunk_inputs(0)
                for c in range(TPB):
                    q = slice(c * P, (c + 1) * P)
                    if c + 1 < TPB:
                        chunk_inputs(c + 1)
                    if c:
                        pe.wait_ge(st_done, at(TPB - 1, c))
                        pe.wait_ge(yo_done, at(TPB - 1, c - 1))
                        nc.tensor.matmul(psO[:], xbc[:, KI + 1, q], st[:], start=True, stop=True).then_inc(yo_ps, 1)
                    if c + 1 < TPB:
                        pe.wait_ge(xdec_done, at(TPB - 1, c + 1))
                        nc.tensor.matmul(psP[:, 0, :], b_tok[:, c % 2, :], xdec[:, c % 2, :],
                                         start=True, stop=True).then_inc(st_ps, 1)
                    pe.wait_ge(m_done, at(TPB, c + 1))
                    pe.wait_ge(y_done, at(TPB, c))
                    for h in range(HM):
                        last = nc.tensor.matmul(psY[:, h * PM:(h + 1) * PM], lt[:, c % 2, h, :],
                                                xdt[:, c % 2, h * PM:(h + 1) * PM], start=True, stop=True)
                    last.then_inc(yd_ps, 1)
                for j in range(TPB):
                    pe.wait_ge(yz_done, at(TPB, j + 1))
                    pe.wait_ge(yT_done, at(TPB, j))
                    for k in range(KI):
                        last = nc.tensor.transpose(psX[:, k * P:(k + 1) * P], y[:, j, k * P:(k + 1) * P], core.ident[:])
                    last.then_inc(yT_ps, 1)
                    pe.wait_ge(yT_done, at(TPB, j + 1))
                    pe.wait_ge(x_done, at(TPB, j))
                    for k in range(KI):
                        last = nc.tensor.matmul(psG[:, 0:D], yT[:, j % 2, k, :], wout[:, k, :],
                                                start=(k == 0), stop=(k == KI - 1))
                    last.then_inc(o_ps, 1)

        @block.scalar
        def _(act):
            a = nc.scalar.activation
            act.wait_ge(loaded, 128)
            a(neg_a[:], neg_a[:], ACT.Exp).then_inc(a_exp, 1)
            with act.Fori(0, B) as b:
                at = lambda per, c: b * per + c
                act.wait_ge(tr_done, at(KD, 0))
                core.apart(act)
                for j in range(TPB):
                    t = at(TPB, j)
                    a(xn[:, j, :], core.X[:, t, :], ACT.Identity, bias=core.shift[:, bass.ds(t, 1)],
                      scale=core.rstd[:, bass.ds(t, 1)]).then_inc(xn_done, 1)
                for k in range(KD):
                    act.wait_ge(tr_done, at(KD, k + 1))
                    a(xnT[:, k, :], psP[:, k, :], ACT.Identity).then_inc(xnT_done, 1)

                def silu(c):
                    act.wait_ge(conv_done, at(NCT, c + 1))
                    a(xbc[:, c, :], acc[:, c % 2, :], ACT.Silu, bias=cb[:, c:c + 1]).then_inc(silu_done, 1)

                act.wait_ge(prep, 1 + KI)
                for p in range(NP_):
                    act.wait_ge(p_ps, at(NP_, p + 1))
                    if p < NCT:
                        act.wait_ge(conv_done, at(NCT, max(p - 1, 0)))
                        a(padded[:, p % 2, TAPS - 1:], psP[:, p % 2, :], ACT.Identity).then_inc(p_done, 1)
                        if p:
                            silu(p - 1)
                    elif p < NCT + TPB:
                        a(z[:, p - NCT, :], psP[:, p % 2, :], ACT.Silu).then_inc(p_done, 1)
                        if p == NCT:
                            silu(NCT - 1)
                    else:
                        a(dtT[0:HM, :], psP[0:HM, p % 2, :], ACT.Identity).then_inc(p_done, 1)
                act.wait_ge(dt_step, at(8, 1))
                a(dv[:, AB], dv[:, XD], ACT.Abs).then_inc(dt_act, 1)
                act.wait_ge(dt_act, at(6, 1))
                a(dv[:, AB], dv[:, AB], ACT.Exp, scale=-1.0).then_inc(dt_act, 1)
                act.wait_ge(dt_act, at(6, 2))
                a(dv[:, AB], dv[:, AB], ACT.Ln, bias=core.ones[:, 0:1]).then_inc(dt_act, 1)
                act.wait_ge(dt_step, at(8, 8))
                for o, i in ((EOUT, CS), (DEC, DIF), (ETOT, TOT)):
                    a(dv[:, o], dv[:, i], ACT.Exp).then_inc(dt_act, 1)
                for c in range(TPB):
                    act.wait_ge(l_done, at(TPB, c + 1))
                    a(lt[:, c % 2], lt[:, c % 2], ACT.Exp).then_inc(lexp_done, 1)
                act.wait_ge(ymv_done, at(1, 1))
                a(yr[:], ymv[:, :, 1], ACT.Sqrt, bias=core.eps[:]).then_inc(yroot_done, 1)
                for j in range(TPB):
                    act.wait_ge(yT_ps, at(TPB, j + 1))
                    act.wait_ge(o_ps, at(TPB, max(j - 1, 0)))
                    a(yT[:, j % 2], psX[:].rearrange("p (k q) -> p k q", k=KI), ACT.Identity).then_inc(yT_done, 1)

        @block.gpsimd
        def _(pool):
            tt = nc.gpsimd.tensor_tensor
            nc.gpsimd.memset(padded[:, :, 0:TAPS - 1], 0.0).then_inc(prep, 1)
            with pool.Fori(0, B) as b:
                at = lambda per, c: b * per + c
                for c in range(TPB):
                    if c == 0:
                        pool.wait_ge(dt_act, at(6, 6))
                    if c + 1 < TPB:
                        pool.wait_ge(xdt_done, at(TPB, c + 1))
                        pool.wait_ge(st_ps, at(TPB - 1, max(c - 1, 0)))
                        tt(xdec[:, c % 2, :].rearrange("p (h q) -> p h q", h=HM),
                           xdt[:, c % 2, :].rearrange("p (h q) -> p h q", h=HM),
                           spread(dv[:, DEC, c, :], [P, HM, PM], 2), ALU.mult).then_inc(xdec_done, 1)
                    pool.wait_ge(lexp_done, at(TPB, c + 1))
                    pool.wait_ge(g_done, at(TPB, c + 1))
                    tt(lt[:, c % 2], lt[:, c % 2], spread(gm[:, c % 2, :], [P, HM, P], 1), ALU.mult).then_inc(m_done, 1)
                for j in range(TPB):
                    pool.wait_ge(yn_done, at(TPB, j + 1))
                    tt(y[:, j, :], y[:, j, :], z[:, j, :], ALU.mult).then_inc(yz_done, 1)

        @block.vector
        def _(dve):
            tt, ts, stt = nc.vector.tensor_tensor, nc.vector.tensor_scalar, nc.vector.scalar_tensor_tensor
            dve.wait_ge(loaded, 128)
            for k in range(KI):
                ts(wout[:, k, :], wout[:, k, :], nw[:, k:k + 1], None, ALU.mult).then_inc(prep, 1)
            dve.wait_ge(prep, 1 + KI)
            dve.wait_ge(a_exp, 1)
            with dve.Fori(0, B) as b:
                at = lambda per, c: b * per + c
                for c in range(NCT):
                    dve.wait_ge(p_done, at(NP_, c + 1))
                    dve.wait_ge(silu_done, at(NCT, max(c - 1, 0)))
                    src, o = padded[:, c % 2], acc[:, c % 2, :]
                    ts(o, src[:, 0:S], cw[:, c, 0:1], None, ALU.mult).then_inc(tap, 1)
                    for j in range(1, TAPS):
                        dve.wait_ge(tap, at(NCT * (TAPS - 1), c * (TAPS - 1) + j))
                        last = stt(o, src[:, j:j + S], cw[:, c, j:j + 1], o, ALU.mult, ALU.add)
                        last.then_inc(tap if j < TAPS - 1 else conv_done, 1)
                dve.wait_ge(dt_ps, at(1, 1))
                raw = psG[:, 0:TPB * HM].rearrange("p (c h) -> p c h", h=HM)
                tt(dv[:, XD], raw, spread(dtb[:], [P, TPB, HM], 1), ALU.add).then_inc(dt_step, 1)
                dve.wait_ge(dt_step, at(8, 1))
                ts(dv[:, RL], dv[:, XD], 0.0, None, ALU.max).then_inc(dt_step, 1)
                dve.wait_ge(dt_step, at(8, 2))
                dve.wait_ge(dt_act, at(6, 3))
                tt(dv[:, DT], dv[:, RL], dv[:, AB], ALU.add).then_inc(dt_step, 1)
                dve.wait_ge(dt_step, at(8, 3))
                stt(dv[:, A], dv[:, DT], -1.0, spread(neg_a[:], [P, TPB, HM], 1), ALU.mult, ALU.mult).then_inc(dt_step, 1)
                dve.wait_ge(cs_ps, at(1, 1))
                cs = psG[:, 64:64 + TPB * HM].rearrange("p (c h) -> p c h", h=HM)
                tot = psG[:, 128:128 + TPB * HM].rearrange("p (c h) -> p c h", h=HM)
                nc.vector.tensor_copy(dv[:, CS], cs).then_inc(dt_step, 1)
                ts(dv[:, NCS], cs, -1.0, None, ALU.mult).then_inc(dt_step, 1)
                nc.vector.tensor_copy(dv[:, TOT], tot).then_inc(dt_step, 1)
                dve.wait_ge(dt_step, at(8, 7))
                tt(dv[:, DIF], dv[:, TOT], dv[:, CS], ALU.subtract).then_inc(dt_step, 1)

                def chunk_inputs(c):
                    dve.wait_ge(x_ps, at(TPB, c + 1))
                    if c >= 2:
                        dve.wait_ge(yd_ps, at(TPB, c - 1))
                    else:
                        dve.wait_ge(yd_ps, at(TPB, 0))
                    if c >= 2:
                        dve.wait_ge(xdec_done, at(TPB - 1, c - 1))
                    tt(xdt[:, c % 2, :].rearrange("p (h q) -> p h q", h=HM), psX[:].rearrange("p (h q) -> p h q", h=HM),
                       spread(dv[:, DT, c, :], [P, HM, PM], 2), ALU.mult).then_inc(xdt_done, 1)
                    dve.wait_ge(g_ps, at(TPB, c + 1))
                    if c >= 2:
                        dve.wait_ge(st_ps, at(TPB - 1, c - 1))
                    nc.vector.tensor_copy(b_tok[:, c % 2, :], psG[:, 0:NST])
                    tt(gm[:, c % 2, :], psG[:, NST:2 * NST], tri[:], ALU.mult).then_inc(g_done, 1)
                    dve.wait_ge(c_ps, at(TPB, c + 1))
                    for h in range(HM):
                        last = ts(lt[:, c % 2, h, :], psC[:, h // 4, (h % 4) * P:(h % 4 + 1) * P],
                                  dv[:, NCS, c, h:h + 1], 0.0, ALU.add, ALU.min)
                    last.then_inc(l_done, 1)

                chunk_inputs(0)
                for c in range(TPB):
                    if c + 1 < TPB:
                        chunk_inputs(c + 1)
                    if c:
                        dve.wait_ge(yo_ps, at(TPB - 1, c))
                        dve.wait_ge(dt_act, at(6, 6))
                        tt(yo[:].rearrange("p (h q) -> p h q", h=HM), psO[:].rearrange("p (h q) -> p h q", h=HM),
                           spread(dv[:, EOUT, c, :], [P, HM, PM], 2), ALU.mult).then_inc(yo_done, 1)
                    if 0 < c < TPB - 1:
                        dve.wait_ge(st_done, at(TPB - 1, c))
                        tt(st2[:].rearrange("p (h q) -> p h q", h=HM), st[:].rearrange("p (h q) -> p h q", h=HM),
                           spread(dv[:, ETOT, c, :], [P, HM, PM], 2), ALU.mult).then_inc(st_step, 1)
                        dve.wait_ge(st_step, at(TPB - 2, c))
                    if c < TPB - 1:
                        dve.wait_ge(st_ps, at(TPB - 1, c + 1))
                        if c:
                            tt(st[:], psP[:, 0, :], st2[:], ALU.add).then_inc(st_done, 1)
                        else:
                            nc.vector.tensor_copy(st[:], psP[:, 0, :]).then_inc(st_done, 1)
                    dve.wait_ge(yd_ps, at(TPB, c + 1))
                    if c:
                        dve.wait_ge(yo_done, at(TPB - 1, c))
                        tt(y[:, c, :], psY[:], yo[:], ALU.add).then_inc(y_done, 1)
                    else:
                        dve.wait_ge(yT_ps, at(TPB, 0))
                        nc.vector.tensor_copy(y[:, c, :], psY[:]).then_inc(y_done, 1)
                    dve.wait_ge(y_done, at(TPB, c + 1))
                    nc.vector.bn_stats(ybn[:, c, :], y[:, c, :]).then_inc(ybn_done, 1)
                dve.wait_ge(ybn_done, at(TPB, TPB))
                core.behind(dve)
                for c in range(TPB):
                    last = nc.vector.bn_aggr(ymv[:, c, :], ybn[:, c, :])
                last.then_inc(ymv_done, 1)
                dve.wait_ge(yroot_done, at(1, 1))
                nc.vector.reciprocal(yr[:], yr[:]).then_inc(yr_done, 1)
                dve.wait_ge(yr_done, at(1, 1))
                for j in range(TPB):
                    ts(y[:, j, :], y[:, j, :], ymv[:, j, 0:1], yr[:, j:j + 1], ALU.subtract, ALU.mult).then_inc(yn_done, 1)
                for j in range(TPB):
                    t = at(TPB, j)
                    dve.wait_ge(o_ps, at(TPB, j + 1))
                    tt(core.X[:, t, :], psG[:, 0:D], core.X[:, t, :], ALU.add).then_inc(x_done, 1)
                    dve.wait_ge(x_done, at(TPB, j + 1))
                    core.apart(dve)
                    nc.vector.bn_stats(core.bn[:, t, :], core.X[:, t, :])
GRP_T = 8
EPS_D = 1e-6


def delta_inputs(nc, core, tag, beta, w_qk, w_vb, tok_qk, seq_k, seq_nbk, seq_v):
    with ExitStack() as ctx:
        sbf = lambda n, s: core.sbuf(f"{tag}_{n}", s, ctx)
        wqk = sbf("wqk", [P, KD, 2 * D])
        wvb = sbf("wvb", [P, KD, D + NH])
        xn = sbf("xn", [P, TPB, D])
        xnT = sbf("xnT", [P, KD, S])
        qk = sbf("qk", [P, 2, TPB, 2 * D])
        v = sbf("v", [P, 2, TPB, D])
        sqr = sbf("sqr", [P, 2, 2 * D])
        ss = sbf("ss", [P, TPB * 2 * NH])
        nbk = sbf("nbk", [P, 2, TPB, D])
        psT = core.psum(f"{tag}_psT", [P, 2, 512], ctx)
        psA = core.psum(f"{tag}_psA", [P, 2, 512], ctx)
        psV = core.psum(f"{tag}_psV", [P, 2, 512], ctx)
        psB = core.psum(f"{tag}_psB", [P, 512], ctx)
        sem = lambda n: core.sem(f"{tag}_{n}", ctx)
        loaded = sem("loaded")
        xn_done, tr_done, xnT_done = sem("xn_done"), sem("tr_done"), sem("xnT_done")
        a_ps, silu_done, b_ps, beta_done = sem("a_ps"), sem("silu_done"), sem("b_ps"), sem("beta_done")
        sq_done, ss_done, root_done, inv_step, norm_done, nbk_done = (
            sem("sq_done"), sem("ss_done"), sem("root_done"), sem("inv_step"), sem("norm_done"), sem("nbk_done"))
        stored = [sem(f"stored{u}") for u in range(2)]
        block = ctx.enter_context(nc.Block())
        NOUT = 1 + 3 * TPB

        @block.sync
        def _(sp):
            sp.dma_start(wqk[:], w_qk.rearrange("(k p) n -> p k n", p=P)).then_inc(loaded, 16)
            sp.dma_start(wvb[:], w_vb.rearrange("(k p) n -> p k n", p=P)).then_inc(loaded, 16)
            with sp.Fori(0, B // 2) as b2:
                for u in range(2):
                    at = at_batch(b2, u)
                    b = b2 * 2 + u

                    def by_sequence(dst, src):
                        rows = dst.rearrange("(b h) (j p) d -> b j p h d", b=B, p=P)
                        for j in range(TPB):
                            sp.dma_start(rows[b, j], src[:, u, j, :].rearrange("p (h d) -> p h d", h=NH)).then_inc(stored[u], 16)

                    sp.wait_ge(silu_done, at(2 * TPB, 2 * TPB))
                    by_sequence(seq_v, v)
                    sp.wait_ge(norm_done, at(TPB, TPB))
                    sp.dma_start(tok_qk.rearrange("(b j p) n -> b p j n", b=B, p=P)[b], qk[:, u]).then_inc(stored[u], 16)
                    by_sequence(seq_k, qk[:, :, :, D:])
                    sp.wait_ge(nbk_done, at(1, 1))
                    by_sequence(seq_nbk, nbk)
            for u in range(2):
                sp.wait_ge(stored[u], 16 * NOUT * (B // 2))

        @block.tensor
        def _(pe):
            pe.wait_ge(loaded, 32)
            with pe.Fori(0, B // 2) as b2:
                for u in range(2):
                    at = at_batch(b2, u)
                    for k in range(KD):
                        for j in range(TPB):
                            if k == 0:
                                pe.wait_ge(xn_done, at(TPB, j + 1))
                            last = nc.tensor.transpose(psT[:, k, j * P:(j + 1) * P], xn[:, j, k * P:(k + 1) * P],
                                                       core.ident[:])
                        last.then_inc(tr_done, 1)
                    pe.wait_ge(xnT_done, at(KD, KD))
                    pe.wait_ge(beta_done, at(1, 0))
                    for j in range(TPB):
                        pe.wait_ge(silu_done, at(2 * TPB, max(2 * j - 2, 0)))
                        for k in range(KD):
                            nc.tensor.matmul(psA[:, j % 2, :], xnT[:, k, j * P:(j + 1) * P], wqk[:, k, :],
                                             start=(k == 0), stop=(k == KD - 1))
                        for k in range(KD):
                            last = nc.tensor.matmul(psV[:, j % 2, 0:D], xnT[:, k, j * P:(j + 1) * P], wvb[:, k, 0:D],
                                                    start=(k == 0), stop=(k == KD - 1))
                        last.then_inc(a_ps, 1)
                        for k in range(KD):
                            last = nc.tensor.matmul(psB[:, j * NH:(j + 1) * NH], xnT[:, k, j * P:(j + 1) * P],
                                                    wvb[:, k, D:], start=(k == 0), stop=(k == KD - 1))
                    last.then_inc(b_ps, 1)

        @block.scalar
        def _(act):
            a = nc.scalar.activation
            with act.Fori(0, B // 2) as b2:
                for u in range(2):
                    at = at_batch(b2, u)
                    act.wait_ge(tr_done, at(KD, 0))
                    core.apart(act)
                    for j in range(TPB):
                        t = at(TPB, j)
                        a(xn[:, j, :], core.X[:, t, :], ACT.Identity, bias=core.shift[:, bass.ds(t, 1)],
                          scale=core.rstd[:, bass.ds(t, 1)]).then_inc(xn_done, 1)
                    for k in range(KD):
                        act.wait_ge(tr_done, at(KD, k + 1))
                        a(xnT[:, k, :], psT[:, k, :], ACT.Identity).then_inc(xnT_done, 1)
                    act.wait_ge(stored[u], b2 * (16 * NOUT))
                    for j in range(TPB):
                        act.wait_ge(a_ps, at(TPB, j + 1))
                        a(qk[:, u, j, :], psA[:, j % 2, :], ACT.Silu).then_inc(silu_done, 1)
                        a(v[:, u, j, :], psV[:, j % 2, 0:D], ACT.Silu).then_inc(silu_done, 1)
                    act.wait_ge(b_ps, at(1, 1))
                    core.apart(act)
                    a(beta[:, bass.ds(at(TPB, 0), TPB), :], psB[:, 0:TPB * NH].rearrange("p (j h) -> p j h", h=NH),
                      ACT.Sigmoid).then_inc(beta_done, 1)
                    act.wait_ge(ss_done, at(TPB, TPB))
                    a(ss[:], ss[:], ACT.Sqrt).then_inc(root_done, 1)

        @block.gpsimd
        def _(pool):
            with pool.Fori(0, B // 2) as b2:
                for u in range(2):
                    at = at_batch(b2, u)
                    for j in range(TPB):
                        pool.wait_ge(silu_done, at(2 * TPB, 2 * j + 1))
                        pool.wait_ge(ss_done, at(TPB, max(j - 1, 0)))
                        nc.gpsimd.tensor_tensor(sqr[:, j % 2, :], qk[:, u, j, :], qk[:, u, j, :], ALU.mult).then_inc(sq_done, 1)

        @block.vector
        def _(dve):
            tt = nc.vector.tensor_tensor
            with dve.Fori(0, B // 2) as b2:
                for u in range(2):
                    at = at_batch(b2, u)
                    ss3 = ss[:].rearrange("p (j h) -> p j h", j=TPB)
                    for j in range(TPB):
                        dve.wait_ge(sq_done, at(TPB, j + 1))
                        nc.vector.tensor_reduce(ss3[:, j, :], sqr[:, j % 2, :].rearrange("p (h d) -> p h d", d=HD),
                                                AX.X, ALU.add).then_inc(ss_done, 1)
                    dve.wait_ge(root_done, at(1, 1))
                    nc.vector.tensor_scalar(ss[:], ss[:], EPS_D, None, ALU.add).then_inc(inv_step, 1)
                    dve.wait_ge(inv_step, at(2, 1))
                    nc.vector.reciprocal(ss[:], ss[:]).then_inc(inv_step, 1)
                    dve.wait_ge(inv_step, at(2, 2))
                    for j in range(TPB):
                        q3 = qk[:, u, j, :].rearrange("p (h d) -> p h d", d=HD)
                        tt(q3, q3, spread(ss3[:, j, :], [P, 2 * NH, HD], 2), ALU.mult).then_inc(norm_done, 1)
                    dve.wait_ge(norm_done, at(TPB, TPB))
                    dve.wait_ge(beta_done, at(1, 1))
                    for j in range(TPB):
                        last = nc.vector.scalar_tensor_tensor(
                            nbk[:, u, j, :].rearrange("p (h d) -> p h d", d=HD),
                            qk[:, u, j, D:].rearrange("p (h d) -> p h d", d=HD), -1.0,
                            beta[:, at(TPB, j), :].unsqueeze(2).broadcast_to([P, NH, HD]), ALU.mult, ALU.mult)
                    last.then_inc(nbk_done, 1)


def delta_scan(nc, core, tag, seq_k, seq_nbk, seq_v, tok_d, beside):
    with ExitStack() as ctx:
        sbf = lambda n, s: core.sbuf(f"{tag}_{n}", s, ctx)
        NCH = S // P
        k_sb = sbf("k", [P, 2, P, HD])
        bk_sb = sbf("bk", [P, 2, P, HD])
        v_sb = sbf("v", [P, 2, P, HD])
        d_sb = sbf("d", [P, 2, P, HD])
        m = sbf("m", [P, HD, HD])
        prod = sbf("prod", [P, 2, GRP_T, HD, HD + 1])
        outer = sbf("outer", [P, HD, HD])
        nd = sbf("nd", [P, 2, GRP_T, HD])
        sem = lambda n: core.sem(f"{tag}_{n}", ctx)
        in_k = [sem(f"in{u}") for u in range(2)]
        m_zero, v_set, nd_out = sem("m_zero"), sem("v_set"), sem("nd_out")
        mul_n, red_n, out_n, add_n = sem("mul_n"), sem("red_n"), sem("out_n"), sem("add_n")
        stored = [sem(f"stored{u}") for u in range(2)]
        beside.allocate(core, ctx)
        block = ctx.enter_context(nc.Block())
        NGT = P // GRP_T
        H2 = HD // 2

        @block.sync
        def _(sp):
            for c in range(NCH):
                u = c % 2
                if c == 2:
                    beside.load(sp)
                if c >= 2:
                    sp.wait_ge(add_n, 2 * P * (c - 1))
                    sp.wait_ge(v_set, (c - 1) * NGT)
                for dst, src in ((k_sb, seq_k), (bk_sb, seq_nbk), (v_sb, seq_v)):
                    sp.dma_start(dst[:, u], src[:, c * P:(c + 1) * P, :]).then_inc(in_k[u], 16)

        @block.scalar
        def _(act):
            rows = tok_d.rearrange("(b t) (h d) -> b h t d", b=B, h=NH)

            def put_v(c, g, w):
                nc.scalar.activation(prod[:, w, :, :, HD], v_sb[:, c % 2, bass.ds(g * GRP_T, GRP_T), :],
                                     ACT.Copy, scale=-1.0).then_inc(v_set, 1)

            def take_d(c, g, w, n):
                act.wait_ge(red_n, n)
                core.apart(act)
                nc.scalar.activation(d_sb[:, c % 2, bass.ds(g * GRP_T, GRP_T), :], nd[:, w], ACT.Copy,
                                     scale=-1.0).then_inc(nd_out, 1)

            act.wait_ge(in_k[0], 48)
            put_v(0, 0, 0)
            put_v(0, 1, 1)
            for c in range(NCH):
                base = 2 * P * c
                per = 2 * GRP_T
                if c >= 2:
                    act.wait_ge(stored[c % 2], 16 * B * (c // 2))
                with act.Fori(0, NGT // 2 - 1) as g2:
                    for w in range(2):
                        done = g2 * (2 * per) + (base + per * (w + 1))
                        take_d(c, g2 * 2 + w, w, done)
                        put_v(c, g2 * 2 + (w + 2), w)
                for w in range(2):
                    done = base + per * (NGT - 1 + w)
                    take_d(c, NGT - 2 + w, w, done)
                    if c + 1 < NCH:
                        act.wait_ge(in_k[(c + 1) % 2], 48 * ((c + 1) // 2 + 1))
                        nc.scalar.activation(prod[:, w, :, :, HD], v_sb[:, (c + 1) % 2, w * GRP_T:(w + 1) * GRP_T, :],
                                             ACT.Copy, scale=-1.0).then_inc(v_set, 1)
                act.wait_ge(nd_out, (c + 1) * NGT)
                for b in range(B):
                    act.dma_start(rows[b, :, c * P:(c + 1) * P, :], d_sb[b * NH:(b + 1) * NH, c % 2]).then_inc(
                        stored[c % 2], 16)
            for u in range(2):
                act.wait_ge(stored[u], 16 * B * NCH // 2)

        @block.gpsimd
        def _(pool):
            nc.gpsimd.memset(m[:], 0.0).then_inc(m_zero, 1)
            beside.work(nc, pool)

        @block.vector
        def _(dve):
            tt = nc.vector.tensor_tensor
            halves = [slice(0, H2), slice(H2, HD)]
            dve.wait_ge(m_zero, 1)
            for c in range(NCH):
                u = c % 2
                dve.wait_ge(in_k[u], 48 * (c // 2 + 1))
                with dve.Fori(0, NGT // 2) as g2:
                    for w in range(2):
                        for s in range(GRP_T):
                            t = g2 * (2 * GRP_T) + (w * GRP_T + s)
                            done = g2 * (4 * GRP_T) + 2 * (c * P + w * GRP_T + s)
                            k_t = k_sb[:, u, t, :].unsqueeze(1).broadcast_to([P, H2, HD])
                            for i, r in enumerate(halves):
                                first = c == 0 and w == 0 and s == 0
                                dve.wait_ge(add_n, done if first else done + (i - 1))
                                tt(prod[:, w, s, r, 0:HD], m[:, r, :], k_t, ALU.mult).then_inc(mul_n, 1)
                            if s == 0:
                                dve.wait_ge(v_set, g2 * 2 + (c * NGT + w + 1))
                            for i, r in enumerate(halves):
                                dve.wait_ge(mul_n, done + (i + 1))
                                nc.vector.tensor_reduce(nd[:, w, s, r], prod[:, w, s, r, :], AX.X, ALU.add).then_inc(red_n, 1)
                            for i, r in enumerate(halves):
                                dve.wait_ge(red_n, done + 2)
                                dve.wait_ge(add_n, done if first else done + (i - 1))
                                tt(outer[:, r, :], bk_sb[:, u, t, r].unsqueeze(2).broadcast_to([P, H2, HD]),
                                   spread(nd[:, w, s, :], [P, H2, HD], 1), ALU.mult).then_inc(out_n, 1)
                            for i, r in enumerate(halves):
                                dve.wait_ge(out_n, done + (i + 1))
                                tt(m[:, r, :], m[:, r, :], outer[:, r, :], ALU.add).then_inc(add_n, 1)


def delta_output(nc, core, tag, beta, tok_qk, tok_d, wo, rms_w, masks):
    with ExitStack() as ctx:
        sbf = lambda n, s: core.sbuf(f"{tag}_{n}", s, ctx)
        wo_sb = sbf("wo", [P, KD, D])
        rw = sbf("rw", [P, KD])
        par = sbf("par", [P, 2])
        before = sbf("before", [P, P])
        own = sbf("own", [P, P])
        eps6 = sbf("eps6", [P, 1])
        qk = sbf("qk", [P, 2, 2 * D])
        d = sbf("d", [P, 2, D])
        bd = sbf("bd", [P, 2, D])
        kT = sbf("kT", [P, KD, P])
        qT = sbf("qT", [P, KD, P])
        q2 = sbf("q2", [P, KD, 2, P])
        aT = sbf("aT", [P, NH, P])
        m0 = sbf("m0", [P, KD, P])
        mt = sbf("mt", [P, KD, P])
        o1 = sbf("o1", [P, KD, P])
        oT = sbf("oT", [P, KD, P])
        osq = sbf("osq", [P, KD, P])
        r = sbf("r", [P, 1])
        psT = core.psum(f"{tag}_psT", [P, 512], ctx)
        psA = core.psum(f"{tag}_psA", [P, 4, 512], ctx)
        psE = core.psum(f"{tag}_psE", [P, KD, 2, P], ctx)
        psM = core.psum(f"{tag}_psM", [P, 512], ctx)
        psY = core.psum(f"{tag}_psY", [P, 512], ctx)
        sem = lambda n: core.sem(f"{tag}_{n}", ctx)
        loaded, prep, wo_done, d_in = sem("loaded"), sem("prep"), sem("wo_done"), [sem("in0"), sem("in1")]
        t_ps, qk_done, a_ps, a_done, bd_done = sem("t_ps"), sem("qk_done"), sem("a_ps"), sem("a_done"), sem("bd_done")
        e_ps, e1_done, e2_done, osq_done, m_ps, mt_done, m0_done = (
            sem("e_ps"), sem("e1_done"), sem("e2_done"), sem("osq_done"), sem("m_ps"), sem("mt_done"), sem("m0_done"))
        y_ps, root_done, r_done, x_done = sem("y_ps"), sem("root_done"), sem("r_done"), sem("x_done")
        block = ctx.enter_context(nc.Block())

        @block.sync
        def _(sp):
            sp.dma_start(wo_sb[:], wo.rearrange("(k p) n -> p k n", p=P)).then_inc(loaded, 16)
            sp.dma_start(rw[:], rms_w).then_inc(loaded, 16)
            for dst, src in ((par, masks[0]), (before, masks[1]), (own, masks[2])):
                sp.dma_start(dst[:], src).then_inc(loaded, 16)
            with sp.Fori(0, B) as b:
                for c in range(TPB):
                    u = c % 2
                    at = lambda per, n: b * per + n
                    sp.wait_ge(y_ps, at(TPB, max(c - 1, 0)))
                    rows = tok_qk.rearrange("(t p) n -> t p n", p=P)
                    sp.dma_start(qk[:, u, :], rows[at(TPB, c)]).then_inc(d_in[u], 16)
                    rows = tok_d.rearrange("(t p) n -> t p n", p=P)
                    sp.dma_start(d[:, u, :], rows[at(TPB, c)]).then_inc(d_in[u], 16)

        @block.gpsimd
        def _(pool):
            nc.gpsimd.memset(eps6[:], EPS_D).then_inc(prep, 1)
            with pool.Fori(0, B) as b:
                for c in range(TPB):
                    u, n = c % 2, b * TPB + c
                    pool.wait_ge(d_in[u], b * (32 * TPB // 2) + 32 * (c // 2 + 1))
                    nc.gpsimd.tensor_tensor(bd[:, u, :].rearrange("p (h d) -> p h d", d=HD),
                                            d[:, u, :].rearrange("p (h d) -> p h d", d=HD),
                                            beta[:, n, :].unsqueeze(2).broadcast_to([P, NH, HD]), ALU.mult).then_inc(bd_done, 1)

        @block.tensor
        def _(pe):
            pe.wait_ge(loaded, 80)
            pe.wait_ge(wo_done, KD)
            with pe.Fori(0, B) as b:
                for c in range(TPB):
                    u = c % 2
                    at = lambda per, n: b * per + n
                    pe.wait_ge(d_in[u], at(32 * TPB // 2, 32 * (c // 2 + 1)))
                    pe.wait_ge(qk_done, at(4 * TPB, 4 * c))
                    for k in range(2 * KD):
                        last = nc.tensor.transpose(psT[:, k * P:(k + 1) * P], qk[:, u, k * P:(k + 1) * P], core.ident[:])
                    last.then_inc(t_ps, 1)
                    pe.wait_ge(qk_done, at(4 * TPB, 4 * c + 4))
                    for k in range(KD):
                        for i in range(4):
                            rr = slice(i * PAD, (i + 1) * PAD)
                            if k == 0:
                                pe.wait_ge(a_done, at(4 * TPB, max(4 * c - 3 + i, 0)))
                            last = nc.tensor.matmul(psA[:, i, k * 2 * P:(k + 1) * 2 * P], kT[rr, k, :],
                                                    q2[rr, k].rearrange("p e t -> p (e t)"), start=True, stop=True)
                            if k:
                                last.then_inc(a_ps, 1)
                    pe.wait_ge(e2_done, at(TPB, c))
                    pe.wait_ge(bd_done, at(TPB, c + 1))
                    if c:
                        pe.wait_ge(m0_done, at(TPB - 1, c))
                    for k in range(KD):
                        if c:
                            nc.tensor.matmul(psE[:, k].rearrange("p e t -> p (e t)"), m0[:, k, :],
                                             qT[:, k, :].unsqueeze(1).broadcast_to([P, 2, P]), start=True, stop=False,
                                             skip_group_check=True)
                        for i in range(4):
                            n = k * 4 + i
                            pe.wait_ge(a_done, at(4 * TPB, 4 * c + i + 1))
                            last = nc.tensor.matmul(psE[i * PAD:(i + 1) * PAD, k].rearrange("p e t -> p (e t)"),
                                                    bd[:, u, k * P + i * PAD:k * P + (i + 1) * PAD],
                                                    aT[:, 2 * n:2 * n + 2, :].rearrange("p h t -> p (h t)"),
                                                    start=(c == 0), stop=True, skip_group_check=True)
                    last.then_inc(e_ps, 1)
                    if c < TPB - 1:
                        if c:
                            pe.wait_ge(mt_done, at(TPB - 1, c))
                        for k in range(KD):
                            last = nc.tensor.matmul(psM[:, k * P:(k + 1) * P], qk[:, u, D + k * P:D + (k + 1) * P],
                                                    bd[:, u, k * P:(k + 1) * P], start=True, stop=True)
                        last.then_inc(m_ps, 1)
                    pe.wait_ge(osq_done, at(TPB, c + 1))
                    pe.wait_ge(x_done, at(TPB, c))
                    for k in range(KD):
                        nc.tensor.matmul(psY[:, 0:D], oT[:, k, :], wo_sb[:, k, :], start=(k == 0), stop=(k == KD - 1))
                    for k in range(KD):
                        last = nc.tensor.matmul(psY[:, D:D + 1], osq[:, k, :], core.ones[:, 0:1],
                                                start=(k == 0), stop=(k == KD - 1))
                    last.then_inc(y_ps, 1)

        @block.scalar
        def _(act):
            a = nc.scalar.activation
            act.wait_ge(loaded, 80)
            act.wait_ge(prep, 1)
            with act.Fori(0, B) as b:
                for c in range(TPB):
                    at = lambda per, n: b * per + n
                    act.wait_ge(t_ps, at(TPB, c + 1))
                    act.wait_ge(e_ps, at(TPB, c))
                    q = psT[:, 0:KD * P].rearrange("p (k t) -> p k t", k=KD)
                    for e in range(2):
                        a(q2[:, :, e, :], q, ACT.Identity, scale=par[:, e:e + 1]).then_inc(qk_done, 1)
                    a(kT[:], psT[:, KD * P:].rearrange("p (k t) -> p k t", k=KD), ACT.Identity).then_inc(qk_done, 1)
                    a(qT[:], q, ACT.Identity).then_inc(qk_done, 1)
                    act.wait_ge(e_ps, at(TPB, c + 1))
                    a(o1[:], psE[:, :, 0, :], ACT.Identity, scale=par[:, 0:1]).then_inc(e1_done, 1)
                    act.wait_ge(e2_done, at(TPB, c + 1))
                    a(osq[:], oT[:], ACT.Square).then_inc(osq_done, 1)
                    act.wait_ge(y_ps, at(TPB, c + 1))
                    a(r[:], psY[:, D:D + 1], ACT.Sqrt, scale=1.0 / D, bias=eps6[:]).then_inc(root_done, 1)

        @block.vector
        def _(dve):
            tt, stt = nc.vector.tensor_tensor, nc.vector.scalar_tensor_tensor
            dve.wait_ge(loaded, 80)
            for k in range(KD):
                nc.vector.tensor_scalar(wo_sb[:, k, :], wo_sb[:, k, :], rw[:, k:k + 1], None, ALU.mult).then_inc(wo_done, 1)
            with dve.Fori(0, B) as b:
                for c in range(TPB):
                    at = lambda per, n: b * per + n
                    t = at(TPB, c)
                    for g in range(4):
                        dve.wait_ge(a_ps, at(4 * TPB, 4 * c + g + 1))
                        if g == 0:
                            dve.wait_ge(e_ps, at(TPB, c))
                        tt(aT[:].rearrange("p (k i e) t -> p k i e t", k=KD, e=2)[:, :, g],
                           psA[:, g, :].rearrange("p (k e t) -> p k e t", k=KD, e=2),
                           spread(before[:], [P, 2 * KD, P], 1).rearrange("p (k e) t -> p k e t", k=KD),
                           ALU.mult).then_inc(a_done, 1)
                    dve.wait_ge(e1_done, at(TPB, c + 1))
                    dve.wait_ge(y_ps, at(TPB, c))
                    stt(oT[:], psE[:, :, 1, :], par[:, 1:2], o1[:], ALU.mult, ALU.add).then_inc(e2_done, 1)
                    if c < TPB - 1:
                        dve.wait_ge(m_ps, at(TPB - 1, c + 1))
                        dst = m0 if c == 0 else mt
                        last = tt(dst[:], psM[:, 0:KD * P].rearrange("p (k t) -> p k t", k=KD),
                                  spread(own[:], [P, KD, P], 1), ALU.mult)
                        last.then_inc(mt_done, 1)
                        if c:
                            dve.wait_ge(mt_done, at(TPB - 1, c + 1))
                            tt(m0[:], m0[:], mt[:], ALU.add).then_inc(m0_done, 1)
                        else:
                            dve.wait_ge(mt_done, at(TPB - 1, 1))
                            core.apart(dve)
                            dve.sem_inc(m0_done, 1)
                    dve.wait_ge(root_done, at(TPB, c + 1))
                    nc.vector.reciprocal(r[:], r[:]).then_inc(r_done, 1)
                    dve.wait_ge(r_done, at(TPB, c + 1))
                    stt(core.X[:, t, :], psY[:, 0:D], r[:], core.X[:, t, :], ALU.mult, ALU.add).then_inc(x_done, 1)
                    dve.wait_ge(x_done, at(TPB, c + 1))
                    core.apart(dve)
                    nc.vector.bn_stats(core.bn[:, t, :], core.X[:, t, :])


def delta_constants():
    import numpy as np

    p = np.arange(P)
    par = np.stack([(p // HD) % 2 == 0, (p // HD) % 2 == 1], 1)
    before = p[:, None] < p[None, :]
    own = p[:, None] // HD == p[None, :] // HD
    return [np.ascontiguousarray(a.astype(np.float32)) for a in (par, before, own)]


def hybrid_layers_program(nc, x, ident, w_qk, w_vb, d_wo, rms_w, par, before, own,
                          w_exp, b_exp, w_con_t, up_w, down_w, up_bias, b_con, down_bias,
                          wq_p, wk_p, bq_p, bk_p, wv, bv, a_wo, bo, sel, sign,
                          fwd, inv, conv_wt, conv_bias, modes, index, chan,
                          weight_t, gate_t, u_t, v,
                          w_in, conv_w, conv_b, dt_bias, a_log, norm_w, w_out, upto, out):
    with ExitStack() as ctx:
        core = Core(nc, ctx)
        tok_qk = nc.dram_tensor("tok_qk", [B * S, 2 * D], F32).ap()
        tok_d = nc.dram_tensor("tok_d", [B * S, D], F32).ap()
        seq = [nc.dram_tensor(f"seq_{n}", [P, S, HD], F32).ap() for n in ("k", "nbk", "v")]

        start(nc, core, x, ident)
        row_scales(nc, core, "r0")
        with ExitStack() as ffn_ctx:
            core.ctx = ffn_ctx
            bf = Butterfly(nc, core, [w_exp, b_exp, w_con_t, up_w, down_w])
            core.ctx = ctx
            with ExitStack() as delta_ctx:
                bf.allocate_folding(core, delta_ctx)
                beta = core.sbuf("beta", [P, NT, NH], delta_ctx)
                delta_inputs(nc, core, "di", beta, w_qk, w_vb, tok_qk, *seq)
                delta_scan(nc, core, "ds", *seq, tok_d, bf)
                delta_output(nc, core, "do", beta, tok_qk, tok_d, d_wo, rms_w, (par, before, own))
                ffn_prepare(nc, core, bf, up_bias, b_con, down_bias)
            row_scales(nc, core, "r1")
            ffn_stage(nc, core, bf, "f1")
            row_scales(nc, core, "r2")
            distance_attention_stage(nc, core, "a1", wq_p, wk_p, bq_p, bk_p, wv, bv, a_wo, bo,
                                     sel, sign)
            row_scales(nc, core, "r3")
            ffn_stage(nc, core, bf, "f2")
        with ExitStack() as conv_ctx:
            lc = LongConv(nc, core, conv_ctx)
            with ExitStack() as load_ctx:
                block = load_ctx.enter_context(nc.Block())

                @block.sync
                def _(sp):
                    lc.load(sp, fwd, inv, conv_wt, conv_bias)
            conv_kernel(nc, core, lc, modes, index, chan)
            row_scales(nc, core, "r4")
            conv_stage(nc, core, lc, "c1")
        core.clear_semaphores()
        mx = MixtureWeights(nc, core)
        with ExitStack() as load_ctx:
            block = load_ctx.enter_context(nc.Block())

            @block.sync
            def _(sp):
                mx.load(sp, weight_t, gate_t, u_t, v)
        row_scales(nc, core, "r5")
        mixture_stage(nc, core, mx, "m1")
        row_scales(nc, core, "r6")
        state_space_stage(nc, core, "s1", w_in, conv_w, conv_b, dt_bias, a_log, norm_w, w_out, upto)
        row_scales(nc, core, "r7")
        mixture_stage(nc, core, mx, "m2")
        finish(nc, core, out)


def kernel(**inputs):
    import numpy as np
    import concourse.bacc as _bacc
    from concourse import mybir as _mybir
    from concourse.bass_utils import run_bass_kernel_spmd as _run

    a = {n: np.asarray(v) for n, v in inputs.items()}
    q, f, g = (lambda n: a["L0_attn_a_" + n]), (lambda n: a["L0_ffn_" + n]), (lambda n: a["L0_attn_b_" + n])
    c, s, m = (lambda n: a["L1_attn_a_" + n]), (lambda n: a["L1_attn_b_" + n]), (lambda n: a["L1_ffn_" + n])
    stages = lambda w: w.reshape(10, 512, 4).transpose(0, 2, 1)
    col = lambda t: t.reshape(4, 128).T
    lay = lambda t: t.reshape(64, 4, 32).transpose(1, 2, 0).reshape(128, 64)
    par, before, own = delta_constants()
    fwd, inv, index, chan = conv_constants()
    sel, sign = attention_constants()
    laid = dict(
        x=q("x"), ident=np.eye(128, dtype=np.float32),
        w_qk=np.concatenate([q("Wq").T, q("Wk").T], 1), w_vb=np.concatenate([q("Wv").T, q("Wbeta").T], 1),
        d_wo=q("Wo").T, rms_w=q("rms_weight").reshape(2, 128).T, par=par, before=before, own=own,
        w_exp=f("W_exp"), b_exp=f("b_exp"), w_con_t=f("W_con").T, up_w=stages(f("up_weights")),
        down_w=stages(f("down_weights").transpose(0, 1, 3, 2))[::-1],
        up_bias=f("up_bias").reshape(8, 128).T, b_con=f("b_con"), down_bias=f("down_bias"),
        wq_p=pad_heads(g("wq").T), wk_p=pad_heads(g("wk").T), bq_p=col(pad_heads(g("bq"), 17)),
        bk_p=col(pad_heads(g("bk"), 16)), wv=g("wv").T, bv=g("bv"), a_wo=g("wo").T, bo=g("bo"),
        sel=sel, sign=sign,
        fwd=fwd, inv=inv, conv_wt=c("W").T, conv_bias=c("b"),
        modes=np.stack([lay(np.repeat(c("log_dt")[:, None], 32, 1)), lay(c("log_A_real")),
                        lay(c("A_imag")), lay(c("C_real")), lay(c("C_imag"))]),
        index=index, chan=chan,
        weight_t=m("weight").T, gate_t=m("gate_w").T, u_t=m("lora_U").reshape(128, 256).T,
        v=m("lora_V").transpose(0, 2, 1).reshape(128, 256),
        w_in=s("W_in"), conv_w=s("conv_w").reshape(6, 128, 4).transpose(1, 0, 2),
        conv_b=s("conv_b").reshape(6, 128).T, dt_bias=s("dt_bias"), a_log=s("A_log"),
        norm_w=s("norm_w").reshape(4, 128).T, w_out=s("W_out"),
        upto=np.triu(np.ones((128, 128), np.float32)))

    nc = _bacc.Bacc("TRN2", target_bir_lowering=False, num_devices=1)
    arrays, args = {}, {}
    for name, value in laid.items():
        arrays[f"in_{name}_dram"] = np.ascontiguousarray(value)
        args[name] = nc.dram_tensor(f"in_{name}_dram", value.shape, _mybir.dt.from_np(value.dtype),
                                    kind="ExternalInput").ap()
    args["out"] = nc.dram_tensor("out_0_dram", (8, 512, 256), _mybir.dt.from_np(np.dtype("float32")),
                                 kind="ExternalOutput").ap()
    hybrid_layers_program(nc, **args)
    r = _run(nc, [arrays], core_ids=[0])
    return r.results[0]["out_0_dram"]
```

```python
from contextlib import ExitStack

import concourse.bass as bass
from concourse import mybir

ALU = mybir.AluOpType
ACT = mybir.ActivationFunctionType
F32 = mybir.dt.float32
AX = mybir.AxisListType

P = 128
B, S, D = 8, 512, 256
TPB = S // P
NT = B * TPB
KD = D // P
HID = 1024
NSTAGE = 10
EPS_LN = 1e-5


class Core:

    def __init__(self, nc, ctx):
        self.nc, self.ctx, self.sems = nc, ctx, []
        sb = self.sbuf
        self.X = sb("X", [P, NT, D])
        self.bn = sb("bn", [P, NT, 6])
        self.mv = sb("mv", [P, NT, 2])
        self.rstd = sb("rstd", [P, NT])
        self.shift = sb("shift", [P, NT])
        self.ident = sb("ident", [P, P])
        self.eps = sb("eps", [P, 1])
        self.ones = sb("ones", [P, P])
        self.begun = self.sem("begun")
        self.passed = self.sem("passed")
        self.sems = []

    def apart(self, eng):
        eng.wait_ge(self.begun, 1)

    def behind(self, eng):
        eng.sem_inc(self.passed, 1)

    def sbuf(self, name, shape, ctx=None):
        return (ctx or self.ctx).enter_context(self.nc.sbuf_tensor(name, shape, F32))

    def psum(self, name, shape, ctx=None):
        return (ctx or self.ctx).enter_context(self.nc.psum_tensor(name, shape, F32))

    def sem(self, name, ctx=None):
        handle = self.nc.alloc_semaphore(name)
        self.sems.append(handle)
        return handle

    def clear_semaphores(self):
        self.nc.all_engine_barrier()
        self.nc.clear_and_free_semaphores(self.sems)
        self.nc.all_engine_barrier()
        self.sems = []


def spread(ap, shape, axis):
    return ap.unsqueeze(axis).broadcast_to(shape)


def start(nc, core, x, ident):
    with ExitStack() as ctx:
        x_in = [core.sem(f"st_x_in{b}") for b in range(2)]
        ident_in = core.sem("st_ident_in")
        const_done = core.sem("st_const_done")
        block = ctx.enter_context(nc.Block())

        @block.sync
        def _(sp):
            xt = x.rearrange("b (t p) d -> p (b t) d", p=P)
            for h in range(2):
                sp.dma_start(core.X[:, h * NT // 2:(h + 1) * NT // 2, :],
                             xt[:, h * NT // 2:(h + 1) * NT // 2, :]).then_inc(x_in[h], 16)
            sp.dma_start(core.ident[:], ident).then_inc(ident_in, 16)
            sp.wait_ge(ident_in, 16)

        @block.gpsimd
        def _(pool):
            nc.gpsimd.memset(core.ones[:], 1.0)
            nc.gpsimd.memset(core.eps[:], EPS_LN).then_inc(const_done, 1)
            pool.wait_ge(const_done, 1)
            pool.sem_inc(core.begun, 1)

        @block.vector
        def _(dve):
            for t in range(NT):
                if t % (NT // 2) == 0:
                    dve.wait_ge(x_in[t // (NT // 2)], 16)
                nc.vector.bn_stats(core.bn[:, t, :], core.X[:, t, :])


def row_scales(nc, core, tag):
    with ExitStack() as ctx:
        mv_done = core.sem(f"{tag}_mv_done")
        root_done = core.sem(f"{tag}_root_done")
        rstd_done = core.sem(f"{tag}_rstd_done")
        block = ctx.enter_context(nc.Block())

        @block.scalar
        def _(act):
            act.wait_ge(mv_done, 1)
            nc.scalar.activation(core.rstd[:], core.mv[:, :, 1], ACT.Sqrt,
                                 bias=core.eps[:]).then_inc(root_done, 1)

        @block.vector
        def _(dve):
            for t in range(NT):
                last = nc.vector.bn_aggr(core.mv[:, t, :], core.bn[:, t, :])
            last.then_inc(mv_done, 1)
            dve.wait_ge(root_done, 1)
            nc.vector.reciprocal(core.rstd[:], core.rstd[:]).then_inc(rstd_done, 1)
            dve.wait_ge(rstd_done, 1)
            nc.vector.scalar_tensor_tensor(core.shift[:], core.mv[:, :, 0], -1.0, core.rstd[:],
                                           ALU.mult, ALU.mult)


class Butterfly:

    def __init__(self, nc, core, sources):
        self.sources = sources
        self.up = core.sbuf("bf_up", [P, KD, HID])
        self.down = core.sbuf("bf_down", [P, HID // P, D])
        self.bias_h = core.sbuf("bf_bias_h", [P, HID // P])
        self.bias_y = core.sbuf("bf_bias_y", [P, D])
        self.loaded = core.sem("bf_loaded")
        self.stage_in = [core.sem(f"bf_stage_in{i}") for i in range(2)]
        self.stage_used = core.sem("bf_stage_used")
        self.zeroed = core.sem("bf_zeroed")
        self.step = core.sem("bf_step")

    def allocate_folding(self, core, ctx):
        self.up_b = core.sbuf("bf_up_b", [P, 1, HID], ctx)
        self.down_t = core.sbuf("bf_down_t", [P, KD, HID], ctx)

    def allocate(self, core, ctx):
        self.w = core.sbuf("bf_w", [P, 2, 4, HID // 2], ctx)
        self.t = core.sbuf("bf_t", [P, 4, 3, HID // 2], ctx)

    def load(self, sp):
        w_exp, b_exp, w_con_t, up_w, down_w = self.sources
        sp.dma_start(self.up[:], w_exp.rearrange("(k p) h -> p k h", p=P)).then_inc(self.loaded, 16)
        sp.dma_start(self.down_t[:], w_con_t.rearrange("(k p) h -> p k h", p=P)).then_inc(self.loaded, 16)
        sp.wait_ge(self.zeroed, 1)
        sp.dma_start(self.up_b[0:1, 0, :], b_exp.unsqueeze(0)).then_inc(self.loaded, 16)
        for n in range(2 * NSTAGE):
            if n >= 2:
                sp.wait_ge(self.stage_used, n - 1)
            src = (up_w if n < NSTAGE else down_w)[n % NSTAGE]
            sp.dma_start(self.w[:, n % 2], src.unsqueeze(0).broadcast_to([P, 4, HID // 2])).then_inc(
                self.stage_in[n % 2], 16)

    def work(self, nc, eng):
        e = nc.gpsimd
        e.memset(self.up_b[:], 0.0).then_inc(self.zeroed, 1)
        eng.wait_ge(self.loaded, 48)
        n_step = 0
        for n in range(2 * NSTAGE):
            up = n < NSTAGE
            rows = [self.up[:, 0, :], self.up[:, 1, :], self.up_b[:, 0, :]] if up else [
                self.down_t[:, 0, :], self.down_t[:, 1, :]]
            s = 1 << (n if up else 2 * NSTAGE - 1 - n)
            nb = HID // (2 * s)
            eng.wait_ge(self.stage_in[n % 2], 16 * (n // 2 + 1))
            for r, row in enumerate(rows):
                v = row.rearrange("p (n two s) -> p n two s", two=2, s=s)
                for i in range(4):
                    w = self.w[:, n % 2, i, :].rearrange("p (n s) -> p n s", s=s)
                    t = self.t[:, i, r, :].rearrange("p (n s) -> p n s", s=s)
                    e.tensor_tensor(t, v[:, :, i % 2, :], w, ALU.mult).then_inc(self.step, 1)
                    n_step += 1
            eng.wait_ge(self.step, n_step)
            for r, row in enumerate(rows):
                v = row.rearrange("p (n two s) -> p n two s", two=2, s=s)
                for o in range(2):
                    t0 = self.t[:, 2 * o, r, :].rearrange("p (n s) -> p n s", s=s)
                    t1 = self.t[:, 2 * o + 1, r, :].rearrange("p (n s) -> p n s", s=s)
                    last = e.tensor_tensor(v[:, :, o, :], t0, t1, ALU.add).then_inc(self.step, 1)
                    n_step += 1
            eng.wait_ge(self.step, n_step)
            eng.sem_inc(self.stage_used, 1)


def ffn_prepare(nc, core, bf, up_bias, b_con, down_bias):
    with ExitStack() as ctx:
        bias_in = core.sbuf("fp_bias_in", [P, 2, D], ctx)
        psT = [core.psum(f"fp_psT{i}", [P, 512], ctx) for i in range(2)]
        psB = core.psum("fp_psB", [P, 512], ctx)
        loaded = core.sem("fp_loaded")
        ub_in = core.sem("fp_ub_in")
        tr_done = core.sem("fp_tr_done")
        ev_done = core.sem("fp_ev_done")
        row_done = core.sem("fp_row_done")
        block = ctx.enter_context(nc.Block())
        NH = HID // P

        @block.sync
        def _(sp):
            sp.dma_start(bf.bias_h[:], up_bias).then_inc(ub_in, 16)
            sp.dma_start(bias_in[:, 0, :], b_con.unsqueeze(0).broadcast_to([P, D])).then_inc(loaded, 16)
            sp.dma_start(bias_in[:, 1, :], down_bias.unsqueeze(0).broadcast_to([P, D])).then_inc(loaded, 16)

        @block.tensor
        def _(pe):
            for g in range(NH // 2):
                if g >= 2:
                    pe.wait_ge(ev_done, g - 1)
                for m in range(2):
                    for k in range(KD):
                        last = nc.tensor.transpose(
                            psT[g % 2][:, (m * KD + k) * P:(m * KD + k + 1) * P],
                            bf.down_t[:, k, (2 * g + m) * P:(2 * g + m + 1) * P], core.ident[:])
                last.then_inc(tr_done, 1)
            for m in range(NH):
                last = nc.tensor.matmul(psB[:, m:m + 1], bf.up_b[0:1, 0, m * P:(m + 1) * P],
                                        core.ones[0:1, 0:1], start=True, stop=True)
            last.then_inc(row_done, 1)

        @block.vector
        def _(dve):
            for g in range(NH // 2):
                dve.wait_ge(tr_done, g + 1)
                nc.vector.tensor_copy(bf.down[:, 2 * g:2 * g + 2, :],
                                      psT[g % 2][:].rearrange("p (m d) -> p m d", m=2)).then_inc(ev_done, 1)
            dve.wait_ge(row_done, 1)
            dve.wait_ge(ub_in, 16)
            nc.vector.tensor_tensor(bf.bias_h[:], bf.bias_h[:], psB[:, 0:NH], ALU.add)
            dve.wait_ge(loaded, 32)
            nc.vector.tensor_tensor(bf.bias_y[:], bias_in[:, 0, :], bias_in[:, 1, :], ALU.add)


def ffn_stage(nc, core, bf, tag):
    with ExitStack() as ctx:
        NH = HID // P
        xn = core.sbuf(f"{tag}_xn", [P, TPB, D], ctx)
        xnT = core.sbuf(f"{tag}_xnT", [P, 2, KD, S], ctx)
        h = core.sbuf(f"{tag}_h", [P, 2, NH, S], ctx)
        psT = [core.psum(f"{tag}_psT{i}", [P, 512], ctx) for i in range(2)]
        psH = [core.psum(f"{tag}_psH{i}", [P, 512], ctx) for i in range(2)]
        psY = [core.psum(f"{tag}_psY{i}", [P, 512], ctx) for i in range(2)]
        xn_done = core.sem(f"{tag}_xn_done")
        xb_done = core.sem(f"{tag}_xb_done")
        tr_done = core.sem(f"{tag}_tr_done")
        xnT_done = core.sem(f"{tag}_xnT_done")
        h_ps = core.sem(f"{tag}_h_ps")
        h_done = core.sem(f"{tag}_h_done")
        y_ps = core.sem(f"{tag}_y_ps")
        x_done = core.sem(f"{tag}_x_done")
        block = ctx.enter_context(nc.Block())

        @block.tensor
        def _(pe):
            with pe.Fori(0, B // 2) as b2:
                for u in range(2):
                    at = lambda per, c: b2 * (2 * per) + (u * per + c)
                    for k in range(KD):
                        pe.wait_ge(xnT_done, at(KD, 0))
                        for j in range(TPB):
                            if k == 0:
                                pe.wait_ge(xn_done, at(TPB, j + 1))
                            last = nc.tensor.transpose(psT[k][:, j * P:(j + 1) * P],
                                                       xn[:, j, k * P:(k + 1) * P], core.ident[:])
                        last.then_inc(tr_done, 1)
                    pe.wait_ge(xnT_done, at(KD, KD))
                    for m in range(NH):
                        if m >= 2:
                            pe.wait_ge(h_done, at(NH, m - 1))
                        for k in range(KD):
                            last = nc.tensor.matmul(psH[m % 2][:], bf.up[:, k, m * P:(m + 1) * P],
                                                    xnT[:, u, k, :], start=(k == 0), stop=(k == KD - 1))
                        last.then_inc(h_ps, 1)
                    pe.wait_ge(h_done, at(NH, NH))
                    for j in range(TPB):
                        pe.wait_ge(x_done, at(TPB, max(j - 1, 0)))
                        for m in range(NH):
                            last = nc.tensor.matmul(psY[j % 2][:, 0:D], h[:, u, m, j * P:(j + 1) * P],
                                                    bf.down[:, m, :], start=(m == 0), stop=(m == NH - 1))
                        last.then_inc(y_ps, 1)

        @block.scalar
        def _(act):
            with act.Fori(0, B // 2) as b2:
                for u in range(2):
                    at = lambda per, c: b2 * (2 * per) + (u * per + c)
                    act.wait_ge(tr_done, at(KD, 0))
                    core.apart(act)
                    for j in range(TPB):
                        t = at(TPB, j)
                        nc.scalar.activation(xn[:, j, :], core.X[:, t, :], ACT.Identity,
                                             bias=core.shift[:, bass.ds(t, 1)],
                                             scale=core.rstd[:, bass.ds(t, 1)]).then_inc(xn_done, 1)
                    for k in range(KD):
                        act.wait_ge(tr_done, at(KD, k + 1))
                        nc.scalar.activation(xnT[:, u, k, :], psT[k][:], ACT.Identity).then_inc(xnT_done, 1)
                    for m in range(NH):
                        act.wait_ge(h_ps, at(NH, m + 1))
                        nc.scalar.activation(h[:, u, m, :], psH[m % 2][:], ACT.Gelu,
                                             bias=bf.bias_h[:, m:m + 1]).then_inc(h_done, 1)

        @block.vector
        def _(dve):
            with dve.Fori(0, B // 2) as b2:
                for u in range(2):
                    for j in range(TPB):
                        at = lambda per, c: b2 * (2 * per) + (u * per + c)
                        t = at(TPB, j)
                        dve.wait_ge(xn_done, at(TPB, j + 1))
                        nc.vector.tensor_tensor(core.X[:, t, :], core.X[:, t, :], bf.bias_y[:], ALU.add).then_inc(xb_done, 1)
                        dve.wait_ge(y_ps, at(TPB, j + 1))
                        dve.wait_ge(xb_done, at(TPB, j + 1))
                        nc.vector.tensor_tensor(core.X[:, t, :], psY[j % 2][:, 0:D], core.X[:, t, :],
                                                ALU.add).then_inc(x_done, 1)
                        dve.wait_ge(x_done, at(TPB, j + 1))
                        core.apart(dve)
                        nc.vector.bn_stats(core.bn[:, t, :], core.X[:, t, :])


def finish(nc, core, out):
    with ExitStack() as ctx:
        stored = core.sem("fin_stored")
        block = ctx.enter_context(nc.Block())

        @block.sync
        def _(sp):
            ot = out.rearrange("b (t p) d -> p (b t) d", p=P)
            sp.dma_start(ot[:, 0:NT // 2, :], core.X[:, 0:NT // 2, :]).then_inc(stored, 16)
            sp.dma_start(ot[:, NT // 2:, :], core.X[:, NT // 2:, :]).then_inc(stored, 16)
            sp.wait_ge(stored, 32)
E_LORA, R_LORA = 8, 16


def at_batch(b2, u):
    return lambda per, c: b2 * (2 * per) + (u * per + c)


class MixtureWeights:

    def __init__(self, nc, core):
        ER = E_LORA * R_LORA
        self.tg = core.sbuf("mx_tg", [P, KD, ER + E_LORA])
        self.base = core.sbuf("mx_base", [P, KD, D])
        self.v = core.sbuf("mx_v", [P, D])
        self.loaded = core.sem("mx_loaded")

    def load(self, sp, weight_t, gate_t, u_t, v):
        ER = E_LORA * R_LORA
        sp.dma_start(self.tg[:, :, 0:ER], u_t.rearrange("(k p) n -> p k n", p=P)).then_inc(self.loaded, 16)
        sp.dma_start(self.tg[:, :, ER:], gate_t.rearrange("(k p) n -> p k n", p=P)).then_inc(self.loaded, 16)
        sp.dma_start(self.base[:], weight_t.rearrange("(k p) n -> p k n", p=P)).then_inc(self.loaded, 16)
        sp.dma_start(self.v[:], v).then_inc(self.loaded, 16)


def mixture_stage(nc, core, mx, tag):
    with ExitStack() as ctx:
        ER = E_LORA * R_LORA
        G = E_LORA
        xn = core.sbuf(f"{tag}_xn", [P, TPB, D], ctx)
        xnT = core.sbuf(f"{tag}_xnT", [P, 2, KD, S], ctx)
        gate = core.sbuf(f"{tag}_gate", [P, TPB, G], ctx)
        gmax = core.sbuf(f"{tag}_gmax", [P, TPB], ctx)
        gsum = core.sbuf(f"{tag}_gsum", [P, TPB], ctx)
        tg = core.sbuf(f"{tag}_tg", [P, TPB, ER], ctx)
        tgT = core.sbuf(f"{tag}_tgT", [P, TPB * P], ctx)
        psT = [core.psum(f"{tag}_psT{i}", [P, 512], ctx) for i in range(2)]
        psG = core.psum(f"{tag}_psG", [P, 2, 512], ctx)
        psB = core.psum(f"{tag}_psB", [P, TPB, 512], ctx)
        xn_done = core.sem(f"{tag}_xn_done")
        tr_done = core.sem(f"{tag}_tr_done")
        xnT_done = core.sem(f"{tag}_xnT_done")
        tg_ps = core.sem(f"{tag}_tg_ps")
        shifted = core.sem(f"{tag}_shifted")
        exp_done = core.sem(f"{tag}_exp_done")
        gate_step = core.sem(f"{tag}_gate_step")
        tg_done = core.sem(f"{tag}_tg_done")
        tgT_ps = core.sem(f"{tag}_tgT_ps")
        tgT_done = core.sem(f"{tag}_tgT_done")
        y_ps = core.sem(f"{tag}_y_ps")
        x_done = core.sem(f"{tag}_x_done")
        pair = [psG[:, g, 0:2 * (ER + G)].rearrange("p (t n) -> p t n", t=2) for g in range(2)]
        block = ctx.enter_context(nc.Block())

        @block.scalar
        def _(act):
            with act.Fori(0, B // 2) as b2:
                for u in range(2):
                    at = at_batch(b2, u)
                    act.wait_ge(tr_done, at(KD, 0))
                    core.apart(act)
                    for j in range(TPB):
                        t = at(TPB, j)
                        nc.scalar.activation(xn[:, j, :], core.X[:, t, :], ACT.Identity,
                                             bias=core.shift[:, bass.ds(t, 1)],
                                             scale=core.rstd[:, bass.ds(t, 1)]).then_inc(xn_done, 1)
                    for k in range(KD):
                        act.wait_ge(tr_done, at(KD, k + 1))
                        nc.scalar.activation(xnT[:, u, k, :], psT[k][:], ACT.Identity).then_inc(xnT_done, 1)
                    act.wait_ge(shifted, at(1, 1))
                    nc.scalar.activation(gate[:], gate[:], ACT.Exp).then_inc(exp_done, 1)
                    act.wait_ge(tgT_ps, at(1, 1))
                    nc.scalar.activation(tgT[:], psT[0][:], ACT.Identity).then_inc(tgT_done, 1)

        @block.tensor
        def _(pe):
            pe.wait_ge(mx.loaded, 64)
            with pe.Fori(0, B // 2) as b2:
                for u in range(2):
                    at = at_batch(b2, u)
                    pe.wait_ge(tgT_done, at(1, 0))
                    for k in range(KD):
                        for j in range(TPB):
                            if k == 0:
                                pe.wait_ge(xn_done, at(TPB, j + 1))
                            last = nc.tensor.transpose(psT[k][:, j * P:(j + 1) * P],
                                                       xn[:, j, k * P:(k + 1) * P], core.ident[:])
                        last.then_inc(tr_done, 1)
                    pe.wait_ge(xnT_done, at(KD, KD))
                    pe.wait_ge(tg_done, at(2, 0))
                    for j in range(TPB):
                        for k in range(KD):
                            last = nc.tensor.matmul(pair[j // 2][:, j % 2, :], xnT[:, u, k, j * P:(j + 1) * P],
                                                    mx.tg[:, k, :], start=(k == 0), stop=(k == KD - 1))
                    last.then_inc(tg_ps, 1)
                    for j in range(TPB):
                        pe.wait_ge(x_done, at(TPB, 0))
                        for k in range(KD):
                            nc.tensor.matmul(psB[:, j, 0:D], xnT[:, u, k, j * P:(j + 1) * P],
                                             mx.base[:, k, :], start=(k == 0), stop=False)
                    for j in range(TPB):
                        pe.wait_ge(tg_done, at(2, j // 2 + 1))
                        last = nc.tensor.transpose(psT[0][:, j * P:(j + 1) * P], tg[:, j, :], core.ident[:])
                    last.then_inc(tgT_ps, 1)
                    pe.wait_ge(tgT_done, at(1, 1))
                    for j in range(TPB):
                        nc.tensor.matmul(psB[:, j, 0:D], tgT[:, j * P:(j + 1) * P], mx.v[:],
                                         start=False, stop=True).then_inc(y_ps, 1)

        @block.vector
        def _(dve):
            with dve.Fori(0, B // 2) as b2:
                for u in range(2):
                    at = at_batch(b2, u)
                    dve.wait_ge(tg_ps, at(1, 1))
                    for g in range(2):
                        nc.vector.tensor_reduce(gmax[:, 2 * g:2 * g + 2], pair[g][:, :, ER:], AX.X,
                                                ALU.max).then_inc(gate_step, 1)
                    for g in range(2):
                        dve.wait_ge(gate_step, at(6, g + 1))
                        last = nc.vector.tensor_tensor(gate[:, 2 * g:2 * g + 2, :], pair[g][:, :, ER:],
                                                       spread(gmax[:, 2 * g:2 * g + 2], [P, 2, G], 2), ALU.subtract)
                    last.then_inc(shifted, 1)
                    dve.wait_ge(exp_done, at(1, 1))
                    nc.vector.tensor_reduce(gsum[:], gate[:], AX.X, ALU.add).then_inc(gate_step, 1)
                    dve.wait_ge(gate_step, at(6, 3))
                    nc.vector.reciprocal(gsum[:], gsum[:]).then_inc(gate_step, 1)
                    dve.wait_ge(gate_step, at(6, 4))
                    nc.vector.scalar_tensor_tensor(gate[:], gate[:], 1.0 / R_LORA,
                                                   spread(gsum[:], [P, TPB, G], 2),
                                                   ALU.mult, ALU.mult).then_inc(gate_step, 2)
                    dve.wait_ge(gate_step, at(6, 6))
                    for j in range(TPB):
                        last = nc.vector.tensor_tensor(
                            tg[:, j, :].rearrange("p (e r) -> p e r", e=G),
                            pair[j // 2][:, j % 2, 0:ER].rearrange("p (e r) -> p e r", e=G),
                            spread(gate[:, j, :], [P, G, R_LORA], 2), ALU.mult)
                        if j % 2:
                            last.then_inc(tg_done, 1)
                    for j in range(TPB):
                        t = at(TPB, j)
                        dve.wait_ge(y_ps, at(TPB, j + 1))
                        nc.vector.tensor_tensor(core.X[:, t, :], psB[:, j, 0:D], core.X[:, t, :],
                                                ALU.add).then_inc(x_done, 1)
                        dve.wait_ge(x_done, at(TPB, j + 1))
                        core.apart(dve)
                        nc.vector.bn_stats(core.bn[:, t, :], core.X[:, t, :])
NMODE = 32
CPT = P // NMODE
NMT = D // CPT
NF = S // P
ROUND = 1.5 * 2.0 ** 23
PI = 3.141592653589793


class LongConv:

    def __init__(self, nc, core, ctx):
        self.fwd = core.sbuf("lc_fwd", [P, TPB, 2 * S], ctx)
        self.inv = core.sbuf("lc_inv", [P, 2 * NF, S], ctx)
        self.w = core.sbuf("lc_w", [P, KD, D], ctx)
        self.b = core.sbuf("lc_b", [P, D], ctx)
        self.k_re = core.sbuf("lc_k_re", [P, NF, D], ctx)
        self.k_im = core.sbuf("lc_k_im", [P, NF, D], ctx)
        self.k_re2 = core.sbuf("lc_k_re2", [P, NF, D], ctx)
        self.loaded = core.sem("lc_loaded")

    def load(self, sp, fwd, inv, w_t, b):
        sp.dma_start(self.fwd[:], fwd.rearrange("(k p) n -> p k n", p=P)).then_inc(self.loaded, 16)
        sp.dma_start(self.inv[:], inv.rearrange("(k p) n -> p k n", p=P)).then_inc(self.loaded, 16)
        sp.dma_start(self.w[:], w_t.rearrange("(k p) n -> p k n", p=P)).then_inc(self.loaded, 16)
        sp.dma_start(self.b[:], b.unsqueeze(0).broadcast_to([P, D])).then_inc(self.loaded, 16)


def conv_kernel(nc, core, lc, modes, index, conv_in):
    with ExitStack() as ctx:
        GRP = 16
        NG = NMT // GRP
        par = core.sbuf("ck_par", [P, 5, NMT], ctx)
        idx = core.sbuf("ck_idx", [P, P + TPB], ctx)
        chan = core.sbuf("ck_chan", [P, CPT], ctx)
        v = core.sbuf("ck_v", [P, 16, NMT], ctx)
        f_ph = core.sbuf("ck_f_ph", [P, 4, NMT * TPB], ctx)
        f_re = core.sbuf("ck_f_re", [P, NMT, TPB], ctx)
        f_im = core.sbuf("ck_f_im", [P, NMT, TPB], ctx)
        fm = core.sbuf("ck_fm", [P, 2, NMT, TPB * CPT], ctx)
        ph = core.sbuf("ck_ph", [P, GRP, P], ctx)
        rnd = core.sbuf("ck_rnd", [P, GRP, P], ctx)
        mag = core.sbuf("ck_mag", [P, GRP, P], ctx)
        g_re = core.sbuf("ck_g_re", [P, GRP, P], ctx)
        g_im = core.sbuf("ck_g_im", [P, GRP, P], ctx)
        kT = core.sbuf("ck_kT", [P, TPB, D], ctx)
        half_pi = core.sbuf("ck_half_pi", [P, 1], ctx)
        psK = core.psum("ck_psK", [P, 2, 512], ctx)
        psF = core.psum("ck_psF", [P, 2, 512], ctx)
        loaded = core.sem("ck_loaded")
        vec = core.sem("ck_vec")
        act_n = core.sem("ck_act")
        pe_g = core.sem("ck_pe_g")
        kT_done = core.sem("ck_kT_done")
        f_ps = core.sem("ck_f_ps")
        f_out = core.sem("ck_f_out")
        block = ctx.enter_context(nc.Block())
        LDT, LAR, AIM, CRE, CIM = range(5)
        (DT, AR, DR, DI, MAG, SIN, COS, TURN, RN, FR, ABS, T0, T1, NRE, NIM, DEN) = range(16)

        @block.sync
        def _(sp):
            sp.dma_start(par[:], modes.rearrange("a p t -> p a t")).then_inc(loaded, 16)
            sp.dma_start(idx[:], index.unsqueeze(0).broadcast_to([P, P + TPB])).then_inc(loaded, 16)
            sp.dma_start(chan[:], conv_in).then_inc(loaded, 16)


        @block.vector
        def _(dve):
            n = [0]

            def step(ins):
                n[0] += 1
                ins.then_inc(vec, 1)
                dve.wait_ge(vec, n[0])

            tt = nc.vector.tensor_tensor
            step(nc.vector.memset(half_pi[:], PI / 2))
            dve.wait_ge(loaded, 48)
            dve.wait_ge(act_n, 2)
            step(nc.vector.scalar_tensor_tensor(v[:, DR, :], v[:, AR, :], -1.0, v[:, DT, :], ALU.mult, ALU.mult))
            step(tt(v[:, DI, :], par[:, AIM, :], v[:, DT, :], ALU.mult))
            step(nc.vector.tensor_scalar(v[:, TURN, :], v[:, DI, :], 1 / (2 * PI), None, ALU.mult))
            step(nc.vector.tensor_scalar(v[:, RN, :], v[:, TURN, :], ROUND, -ROUND, ALU.add, ALU.add))
            step(tt(v[:, FR, :], v[:, TURN, :], v[:, RN, :], ALU.subtract))
            dve.wait_ge(act_n, 6)
            step(tt(v[:, T0, :], v[:, MAG, :], v[:, COS, :], ALU.mult))
            step(nc.vector.tensor_scalar(v[:, T0, :], v[:, T0, :], -1.0, None, ALU.add))
            step(tt(v[:, T1, :], v[:, MAG, :], v[:, SIN, :], ALU.mult))

            def cmul(o_re, o_im, a_re, a_im, b_re, b_im, s0, s1):
                step(tt(s0, a_re, b_re, ALU.mult))
                step(tt(s1, a_im, b_im, ALU.mult))
                step(tt(o_re, s0, s1, ALU.subtract))
                step(tt(s0, a_re, b_im, ALU.mult))
                step(tt(s1, a_im, b_re, ALU.mult))
                step(tt(o_im, s0, s1, ALU.add))

            cmul(v[:, NRE, :], v[:, NIM, :], par[:, CRE, :], par[:, CIM, :], v[:, T0, :], v[:, T1, :],
                 v[:, RN, :], v[:, FR, :])
            step(nc.vector.tensor_scalar(v[:, AR, :], v[:, AR, :], -1.0, None, ALU.mult))
            step(nc.vector.tensor_scalar(v[:, ABS, :], par[:, AIM, :], -1.0, None, ALU.mult))
            step(tt(v[:, T0, :], v[:, AR, :], v[:, AR, :], ALU.mult))
            step(tt(v[:, T1, :], par[:, AIM, :], par[:, AIM, :], ALU.mult))
            step(tt(v[:, DEN, :], v[:, T0, :], v[:, T1, :], ALU.add))
            step(nc.vector.reciprocal(v[:, DEN, :], v[:, DEN, :]))
            cmul(v[:, T0, :], v[:, T1, :], v[:, NRE, :], v[:, NIM, :], v[:, AR, :], v[:, ABS, :],
                 v[:, RN, :], v[:, FR, :])
            for o, i in ((NRE, T0), (NIM, T1)):
                step(nc.vector.scalar_tensor_tensor(v[:, o, :], v[:, i, :], 2.0, v[:, DEN, :], ALU.mult, ALU.mult))
            f3 = [f_ph[:, q, :].rearrange("p (t i) -> p t i", i=TPB) for q in range(4)]
            ix = spread(idx[:, P:], [P, NMT, TPB], 1)
            step(tt(f3[0], spread(v[:, TURN, :], [P, NMT, TPB], 2), ix, ALU.mult))
            step(nc.vector.tensor_scalar(f_ph[:, 1, :], f_ph[:, 0, :], ROUND, -ROUND, ALU.add, ALU.add))
            step(tt(f_ph[:, 0, :], f_ph[:, 0, :], f_ph[:, 1, :], ALU.subtract))
            step(tt(f3[1], spread(v[:, DR, :], [P, NMT, TPB], 2), ix, ALU.mult))
            assert n[0] == 33, n
            dve.wait_ge(act_n, 10)
            step(tt(f_ph[:, 2, :], f_ph[:, 2, :], f_ph[:, 1, :], ALU.mult))
            step(tt(f_ph[:, 3, :], f_ph[:, 3, :], f_ph[:, 1, :], ALU.mult))
            s0 = ph[:, 0:2, :].rearrange("p a (t i) -> p (a t) i", i=TPB)
            s1 = rnd[:, 0:2, :].rearrange("p a (t i) -> p (a t) i", i=TPB)
            cmul(f_re[:], f_im[:], spread(v[:, NRE, :], [P, NMT, TPB], 2), spread(v[:, NIM, :], [P, NMT, TPB], 2),
                 f3[3], f3[2], s0, s1)
            step(nc.vector.tensor_scalar(f_im[:], f_im[:], -1.0, None, ALU.mult))
            for c in range(CPT):
                for q, f in ((0, f_re), (1, f_im)):
                    dst = fm[:, q].rearrange("p t (i c) -> p t i c", c=CPT)[:, :, :, c]
                    step(nc.vector.tensor_scalar(dst, f[:], chan[:, c:c + 1], None, ALU.mult))
            assert n[0] == 50, n
            jx = spread(idx[:, 0:P], [P, GRP, P], 1)
            for g in range(NG):
                t = slice(g * GRP, (g + 1) * GRP)
                step(tt(ph[:], spread(v[:, TURN, t], [P, GRP, P], 2), jx, ALU.mult))
                step(nc.vector.tensor_scalar(rnd[:], ph[:], ROUND, -ROUND, ALU.add, ALU.add))
                step(tt(ph[:], ph[:], rnd[:], ALU.subtract))
                step(tt(mag[:], spread(v[:, DR, t], [P, GRP, P], 2), jx, ALU.mult))
                if g:
                    dve.wait_ge(pe_g, g)
                dve.wait_ge(act_n, 10 + 4 * (g + 1))
                step(tt(g_im[:], g_im[:], mag[:], ALU.mult))
                step(tt(g_re[:], g_re[:], mag[:], ALU.mult))
            dve.wait_ge(pe_g, NG)
            for h in range(2):
                t = NMT // 2
                dst = kT[:, :, h * D // 2:(h + 1) * D // 2].rearrange("p i (t c) -> p i t c", c=CPT)
                src = psK[:, h, :].rearrange("p (t i c) -> p i t c", i=TPB, c=CPT)
                for i in range(TPB):
                    last = nc.vector.tensor_copy(dst[:, i], src[:, i])
            last.then_inc(kT_done, 1)
            for m in range(2 * NF):
                dst = (lc.k_re if m < NF else lc.k_im)[:, m % NF, :]
                dve.wait_ge(f_ps, m + 1)
                nc.vector.tensor_copy(dst, psF[:, m % 2, 0:D]).then_inc(f_out, 1)
            dve.wait_ge(f_out, 2 * NF)
            step(nc.vector.tensor_copy(lc.k_re2[:], lc.k_re[:]))
            step(nc.vector.tensor_copy(lc.k_re2[0:1, 0, :], lc.k_im[0:1, 0, :]))
            step(nc.vector.memset(lc.k_im[0:1, 0, :], 0.0))

        @block.scalar
        def _(act):
            a = nc.scalar.activation
            act.wait_ge(loaded, 48)
            a(v[:, DT, :], par[:, LDT, :], ACT.Exp).then_inc(act_n, 1)
            a(v[:, AR, :], par[:, LAR, :], ACT.Exp).then_inc(act_n, 1)
            act.wait_ge(vec, 6)
            a(v[:, MAG, :], v[:, DR, :], ACT.Exp).then_inc(act_n, 1)
            a(v[:, SIN, :], v[:, FR, :], ACT.Sin, scale=2 * PI).then_inc(act_n, 1)
            a(v[:, ABS, :], v[:, FR, :], ACT.Abs).then_inc(act_n, 1)
            act.wait_ge(act_n, 5)
            a(v[:, COS, :], v[:, ABS, :], ACT.Sin, scale=-2 * PI, bias=half_pi[:]).then_inc(act_n, 1)
            act.wait_ge(vec, 33)
            a(f_ph[:, 2, :], f_ph[:, 0, :], ACT.Sin, scale=2 * PI).then_inc(act_n, 1)
            a(f_ph[:, 3, :], f_ph[:, 0, :], ACT.Abs).then_inc(act_n, 1)
            act.wait_ge(act_n, 8)
            a(f_ph[:, 3, :], f_ph[:, 3, :], ACT.Sin, scale=-2 * PI, bias=half_pi[:]).then_inc(act_n, 1)
            a(f_ph[:, 1, :], f_ph[:, 1, :], ACT.Exp).then_inc(act_n, 1)
            for g in range(NG):
                act.wait_ge(vec, 50 + 6 * g + 4)
                if g:
                    act.wait_ge(pe_g, g)
                n = 10 + 4 * g
                a(g_im[:], ph[:], ACT.Sin, scale=2 * PI).then_inc(act_n, 1)
                a(g_re[:], ph[:], ACT.Abs).then_inc(act_n, 1)
                act.wait_ge(act_n, n + 2)
                a(g_re[:], g_re[:], ACT.Sin, scale=-2 * PI, bias=half_pi[:]).then_inc(act_n, 1)
                a(mag[:], mag[:], ACT.Exp).then_inc(act_n, 1)

        @block.tensor
        def _(pe):
            for g in range(NG):
                pe.wait_ge(vec, 50 + 6 * (g + 1))
                for t in range(GRP):
                    tt_ = g * GRP + t
                    h, o = tt_ // (NMT // 2), (tt_ % (NMT // 2)) * TPB * CPT
                    for q, gg in ((0, g_re), (1, g_im)):
                        last = nc.tensor.matmul(psK[:, h, o:o + TPB * CPT], gg[:, t, :], fm[:, q, tt_, :],
                                                start=(q == 0), stop=(q == 1))
                last.then_inc(pe_g, 1)
            pe.wait_ge(lc.loaded, 64)
            pe.wait_ge(kT_done, 1)
            for m in range(2 * NF):
                if m >= 2:
                    pe.wait_ge(f_out, m - 1)
                for k in range(TPB):
                    last = nc.tensor.matmul(psF[:, m % 2, 0:D], lc.fwd[:, k, m * P:(m + 1) * P], kT[:, k, :],
                                            start=(k == 0), stop=(k == TPB - 1))
                last.then_inc(f_ps, 1)


def conv_stage(nc, core, lc, tag):
    with ExitStack() as ctx:
        xn = core.sbuf(f"{tag}_xn", [P, TPB, 2, D], ctx)
        y = core.sbuf(f"{tag}_y", [P, 2 * NF, 2 * D], ctx)
        prod = core.sbuf(f"{tag}_prod", [P, 2, 4, 2 * D], ctx)
        g = core.sbuf(f"{tag}_g", [P, 2, 2 * D], ctx)
        gT = core.sbuf(f"{tag}_gT", [P, 2, 2 * KD, P], ctx)
        psF = core.psum(f"{tag}_psF", [P, 2, 2, 512], ctx)
        psY = core.psum(f"{tag}_psY", [P, 2, 512], ctx)
        psT = core.psum(f"{tag}_psT", [P, 512], ctx)
        psO = core.psum(f"{tag}_psO", [P, 512], ctx)
        xn_done = core.sem(f"{tag}_xn_done")
        f_ps = core.sem(f"{tag}_f_ps")
        prod_done = core.sem(f"{tag}_prod_done")
        y_done = core.sem(f"{tag}_y_done")
        c_ps = core.sem(f"{tag}_c_ps")
        g_done = core.sem(f"{tag}_g_done")
        gT_ps = core.sem(f"{tag}_gT_ps")
        gT_done = core.sem(f"{tag}_gT_done")
        o_ps = core.sem(f"{tag}_o_ps")
        xb_done = core.sem(f"{tag}_xb_done")
        x_done = core.sem(f"{tag}_x_done")
        block = ctx.enter_context(nc.Block())

        @block.scalar
        def _(act):
            with act.Fori(0, B // 2) as i:
                act.wait_ge(f_ps, i * NF)
                core.apart(act)
                for k in range(TPB):
                    for b in range(2):
                        t = i * (2 * TPB) + (b * TPB + k)
                        nc.scalar.activation(xn[:, k, b, :], core.X[:, t, :], ACT.Identity,
                                             bias=core.shift[:, bass.ds(t, 1)],
                                             scale=core.rstd[:, bass.ds(t, 1)]).then_inc(xn_done, 1)
                for l in range(TPB):
                    act.wait_ge(c_ps, i * TPB + (l + 1))
                    act.wait_ge(gT_ps, i * TPB + max(l - 1, 0))
                    nc.scalar.activation(g[:, l % 2, :], psY[:, l % 2, :], ACT.Gelu).then_inc(g_done, 1)
                    act.wait_ge(gT_ps, i * TPB + (l + 1))
                    nc.scalar.activation(gT[:, l % 2], psT[:].rearrange("p (a q) -> p a q", q=P),
                                         ACT.Identity).then_inc(gT_done, 1)

        @block.tensor
        def _(pe):
            with pe.Fori(0, B // 2) as i:
                for f in range(NF):
                    pe.wait_ge(prod_done, i * NF + max(f - 1, 0))
                    for c in range(2):
                        for k in range(TPB):
                            if f == 0 and c == 0:
                                pe.wait_ge(xn_done, i * (2 * TPB) + 2 * (k + 1))
                            m = c * NF + f
                            last = nc.tensor.matmul(psF[:, f % 2, c, :], lc.fwd[:, k, m * P:(m + 1) * P],
                                                    xn[:, k].rearrange("p b d -> p (b d)"),
                                                    start=(k == 0), stop=(k == TPB - 1))
                    last.then_inc(f_ps, 1)

                def project(l):
                    pe.wait_ge(g_done, i * TPB + (l + 1))
                    pe.wait_ge(gT_done, i * TPB + l)
                    for a in range(2 * KD):
                        last = nc.tensor.transpose(psT[:, a * P:(a + 1) * P], g[:, l % 2, a * P:(a + 1) * P],
                                                   core.ident[:])
                    last.then_inc(gT_ps, 1)
                    pe.wait_ge(gT_done, i * TPB + (l + 1))
                    pe.wait_ge(x_done, i * (2 * TPB) + 2 * l)
                    for b in range(2):
                        for k in range(KD):
                            last = nc.tensor.matmul(psO[:, b * D:(b + 1) * D], gT[:, l % 2, b * KD + k, :],
                                                    lc.w[:, k, :], start=(k == 0), stop=(k == KD - 1))
                    last.then_inc(o_ps, 1)

                for l in range(TPB):
                    pe.wait_ge(g_done, i * TPB + max(l - 1, 0))
                    for n, (f, c) in enumerate((f, c) for f in range(NF) for c in range(2)):
                        pe.wait_ge(y_done, i * NF + (f + 1))
                        last = nc.tensor.matmul(psY[:, l % 2, :], lc.inv[:, c * NF + f, l * P:(l + 1) * P],
                                                y[:, c * NF + f, :], start=(n == 0), stop=(n == 2 * NF - 1))
                    last.then_inc(c_ps, 1)
                    if l:
                        project(l - 1)
                project(TPB - 1)

        @block.gpsimd
        def _(pool):
            with pool.Fori(0, B // 2) as i:
                for f in range(NF):
                    pool.wait_ge(prod_done, i * NF + (f + 1))
                    if f == 0:
                        pool.wait_ge(c_ps, i * TPB)
                    p4 = prod[:, f % 2]
                    nc.gpsimd.tensor_tensor(y[:, f, :], p4[:, 0, :], p4[:, 1, :], ALU.subtract)
                    nc.gpsimd.tensor_tensor(y[:, NF + f, :], p4[:, 2, :], p4[:, 3, :], ALU.add).then_inc(y_done, 1)

        @block.vector
        def _(dve):
            with dve.Fori(0, B // 2) as i:
                for f in range(NF):
                    dve.wait_ge(y_done, i * NF + max(f - 1, 0))
                    dve.wait_ge(f_ps, i * NF + (f + 1))
                    for q, (c, kk) in enumerate(((0, lc.k_re), (1, lc.k_im), (0, lc.k_im), (1, lc.k_re2))):
                        last = nc.vector.tensor_tensor(
                            prod[:, f % 2, q, :].rearrange("p (b d) -> p b d", b=2),
                            psF[:, f % 2, c, :].rearrange("p (b d) -> p b d", b=2),
                            spread(kk[:, f, :], [P, 2, D], 1), ALU.mult)
                    last.then_inc(prod_done, 1)
                dve.wait_ge(xn_done, i * (2 * TPB) + 2 * TPB)
                for l in range(TPB):
                    for b in range(2):
                        t = i * (2 * TPB) + (b * TPB + l)
                        nc.vector.tensor_tensor(core.X[:, t, :], core.X[:, t, :], lc.b[:], ALU.add).then_inc(xb_done, 1)
                for l in range(TPB):
                    for b in range(2):
                        t = i * (2 * TPB) + (b * TPB + l)
                        n = 2 * l + b + 1
                        dve.wait_ge(xb_done, i * (2 * TPB) + n)
                        dve.wait_ge(o_ps, i * TPB + (l + 1))
                        nc.vector.tensor_tensor(core.X[:, t, :], psO[:, b * D:(b + 1) * D], core.X[:, t, :],
                                                ALU.add).then_inc(x_done, 1)
                        dve.wait_ge(x_done, i * (2 * TPB) + n)
                        core.apart(dve)
                        nc.vector.bn_stats(core.bn[:, t, :], core.X[:, t, :])


def conv_constants():
    import numpy as np

    l = np.arange(S)[:, None]
    f = np.arange(S)[None, :]
    turn = 2 * np.pi * ((l * f) % (2 * S)) / (2 * S)
    fwd = np.concatenate([np.cos(turn), -np.sin(turn)], 1)
    fwd[:, S] = (-1.0) ** np.arange(S)
    inv = fwd.T / S
    inv[0] /= 2
    inv[S] /= 2
    index = np.concatenate([np.arange(P), P * np.arange(TPB)])
    chan = np.arange(P)[:, None] // NMODE == np.arange(CPT)[None, :]
    return [np.ascontiguousarray(a.astype(np.float32)) for a in (fwd, inv, index, chan)]
NH = 16
HD = D // NH
PAD = 32
HPT = P // PAD
NG_H = NH // HPT
BF16 = mybir.dt.bfloat16
Q_PART = (0, 0, 0, 1, 1, 2)
K_PART = (0, 1, 2, 0, 1, 0)
NSLOT = len(Q_PART)
NROW = NSLOT * HD + 6
NLOAD = 2 * NSLOT + 2


def distance_attention_stage(nc, core, tag, wq, wk, bq, bk, wv, bv, wo, bo, sel):
    with ExitStack() as ctx:
        sbf = lambda n, s: core.sbuf(f"{tag}_{n}", s, ctx)
        sb16 = lambda n, s: ctx.enter_context(nc.sbuf_tensor(f"{tag}_{n}", s, BF16))
        parts_d = nc.dram_tensor(f"{tag}_parts_dram", [B * 2 * KD * 3, P, S], BF16).ap()
        lens_d = nc.dram_tensor(f"{tag}_lens_dram", [B, 3, 2 * NH, S], BF16).ap()
        wqk = sbf("wqk", [P, 2, KD, D])
        bqk = sbf("bqk", [P, 2, KD])
        nbq = sbf("nbq", [P, KD])
        wv_sb, wo_sb = sbf("wv", [P, KD, D]), sbf("wo", [P, KD, D])
        bv_sb, bo_sb = sbf("bv", [P, D]), sbf("bo", [P, D])
        sel_sb = sbf("sel", [P, 2 * KD, 2 * NH])
        sq = sbf("sq", [P, 2 * KD, S])
        xn = sq[:, 0:KD, :].rearrange("p k s -> p (k s)").rearrange("p (j d) -> p j d", d=D)
        xnT = sbf("xnT", [P, KD, S])
        raw = sbf("raw", [P, 2, S])
        parts = sb16("parts", [P, 2 * KD, 3, S])
        lens = sb16("lens", [2 * NH, 3, S])
        stack = sb16("stack", [P, 2, 2, HPT, S])
        va = sbf("va", [P, TPB, NH, PAD])
        dist = sbf("dist", [P, 2, HPT, TPB, S])
        fold = sbf("fold", [P, 2, S])
        least = sbf("least", [P, 2, S])
        mq = sbf("mq", [P, 2, HPT, TPB])
        mb = sbf("mb", [P, HPT, S])
        oT = sbf("oT", [P, NG_H, S])
        rec = sbf("rec", [P, NH])
        on = sbf("on", [P, D])
        onT = sbf("onT", [P, KD, P])
        psS = core.psum(f"{tag}_psS", [P, TPB, 512], ctx)
        psM, psB, psO, psX = (core.psum(f"{tag}_{n}", [P, 512], ctx) for n in ("psM", "psB", "psO", "psX"))
        sem = lambda n: core.sem(f"{tag}_{n}", ctx)
        loaded, va_set, nbq_done = sem("loaded"), sem("va_set"), sem("nbq_done")
        xn_done, tr_done, xnT_done = sem("xn_done"), sem("tr_done"), sem("xnT_done")
        pr_ps, raw_done, split_step, split_done = sem("pr_ps"), sem("raw_done"), sem("split_step"), sem("split_done")
        len_ps, len_step, len_done, parts_out, stack_in = sem("len_ps"), sem("len_step"), sem("len_done"), sem("parts_out"), [sem("stack0"), sem("stack1")]
        v_ps, v_done = sem("v_ps"), sem("v_done")
        s_ps, clamp_done, fold_done, least_done = sem("s_ps"), sem("clamp_done"), sem("fold_done"), sem("least_done")
        m_ps, mq_done, root_done, mroot_done = sem("m_ps"), sem("mq_done"), sem("root_done"), sem("mroot_done")
        b_ps, mb_done, sub_done, exp_done = sem("b_ps"), sem("mb_done"), sem("sub_done"), sem("exp_done")
        o_ps, oT_done = sem("o_ps"), sem("oT_done")
        q_ps, rec_done, on_done, onT_ps, onT_done = sem("q_ps"), sem("rec_done"), sem("on_done"), sem("onT_ps"), sem("onT_done")
        y_ps, xb_done, x_done = sem("y_ps"), sem("xb_done"), sem("x_done")
        block = ctx.enter_context(nc.Block())
        NPR = 2 * KD

        def at(b, per, c):
            v = b * per + c
            return max(v, 0) if type(b) is int else v

        def batches(eng, body):
            body(0, True, False)
            with eng.Fori(1, B - 1) as b:
                body(b, False, False)
            body(B - 1, False, True)

        def before(b, g):
            return (b - 1, NG_H - 1) if g == 0 else (b, g - 1)

        @block.sync
        def _(sp):
            for n, w in enumerate((wq, wk)):
                sp.dma_start(wqk[:, n], w.rearrange("(k p) n -> p k n", p=P)).then_inc(loaded, 16)
            for n, b in enumerate((bq, bk)):
                sp.dma_start(bqk[:, n], b).then_inc(loaded, 16)
            sp.dma_start(wv_sb[:], wv.rearrange("(k p) n -> p k n", p=P)).then_inc(loaded, 16)
            sp.dma_start(wo_sb[:], wo.rearrange("(k p) n -> p k n", p=P)).then_inc(loaded, 16)
            sp.dma_start(bv_sb[:], bv.unsqueeze(0).broadcast_to([P, D])).then_inc(loaded, 16)
            sp.dma_start(bo_sb[:], bo.unsqueeze(0).broadcast_to([P, D])).then_inc(loaded, 16)
            sp.dma_start(sel_sb[:], sel).then_inc(loaded, 16)
            sp.wait_ge(va_set, 3)

            def store(b):
                for p in range(NPR):
                    sp.wait_ge(split_done, at(b, NPR, p + 1))
                    sp.dma_start(parts_d[bass.ds((b * NPR + p) * 3, 3)].rearrange("k p s -> p k s"),
                                 parts[:, p]).then_inc(parts_out, 16)
                sp.wait_ge(len_done, at(b, 1, 1))
                sp.dma_start(lens_d[b].rearrange("k h s -> h k s"), lens[:]).then_inc(parts_out, 16)

            def load(b, g):
                u, half = g % 2, slice(g % 2 * P // 2, (g % 2 + 1) * P // 2)
                if type(b) is not int or b or g >= 2:
                    sp.wait_ge(s_ps, at(b, 2 * NH, 2 * HPT * (g - 1)))
                for n, part in ((0, Q_PART), (1, K_PART)):
                    for s in range(NSLOT):
                        src = parts_d[(b * NPR + (n * KD + g // 2)) * 3 + part[s]]
                        sp.dma_start(stack[s * HD:(s + 1) * HD, u, n],
                                     src[half, :].rearrange("(i d) s -> d i s", i=HPT)).then_inc(stack_in[u], 16)
                    r = NSLOT * HD + 3 * n
                    sp.dma_start(stack[r:r + 3, u, n],
                                 lens_d[b][:, n * NH + g * HPT:n * NH + (g + 1) * HPT, :]).then_inc(stack_in[u], 16)

            def body(b, first, last):
                for g in range(NG_H):
                    if g == 0:
                        sp.wait_ge(parts_out, at(b, 16 * (NPR + 1), 16 * (NPR + 1)))
                    load(b, g)
                if not last:
                    store(b + 1)

            store(0)
            batches(sp, body)

        @block.tensor
        def _(pe):
            mm, turn = nc.tensor.matmul, nc.tensor.transpose
            pe.wait_ge(loaded, 144)

            def scores(b, g, i):
                h, u = g * HPT + i, g % 2
                if i == 0:
                    pe.wait_ge(stack_in[u], at(b, 2 * 16 * NLOAD, (g // 2 + 1) * 16 * NLOAD))
                for kb in range(TPB):
                    if kb % 2 == 0:
                        pe.wait_ge(clamp_done, at(b, 2 * NH, 2 * h - 1 + kb // 2))
                    last = mm(psS[:, kb, :], stack[0:NROW, u, 1, i, kb * P:(kb + 1) * P],
                              stack[0:NROW, u, 0, i, :], start=True, stop=True)
                    if kb % 2:
                        last.then_inc(s_ps, 1)

            def turn_least(b, g, i):
                h = g * HPT + i
                pe.wait_ge(least_done, at(b, NH, h + 1))
                pe.wait_ge(mq_done, at(b, NH, h))
                if i == 0:
                    pe.wait_ge(mb_done, at(b, NH, h))
                for q in range(TPB):
                    last = turn(psM[:, q * P:(q + 1) * P], least[:, h % 2, q * P:(q + 1) * P], core.ident[:])
                last.then_inc(m_ps, 1)

            def spread_least(b, g, i, last_batch):
                h, bank = g * HPT + i, (psB, psM)[i % 2]
                if i == 0:
                    pe.wait_ge(mroot_done, at(b, NG_H, g + 1))
                    if g == 1:
                        pe.wait_ge(onT_done, at(b, TPB, 0))
                    if g == 2:
                        pe.wait_ge(x_done, at(b, TPB, 0))
                        if not last_batch:
                            pe.wait_ge(raw_done, at(b, NPR, 2 * NPR))
                if i >= 2:
                    pe.wait_ge(mb_done, at(b, NH, h - 1))
                for q in range(TPB):
                    last = turn(bank[:, q * P:(q + 1) * P], mq[:, g % 2, i, q:q + 1].broadcast_to([P, P]), core.ident[:])
                last.then_inc(b_ps, 1)

            def weigh_v(b, g, i):
                h = g * HPT + i
                if i == 0:
                    pe.wait_ge(oT_done, at(b, NG_H, g))
                    if g == 0:
                        pe.wait_ge(v_done, at(b, 2, 2))
                pe.wait_ge(exp_done, at(b, NH, h + 1))
                for kb in range(TPB):
                    last = mm(psO[i * PAD:(i + 1) * PAD, :], va[:, kb, h, :], dist[:, g % 2, i, kb, :],
                              start=(kb == 0), stop=(kb == TPB - 1))
                last.then_inc(o_ps, 1)

            def project_v(b, half):
                if half == 0:
                    pe.wait_ge(len_done, at(b, 1, 1))
                else:
                    pe.wait_ge(v_done, at(b, 2, 1))
                for j in (2 * half, 2 * half + 1):
                    for k in range(KD):
                        last = mm(psX[:, (j % 2) * D:(j % 2 + 1) * D], xnT[:, k, j * P:(j + 1) * P], wv_sb[:, k, :],
                                  start=(k == 0), stop=(k == KD - 1))
                last.then_inc(v_ps, 1)

            def turn_rows(b, k, first):
                if k == 0:
                    pe.wait_ge(xn_done, at(b, TPB, TPB))
                    if not first:
                        pe.wait_ge(v_done, at(b, 2, 0))
                        pe.wait_ge(on_done, at(b, TPB, -TPB))
                elif not first:
                    pe.wait_ge(mb_done, at(b, NH, -NH + 2 * HPT))
                    pe.wait_ge(x_done, at(b, TPB, -TPB))
                for j in range(TPB):
                    last = turn((psX, psB)[k][:, j * P:(j + 1) * P], xn[:, j, k * P:(k + 1) * P], core.ident[:])
                last.then_inc(tr_done, 1)

            def project(b, p):
                pe.wait_ge(xnT_done, at(b, KD, KD))
                if p >= 2:
                    pe.wait_ge(raw_done, at(b, NPR, p - 1))
                for k in range(KD):
                    last = mm((psX, psB)[p % 2][:], wqk[:, p // KD, k, (p % KD) * P:(p % KD + 1) * P], xnT[:, k, :],
                              start=(k == 0), stop=(k == KD - 1))
                last.then_inc(pr_ps, 1)

            def lengths(b):
                pe.wait_ge(raw_done, at(b, NPR, NPR))
                for p in range(NPR):
                    last = mm(psX[0:2 * NH, :], sel_sb[:, p, :], sq[:, p, :], start=(p == 0), stop=(p == NPR - 1))
                last.then_inc(len_ps, 1)

            def out_turn(b, j):
                if j == 0:
                    pe.wait_ge(oT_done, at(b, NG_H, NG_H))
                pe.wait_ge(on_done, at(b, TPB, j))
                for g in range(NG_H):
                    last = turn(psX[:, g * P:(g + 1) * P], oT[:, g, j * P:(j + 1) * P], core.ident[:])
                last.then_inc(q_ps, 1)

            def out_turn_back(b, j):
                pe.wait_ge(on_done, at(b, TPB, j + 1))
                pe.wait_ge(x_done, at(b, TPB, j))
                for k in range(KD):
                    last = turn(psB[:, k * P:(k + 1) * P], on[:, k * P:(k + 1) * P], core.ident[:])
                last.then_inc(onT_ps, 1)

            def out_project(b, j):
                pe.wait_ge(onT_done, at(b, TPB, j + 1))
                for k in range(KD):
                    last = mm(psB[:, 0:D], onT[:, k, :], wo_sb[:, k, :], start=(k == 0), stop=(k == KD - 1))
                last.then_inc(y_ps, 1)

            def body(b, first, last):
                for g in range(NG_H):
                    for i in range(HPT):
                        if g == 1 and not first:
                            if i:
                                out_project(b - 1, i - 1)
                            if i == 0:
                                pe.wait_ge(v_done, at(b, 2, 2))
                            out_turn(b - 1, i)
                        if g == 2:
                            if i == 0 and not first:
                                pe.wait_ge(mb_done, at(b, NH, 2 * HPT))
                                out_project(b - 1, TPB - 1)
                            if not last:
                                if i == 1:
                                    turn_rows(b + 1, 1, False)
                                elif i:
                                    project(b + 1, 2 * i - 3)
                        if i:
                            turn_least(b, g, i - 1)
                        if i < HPT - 1:
                            scores(b, g, i + 1)
                        if g or not first:
                            weigh_v(*before(b, g), i)
                        if g == 0 and i == HPT - 1:
                            project_v(b, 0)
                        if g == 1 and not first:
                            if i == 0:
                                pe.wait_ge(mb_done, at(b, NH, HPT))
                            out_turn_back(b - 1, i)
                        if g == 2 and not last:
                            if i == 0:
                                turn_rows(b + 1, 0, False)
                            elif i < HPT - 1:
                                project(b + 1, 2 * i - 2)
                            else:
                                lengths(b + 1)
                    turn_least(b, g, HPT - 1)
                    if g < NG_H - 1:
                        scores(b, g + 1, 0)
                    elif not last:
                        scores(b + 1, 0, 0)
                    for i in range(HPT):
                        spread_least(b, g, i, last)
                    if g == 0:
                        project_v(b, 1)

            for k in range(KD):
                turn_rows(0, k, True)
            for p in range(NPR):
                project(0, p)
            lengths(0)
            scores(0, 0, 0)
            batches(pe, body)
            for i in range(HPT):
                weigh_v(B - 1, NG_H - 1, i)
            pe.wait_ge(mb_done, B * NH)
            for j in range(TPB):
                out_turn(B - 1, j)
                out_turn_back(B - 1, j)
                out_project(B - 1, j)

        @block.scalar
        def _(act):
            a = nc.scalar.activation
            act.wait_ge(loaded, 144)
            act.wait_ge(nbq_done, 1)

            def normalise(b):
                act.wait_ge(len_ps, at(b, 1, 0))
                core.apart(act)
                for j in range(TPB):
                    t = b * TPB + j
                    a(xn[:, j, :], core.X[:, t, :], ACT.Identity, bias=core.shift[:, bass.ds(t, 1)],
                      scale=core.rstd[:, bass.ds(t, 1)]).then_inc(xn_done, 1)

            def take_rows(b):
                for k in range(KD):
                    act.wait_ge(tr_done, at(b, KD, k + 1))
                    a(xnT[:, k, :], (psX, psB)[k][:], ACT.Identity).then_inc(xnT_done, 1)

            def take_projection(b, p):
                ps, q = (psX, psB)[p % 2], p < KD
                act.wait_ge(pr_ps, at(b, NPR, p + 1))
                act.wait_ge(split_done, at(b, NPR, p - 1))
                act.wait_ge(parts_out, at(b, 16 * (NPR + 1), 0))
                scale, bias = (-2.0, nbq[:, p:p + 1]) if q else (1.0, bqk[:, 1, p - KD:p - KD + 1])
                a(raw[:, p % 2, :], ps[:], ACT.Identity, scale=scale, bias=bias)
                a(parts[:, p, 0, :], ps[:], ACT.Identity, scale=scale, bias=bias)
                a(sq[:, p, :], ps[:], ACT.Square, bias=bqk[:, p // KD, p % KD:p % KD + 1]).then_inc(raw_done, 1)

            def root(b, g, i):
                h = g * HPT + i
                act.wait_ge(clamp_done, at(b, 2 * NH, 2 * h + 2))
                act.wait_ge(least_done, at(b, NH, h + 1))
                a(dist[:, g % 2, i], dist[:, g % 2, i], ACT.Sqrt).then_inc(root_done, 1)

            def weights(b, g, i):
                act.wait_ge(sub_done, at(b, NH, g * HPT + i + 1))
                a(dist[:, g % 2, i], dist[:, g % 2, i], ACT.Exp, scale=-1.0).then_inc(exp_done, 1)

            def take_sums(b, g):
                act.wait_ge(o_ps, at(b, NH, (g + 1) * HPT))
                act.wait_ge(q_ps, at(b, TPB, 0))
                a(oT[:, g, :], psO[:], ACT.Identity).then_inc(oT_done, 1)

            def take_turned(b, j):
                act.wait_ge(onT_ps, at(b, TPB, j + 1))
                act.wait_ge(y_ps, at(b, TPB, j))
                a(onT[:], psB[:, 0:D].rearrange("p (k q) -> p k q", k=KD), ACT.Identity).then_inc(onT_done, 1)

            def body(b, first, last):
                for g in range(NG_H):
                    prev = g or not first
                    out, prep = g == 1 and not first, g == 2 and not last
                    if prep:
                        normalise(b + 1)
                    for two in range(2):
                        for i in (2 * two, 2 * two + 1):
                            if prev:
                                weights(*before(b, g), i)
                        if prep:
                            if two == 0:
                                take_rows(b + 1)
                            else:
                                take_projection(b + 1, 2)
                        if out:
                            take_turned(b - 1, 2 * two)
                        root(b, g, 2 * two)
                        if prep and two:
                            take_projection(b + 1, 3)
                        root(b, g, 2 * two + 1)
                        if prep and two == 0:
                            take_projection(b + 1, 0)
                            take_projection(b + 1, 1)
                        if out:
                            take_turned(b - 1, 2 * two + 1)
                    if prev:
                        take_sums(*before(b, g))
                    act.wait_ge(mq_done, at(b, NH, (g + 1) * HPT))
                    a(mq[:, g % 2], mq[:, g % 2], ACT.Sqrt).then_inc(mroot_done, 1)
                    for i in range(HPT):
                        act.wait_ge(b_ps, at(b, NH, g * HPT + i + 1))
                        act.wait_ge(sub_done, at(b, NH, g * HPT))
                        a(mb[:, i, :], (psB, psM)[i % 2][:], ACT.Identity).then_inc(mb_done, 1)

            normalise(0)
            take_rows(0)
            for p in range(NPR):
                take_projection(0, p)
            batches(act, body)
            for i in range(HPT):
                weights(B - 1, NG_H - 1, i)
            take_sums(B - 1, NG_H - 1)
            for j in range(TPB):
                take_turned(B - 1, j)

        @block.gpsimd
        def _(pool):
            nc.gpsimd.memset(va[:], 0.0).then_inc(va_set, 1)
            pool.wait_ge(va_set, 1)
            nc.gpsimd.memset(va[:, :, :, HD:HD + 1], 1.0).then_inc(va_set, 1)
            pool.wait_ge(va_set, 2)
            nc.gpsimd.memset(stack[NSLOT * HD:], 1.0).then_inc(va_set, 1)
            with pool.Fori(0, B) as b:
                for h in range(NH):
                    g, i = h // HPT, h % HPT
                    pool.wait_ge(root_done, b * NH + (h + 1))
                    pool.wait_ge(mb_done, b * NH + (h + 1))
                    d = dist[:, g % 2, i]
                    nc.gpsimd.tensor_tensor(d, d, spread(mb[:, i, :], [P, TPB, S], 1),
                                            ALU.subtract).then_inc(sub_done, 1)

        @block.vector
        def _(dve):
            tt, copy = nc.vector.tensor_tensor, nc.vector.tensor_copy
            dve.wait_ge(loaded, 144)
            nc.vector.tensor_scalar(nbq[:], bqk[:, 0], -2.0, None, ALU.mult).then_inc(nbq_done, 1)
            dve.wait_ge(va_set, 2)

            def split(b, p):
                r = raw[:, p % 2, :]
                dve.wait_ge(raw_done, at(b, NPR, p + 1))
                tt(r, r, parts[:, p, 0, :], ALU.subtract).then_inc(split_step, 1)
                dve.wait_ge(split_step, at(b, 2 * NPR, 2 * p + 1))
                copy(parts[:, p, 1, :], r).then_inc(split_step, 1)
                dve.wait_ge(split_step, at(b, 2 * NPR, 2 * p + 2))
                tt(parts[:, p, 2, :], r, parts[:, p, 1, :], ALU.subtract).then_inc(split_done, 1)

            def split_lengths(b):
                ps, r = psX[0:2 * NH, :], raw[0:2 * NH, 0, :]
                dve.wait_ge(len_ps, at(b, 1, 1))
                dve.wait_ge(parts_out, at(b, 16 * (NPR + 1), 0))
                dve.wait_ge(split_done, at(b, NPR, NPR))
                copy(lens[:, 0, :], ps).then_inc(len_step, 1)
                dve.wait_ge(len_step, at(b, 3, 1))
                tt(r, ps, lens[:, 0, :], ALU.subtract).then_inc(len_step, 1)
                dve.wait_ge(len_step, at(b, 3, 2))
                copy(lens[:, 1, :], r).then_inc(len_step, 1)
                dve.wait_ge(len_step, at(b, 3, 3))
                tt(lens[:, 2, :], r, lens[:, 1, :], ALU.subtract).then_inc(len_done, 1)

            def take_v(b, half):
                dve.wait_ge(v_ps, at(b, 2, half + 1))
                dve.wait_ge(o_ps, at(b, NH, 0))
                tt(va[:, 2 * half:2 * half + 2, :, 0:HD], psX[:].rearrange("p (j h d) -> p j h d", j=2, h=NH),
                   spread(bv_sb[:].rearrange("p (h d) -> p h d", h=NH), [P, 2, NH, HD], 1), ALU.add).then_inc(v_done, 1)

            def reduce_least(b, h):
                dve.wait_ge(m_ps, at(b, NH, h + 1))
                nc.vector.tensor_reduce(mq[:, h // HPT % 2, h % HPT, :], psM[:].rearrange("p (q k) -> p q k", k=P),
                                        AX.X, ALU.min).then_inc(mq_done, 1)

            def norm_rows(b, j):
                t = b * TPB + j
                heads = psX[:].rearrange("p (h c) -> p h c", c=PAD)
                dve.wait_ge(q_ps, at(b, TPB, j + 1))
                nc.vector.reciprocal(rec[:], heads[:, :, HD]).then_inc(rec_done, 1)
                tt(core.X[:, t, :], core.X[:, t, :], bo_sb[:], ALU.add).then_inc(xb_done, 1)
                dve.wait_ge(rec_done, at(b, TPB, j + 1))
                dve.wait_ge(onT_ps, at(b, TPB, j))
                tt(on[:].rearrange("p (h d) -> p h d", h=NH), heads[:, :, 0:HD],
                   spread(rec[:], [P, NH, HD], 2), ALU.mult).then_inc(on_done, 1)

            def add_rows(b, j):
                t = b * TPB + j
                dve.wait_ge(xb_done, at(b, TPB, j + 1))
                dve.wait_ge(y_ps, at(b, TPB, j + 1))
                tt(core.X[:, t, :], psB[:, 0:D], core.X[:, t, :], ALU.add).then_inc(x_done, 1)
                dve.wait_ge(x_done, at(b, TPB, j + 1))
                core.apart(dve)
                nc.vector.bn_stats(core.bn[:, t, :], core.X[:, t, :])

            def body(b, first, last):
                for g in range(NG_H):
                    out, prep = g == 1 and not first, g == 2 and not last
                    for i in range(HPT):
                        h = g * HPT + i
                        d = dist[:, g % 2, i]
                        if g == 1 and i == 0:
                            take_v(b, 1)
                        dve.wait_ge(o_ps, at(b, NH, h - 2 * HPT + 1))
                        for c in range(2):
                            dve.wait_ge(s_ps, at(b, 2 * NH, 2 * h + c + 1))
                            nc.vector.tensor_scalar(d[:, 2 * c:2 * c + 2, :], psS[:, 2 * c:2 * c + 2, :], 1e-12, None,
                                                    ALU.max).then_inc(clamp_done, 1)
                        if out:
                            norm_rows(b - 1, i)
                        dve.wait_ge(clamp_done, at(b, 2 * NH, 2 * h + 2))
                        tt(fold[:], d[:, 0:2, :], d[:, 2:4, :], ALU.min).then_inc(fold_done, 1)
                        if i:
                            reduce_least(b, h - 1)
                        dve.wait_ge(fold_done, at(b, NH, h + 1))
                        dve.wait_ge(m_ps, at(b, NH, h - 1))
                        tt(least[:, h % 2, :], fold[:, 0, :], fold[:, 1, :], ALU.min).then_inc(least_done, 1)
                        if out and i:
                            add_rows(b - 1, i - 1)
                        if g == 2 and i == 0 and not first:
                            add_rows(b - 1, TPB - 1)
                        if prep and i == 2:
                            split(b + 1, 0)
                            split(b + 1, 1)
                        if prep and i == 3:
                            split(b + 1, 2)
                    if g == 0:
                        take_v(b, 0)
                    reduce_least(b, (g + 1) * HPT - 1)
                    if prep:
                        split(b + 1, 3)
                        split_lengths(b + 1)

            for p in range(NPR):
                split(0, p)
            split_lengths(0)
            batches(dve, body)
            for j in range(TPB):
                norm_rows(B - 1, j)
                add_rows(B - 1, j)


def attention_constants():
    import numpy as np

    sel = np.zeros((P, 2 * KD, 2 * NH), np.float32)
    for p in range(2 * KD):
        sel[np.arange(P), p, (p // KD) * NH + (p % KD) * (P // HD) + np.arange(P) // HD] = 1.0
    return sel
DI = 512
HM, PM = 8, 64
NST = 128
TAPS = 4
NCT = (DI + 2 * NST) // P
KI = DI // P


def state_space_stage(nc, core, tag, w_in, conv_w, conv_b, dt_bias, a_log, norm_w, w_out, upto):
    with ExitStack() as ctx:
        WIN = 2 * DI + 2 * NST + HM
        sbf = lambda n, s: core.sbuf(f"{tag}_{n}", s, ctx)
        win = sbf("win", [P, KD, WIN])
        wout = sbf("wout", [P, KI, D])
        cw = sbf("cw", [P, NCT, TAPS])
        cb = sbf("cb", [P, NCT])
        nw = sbf("nw", [P, KI])
        dtb = sbf("dtb", [P, HM])
        neg_a = sbf("neg_a", [P, HM])
        tri = sbf("tri", [P, P])
        xn = sbf("xn", [P, TPB, D])
        xnT = sbf("xnT", [P, KD, S])
        padded = sbf("padded", [P, 2, TAPS - 1 + S])
        acc = sbf("acc", [P, 2, S])
        xbc = sbf("xbc", [P, NCT, S])
        z = sbf("z", [P, TPB, DI])
        dtT = sbf("dtT", [P, S])
        dv = sbf("dv", [P, 12, TPB, HM])
        xdt = sbf("xdt", [P, 2, DI])
        xdec = sbf("xdec", [P, 2, DI])
        b_tok = sbf("b_tok", [P, 2, NST])
        gm = sbf("gm", [P, 2, P])
        lt = sbf("lt", [P, 2, HM, P])
        st = sbf("st", [P, DI])
        st2 = sbf("st2", [P, DI])
        yo = sbf("yo", [P, DI])
        y = sbf("y", [P, TPB, DI])
        ybn = sbf("ybn", [P, TPB, 6])
        ymv = sbf("ymv", [P, TPB, 2])
        yr = sbf("yr", [P, TPB])
        yT = sbf("yT", [P, 2, KI, P])
        psP = core.psum(f"{tag}_psP", [P, 2, 512], ctx)
        psX = core.psum(f"{tag}_psX", [P, 512], ctx)
        psG = core.psum(f"{tag}_psG", [P, 512], ctx)
        psC = core.psum(f"{tag}_psC", [P, 2, 512], ctx)
        psY = core.psum(f"{tag}_psY", [P, 512], ctx)
        psO = core.psum(f"{tag}_psO", [P, 512], ctx)
        sem = lambda n: core.sem(f"{tag}_{n}", ctx)
        loaded, prep = sem("loaded"), sem("prep")
        a_exp = sem("a_exp")
        xn_done, tr_done, xnT_done = sem("xn_done"), sem("tr_done"), sem("xnT_done")
        p_ps, p_done, tap, conv_done, silu_done = sem("p_ps"), sem("p_done"), sem("tap"), sem("conv_done"), sem("silu_done")
        dt_ps, dt_step, dt_act, cs_ps = sem("dt_ps"), sem("dt_step"), sem("dt_act"), sem("cs_ps")
        x_ps, g_ps, c_ps = sem("x_ps"), sem("g_ps"), sem("c_ps")
        xdt_done, xdec_done, g_done, l_done, lexp_done, m_done = (
            sem("xdt_done"), sem("xdec_done"), sem("g_done"), sem("l_done"), sem("lexp_done"), sem("m_done"))
        yo_ps, yd_ps, st_ps, yo_done, y_done, st_done, st_step = (
            sem("yo_ps"), sem("yd_ps"), sem("st_ps"), sem("yo_done"), sem("y_done"), sem("st_done"), sem("st_step"))
        ybn_done, ymv_done, yroot_done, yr_done, yn_done, yz_done = (
            sem("ybn_done"), sem("ymv_done"), sem("yroot_done"), sem("yr_done"), sem("yn_done"), sem("yz_done"))
        yT_ps, yT_done, o_ps, x_done = sem("yT_ps"), sem("yT_done"), sem("o_ps"), sem("x_done")
        block = ctx.enter_context(nc.Block())
        NP_ = NCT + TPB + 1
        (XD, AB, RL, DT, A, CS, NCS, TOT, DIF, EOUT, DEC, ETOT) = range(12)

        @block.sync
        def _(sp):
            for dst, src in ((win[:], w_in.rearrange("(k p) n -> p k n", p=P)),
                             (wout[:], w_out.rearrange("(k p) n -> p k n", p=P)),
                             (cw[:], conv_w), (cb[:], conv_b), (nw[:], norm_w),
                             (dtb[:], dt_bias.unsqueeze(0).broadcast_to([P, HM])),
                             (neg_a[:], a_log.unsqueeze(0).broadcast_to([P, HM])), (tri[:], upto)):
                sp.dma_start(dst, src).then_inc(loaded, 16)

        @block.tensor
        def _(pe):
            pe.wait_ge(loaded, 128)
            pe.wait_ge(prep, 1 + KI)
            with pe.Fori(0, B) as b:
                at = lambda per, c: b * per + c
                for k in range(KD):
                    pe.wait_ge(p_done, at(NP_, 0))
                    pe.wait_ge(st_done, at(TPB - 1, 0))
                    for j in range(TPB):
                        if k == 0:
                            pe.wait_ge(xn_done, at(TPB, j + 1))
                        last = nc.tensor.transpose(psP[:, k, j * P:(j + 1) * P], xn[:, j, k * P:(k + 1) * P],
                                                   core.ident[:])
                    last.then_inc(tr_done, 1)
                pe.wait_ge(xnT_done, at(KD, KD))
                for p in range(NP_):
                    if p >= 2:
                        pe.wait_ge(p_done, at(NP_, p - 1))
                    for k in range(KD):
                        if p < NCT:
                            lhsT, rhs = win[:, k, DI + p * P:DI + (p + 1) * P], xnT[:, k, :]
                            out = psP[:, p % 2, :]
                        elif p < NCT + TPB:
                            j = p - NCT
                            lhsT, rhs = xnT[:, k, j * P:(j + 1) * P], win[:, k, 0:DI]
                            out = psP[:, p % 2, :]
                        else:
                            lhsT, rhs = win[:, k, WIN - HM:WIN], xnT[:, k, :]
                            out = psP[0:HM, p % 2, :]
                        last = nc.tensor.matmul(out, lhsT, rhs, start=(k == 0), stop=(k == KD - 1))
                    last.then_inc(p_ps, 1)
                pe.wait_ge(p_done, at(NP_, NP_))
                pe.wait_ge(x_done, at(TPB, 0))
                core.behind(pe)
                for j in range(TPB):
                    last = nc.tensor.transpose(psG[:, j * HM:(j + 1) * HM], dtT[0:HM, j * P:(j + 1) * P],
                                               core.ident[0:HM, 0:HM])
                last.then_inc(dt_ps, 1)
                pe.wait_ge(dt_step, at(8, 4))
                nc.tensor.matmul(psG[:, 64:64 + TPB * HM], tri[:], dv[:, A].rearrange("p c h -> p (c h)"),
                                 start=True, stop=True)
                nc.tensor.matmul(psG[:, 128:128 + TPB * HM], core.ones[:], dv[:, A].rearrange("p c h -> p (c h)"),
                                 start=True, stop=True).then_inc(cs_ps, 1)
                pe.wait_ge(silu_done, at(NCT, NCT))
                pe.wait_ge(dt_step, at(8, 8))

                def chunk_inputs(c):
                    q = slice(c * P, (c + 1) * P)
                    pe.wait_ge(xdt_done, at(TPB, c))
                    for k in range(KI):
                        last = nc.tensor.transpose(psX[:, k * P:(k + 1) * P], xbc[:, k, q], core.ident[:])
                    last.then_inc(x_ps, 1)
                    pe.wait_ge(g_done, at(TPB, c))
                    nc.tensor.transpose(psG[:, 0:NST], xbc[:, KI, q], core.ident[:])
                    nc.tensor.matmul(psG[:, NST:2 * NST], xbc[:, KI, q], xbc[:, KI + 1, q],
                                     start=True, stop=True).then_inc(g_ps, 1)
                    pe.wait_ge(l_done, at(TPB, c))
                    for h in range(HM):
                        last = nc.tensor.transpose(psC[:, h // 4, (h % 4) * P:(h % 4 + 1) * P],
                                                   dv[:, CS, c, h:h + 1].broadcast_to([P, P]), core.ident[:])
                    last.then_inc(c_ps, 1)

                chunk_inputs(0)
                for c in range(TPB):
                    q = slice(c * P, (c + 1) * P)
                    if c + 1 < TPB:
                        chunk_inputs(c + 1)
                    if c:
                        pe.wait_ge(st_done, at(TPB - 1, c))
                        pe.wait_ge(yo_done, at(TPB - 1, c - 1))
                        nc.tensor.matmul(psO[:], xbc[:, KI + 1, q], st[:], start=True, stop=True).then_inc(yo_ps, 1)
                    if c + 1 < TPB:
                        pe.wait_ge(xdec_done, at(TPB - 1, c + 1))
                        nc.tensor.matmul(psP[:, 0, :], b_tok[:, c % 2, :], xdec[:, c % 2, :],
                                         start=True, stop=True).then_inc(st_ps, 1)
                    pe.wait_ge(m_done, at(TPB, c + 1))
                    pe.wait_ge(y_done, at(TPB, c))
                    for h in range(HM):
                        last = nc.tensor.matmul(psY[:, h * PM:(h + 1) * PM], lt[:, c % 2, h, :],
                                                xdt[:, c % 2, h * PM:(h + 1) * PM], start=True, stop=True)
                    last.then_inc(yd_ps, 1)
                for j in range(TPB):
                    pe.wait_ge(yz_done, at(TPB, j + 1))
                    pe.wait_ge(yT_done, at(TPB, j))
                    for k in range(KI):
                        last = nc.tensor.transpose(psX[:, k * P:(k + 1) * P], y[:, j, k * P:(k + 1) * P], core.ident[:])
                    last.then_inc(yT_ps, 1)
                    pe.wait_ge(yT_done, at(TPB, j + 1))
                    pe.wait_ge(x_done, at(TPB, j))
                    for k in range(KI):
                        last = nc.tensor.matmul(psG[:, 0:D], yT[:, j % 2, k, :], wout[:, k, :],
                                                start=(k == 0), stop=(k == KI - 1))
                    last.then_inc(o_ps, 1)

        @block.scalar
        def _(act):
            a = nc.scalar.activation
            act.wait_ge(loaded, 128)
            a(neg_a[:], neg_a[:], ACT.Exp).then_inc(a_exp, 1)
            with act.Fori(0, B) as b:
                at = lambda per, c: b * per + c
                act.wait_ge(tr_done, at(KD, 0))
                core.apart(act)
                for j in range(TPB):
                    t = at(TPB, j)
                    a(xn[:, j, :], core.X[:, t, :], ACT.Identity, bias=core.shift[:, bass.ds(t, 1)],
                      scale=core.rstd[:, bass.ds(t, 1)]).then_inc(xn_done, 1)
                for k in range(KD):
                    act.wait_ge(tr_done, at(KD, k + 1))
                    a(xnT[:, k, :], psP[:, k, :], ACT.Identity).then_inc(xnT_done, 1)

                def silu(c):
                    act.wait_ge(conv_done, at(NCT, c + 1))
                    a(xbc[:, c, :], acc[:, c % 2, :], ACT.Silu, bias=cb[:, c:c + 1]).then_inc(silu_done, 1)

                act.wait_ge(prep, 1 + KI)
                for p in range(NP_):
                    act.wait_ge(p_ps, at(NP_, p + 1))
                    if p < NCT:
                        act.wait_ge(conv_done, at(NCT, max(p - 1, 0)))
                        a(padded[:, p % 2, TAPS - 1:], psP[:, p % 2, :], ACT.Identity).then_inc(p_done, 1)
                        if p:
                            silu(p - 1)
                    elif p < NCT + TPB:
                        a(z[:, p - NCT, :], psP[:, p % 2, :], ACT.Silu).then_inc(p_done, 1)
                        if p == NCT:
                            silu(NCT - 1)
                    else:
                        a(dtT[0:HM, :], psP[0:HM, p % 2, :], ACT.Identity).then_inc(p_done, 1)
                act.wait_ge(dt_step, at(8, 1))
                a(dv[:, AB], dv[:, XD], ACT.Abs).then_inc(dt_act, 1)
                act.wait_ge(dt_act, at(6, 1))
                a(dv[:, AB], dv[:, AB], ACT.Exp, scale=-1.0).then_inc(dt_act, 1)
                act.wait_ge(dt_act, at(6, 2))
                a(dv[:, AB], dv[:, AB], ACT.Ln, bias=core.ones[:, 0:1]).then_inc(dt_act, 1)
                act.wait_ge(dt_step, at(8, 8))
                for o, i in ((EOUT, CS), (DEC, DIF), (ETOT, TOT)):
                    a(dv[:, o], dv[:, i], ACT.Exp).then_inc(dt_act, 1)
                for c in range(TPB):
                    act.wait_ge(l_done, at(TPB, c + 1))
                    a(lt[:, c % 2], lt[:, c % 2], ACT.Exp).then_inc(lexp_done, 1)
                act.wait_ge(ymv_done, at(1, 1))
                a(yr[:], ymv[:, :, 1], ACT.Sqrt, bias=core.eps[:]).then_inc(yroot_done, 1)
                for j in range(TPB):
                    act.wait_ge(yT_ps, at(TPB, j + 1))
                    act.wait_ge(o_ps, at(TPB, max(j - 1, 0)))
                    a(yT[:, j % 2], psX[:].rearrange("p (k q) -> p k q", k=KI), ACT.Identity).then_inc(yT_done, 1)

        @block.gpsimd
        def _(pool):
            tt = nc.gpsimd.tensor_tensor
            nc.gpsimd.memset(padded[:, :, 0:TAPS - 1], 0.0).then_inc(prep, 1)
            with pool.Fori(0, B) as b:
                at = lambda per, c: b * per + c
                for c in range(TPB):
                    if c == 0:
                        pool.wait_ge(dt_act, at(6, 6))
                    if c + 1 < TPB:
                        pool.wait_ge(xdt_done, at(TPB, c + 1))
                        pool.wait_ge(st_ps, at(TPB - 1, max(c - 1, 0)))
                        tt(xdec[:, c % 2, :].rearrange("p (h q) -> p h q", h=HM),
                           xdt[:, c % 2, :].rearrange("p (h q) -> p h q", h=HM),
                           spread(dv[:, DEC, c, :], [P, HM, PM], 2), ALU.mult).then_inc(xdec_done, 1)
                    pool.wait_ge(lexp_done, at(TPB, c + 1))
                    pool.wait_ge(g_done, at(TPB, c + 1))
                    tt(lt[:, c % 2], lt[:, c % 2], spread(gm[:, c % 2, :], [P, HM, P], 1), ALU.mult).then_inc(m_done, 1)
                for j in range(TPB):
                    pool.wait_ge(yn_done, at(TPB, j + 1))
                    tt(y[:, j, :], y[:, j, :], z[:, j, :], ALU.mult).then_inc(yz_done, 1)

        @block.vector
        def _(dve):
            tt, ts, stt = nc.vector.tensor_tensor, nc.vector.tensor_scalar, nc.vector.scalar_tensor_tensor
            dve.wait_ge(loaded, 128)
            for k in range(KI):
                ts(wout[:, k, :], wout[:, k, :], nw[:, k:k + 1], None, ALU.mult).then_inc(prep, 1)
            dve.wait_ge(prep, 1 + KI)
            dve.wait_ge(a_exp, 1)
            with dve.Fori(0, B) as b:
                at = lambda per, c: b * per + c
                for c in range(NCT):
                    dve.wait_ge(p_done, at(NP_, c + 1))
                    dve.wait_ge(silu_done, at(NCT, max(c - 1, 0)))
                    src, o = padded[:, c % 2], acc[:, c % 2, :]
                    ts(o, src[:, 0:S], cw[:, c, 0:1], None, ALU.mult).then_inc(tap, 1)
                    for j in range(1, TAPS):
                        dve.wait_ge(tap, at(NCT * (TAPS - 1), c * (TAPS - 1) + j))
                        last = stt(o, src[:, j:j + S], cw[:, c, j:j + 1], o, ALU.mult, ALU.add)
                        last.then_inc(tap if j < TAPS - 1 else conv_done, 1)
                dve.wait_ge(dt_ps, at(1, 1))
                raw = psG[:, 0:TPB * HM].rearrange("p (c h) -> p c h", h=HM)
                tt(dv[:, XD], raw, spread(dtb[:], [P, TPB, HM], 1), ALU.add).then_inc(dt_step, 1)
                dve.wait_ge(dt_step, at(8, 1))
                ts(dv[:, RL], dv[:, XD], 0.0, None, ALU.max).then_inc(dt_step, 1)
                dve.wait_ge(dt_step, at(8, 2))
                dve.wait_ge(dt_act, at(6, 3))
                tt(dv[:, DT], dv[:, RL], dv[:, AB], ALU.add).then_inc(dt_step, 1)
                dve.wait_ge(dt_step, at(8, 3))
                stt(dv[:, A], dv[:, DT], -1.0, spread(neg_a[:], [P, TPB, HM], 1), ALU.mult, ALU.mult).then_inc(dt_step, 1)
                dve.wait_ge(cs_ps, at(1, 1))
                cs = psG[:, 64:64 + TPB * HM].rearrange("p (c h) -> p c h", h=HM)
                tot = psG[:, 128:128 + TPB * HM].rearrange("p (c h) -> p c h", h=HM)
                nc.vector.tensor_copy(dv[:, CS], cs).then_inc(dt_step, 1)
                ts(dv[:, NCS], cs, -1.0, None, ALU.mult).then_inc(dt_step, 1)
                nc.vector.tensor_copy(dv[:, TOT], tot).then_inc(dt_step, 1)
                dve.wait_ge(dt_step, at(8, 7))
                tt(dv[:, DIF], dv[:, TOT], dv[:, CS], ALU.subtract).then_inc(dt_step, 1)

                def chunk_inputs(c):
                    dve.wait_ge(x_ps, at(TPB, c + 1))
                    if c >= 2:
                        dve.wait_ge(yd_ps, at(TPB, c - 1))
                    else:
                        dve.wait_ge(yd_ps, at(TPB, 0))
                    if c >= 2:
                        dve.wait_ge(xdec_done, at(TPB - 1, c - 1))
                    tt(xdt[:, c % 2, :].rearrange("p (h q) -> p h q", h=HM), psX[:].rearrange("p (h q) -> p h q", h=HM),
                       spread(dv[:, DT, c, :], [P, HM, PM], 2), ALU.mult).then_inc(xdt_done, 1)
                    dve.wait_ge(g_ps, at(TPB, c + 1))
                    if c >= 2:
                        dve.wait_ge(st_ps, at(TPB - 1, c - 1))
                    nc.vector.tensor_copy(b_tok[:, c % 2, :], psG[:, 0:NST])
                    tt(gm[:, c % 2, :], psG[:, NST:2 * NST], tri[:], ALU.mult).then_inc(g_done, 1)
                    dve.wait_ge(c_ps, at(TPB, c + 1))
                    for h in range(HM):
                        last = ts(lt[:, c % 2, h, :], psC[:, h // 4, (h % 4) * P:(h % 4 + 1) * P],
                                  dv[:, NCS, c, h:h + 1], 0.0, ALU.add, ALU.min)
                    last.then_inc(l_done, 1)

                chunk_inputs(0)
                for c in range(TPB):
                    if c + 1 < TPB:
                        chunk_inputs(c + 1)
                    if c:
                        dve.wait_ge(yo_ps, at(TPB - 1, c))
                        dve.wait_ge(dt_act, at(6, 6))
                        tt(yo[:].rearrange("p (h q) -> p h q", h=HM), psO[:].rearrange("p (h q) -> p h q", h=HM),
                           spread(dv[:, EOUT, c, :], [P, HM, PM], 2), ALU.mult).then_inc(yo_done, 1)
                    if 0 < c < TPB - 1:
                        dve.wait_ge(st_done, at(TPB - 1, c))
                        tt(st2[:].rearrange("p (h q) -> p h q", h=HM), st[:].rearrange("p (h q) -> p h q", h=HM),
                           spread(dv[:, ETOT, c, :], [P, HM, PM], 2), ALU.mult).then_inc(st_step, 1)
                        dve.wait_ge(st_step, at(TPB - 2, c))
                    if c < TPB - 1:
                        dve.wait_ge(st_ps, at(TPB - 1, c + 1))
                        if c:
                            tt(st[:], psP[:, 0, :], st2[:], ALU.add).then_inc(st_done, 1)
                        else:
                            nc.vector.tensor_copy(st[:], psP[:, 0, :]).then_inc(st_done, 1)
                    dve.wait_ge(yd_ps, at(TPB, c + 1))
                    if c:
                        dve.wait_ge(yo_done, at(TPB - 1, c))
                        tt(y[:, c, :], psY[:], yo[:], ALU.add).then_inc(y_done, 1)
                    else:
                        dve.wait_ge(yT_ps, at(TPB, 0))
                        nc.vector.tensor_copy(y[:, c, :], psY[:]).then_inc(y_done, 1)
                    dve.wait_ge(y_done, at(TPB, c + 1))
                    nc.vector.bn_stats(ybn[:, c, :], y[:, c, :]).then_inc(ybn_done, 1)
                dve.wait_ge(ybn_done, at(TPB, TPB))
                core.behind(dve)
                for c in range(TPB):
                    last = nc.vector.bn_aggr(ymv[:, c, :], ybn[:, c, :])
                last.then_inc(ymv_done, 1)
                dve.wait_ge(yroot_done, at(1, 1))
                nc.vector.reciprocal(yr[:], yr[:]).then_inc(yr_done, 1)
                dve.wait_ge(yr_done, at(1, 1))
                for j in range(TPB):
                    ts(y[:, j, :], y[:, j, :], ymv[:, j, 0:1], yr[:, j:j + 1], ALU.subtract, ALU.mult).then_inc(yn_done, 1)
                for j in range(TPB):
                    t = at(TPB, j)
                    dve.wait_ge(o_ps, at(TPB, j + 1))
                    tt(core.X[:, t, :], psG[:, 0:D], core.X[:, t, :], ALU.add).then_inc(x_done, 1)
                    dve.wait_ge(x_done, at(TPB, j + 1))
                    core.apart(dve)
                    nc.vector.bn_stats(core.bn[:, t, :], core.X[:, t, :])
GRP_T = 8
EPS_D = 1e-6


def delta_inputs(nc, core, tag, beta, w_qk, w_vb, tok_qk, seq_k, seq_nbk, seq_v):
    with ExitStack() as ctx:
        sbf = lambda n, s: core.sbuf(f"{tag}_{n}", s, ctx)
        wqk = sbf("wqk", [P, KD, 2 * D])
        wvb = sbf("wvb", [P, KD, D + NH])
        xn = sbf("xn", [P, TPB, D])
        xnT = sbf("xnT", [P, KD, S])
        qk = sbf("qk", [P, 2, TPB, 2 * D])
        v = sbf("v", [P, 2, TPB, D])
        sqr = sbf("sqr", [P, 2, 2 * D])
        ss = sbf("ss", [P, TPB * 2 * NH])
        nbk = sbf("nbk", [P, 2, TPB, D])
        psT = core.psum(f"{tag}_psT", [P, 2, 512], ctx)
        psA = core.psum(f"{tag}_psA", [P, 2, 512], ctx)
        psV = core.psum(f"{tag}_psV", [P, 2, 512], ctx)
        psB = core.psum(f"{tag}_psB", [P, 512], ctx)
        sem = lambda n: core.sem(f"{tag}_{n}", ctx)
        loaded = sem("loaded")
        xn_done, tr_done, xnT_done = sem("xn_done"), sem("tr_done"), sem("xnT_done")
        a_ps, silu_done, b_ps, beta_done = sem("a_ps"), sem("silu_done"), sem("b_ps"), sem("beta_done")
        sq_done, ss_done, root_done, inv_step, norm_done, nbk_done = (
            sem("sq_done"), sem("ss_done"), sem("root_done"), sem("inv_step"), sem("norm_done"), sem("nbk_done"))
        stored = [sem(f"stored{u}") for u in range(2)]
        block = ctx.enter_context(nc.Block())
        NOUT = 1 + 3 * TPB

        @block.sync
        def _(sp):
            sp.dma_start(wqk[:], w_qk.rearrange("(k p) n -> p k n", p=P)).then_inc(loaded, 16)
            sp.dma_start(wvb[:], w_vb.rearrange("(k p) n -> p k n", p=P)).then_inc(loaded, 16)
            with sp.Fori(0, B // 2) as b2:
                for u in range(2):
                    at = at_batch(b2, u)
                    b = b2 * 2 + u

                    def by_sequence(dst, src):
                        rows = dst.rearrange("(b h) (j p) d -> b j p h d", b=B, p=P)
                        for j in range(TPB):
                            sp.dma_start(rows[b, j], src[:, u, j, :].rearrange("p (h d) -> p h d", h=NH)).then_inc(stored[u], 16)

                    sp.wait_ge(silu_done, at(2 * TPB, 2 * TPB))
                    by_sequence(seq_v, v)
                    sp.wait_ge(norm_done, at(TPB, TPB))
                    sp.dma_start(tok_qk.rearrange("(b j p) n -> b p j n", b=B, p=P)[b], qk[:, u]).then_inc(stored[u], 16)
                    by_sequence(seq_k, qk[:, :, :, D:])
                    sp.wait_ge(nbk_done, at(1, 1))
                    by_sequence(seq_nbk, nbk)
            for u in range(2):
                sp.wait_ge(stored[u], 16 * NOUT * (B // 2))

        @block.tensor
        def _(pe):
            pe.wait_ge(loaded, 32)
            with pe.Fori(0, B // 2) as b2:
                for u in range(2):
                    at = at_batch(b2, u)
                    for k in range(KD):
                        for j in range(TPB):
                            if k == 0:
                                pe.wait_ge(xn_done, at(TPB, j + 1))
                            last = nc.tensor.transpose(psT[:, k, j * P:(j + 1) * P], xn[:, j, k * P:(k + 1) * P],
                                                       core.ident[:])
                        last.then_inc(tr_done, 1)
                    pe.wait_ge(xnT_done, at(KD, KD))
                    pe.wait_ge(beta_done, at(1, 0))
                    for j in range(TPB):
                        pe.wait_ge(silu_done, at(2 * TPB, max(2 * j - 2, 0)))
                        for k in range(KD):
                            nc.tensor.matmul(psA[:, j % 2, :], xnT[:, k, j * P:(j + 1) * P], wqk[:, k, :],
                                             start=(k == 0), stop=(k == KD - 1))
                        for k in range(KD):
                            last = nc.tensor.matmul(psV[:, j % 2, 0:D], xnT[:, k, j * P:(j + 1) * P], wvb[:, k, 0:D],
                                                    start=(k == 0), stop=(k == KD - 1))
                        last.then_inc(a_ps, 1)
                        for k in range(KD):
                            last = nc.tensor.matmul(psB[:, j * NH:(j + 1) * NH], xnT[:, k, j * P:(j + 1) * P],
                                                    wvb[:, k, D:], start=(k == 0), stop=(k == KD - 1))
                    last.then_inc(b_ps, 1)

        @block.scalar
        def _(act):
            a = nc.scalar.activation
            with act.Fori(0, B // 2) as b2:
                for u in range(2):
                    at = at_batch(b2, u)
                    act.wait_ge(tr_done, at(KD, 0))
                    core.apart(act)
                    for j in range(TPB):
                        t = at(TPB, j)
                        a(xn[:, j, :], core.X[:, t, :], ACT.Identity, bias=core.shift[:, bass.ds(t, 1)],
                          scale=core.rstd[:, bass.ds(t, 1)]).then_inc(xn_done, 1)
                    for k in range(KD):
                        act.wait_ge(tr_done, at(KD, k + 1))
                        a(xnT[:, k, :], psT[:, k, :], ACT.Identity).then_inc(xnT_done, 1)
                    act.wait_ge(stored[u], b2 * (16 * NOUT))
                    for j in range(TPB):
                        act.wait_ge(a_ps, at(TPB, j + 1))
                        a(qk[:, u, j, :], psA[:, j % 2, :], ACT.Silu).then_inc(silu_done, 1)
                        a(v[:, u, j, :], psV[:, j % 2, 0:D], ACT.Silu).then_inc(silu_done, 1)
                    act.wait_ge(b_ps, at(1, 1))
                    core.apart(act)
                    a(beta[:, bass.ds(at(TPB, 0), TPB), :], psB[:, 0:TPB * NH].rearrange("p (j h) -> p j h", h=NH),
                      ACT.Sigmoid).then_inc(beta_done, 1)
                    act.wait_ge(ss_done, at(TPB, TPB))
                    a(ss[:], ss[:], ACT.Sqrt).then_inc(root_done, 1)

        @block.gpsimd
        def _(pool):
            with pool.Fori(0, B // 2) as b2:
                for u in range(2):
                    at = at_batch(b2, u)
                    for j in range(TPB):
                        pool.wait_ge(silu_done, at(2 * TPB, 2 * j + 1))
                        pool.wait_ge(ss_done, at(TPB, max(j - 1, 0)))
                        nc.gpsimd.tensor_tensor(sqr[:, j % 2, :], qk[:, u, j, :], qk[:, u, j, :], ALU.mult).then_inc(sq_done, 1)

        @block.vector
        def _(dve):
            tt = nc.vector.tensor_tensor
            with dve.Fori(0, B // 2) as b2:
                for u in range(2):
                    at = at_batch(b2, u)
                    ss3 = ss[:].rearrange("p (j h) -> p j h", j=TPB)
                    for j in range(TPB):
                        dve.wait_ge(sq_done, at(TPB, j + 1))
                        nc.vector.tensor_reduce(ss3[:, j, :], sqr[:, j % 2, :].rearrange("p (h d) -> p h d", d=HD),
                                                AX.X, ALU.add).then_inc(ss_done, 1)
                    dve.wait_ge(root_done, at(1, 1))
                    nc.vector.tensor_scalar(ss[:], ss[:], EPS_D, None, ALU.add).then_inc(inv_step, 1)
                    dve.wait_ge(inv_step, at(2, 1))
                    nc.vector.reciprocal(ss[:], ss[:]).then_inc(inv_step, 1)
                    dve.wait_ge(inv_step, at(2, 2))
                    for j in range(TPB):
                        q3 = qk[:, u, j, :].rearrange("p (h d) -> p h d", d=HD)
                        tt(q3, q3, spread(ss3[:, j, :], [P, 2 * NH, HD], 2), ALU.mult).then_inc(norm_done, 1)
                    dve.wait_ge(norm_done, at(TPB, TPB))
                    dve.wait_ge(beta_done, at(1, 1))
                    for j in range(TPB):
                        last = nc.vector.scalar_tensor_tensor(
                            nbk[:, u, j, :].rearrange("p (h d) -> p h d", d=HD),
                            qk[:, u, j, D:].rearrange("p (h d) -> p h d", d=HD), -1.0,
                            beta[:, at(TPB, j), :].unsqueeze(2).broadcast_to([P, NH, HD]), ALU.mult, ALU.mult)
                    last.then_inc(nbk_done, 1)


def delta_scan(nc, core, tag, seq_k, seq_nbk, seq_v, tok_d, beside):
    with ExitStack() as ctx:
        sbf = lambda n, s: core.sbuf(f"{tag}_{n}", s, ctx)
        NCH = S // P
        k_sb = sbf("k", [P, 2, P, HD])
        bk_sb = sbf("bk", [P, 2, P, HD])
        v_sb = sbf("v", [P, 2, P, HD])
        d_sb = sbf("d", [P, 2, P, HD])
        m = sbf("m", [P, HD, HD])
        prod = sbf("prod", [P, 2, GRP_T, HD, HD + 1])
        outer = sbf("outer", [P, 2, HD, HD])
        ndm = sbf("ndm", [P, HD])
        dots, dot = sbf("dots", [P, HD]), sbf("dot", [P, 1])
        nd = sbf("nd", [P, 2, GRP_T, HD])
        sem = lambda n: core.sem(f"{tag}_{n}", ctx)
        in_k = [sem(f"in{u}") for u in range(2)]
        m_zero, v_set, nd_out = sem("m_zero"), sem("v_set"), sem("nd_out")
        mul_n, red_n, dot_n, d_n, out_n, add_n = (
            sem("mul_n"), sem("red_n"), sem("dot_n"), sem("d_n"), sem("out_n"), sem("add_n"))
        stored = [sem(f"stored{u}") for u in range(2)]
        beside.allocate(core, ctx)
        block = ctx.enter_context(nc.Block())
        NGT = P // GRP_T
        H2 = HD // 2

        @block.sync
        def _(sp):
            for c in range(NCH):
                u = c % 2
                if c == 2:
                    beside.load(sp)
                if c >= 2:
                    sp.wait_ge(add_n, 3 * P // 2 * (c - 1))
                    sp.wait_ge(v_set, (c - 1) * NGT)
                for dst, src in ((k_sb, seq_k), (bk_sb, seq_nbk), (v_sb, seq_v)):
                    sp.dma_start(dst[:, u], src[:, c * P:(c + 1) * P, :]).then_inc(in_k[u], 16)

        @block.scalar
        def _(act):
            rows = tok_d.rearrange("(b t) (h d) -> b h t d", b=B, h=NH)

            def put_v(c, g, w):
                nc.scalar.activation(prod[:, w, :, :, HD], v_sb[:, c % 2, bass.ds(g * GRP_T, GRP_T), :],
                                     ACT.Copy, scale=-1.0).then_inc(v_set, 1)

            def take_d(c, g, w, n):
                act.wait_ge(d_n, n)
                core.apart(act)
                nc.scalar.activation(d_sb[:, c % 2, bass.ds(g * GRP_T, GRP_T), :], nd[:, w], ACT.Copy,
                                     scale=-1.0).then_inc(nd_out, 1)

            act.wait_ge(in_k[0], 48)
            put_v(0, 0, 0)
            put_v(0, 1, 1)
            for c in range(NCH):
                base = P // 2 * c
                per = GRP_T // 2
                if c >= 2:
                    act.wait_ge(stored[c % 2], 16 * B * (c // 2))
                with act.Fori(0, NGT // 2 - 1) as g2:
                    for w in range(2):
                        done = g2 * (2 * per) + (base + per * (w + 1))
                        take_d(c, g2 * 2 + w, w, done)
                        put_v(c, g2 * 2 + (w + 2), w)
                for w in range(2):
                    done = base + per * (NGT - 1 + w)
                    take_d(c, NGT - 2 + w, w, done)
                    if c + 1 < NCH:
                        act.wait_ge(in_k[(c + 1) % 2], 48 * ((c + 1) // 2 + 1))
                        nc.scalar.activation(prod[:, w, :, :, HD], v_sb[:, (c + 1) % 2, w * GRP_T:(w + 1) * GRP_T, :],
                                             ACT.Copy, scale=-1.0).then_inc(v_set, 1)
                act.wait_ge(nd_out, (c + 1) * NGT)
                for b in range(B):
                    act.dma_start(rows[b, :, c * P:(c + 1) * P, :], d_sb[b * NH:(b + 1) * NH, c % 2]).then_inc(
                        stored[c % 2], 16)
            for u in range(2):
                act.wait_ge(stored[u], 16 * B * NCH // 2)

        @block.gpsimd
        def _(pool):
            nc.gpsimd.memset(m[:], 0.0).then_inc(m_zero, 1)
            beside.work(nc, pool)

        @block.vector
        def _(dve):
            tt, red = nc.vector.tensor_tensor, nc.vector.tensor_reduce
            halves = [slice(0, H2), slice(H2, HD)]
            dve.wait_ge(m_zero, 1)

            def outer_half(i, bk, nd_t, which):
                r = halves[i]
                tt(outer[:, which, r, :], bk[:, r].unsqueeze(2).broadcast_to([P, H2, HD]),
                   spread(nd_t, [P, H2, HD], 1), ALU.mult).then_inc(out_n, 1)

            for c in range(NCH):
                u = c % 2
                dve.wait_ge(in_k[u], 48 * (c // 2 + 1))
                with dve.Fori(0, NGT // 2) as g2:
                    for w in range(2):
                        for s in range(0, GRP_T, 2):
                            at = lambda per, n: g2 * (per * GRP_T) + (per * (c * P + w * GRP_T + s) // 2 + n)
                            t = g2 * (2 * GRP_T) + (w * GRP_T + s)
                            k0, k1 = k_sb[:, u, t, :], k_sb[:, u, t + 1, :]
                            bk0, bk1 = bk_sb[:, u, t, :], bk_sb[:, u, t + 1, :]
                            nd0, nd1 = nd[:, w, s, :], nd[:, w, s + 1, :]
                            for i, r in enumerate(halves):
                                if c or w or s:
                                    dve.wait_ge(add_n, at(3, i - 1))
                                else:
                                    dve.wait_ge(add_n, at(3, 0))
                                tt(prod[:, w, s, r, 0:HD], m[:, r, :], k0.unsqueeze(1).broadcast_to([P, H2, HD]),
                                   ALU.mult).then_inc(mul_n, 1)
                            tt(prod[:, w, s + 1, :, 0:HD], m[:], k1.unsqueeze(1).broadcast_to([P, HD, HD]),
                               ALU.mult).then_inc(mul_n, 1)
                            if s == 0:
                                dve.wait_ge(v_set, g2 * 2 + (c * NGT + w + 1))
                            dve.wait_ge(mul_n, at(3, 2))
                            red(nd0, prod[:, w, s], AX.X, ALU.add).then_inc(red_n, 1)
                            dve.wait_ge(mul_n, at(3, 3))
                            red(ndm[:], prod[:, w, s + 1], AX.X, ALU.add).then_inc(red_n, 1)
                            dve.wait_ge(red_n, at(2, 1))
                            tt(dots[:], nd0, k1, ALU.mult).then_inc(dot_n, 1)
                            outer_half(0, bk0, nd0, 0)
                            dve.wait_ge(dot_n, at(2, 1))
                            red(dot[:], dots[:], AX.X, ALU.add).then_inc(dot_n, 1)
                            outer_half(1, bk0, nd0, 0)
                            dve.wait_ge(dot_n, at(2, 2))
                            dve.wait_ge(red_n, at(2, 2))
                            nc.vector.scalar_tensor_tensor(nd1, bk0, dot[:], ndm[:], ALU.mult, ALU.add).then_inc(d_n, 1)
                            dve.wait_ge(out_n, at(4, 2))
                            tt(m[:], m[:], outer[:, 0], ALU.add).then_inc(add_n, 1)
                            dve.wait_ge(d_n, at(1, 1))
                            for i in range(2):
                                outer_half(i, bk1, nd1, 1)
                            dve.wait_ge(add_n, at(3, 1))
                            for i, r in enumerate(halves):
                                dve.wait_ge(out_n, at(4, 3 + i))
                                tt(m[:, r, :], m[:, r, :], outer[:, 1, r, :], ALU.add).then_inc(add_n, 1)


def delta_output(nc, core, tag, beta, tok_qk, tok_d, wo, rms_w, masks):
    with ExitStack() as ctx:
        sbf = lambda n, s: core.sbuf(f"{tag}_{n}", s, ctx)
        wo_sb = sbf("wo", [P, KD, D])
        rw = sbf("rw", [P, KD])
        par = sbf("par", [P, 2])
        before = sbf("before", [P, P])
        own = sbf("own", [P, P])
        eps6 = sbf("eps6", [P, 1])
        qk = sbf("qk", [P, 2, 2 * D])
        d = sbf("d", [P, 2, D])
        bd = sbf("bd", [P, 2, D])
        kT = sbf("kT", [P, KD, P])
        qT = sbf("qT", [P, KD, P])
        q2 = sbf("q2", [P, KD, 2, P])
        aT = sbf("aT", [P, NH, P])
        m0 = sbf("m0", [P, KD, P])
        mt = sbf("mt", [P, KD, P])
        o1 = sbf("o1", [P, KD, P])
        oT = sbf("oT", [P, KD, P])
        osq = sbf("osq", [P, KD, P])
        r = sbf("r", [P, 1])
        psT = core.psum(f"{tag}_psT", [P, 512], ctx)
        psA = core.psum(f"{tag}_psA", [P, 4, 512], ctx)
        psE = core.psum(f"{tag}_psE", [P, KD, 2, P], ctx)
        psM = core.psum(f"{tag}_psM", [P, 512], ctx)
        psY = core.psum(f"{tag}_psY", [P, 512], ctx)
        sem = lambda n: core.sem(f"{tag}_{n}", ctx)
        loaded, prep, wo_done, d_in = sem("loaded"), sem("prep"), sem("wo_done"), [sem("in0"), sem("in1")]
        t_ps, qk_done, a_ps, a_done, bd_done = sem("t_ps"), sem("qk_done"), sem("a_ps"), sem("a_done"), sem("bd_done")
        e_ps, e1_done, e2_done, osq_done, m_ps, mt_done, m0_done = (
            sem("e_ps"), sem("e1_done"), sem("e2_done"), sem("osq_done"), sem("m_ps"), sem("mt_done"), sem("m0_done"))
        y_ps, root_done, r_done, x_done = sem("y_ps"), sem("root_done"), sem("r_done"), sem("x_done")
        block = ctx.enter_context(nc.Block())

        @block.sync
        def _(sp):
            sp.dma_start(wo_sb[:], wo.rearrange("(k p) n -> p k n", p=P)).then_inc(loaded, 16)
            sp.dma_start(rw[:], rms_w).then_inc(loaded, 16)
            for dst, src in ((par, masks[0]), (before, masks[1]), (own, masks[2])):
                sp.dma_start(dst[:], src).then_inc(loaded, 16)
            with sp.Fori(0, B) as b:
                for c in range(TPB):
                    u = c % 2
                    at = lambda per, n: b * per + n
                    sp.wait_ge(y_ps, at(TPB, max(c - 1, 0)))
                    rows = tok_qk.rearrange("(t p) n -> t p n", p=P)
                    sp.dma_start(qk[:, u, :], rows[at(TPB, c)]).then_inc(d_in[u], 16)
                    rows = tok_d.rearrange("(t p) n -> t p n", p=P)
                    sp.dma_start(d[:, u, :], rows[at(TPB, c)]).then_inc(d_in[u], 16)

        @block.gpsimd
        def _(pool):
            nc.gpsimd.memset(eps6[:], EPS_D).then_inc(prep, 1)
            with pool.Fori(0, B) as b:
                for c in range(TPB):
                    u, n = c % 2, b * TPB + c
                    pool.wait_ge(d_in[u], b * (32 * TPB // 2) + 32 * (c // 2 + 1))
                    nc.gpsimd.tensor_tensor(bd[:, u, :].rearrange("p (h d) -> p h d", d=HD),
                                            d[:, u, :].rearrange("p (h d) -> p h d", d=HD),
                                            beta[:, n, :].unsqueeze(2).broadcast_to([P, NH, HD]), ALU.mult).then_inc(bd_done, 1)

        @block.tensor
        def _(pe):
            pe.wait_ge(loaded, 80)
            pe.wait_ge(wo_done, KD)
            with pe.Fori(0, B) as b:
                for c in range(TPB):
                    u = c % 2
                    at = lambda per, n: b * per + n
                    pe.wait_ge(d_in[u], at(32 * TPB // 2, 32 * (c // 2 + 1)))
                    pe.wait_ge(qk_done, at(4 * TPB, 4 * c))
                    for k in range(2 * KD):
                        last = nc.tensor.transpose(psT[:, k * P:(k + 1) * P], qk[:, u, k * P:(k + 1) * P], core.ident[:])
                    last.then_inc(t_ps, 1)
                    pe.wait_ge(qk_done, at(4 * TPB, 4 * c + 4))
                    for k in range(KD):
                        for i in range(4):
                            rr = slice(i * PAD, (i + 1) * PAD)
                            if k == 0:
                                pe.wait_ge(a_done, at(4 * TPB, max(4 * c - 3 + i, 0)))
                            last = nc.tensor.matmul(psA[:, i, k * 2 * P:(k + 1) * 2 * P], kT[rr, k, :],
                                                    q2[rr, k].rearrange("p e t -> p (e t)"), start=True, stop=True)
                            if k:
                                last.then_inc(a_ps, 1)
                    pe.wait_ge(e2_done, at(TPB, c))
                    pe.wait_ge(bd_done, at(TPB, c + 1))
                    if c:
                        pe.wait_ge(m0_done, at(TPB - 1, c))
                    for k in range(KD):
                        if c:
                            nc.tensor.matmul(psE[:, k].rearrange("p e t -> p (e t)"), m0[:, k, :],
                                             qT[:, k, :].unsqueeze(1).broadcast_to([P, 2, P]), start=True, stop=False,
                                             skip_group_check=True)
                        for i in range(4):
                            n = k * 4 + i
                            pe.wait_ge(a_done, at(4 * TPB, 4 * c + i + 1))
                            last = nc.tensor.matmul(psE[i * PAD:(i + 1) * PAD, k].rearrange("p e t -> p (e t)"),
                                                    bd[:, u, k * P + i * PAD:k * P + (i + 1) * PAD],
                                                    aT[:, 2 * n:2 * n + 2, :].rearrange("p h t -> p (h t)"),
                                                    start=(c == 0), stop=True, skip_group_check=True)
                    last.then_inc(e_ps, 1)
                    if c < TPB - 1:
                        if c:
                            pe.wait_ge(mt_done, at(TPB - 1, c))
                        for k in range(KD):
                            last = nc.tensor.matmul(psM[:, k * P:(k + 1) * P], qk[:, u, D + k * P:D + (k + 1) * P],
                                                    bd[:, u, k * P:(k + 1) * P], start=True, stop=True)
                        last.then_inc(m_ps, 1)
                    pe.wait_ge(osq_done, at(TPB, c + 1))
                    pe.wait_ge(x_done, at(TPB, c))
                    for k in range(KD):
                        nc.tensor.matmul(psY[:, 0:D], oT[:, k, :], wo_sb[:, k, :], start=(k == 0), stop=(k == KD - 1))
                    for k in range(KD):
                        last = nc.tensor.matmul(psY[:, D:D + 1], osq[:, k, :], core.ones[:, 0:1],
                                                start=(k == 0), stop=(k == KD - 1))
                    last.then_inc(y_ps, 1)

        @block.scalar
        def _(act):
            a = nc.scalar.activation
            act.wait_ge(loaded, 80)
            act.wait_ge(prep, 1)
            with act.Fori(0, B) as b:
                for c in range(TPB):
                    at = lambda per, n: b * per + n
                    act.wait_ge(t_ps, at(TPB, c + 1))
                    act.wait_ge(e_ps, at(TPB, c))
                    q = psT[:, 0:KD * P].rearrange("p (k t) -> p k t", k=KD)
                    for e in range(2):
                        a(q2[:, :, e, :], q, ACT.Identity, scale=par[:, e:e + 1]).then_inc(qk_done, 1)
                    a(kT[:], psT[:, KD * P:].rearrange("p (k t) -> p k t", k=KD), ACT.Identity).then_inc(qk_done, 1)
                    a(qT[:], q, ACT.Identity).then_inc(qk_done, 1)
                    act.wait_ge(e_ps, at(TPB, c + 1))
                    a(o1[:], psE[:, :, 0, :], ACT.Identity, scale=par[:, 0:1]).then_inc(e1_done, 1)
                    act.wait_ge(e2_done, at(TPB, c + 1))
                    a(osq[:], oT[:], ACT.Square).then_inc(osq_done, 1)
                    act.wait_ge(y_ps, at(TPB, c + 1))
                    a(r[:], psY[:, D:D + 1], ACT.Sqrt, scale=1.0 / D, bias=eps6[:]).then_inc(root_done, 1)

        @block.vector
        def _(dve):
            tt, stt = nc.vector.tensor_tensor, nc.vector.scalar_tensor_tensor
            dve.wait_ge(loaded, 80)
            for k in range(KD):
                nc.vector.tensor_scalar(wo_sb[:, k, :], wo_sb[:, k, :], rw[:, k:k + 1], None, ALU.mult).then_inc(wo_done, 1)
            with dve.Fori(0, B) as b:
                for c in range(TPB):
                    at = lambda per, n: b * per + n
                    t = at(TPB, c)
                    for g in range(4):
                        dve.wait_ge(a_ps, at(4 * TPB, 4 * c + g + 1))
                        if g == 0:
                            dve.wait_ge(e_ps, at(TPB, c))
                        tt(aT[:].rearrange("p (k i e) t -> p k i e t", k=KD, e=2)[:, :, g],
                           psA[:, g, :].rearrange("p (k e t) -> p k e t", k=KD, e=2),
                           spread(before[:], [P, 2 * KD, P], 1).rearrange("p (k e) t -> p k e t", k=KD),
                           ALU.mult).then_inc(a_done, 1)
                    dve.wait_ge(e1_done, at(TPB, c + 1))
                    dve.wait_ge(y_ps, at(TPB, c))
                    stt(oT[:], psE[:, :, 1, :], par[:, 1:2], o1[:], ALU.mult, ALU.add).then_inc(e2_done, 1)
                    if c < TPB - 1:
                        dve.wait_ge(m_ps, at(TPB - 1, c + 1))
                        dst = m0 if c == 0 else mt
                        last = tt(dst[:], psM[:, 0:KD * P].rearrange("p (k t) -> p k t", k=KD),
                                  spread(own[:], [P, KD, P], 1), ALU.mult)
                        last.then_inc(mt_done, 1)
                        if c:
                            dve.wait_ge(mt_done, at(TPB - 1, c + 1))
                            tt(m0[:], m0[:], mt[:], ALU.add).then_inc(m0_done, 1)
                        else:
                            dve.wait_ge(mt_done, at(TPB - 1, 1))
                            core.apart(dve)
                            dve.sem_inc(m0_done, 1)
                    dve.wait_ge(root_done, at(TPB, c + 1))
                    nc.vector.reciprocal(r[:], r[:]).then_inc(r_done, 1)
                    dve.wait_ge(r_done, at(TPB, c + 1))
                    stt(core.X[:, t, :], psY[:, 0:D], r[:], core.X[:, t, :], ALU.mult, ALU.add).then_inc(x_done, 1)
                    dve.wait_ge(x_done, at(TPB, c + 1))
                    core.apart(dve)
                    nc.vector.bn_stats(core.bn[:, t, :], core.X[:, t, :])


def delta_constants():
    import numpy as np

    p = np.arange(P)
    par = np.stack([(p // HD) % 2 == 0, (p // HD) % 2 == 1], 1)
    before = p[:, None] < p[None, :]
    own = p[:, None] // HD == p[None, :] // HD
    return [np.ascontiguousarray(a.astype(np.float32)) for a in (par, before, own)]


def hybrid_layers_program(nc, x, ident, w_qk, w_vb, d_wo, rms_w, par, before, own,
                          w_exp, b_exp, w_con_t, up_w, down_w, up_bias, b_con, down_bias,
                          wq, wk, bq, bk, wv, bv, a_wo, bo, sel,
                          fwd, inv, conv_wt, conv_bias, modes, index, chan,
                          weight_t, gate_t, u_t, v,
                          w_in, conv_w, conv_b, dt_bias, a_log, norm_w, w_out, upto, out):
    with ExitStack() as ctx:
        core = Core(nc, ctx)
        tok_qk = nc.dram_tensor("tok_qk", [B * S, 2 * D], F32).ap()
        tok_d = nc.dram_tensor("tok_d", [B * S, D], F32).ap()
        seq = [nc.dram_tensor(f"seq_{n}", [P, S, HD], F32).ap() for n in ("k", "nbk", "v")]

        start(nc, core, x, ident)
        row_scales(nc, core, "r0")
        with ExitStack() as ffn_ctx:
            core.ctx = ffn_ctx
            bf = Butterfly(nc, core, [w_exp, b_exp, w_con_t, up_w, down_w])
            core.ctx = ctx
            with ExitStack() as delta_ctx:
                bf.allocate_folding(core, delta_ctx)
                beta = core.sbuf("beta", [P, NT, NH], delta_ctx)
                delta_inputs(nc, core, "di", beta, w_qk, w_vb, tok_qk, *seq)
                delta_scan(nc, core, "ds", *seq, tok_d, bf)
                delta_output(nc, core, "do", beta, tok_qk, tok_d, d_wo, rms_w, (par, before, own))
                ffn_prepare(nc, core, bf, up_bias, b_con, down_bias)
            row_scales(nc, core, "r1")
            ffn_stage(nc, core, bf, "f1")
            row_scales(nc, core, "r2")
            distance_attention_stage(nc, core, "a1", wq, wk, bq, bk, wv, bv, a_wo, bo,
                                     sel)
            row_scales(nc, core, "r3")
            ffn_stage(nc, core, bf, "f2")
        with ExitStack() as conv_ctx:
            lc = LongConv(nc, core, conv_ctx)
            with ExitStack() as load_ctx:
                block = load_ctx.enter_context(nc.Block())

                @block.sync
                def _(sp):
                    lc.load(sp, fwd, inv, conv_wt, conv_bias)
            conv_kernel(nc, core, lc, modes, index, chan)
            row_scales(nc, core, "r4")
            conv_stage(nc, core, lc, "c1")
        core.clear_semaphores()
        mx = MixtureWeights(nc, core)
        with ExitStack() as load_ctx:
            block = load_ctx.enter_context(nc.Block())

            @block.sync
            def _(sp):
                mx.load(sp, weight_t, gate_t, u_t, v)
        row_scales(nc, core, "r5")
        mixture_stage(nc, core, mx, "m1")
        row_scales(nc, core, "r6")
        state_space_stage(nc, core, "s1", w_in, conv_w, conv_b, dt_bias, a_log, norm_w, w_out, upto)
        row_scales(nc, core, "r7")
        mixture_stage(nc, core, mx, "m2")
        finish(nc, core, out)


def kernel(**inputs):
    import numpy as np
    import concourse.bacc as _bacc
    from concourse import mybir as _mybir
    from concourse.bass_utils import run_bass_kernel_spmd as _run

    a = {n: np.asarray(v) for n, v in inputs.items()}
    q, f, g = (lambda n: a["L0_attn_a_" + n]), (lambda n: a["L0_ffn_" + n]), (lambda n: a["L0_attn_b_" + n])
    c, s, m = (lambda n: a["L1_attn_a_" + n]), (lambda n: a["L1_attn_b_" + n]), (lambda n: a["L1_ffn_" + n])
    stages = lambda w: w.reshape(10, 512, 4).transpose(0, 2, 1)
    lay = lambda t: t.reshape(64, 4, 32).transpose(1, 2, 0).reshape(128, 64)
    par, before, own = delta_constants()
    fwd, inv, index, chan = conv_constants()
    sel = attention_constants()
    laid = dict(
        x=q("x"), ident=np.eye(128, dtype=np.float32),
        w_qk=np.concatenate([q("Wq").T, q("Wk").T], 1), w_vb=np.concatenate([q("Wv").T, q("Wbeta").T], 1),
        d_wo=q("Wo").T, rms_w=q("rms_weight").reshape(2, 128).T, par=par, before=before, own=own,
        w_exp=f("W_exp"), b_exp=f("b_exp"), w_con_t=f("W_con").T, up_w=stages(f("up_weights")),
        down_w=stages(f("down_weights").transpose(0, 1, 3, 2))[::-1],
        up_bias=f("up_bias").reshape(8, 128).T, b_con=f("b_con"), down_bias=f("down_bias"),
        wq=g("wq").T, wk=g("wk").T, bq=g("bq").reshape(2, 128).T, bk=g("bk").reshape(2, 128).T, wv=g("wv").T, bv=g("bv"), a_wo=g("wo").T, bo=g("bo"),
        sel=sel, fwd=fwd, inv=inv, conv_wt=c("W").T, conv_bias=c("b"),
        modes=np.stack([lay(np.repeat(c("log_dt")[:, None], 32, 1)), lay(c("log_A_real")),
                        lay(c("A_imag")), lay(c("C_real")), lay(c("C_imag"))]),
        index=index, chan=chan,
        weight_t=m("weight").T, gate_t=m("gate_w").T, u_t=m("lora_U").reshape(128, 256).T,
        v=m("lora_V").transpose(0, 2, 1).reshape(128, 256),
        w_in=s("W_in"), conv_w=s("conv_w").reshape(6, 128, 4).transpose(1, 0, 2),
        conv_b=s("conv_b").reshape(6, 128).T, dt_bias=s("dt_bias"), a_log=s("A_log"),
        norm_w=s("norm_w").reshape(4, 128).T, w_out=s("W_out"),
        upto=np.triu(np.ones((128, 128), np.float32)))

    nc = _bacc.Bacc("TRN2", target_bir_lowering=False, num_devices=1)
    arrays, args = {}, {}
    for name, value in laid.items():
        arrays[f"in_{name}_dram"] = np.ascontiguousarray(value)
        args[name] = nc.dram_tensor(f"in_{name}_dram", value.shape, _mybir.dt.from_np(value.dtype),
                                    kind="ExternalInput").ap()
    args["out"] = nc.dram_tensor("out_0_dram", (8, 512, 256), _mybir.dt.from_np(np.dtype("float32")),
                                 kind="ExternalOutput").ap()
    hybrid_layers_program(nc, **args)
    r = _run(nc, [arrays], core_ids=[0])
    return r.results[0]["out_0_dram"]
```

```python
from contextlib import ExitStack

import concourse.bass as bass
from concourse import mybir

ALU = mybir.AluOpType
ACT = mybir.ActivationFunctionType
F32 = mybir.dt.float32
AX = mybir.AxisListType

P = 128
B, S, D = 8, 512, 256
TPB = S // P
NT = B * TPB
KD = D // P
HID = 1024
NSTAGE = 10
EPS_LN = 1e-5


class Core:

    def __init__(self, nc, ctx):
        self.nc, self.ctx, self.sems = nc, ctx, []
        sb = self.sbuf
        self.X = sb("X", [P, NT, D])
        self.bn = sb("bn", [P, NT, 6])
        self.mv = sb("mv", [P, NT, 2])
        self.rstd = sb("rstd", [P, NT])
        self.shift = sb("shift", [P, NT])
        self.ident = sb("ident", [P, P])
        self.eps = sb("eps", [P, 1])
        self.ones = sb("ones", [P, P])
        self.begun = self.sem("begun")
        self.passed = self.sem("passed")
        self.sems = []

    def apart(self, eng):
        eng.wait_ge(self.begun, 1)

    def behind(self, eng):
        eng.sem_inc(self.passed, 1)

    def sbuf(self, name, shape, ctx=None):
        return (ctx or self.ctx).enter_context(self.nc.sbuf_tensor(name, shape, F32))

    def psum(self, name, shape, ctx=None):
        return (ctx or self.ctx).enter_context(self.nc.psum_tensor(name, shape, F32))

    def sem(self, name, ctx=None):
        handle = self.nc.alloc_semaphore(name)
        self.sems.append(handle)
        return handle

    def clear_semaphores(self):
        self.nc.all_engine_barrier()
        self.nc.clear_and_free_semaphores(self.sems)
        self.nc.all_engine_barrier()
        self.sems = []


def spread(ap, shape, axis):
    return ap.unsqueeze(axis).broadcast_to(shape)


def start(nc, core, x, ident):
    with ExitStack() as ctx:
        x_in = [core.sem(f"st_x_in{b}") for b in range(2)]
        ident_in = core.sem("st_ident_in")
        const_done = core.sem("st_const_done")
        block = ctx.enter_context(nc.Block())

        @block.sync
        def _(sp):
            xt = x.rearrange("b (t p) d -> p (b t) d", p=P)
            for h in range(2):
                sp.dma_start(core.X[:, h * NT // 2:(h + 1) * NT // 2, :],
                             xt[:, h * NT // 2:(h + 1) * NT // 2, :]).then_inc(x_in[h], 16)
            sp.dma_start(core.ident[:], ident).then_inc(ident_in, 16)
            sp.wait_ge(ident_in, 16)

        @block.gpsimd
        def _(pool):
            nc.gpsimd.memset(core.ones[:], 1.0)
            nc.gpsimd.memset(core.eps[:], EPS_LN).then_inc(const_done, 1)
            pool.wait_ge(const_done, 1)
            pool.sem_inc(core.begun, 1)

        @block.vector
        def _(dve):
            for t in range(NT):
                if t % (NT // 2) == 0:
                    dve.wait_ge(x_in[t // (NT // 2)], 16)
                nc.vector.bn_stats(core.bn[:, t, :], core.X[:, t, :])


def row_scales(nc, core, tag):
    with ExitStack() as ctx:
        mv_done = core.sem(f"{tag}_mv_done")
        root_done = core.sem(f"{tag}_root_done")
        rstd_done = core.sem(f"{tag}_rstd_done")
        block = ctx.enter_context(nc.Block())

        @block.scalar
        def _(act):
            act.wait_ge(mv_done, 1)
            nc.scalar.activation(core.rstd[:], core.mv[:, :, 1], ACT.Sqrt,
                                 bias=core.eps[:]).then_inc(root_done, 1)

        @block.vector
        def _(dve):
            for t in range(NT):
                last = nc.vector.bn_aggr(core.mv[:, t, :], core.bn[:, t, :])
            last.then_inc(mv_done, 1)
            dve.wait_ge(root_done, 1)
            nc.vector.reciprocal(core.rstd[:], core.rstd[:]).then_inc(rstd_done, 1)
            dve.wait_ge(rstd_done, 1)
            nc.vector.scalar_tensor_tensor(core.shift[:], core.mv[:, :, 0], -1.0, core.rstd[:],
                                           ALU.mult, ALU.mult)


class Butterfly:

    def __init__(self, nc, core, sources):
        self.sources = sources
        self.up = core.sbuf("bf_up", [P, KD, HID])
        self.down = core.sbuf("bf_down", [P, HID // P, D])
        self.bias_h = core.sbuf("bf_bias_h", [P, HID // P])
        self.bias_y = core.sbuf("bf_bias_y", [P, D])
        self.loaded = core.sem("bf_loaded")
        self.stage_in = [core.sem(f"bf_stage_in{i}") for i in range(2)]
        self.zeroed = core.sem("bf_zeroed")
        self.step = core.sem("bf_step")

    def allocate_folding(self, core, ctx):
        self.up_b = core.sbuf("bf_up_b", [P, 1, HID], ctx)
        self.down_t = core.sbuf("bf_down_t", [P, KD, HID], ctx)

    def allocate(self, core, ctx):
        self.w = core.sbuf("bf_w", [P, 2, 4, HID // 2], ctx)
        self.t = core.sbuf("bf_t", [P, 4, HID // 2], ctx)

    def run(self, nc, pool):
        e = nc.gpsimd
        w_exp, b_exp, w_con_t, up_w, down_w = self.sources

        def load_stage(n):
            src = (up_w if n < NSTAGE else down_w)[n % NSTAGE]
            pool.dma_start(self.w[:, n % 2], src.unsqueeze(0).broadcast_to([P, 4, HID // 2])).then_inc(
                self.stage_in[n % 2], 16)

        e.memset(self.up_b[:], 0.0).then_inc(self.zeroed, 1)
        pool.dma_start(self.up[:], w_exp.rearrange("(k p) h -> p k h", p=P)).then_inc(self.loaded, 16)
        pool.dma_start(self.down_t[:], w_con_t.rearrange("(k p) h -> p k h", p=P)).then_inc(self.loaded, 16)
        pool.wait_ge(self.zeroed, 1)
        pool.dma_start(self.up_b[0:1, 0, :], b_exp.unsqueeze(0)).then_inc(self.loaded, 16)
        load_stage(0)
        load_stage(1)
        pool.wait_ge(self.loaded, 48)
        n_step = 0
        for n in range(2 * NSTAGE):
            up = n < NSTAGE
            rows = [self.up[:, 0, :], self.up[:, 1, :], self.up_b[:, 0, :]] if up else [
                self.down_t[:, 0, :], self.down_t[:, 1, :]]
            s = 1 << (n if up else 2 * NSTAGE - 1 - n)
            pool.wait_ge(self.stage_in[n % 2], 16 * (n // 2 + 1))
            for r, row in enumerate(rows):
                v = row.rearrange("p (n two s) -> p n two s", two=2, s=s)
                for i in range(4):
                    w = self.w[:, n % 2, i, :].rearrange("p (n s) -> p n s", s=s)
                    t = self.t[:, i, :].rearrange("p (n s) -> p n s", s=s)
                    e.tensor_tensor(t, v[:, :, i % 2, :], w, ALU.mult).then_inc(self.step, 1)
                    n_step += 1
                pool.wait_ge(self.step, n_step)
                if n + 2 < 2 * NSTAGE and r == len(rows) - 1:
                    load_stage(n + 2)
                for o in range(2):
                    t0 = self.t[:, 2 * o, :].rearrange("p (n s) -> p n s", s=s)
                    t1 = self.t[:, 2 * o + 1, :].rearrange("p (n s) -> p n s", s=s)
                    e.tensor_tensor(v[:, :, o, :], t0, t1, ALU.add).then_inc(self.step, 1)
                    n_step += 1
                pool.wait_ge(self.step, n_step)
        pool.wait_ge(self.step, n_step)


def ffn_prepare(nc, core, bf, up_bias, b_con, down_bias):
    with ExitStack() as ctx:
        bias_in = core.sbuf("fp_bias_in", [P, 2, D], ctx)
        psT = [core.psum(f"fp_psT{i}", [P, 512], ctx) for i in range(2)]
        psB = core.psum("fp_psB", [P, 512], ctx)
        loaded = core.sem("fp_loaded")
        ub_in = core.sem("fp_ub_in")
        tr_done = core.sem("fp_tr_done")
        ev_done = core.sem("fp_ev_done")
        row_done = core.sem("fp_row_done")
        block = ctx.enter_context(nc.Block())
        NH = HID // P

        @block.sync
        def _(sp):
            sp.dma_start(bf.bias_h[:], up_bias).then_inc(ub_in, 16)
            sp.dma_start(bias_in[:, 0, :], b_con.unsqueeze(0).broadcast_to([P, D])).then_inc(loaded, 16)
            sp.dma_start(bias_in[:, 1, :], down_bias.unsqueeze(0).broadcast_to([P, D])).then_inc(loaded, 16)

        @block.tensor
        def _(pe):
            for g in range(NH // 2):
                if g >= 2:
                    pe.wait_ge(ev_done, g - 1)
                for m in range(2):
                    for k in range(KD):
                        last = nc.tensor.transpose(
                            psT[g % 2][:, (m * KD + k) * P:(m * KD + k + 1) * P],
                            bf.down_t[:, k, (2 * g + m) * P:(2 * g + m + 1) * P], core.ident[:])
                last.then_inc(tr_done, 1)
            for m in range(NH):
                last = nc.tensor.matmul(psB[:, m:m + 1], bf.up_b[0:1, 0, m * P:(m + 1) * P],
                                        core.ones[0:1, 0:1], start=True, stop=True)
            last.then_inc(row_done, 1)

        @block.vector
        def _(dve):
            for g in range(NH // 2):
                dve.wait_ge(tr_done, g + 1)
                nc.vector.tensor_copy(bf.down[:, 2 * g:2 * g + 2, :],
                                      psT[g % 2][:].rearrange("p (m d) -> p m d", m=2)).then_inc(ev_done, 1)
            dve.wait_ge(row_done, 1)
            dve.wait_ge(ub_in, 16)
            nc.vector.tensor_tensor(bf.bias_h[:], bf.bias_h[:], psB[:, 0:NH], ALU.add)
            dve.wait_ge(loaded, 32)
            nc.vector.tensor_tensor(bf.bias_y[:], bias_in[:, 0, :], bias_in[:, 1, :], ALU.add)


def ffn_stage(nc, core, bf, tag):
    with ExitStack() as ctx:
        NH = HID // P
        xn = core.sbuf(f"{tag}_xn", [P, TPB, D], ctx)
        xnT = core.sbuf(f"{tag}_xnT", [P, 2, KD, S], ctx)
        h = core.sbuf(f"{tag}_h", [P, 2, NH, S], ctx)
        psT = [core.psum(f"{tag}_psT{i}", [P, 512], ctx) for i in range(2)]
        psH = [core.psum(f"{tag}_psH{i}", [P, 512], ctx) for i in range(2)]
        psY = [core.psum(f"{tag}_psY{i}", [P, 512], ctx) for i in range(2)]
        xn_done = core.sem(f"{tag}_xn_done")
        xb_done = core.sem(f"{tag}_xb_done")
        tr_done = core.sem(f"{tag}_tr_done")
        xnT_done = core.sem(f"{tag}_xnT_done")
        h_ps = core.sem(f"{tag}_h_ps")
        h_done = core.sem(f"{tag}_h_done")
        y_ps = core.sem(f"{tag}_y_ps")
        x_done = core.sem(f"{tag}_x_done")
        block = ctx.enter_context(nc.Block())

        @block.tensor
        def _(pe):
            with pe.Fori(0, B // 2) as b2:
                for u in range(2):
                    at = lambda per, c: b2 * (2 * per) + (u * per + c)
                    for k in range(KD):
                        pe.wait_ge(xnT_done, at(KD, 0))
                        for j in range(TPB):
                            if k == 0:
                                pe.wait_ge(xn_done, at(TPB, j + 1))
                            last = nc.tensor.transpose(psT[k][:, j * P:(j + 1) * P],
                                                       xn[:, j, k * P:(k + 1) * P], core.ident[:])
                        last.then_inc(tr_done, 1)
                    pe.wait_ge(xnT_done, at(KD, KD))
                    for m in range(NH):
                        if m >= 2:
                            pe.wait_ge(h_done, at(NH, m - 1))
                        for k in range(KD):
                            last = nc.tensor.matmul(psH[m % 2][:], bf.up[:, k, m * P:(m + 1) * P],
                                                    xnT[:, u, k, :], start=(k == 0), stop=(k == KD - 1))
                        last.then_inc(h_ps, 1)
                    pe.wait_ge(h_done, at(NH, NH))
                    for j in range(TPB):
                        pe.wait_ge(x_done, at(TPB, max(j - 1, 0)))
                        for m in range(NH):
                            last = nc.tensor.matmul(psY[j % 2][:, 0:D], h[:, u, m, j * P:(j + 1) * P],
                                                    bf.down[:, m, :], start=(m == 0), stop=(m == NH - 1))
                        last.then_inc(y_ps, 1)

        @block.scalar
        def _(act):
            with act.Fori(0, B // 2) as b2:
                for u in range(2):
                    at = lambda per, c: b2 * (2 * per) + (u * per + c)
                    act.wait_ge(tr_done, at(KD, 0))
                    core.apart(act)
                    for j in range(TPB):
                        t = at(TPB, j)
                        nc.scalar.activation(xn[:, j, :], core.X[:, t, :], ACT.Identity,
                                             bias=core.shift[:, bass.ds(t, 1)],
                                             scale=core.rstd[:, bass.ds(t, 1)]).then_inc(xn_done, 1)
                    for k in range(KD):
                        act.wait_ge(tr_done, at(KD, k + 1))
                        nc.scalar.activation(xnT[:, u, k, :], psT[k][:], ACT.Identity).then_inc(xnT_done, 1)
                    for m in range(NH):
                        act.wait_ge(h_ps, at(NH, m + 1))
                        nc.scalar.activation(h[:, u, m, :], psH[m % 2][:], ACT.Gelu,
                                             bias=bf.bias_h[:, m:m + 1]).then_inc(h_done, 1)

        @block.vector
        def _(dve):
            with dve.Fori(0, B // 2) as b2:
                for u in range(2):
                    for j in range(TPB):
                        at = lambda per, c: b2 * (2 * per) + (u * per + c)
                        t = at(TPB, j)
                        dve.wait_ge(xn_done, at(TPB, j + 1))
                        nc.vector.tensor_tensor(core.X[:, t, :], core.X[:, t, :], bf.bias_y[:], ALU.add).then_inc(xb_done, 1)
                        dve.wait_ge(y_ps, at(TPB, j + 1))
                        dve.wait_ge(xb_done, at(TPB, j + 1))
                        nc.vector.tensor_tensor(core.X[:, t, :], psY[j % 2][:, 0:D], core.X[:, t, :],
                                                ALU.add).then_inc(x_done, 1)
                        dve.wait_ge(x_done, at(TPB, j + 1))
                        core.apart(dve)
                        nc.vector.bn_stats(core.bn[:, t, :], core.X[:, t, :])


def finish(nc, core, out):
    with ExitStack() as ctx:
        stored = core.sem("fin_stored")
        block = ctx.enter_context(nc.Block())

        @block.sync
        def _(sp):
            ot = out.rearrange("b (t p) d -> p (b t) d", p=P)
            sp.dma_start(ot[:, 0:NT // 2, :], core.X[:, 0:NT // 2, :]).then_inc(stored, 16)
            sp.dma_start(ot[:, NT // 2:, :], core.X[:, NT // 2:, :]).then_inc(stored, 16)
            sp.wait_ge(stored, 32)
E_LORA, R_LORA = 8, 16


def at_batch(b2, u):
    return lambda per, c: b2 * (2 * per) + (u * per + c)


class MixtureWeights:

    def __init__(self, nc, core):
        ER = E_LORA * R_LORA
        self.tg = core.sbuf("mx_tg", [P, KD, ER + E_LORA])
        self.base = core.sbuf("mx_base", [P, KD, D])
        self.v = core.sbuf("mx_v", [P, D])
        self.loaded = core.sem("mx_loaded")

    def load(self, sp, weight_t, gate_t, u_t, v):
        ER = E_LORA * R_LORA
        sp.dma_start(self.tg[:, :, 0:ER], u_t.rearrange("(k p) n -> p k n", p=P)).then_inc(self.loaded, 16)
        sp.dma_start(self.tg[:, :, ER:], gate_t.rearrange("(k p) n -> p k n", p=P)).then_inc(self.loaded, 16)
        sp.dma_start(self.base[:], weight_t.rearrange("(k p) n -> p k n", p=P)).then_inc(self.loaded, 16)
        sp.dma_start(self.v[:], v).then_inc(self.loaded, 16)


def mixture_stage(nc, core, mx, tag):
    with ExitStack() as ctx:
        ER = E_LORA * R_LORA
        G = E_LORA
        xn = core.sbuf(f"{tag}_xn", [P, TPB, D], ctx)
        xnT = core.sbuf(f"{tag}_xnT", [P, 2, KD, S], ctx)
        gate = core.sbuf(f"{tag}_gate", [P, TPB, G], ctx)
        gmax = core.sbuf(f"{tag}_gmax", [P, TPB], ctx)
        gsum = core.sbuf(f"{tag}_gsum", [P, TPB], ctx)
        tg = core.sbuf(f"{tag}_tg", [P, TPB, ER], ctx)
        tgT = core.sbuf(f"{tag}_tgT", [P, TPB * P], ctx)
        psT = [core.psum(f"{tag}_psT{i}", [P, 512], ctx) for i in range(2)]
        psG = core.psum(f"{tag}_psG", [P, 2, 512], ctx)
        psB = core.psum(f"{tag}_psB", [P, TPB, 512], ctx)
        xn_done = core.sem(f"{tag}_xn_done")
        tr_done = core.sem(f"{tag}_tr_done")
        xnT_done = core.sem(f"{tag}_xnT_done")
        tg_ps = core.sem(f"{tag}_tg_ps")
        shifted = core.sem(f"{tag}_shifted")
        exp_done = core.sem(f"{tag}_exp_done")
        gate_step = core.sem(f"{tag}_gate_step")
        tg_done = core.sem(f"{tag}_tg_done")
        tgT_ps = core.sem(f"{tag}_tgT_ps")
        tgT_done = core.sem(f"{tag}_tgT_done")
        y_ps = core.sem(f"{tag}_y_ps")
        x_done = core.sem(f"{tag}_x_done")
        pair = [psG[:, g, 0:2 * (ER + G)].rearrange("p (t n) -> p t n", t=2) for g in range(2)]
        block = ctx.enter_context(nc.Block())

        @block.scalar
        def _(act):
            with act.Fori(0, B // 2) as b2:
                for u in range(2):
                    at = at_batch(b2, u)
                    act.wait_ge(tr_done, at(KD, 0))
                    core.apart(act)
                    for j in range(TPB):
                        t = at(TPB, j)
                        nc.scalar.activation(xn[:, j, :], core.X[:, t, :], ACT.Identity,
                                             bias=core.shift[:, bass.ds(t, 1)],
                                             scale=core.rstd[:, bass.ds(t, 1)]).then_inc(xn_done, 1)
                    for k in range(KD):
                        act.wait_ge(tr_done, at(KD, k + 1))
                        nc.scalar.activation(xnT[:, u, k, :], psT[k][:], ACT.Identity).then_inc(xnT_done, 1)
                    act.wait_ge(shifted, at(1, 1))
                    nc.scalar.activation(gate[:], gate[:], ACT.Exp).then_inc(exp_done, 1)
                    act.wait_ge(tgT_ps, at(1, 1))
                    nc.scalar.activation(tgT[:], psT[0][:], ACT.Identity).then_inc(tgT_done, 1)

        @block.tensor
        def _(pe):
            pe.wait_ge(mx.loaded, 64)
            with pe.Fori(0, B // 2) as b2:
                for u in range(2):
                    at = at_batch(b2, u)
                    pe.wait_ge(tgT_done, at(1, 0))
                    for k in range(KD):
                        for j in range(TPB):
                            if k == 0:
                                pe.wait_ge(xn_done, at(TPB, j + 1))
                            last = nc.tensor.transpose(psT[k][:, j * P:(j + 1) * P],
                                                       xn[:, j, k * P:(k + 1) * P], core.ident[:])
                        last.then_inc(tr_done, 1)
                    pe.wait_ge(xnT_done, at(KD, KD))
                    pe.wait_ge(tg_done, at(2, 0))
                    for j in range(TPB):
                        for k in range(KD):
                            last = nc.tensor.matmul(pair[j // 2][:, j % 2, :], xnT[:, u, k, j * P:(j + 1) * P],
                                                    mx.tg[:, k, :], start=(k == 0), stop=(k == KD - 1))
                    last.then_inc(tg_ps, 1)
                    for j in range(TPB):
                        pe.wait_ge(x_done, at(TPB, 0))
                        for k in range(KD):
                            nc.tensor.matmul(psB[:, j, 0:D], xnT[:, u, k, j * P:(j + 1) * P],
                                             mx.base[:, k, :], start=(k == 0), stop=False)
                    for j in range(TPB):
                        pe.wait_ge(tg_done, at(2, j // 2 + 1))
                        last = nc.tensor.transpose(psT[0][:, j * P:(j + 1) * P], tg[:, j, :], core.ident[:])
                    last.then_inc(tgT_ps, 1)
                    pe.wait_ge(tgT_done, at(1, 1))
                    for j in range(TPB):
                        nc.tensor.matmul(psB[:, j, 0:D], tgT[:, j * P:(j + 1) * P], mx.v[:],
                                         start=False, stop=True).then_inc(y_ps, 1)

        @block.vector
        def _(dve):
            with dve.Fori(0, B // 2) as b2:
                for u in range(2):
                    at = at_batch(b2, u)
                    dve.wait_ge(tg_ps, at(1, 1))
                    for g in range(2):
                        nc.vector.tensor_reduce(gmax[:, 2 * g:2 * g + 2], pair[g][:, :, ER:], AX.X,
                                                ALU.max).then_inc(gate_step, 1)
                    for g in range(2):
                        dve.wait_ge(gate_step, at(6, g + 1))
                        last = nc.vector.tensor_tensor(gate[:, 2 * g:2 * g + 2, :], pair[g][:, :, ER:],
                                                       spread(gmax[:, 2 * g:2 * g + 2], [P, 2, G], 2), ALU.subtract)
                    last.then_inc(shifted, 1)
                    dve.wait_ge(exp_done, at(1, 1))
                    nc.vector.tensor_reduce(gsum[:], gate[:], AX.X, ALU.add).then_inc(gate_step, 1)
                    dve.wait_ge(gate_step, at(6, 3))
                    nc.vector.reciprocal(gsum[:], gsum[:]).then_inc(gate_step, 1)
                    dve.wait_ge(gate_step, at(6, 4))
                    nc.vector.scalar_tensor_tensor(gate[:], gate[:], 1.0 / R_LORA,
                                                   spread(gsum[:], [P, TPB, G], 2),
                                                   ALU.mult, ALU.mult).then_inc(gate_step, 2)
                    dve.wait_ge(gate_step, at(6, 6))
                    for j in range(TPB):
                        last = nc.vector.tensor_tensor(
                            tg[:, j, :].rearrange("p (e r) -> p e r", e=G),
                            pair[j // 2][:, j % 2, 0:ER].rearrange("p (e r) -> p e r", e=G),
                            spread(gate[:, j, :], [P, G, R_LORA], 2), ALU.mult)
                        if j % 2:
                            last.then_inc(tg_done, 1)
                    for j in range(TPB):
                        t = at(TPB, j)
                        dve.wait_ge(y_ps, at(TPB, j + 1))
                        nc.vector.tensor_tensor(core.X[:, t, :], psB[:, j, 0:D], core.X[:, t, :],
                                                ALU.add).then_inc(x_done, 1)
                        dve.wait_ge(x_done, at(TPB, j + 1))
                        core.apart(dve)
                        nc.vector.bn_stats(core.bn[:, t, :], core.X[:, t, :])
NMODE = 32
CPT = P // NMODE
NMT = D // CPT
NF = S // P
ROUND = 1.5 * 2.0 ** 23
PI = 3.141592653589793


class LongConv:

    def __init__(self, nc, core, ctx):
        self.fwd = core.sbuf("lc_fwd", [P, TPB, 2 * S], ctx)
        self.inv = core.sbuf("lc_inv", [P, 2 * NF, S], ctx)
        self.w = core.sbuf("lc_w", [P, KD, D], ctx)
        self.b = core.sbuf("lc_b", [P, D], ctx)
        self.k_re = core.sbuf("lc_k_re", [P, NF, D], ctx)
        self.k_im = core.sbuf("lc_k_im", [P, NF, D], ctx)
        self.k_re2 = core.sbuf("lc_k_re2", [P, NF, D], ctx)
        self.loaded = core.sem("lc_loaded")

    def load(self, sp, fwd, inv, w_t, b):
        sp.dma_start(self.fwd[:], fwd.rearrange("(k p) n -> p k n", p=P)).then_inc(self.loaded, 16)
        sp.dma_start(self.inv[:], inv.rearrange("(k p) n -> p k n", p=P)).then_inc(self.loaded, 16)
        sp.dma_start(self.w[:], w_t.rearrange("(k p) n -> p k n", p=P)).then_inc(self.loaded, 16)
        sp.dma_start(self.b[:], b.unsqueeze(0).broadcast_to([P, D])).then_inc(self.loaded, 16)


def conv_kernel(nc, core, lc, tables, modes, index, conv_in):
    with ExitStack() as ctx:
        GRP = 16
        NG = NMT // GRP
        par = core.sbuf("ck_par", [P, 5, NMT], ctx)
        idx = core.sbuf("ck_idx", [P, P + TPB], ctx)
        chan = core.sbuf("ck_chan", [P, CPT], ctx)
        v = core.sbuf("ck_v", [P, 16, NMT], ctx)
        f_ph = core.sbuf("ck_f_ph", [P, 4, NMT * TPB], ctx)
        f_re = core.sbuf("ck_f_re", [P, NMT, TPB], ctx)
        f_im = core.sbuf("ck_f_im", [P, NMT, TPB], ctx)
        fm = core.sbuf("ck_fm", [P, 2, NMT, TPB * CPT], ctx)
        ph2 = core.sbuf("ck_ph", [P, 2, GRP, P], ctx)
        rnd = core.sbuf("ck_rnd", [P, GRP, P], ctx)
        mag2 = core.sbuf("ck_mag", [P, 2, GRP, P], ctx)
        g_re2 = core.sbuf("ck_g_re", [P, 2, GRP, P], ctx)
        g_im2 = core.sbuf("ck_g_im", [P, 2, GRP, P], ctx)
        kT = core.sbuf("ck_kT", [P, TPB, D], ctx)
        half_pi = core.sbuf("ck_half_pi", [P, 1], ctx)
        psK = core.psum("ck_psK", [P, 2, 512], ctx)
        psF = core.psum("ck_psF", [P, 2, 512], ctx)
        loaded = core.sem("ck_loaded")
        vec = core.sem("ck_vec")
        act_n = core.sem("ck_act")
        pe_g = core.sem("ck_pe_g")
        kT_done = core.sem("ck_kT_done")
        f_ps = core.sem("ck_f_ps")
        f_out = core.sem("ck_f_out")
        block = ctx.enter_context(nc.Block())
        LDT, LAR, AIM, CRE, CIM = range(5)
        phases_at = lambda g: 54 + 6 * g - 2 * (g > 0)
        powers_at = lambda g: min(60 + 6 * g, 50 + 6 * NG)
        (DT, AR, DR, DI, MAG, SIN, COS, TURN, RN, FR, ABS, T0, T1, NRE, NIM, DEN) = range(16)

        @block.sync
        def _(sp):
            sp.dma_start(par[:], modes.rearrange("a p t -> p a t")).then_inc(loaded, 16)
            sp.dma_start(idx[:], index.unsqueeze(0).broadcast_to([P, P + TPB])).then_inc(loaded, 16)
            sp.dma_start(chan[:], conv_in).then_inc(loaded, 16)
            lc.load(sp, *tables)

        @block.vector
        def _(dve):
            n = [0]

            def step(ins):
                n[0] += 1
                ins.then_inc(vec, 1)
                dve.wait_ge(vec, n[0])

            tt = nc.vector.tensor_tensor
            step(nc.vector.memset(half_pi[:], PI / 2))
            dve.wait_ge(loaded, 48)
            dve.wait_ge(act_n, 2)
            step(nc.vector.scalar_tensor_tensor(v[:, DR, :], v[:, AR, :], -1.0, v[:, DT, :], ALU.mult, ALU.mult))
            step(tt(v[:, DI, :], par[:, AIM, :], v[:, DT, :], ALU.mult))
            step(nc.vector.tensor_scalar(v[:, TURN, :], v[:, DI, :], 1 / (2 * PI), None, ALU.mult))
            step(nc.vector.tensor_scalar(v[:, RN, :], v[:, TURN, :], ROUND, -ROUND, ALU.add, ALU.add))
            step(tt(v[:, FR, :], v[:, TURN, :], v[:, RN, :], ALU.subtract))
            dve.wait_ge(act_n, 6)
            step(tt(v[:, T0, :], v[:, MAG, :], v[:, COS, :], ALU.mult))
            step(nc.vector.tensor_scalar(v[:, T0, :], v[:, T0, :], -1.0, None, ALU.add))
            step(tt(v[:, T1, :], v[:, MAG, :], v[:, SIN, :], ALU.mult))

            def cmul(o_re, o_im, a_re, a_im, b_re, b_im, s0, s1):
                step(tt(s0, a_re, b_re, ALU.mult))
                step(tt(s1, a_im, b_im, ALU.mult))
                step(tt(o_re, s0, s1, ALU.subtract))
                step(tt(s0, a_re, b_im, ALU.mult))
                step(tt(s1, a_im, b_re, ALU.mult))
                step(tt(o_im, s0, s1, ALU.add))

            cmul(v[:, NRE, :], v[:, NIM, :], par[:, CRE, :], par[:, CIM, :], v[:, T0, :], v[:, T1, :],
                 v[:, RN, :], v[:, FR, :])
            step(nc.vector.tensor_scalar(v[:, AR, :], v[:, AR, :], -1.0, None, ALU.mult))
            step(nc.vector.tensor_scalar(v[:, ABS, :], par[:, AIM, :], -1.0, None, ALU.mult))
            step(tt(v[:, T0, :], v[:, AR, :], v[:, AR, :], ALU.mult))
            step(tt(v[:, T1, :], par[:, AIM, :], par[:, AIM, :], ALU.mult))
            step(tt(v[:, DEN, :], v[:, T0, :], v[:, T1, :], ALU.add))
            step(nc.vector.reciprocal(v[:, DEN, :], v[:, DEN, :]))
            cmul(v[:, T0, :], v[:, T1, :], v[:, NRE, :], v[:, NIM, :], v[:, AR, :], v[:, ABS, :],
                 v[:, RN, :], v[:, FR, :])
            for o, i in ((NRE, T0), (NIM, T1)):
                step(nc.vector.scalar_tensor_tensor(v[:, o, :], v[:, i, :], 2.0, v[:, DEN, :], ALU.mult, ALU.mult))
            f3 = [f_ph[:, q, :].rearrange("p (t i) -> p t i", i=TPB) for q in range(4)]
            ix = spread(idx[:, P:], [P, NMT, TPB], 1)
            step(tt(f3[0], spread(v[:, TURN, :], [P, NMT, TPB], 2), ix, ALU.mult))
            step(nc.vector.tensor_scalar(f_ph[:, 1, :], f_ph[:, 0, :], ROUND, -ROUND, ALU.add, ALU.add))
            step(tt(f_ph[:, 0, :], f_ph[:, 0, :], f_ph[:, 1, :], ALU.subtract))
            step(tt(f3[1], spread(v[:, DR, :], [P, NMT, TPB], 2), ix, ALU.mult))
            assert n[0] == 33, n
            dve.wait_ge(act_n, 10)
            step(tt(f_ph[:, 2, :], f_ph[:, 2, :], f_ph[:, 1, :], ALU.mult))
            step(tt(f_ph[:, 3, :], f_ph[:, 3, :], f_ph[:, 1, :], ALU.mult))
            s0 = ph2[:, 0, 0:2, :].rearrange("p a (t i) -> p (a t) i", i=TPB)
            s1 = rnd[:, 0:2, :].rearrange("p a (t i) -> p (a t) i", i=TPB)
            cmul(f_re[:], f_im[:], spread(v[:, NRE, :], [P, NMT, TPB], 2), spread(v[:, NIM, :], [P, NMT, TPB], 2),
                 f3[3], f3[2], s0, s1)
            step(nc.vector.tensor_scalar(f_im[:], f_im[:], -1.0, None, ALU.mult))
            for c in range(CPT):
                for q, f in ((0, f_re), (1, f_im)):
                    dst = fm[:, q].rearrange("p t (i c) -> p t i c", c=CPT)[:, :, :, c]
                    step(nc.vector.tensor_scalar(dst, f[:], chan[:, c:c + 1], None, ALU.mult))
            assert n[0] == 50, n
            jx = spread(idx[:, 0:P], [P, GRP, P], 1)

            def phases(g):
                t = slice(g * GRP, (g + 1) * GRP)
                ph, mag = ph2[:, g % 2], mag2[:, g % 2]
                if g >= 2:
                    dve.wait_ge(act_n, 10 + 4 * (g - 1))
                step(tt(ph, spread(v[:, TURN, t], [P, GRP, P], 2), jx, ALU.mult))
                step(nc.vector.tensor_scalar(rnd[:], ph, ROUND, -ROUND, ALU.add, ALU.add))
                step(tt(ph, ph, rnd[:], ALU.subtract))
                step(tt(mag, spread(v[:, DR, t], [P, GRP, P], 2), jx, ALU.mult))

            phases(0)
            for g in range(NG):
                if g + 1 < NG:
                    phases(g + 1)
                dve.wait_ge(act_n, 10 + 4 * (g + 1))
                step(tt(g_im2[:, g % 2], g_im2[:, g % 2], mag2[:, g % 2], ALU.mult))
                step(tt(g_re2[:, g % 2], g_re2[:, g % 2], mag2[:, g % 2], ALU.mult))
            dve.wait_ge(pe_g, NG)
            for h in range(2):
                t = NMT // 2
                dst = kT[:, :, h * D // 2:(h + 1) * D // 2].rearrange("p i (t c) -> p i t c", c=CPT)
                src = psK[:, h, :].rearrange("p (t i c) -> p i t c", i=TPB, c=CPT)
                for i in range(TPB):
                    last = nc.vector.tensor_copy(dst[:, i], src[:, i])
            last.then_inc(kT_done, 1)
            for m in range(2 * NF):
                dst = (lc.k_re if m < NF else lc.k_im)[:, m % NF, :]
                dve.wait_ge(f_ps, m + 1)
                nc.vector.tensor_copy(dst, psF[:, m % 2, 0:D]).then_inc(f_out, 1)
            dve.wait_ge(f_out, 2 * NF)
            step(nc.vector.tensor_copy(lc.k_re2[:], lc.k_re[:]))
            step(nc.vector.tensor_copy(lc.k_re2[0:1, 0, :], lc.k_im[0:1, 0, :]))
            step(nc.vector.memset(lc.k_im[0:1, 0, :], 0.0))

        @block.scalar
        def _(act):
            a = nc.scalar.activation
            act.wait_ge(loaded, 48)
            a(v[:, DT, :], par[:, LDT, :], ACT.Exp).then_inc(act_n, 1)
            a(v[:, AR, :], par[:, LAR, :], ACT.Exp).then_inc(act_n, 1)
            act.wait_ge(vec, 6)
            a(v[:, MAG, :], v[:, DR, :], ACT.Exp).then_inc(act_n, 1)
            a(v[:, SIN, :], v[:, FR, :], ACT.Sin, scale=2 * PI).then_inc(act_n, 1)
            a(v[:, ABS, :], v[:, FR, :], ACT.Abs).then_inc(act_n, 1)
            act.wait_ge(act_n, 5)
            a(v[:, COS, :], v[:, ABS, :], ACT.Sin, scale=-2 * PI, bias=half_pi[:]).then_inc(act_n, 1)
            act.wait_ge(vec, 33)
            a(f_ph[:, 2, :], f_ph[:, 0, :], ACT.Sin, scale=2 * PI).then_inc(act_n, 1)
            a(f_ph[:, 3, :], f_ph[:, 0, :], ACT.Abs).then_inc(act_n, 1)
            act.wait_ge(act_n, 8)
            a(f_ph[:, 3, :], f_ph[:, 3, :], ACT.Sin, scale=-2 * PI, bias=half_pi[:]).then_inc(act_n, 1)
            a(f_ph[:, 1, :], f_ph[:, 1, :], ACT.Exp).then_inc(act_n, 1)
            for g in range(NG):
                act.wait_ge(vec, phases_at(g))
                if g >= 2:
                    act.wait_ge(pe_g, g - 1)
                n = 10 + 4 * g
                ph, mag, g_re, g_im = ph2[:, g % 2], mag2[:, g % 2], g_re2[:, g % 2], g_im2[:, g % 2]
                if g % 2:
                    a(mag, mag, ACT.Exp).then_inc(act_n, 1)
                a(g_im, ph, ACT.Sin, scale=2 * PI).then_inc(act_n, 1)
                a(g_re, ph, ACT.Abs).then_inc(act_n, 1)
                act.wait_ge(act_n, n + 2 + g % 2)
                a(g_re, g_re, ACT.Sin, scale=-2 * PI, bias=half_pi[:]).then_inc(act_n, 1)
                if g % 2 == 0:
                    a(mag, mag, ACT.Exp).then_inc(act_n, 1)

        @block.tensor
        def _(pe):
            for g in range(NG):
                pe.wait_ge(vec, powers_at(g))
                for t in range(GRP):
                    tt_ = g * GRP + t
                    h, o = tt_ // (NMT // 2), (tt_ % (NMT // 2)) * TPB * CPT
                    for q, gg in ((0, g_re2[:, g % 2]), (1, g_im2[:, g % 2])):
                        last = nc.tensor.matmul(psK[:, h, o:o + TPB * CPT], gg[:, t, :], fm[:, q, tt_, :],
                                                start=(q == 0), stop=(q == 1))
                last.then_inc(pe_g, 1)
            pe.wait_ge(lc.loaded, 64)
            pe.wait_ge(kT_done, 1)
            for m in range(2 * NF):
                if m >= 2:
                    pe.wait_ge(f_out, m - 1)
                for k in range(TPB):
                    last = nc.tensor.matmul(psF[:, m % 2, 0:D], lc.fwd[:, k, m * P:(m + 1) * P], kT[:, k, :],
                                            start=(k == 0), stop=(k == TPB - 1))
                last.then_inc(f_ps, 1)


def conv_stage(nc, core, lc, tag):
    with ExitStack() as ctx:
        xn = core.sbuf(f"{tag}_xn", [P, TPB, 2, D], ctx)
        y = core.sbuf(f"{tag}_y", [P, 2 * NF, 2 * D], ctx)
        prod = core.sbuf(f"{tag}_prod", [P, 2, 4, 2 * D], ctx)
        g = core.sbuf(f"{tag}_g", [P, 2, 2 * D], ctx)
        gT = core.sbuf(f"{tag}_gT", [P, 2, 2 * KD, P], ctx)
        psF = core.psum(f"{tag}_psF", [P, 2, 2, 512], ctx)
        psY = core.psum(f"{tag}_psY", [P, 2, 512], ctx)
        psT = core.psum(f"{tag}_psT", [P, 512], ctx)
        psO = core.psum(f"{tag}_psO", [P, 512], ctx)
        xn_done = core.sem(f"{tag}_xn_done")
        f_ps = core.sem(f"{tag}_f_ps")
        prod_done = core.sem(f"{tag}_prod_done")
        y_done = core.sem(f"{tag}_y_done")
        c_ps = core.sem(f"{tag}_c_ps")
        g_done = core.sem(f"{tag}_g_done")
        gT_ps = core.sem(f"{tag}_gT_ps")
        gT_done = core.sem(f"{tag}_gT_done")
        o_ps = core.sem(f"{tag}_o_ps")
        xb_done = core.sem(f"{tag}_xb_done")
        x_done = core.sem(f"{tag}_x_done")
        block = ctx.enter_context(nc.Block())

        @block.scalar
        def _(act):
            with act.Fori(0, B // 2) as i:
                act.wait_ge(f_ps, i * NF)
                core.apart(act)
                for k in range(TPB):
                    for b in range(2):
                        t = i * (2 * TPB) + (b * TPB + k)
                        nc.scalar.activation(xn[:, k, b, :], core.X[:, t, :], ACT.Identity,
                                             bias=core.shift[:, bass.ds(t, 1)],
                                             scale=core.rstd[:, bass.ds(t, 1)]).then_inc(xn_done, 1)
                for l in range(TPB):
                    act.wait_ge(c_ps, i * TPB + (l + 1))
                    act.wait_ge(gT_ps, i * TPB + max(l - 1, 0))
                    nc.scalar.activation(g[:, l % 2, :], psY[:, l % 2, :], ACT.Gelu).then_inc(g_done, 1)
                    act.wait_ge(gT_ps, i * TPB + (l + 1))
                    nc.scalar.activation(gT[:, l % 2], psT[:].rearrange("p (a q) -> p a q", q=P),
                                         ACT.Identity).then_inc(gT_done, 1)

        @block.tensor
        def _(pe):
            with pe.Fori(0, B // 2) as i:
                for f in range(NF):
                    pe.wait_ge(prod_done, i * NF + max(f - 1, 0))
                    for c in range(2):
                        for k in range(TPB):
                            if f == 0 and c == 0:
                                pe.wait_ge(xn_done, i * (2 * TPB) + 2 * (k + 1))
                            m = c * NF + f
                            last = nc.tensor.matmul(psF[:, f % 2, c, :], lc.fwd[:, k, m * P:(m + 1) * P],
                                                    xn[:, k].rearrange("p b d -> p (b d)"),
                                                    start=(k == 0), stop=(k == TPB - 1))
                    last.then_inc(f_ps, 1)

                def project(l):
                    pe.wait_ge(g_done, i * TPB + (l + 1))
                    pe.wait_ge(gT_done, i * TPB + l)
                    for a in range(2 * KD):
                        last = nc.tensor.transpose(psT[:, a * P:(a + 1) * P], g[:, l % 2, a * P:(a + 1) * P],
                                                   core.ident[:])
                    last.then_inc(gT_ps, 1)
                    pe.wait_ge(gT_done, i * TPB + (l + 1))
                    pe.wait_ge(x_done, i * (2 * TPB) + 2 * l)
                    for b in range(2):
                        for k in range(KD):
                            last = nc.tensor.matmul(psO[:, b * D:(b + 1) * D], gT[:, l % 2, b * KD + k, :],
                                                    lc.w[:, k, :], start=(k == 0), stop=(k == KD - 1))
                    last.then_inc(o_ps, 1)

                for l in range(TPB):
                    pe.wait_ge(g_done, i * TPB + max(l - 1, 0))
                    for n, (f, c) in enumerate((f, c) for f in range(NF) for c in range(2)):
                        pe.wait_ge(y_done, i * NF + (f + 1))
                        last = nc.tensor.matmul(psY[:, l % 2, :], lc.inv[:, c * NF + f, l * P:(l + 1) * P],
                                                y[:, c * NF + f, :], start=(n == 0), stop=(n == 2 * NF - 1))
                    last.then_inc(c_ps, 1)
                    if l:
                        project(l - 1)
                project(TPB - 1)

        @block.gpsimd
        def _(pool):
            with pool.Fori(0, B // 2) as i:
                for f in range(NF):
                    pool.wait_ge(prod_done, i * NF + (f + 1))
                    if f == 0:
                        pool.wait_ge(c_ps, i * TPB)
                    p4 = prod[:, f % 2]
                    nc.gpsimd.tensor_tensor(y[:, f, :], p4[:, 0, :], p4[:, 1, :], ALU.subtract)
                    nc.gpsimd.tensor_tensor(y[:, NF + f, :], p4[:, 2, :], p4[:, 3, :], ALU.add).then_inc(y_done, 1)

        @block.vector
        def _(dve):
            with dve.Fori(0, B // 2) as i:
                for f in range(NF):
                    dve.wait_ge(y_done, i * NF + max(f - 1, 0))
                    dve.wait_ge(f_ps, i * NF + (f + 1))
                    for q, (c, kk) in enumerate(((0, lc.k_re), (1, lc.k_im), (0, lc.k_im), (1, lc.k_re2))):
                        last = nc.vector.tensor_tensor(
                            prod[:, f % 2, q, :].rearrange("p (b d) -> p b d", b=2),
                            psF[:, f % 2, c, :].rearrange("p (b d) -> p b d", b=2),
                            spread(kk[:, f, :], [P, 2, D], 1), ALU.mult)
                    last.then_inc(prod_done, 1)
                dve.wait_ge(xn_done, i * (2 * TPB) + 2 * TPB)
                for l in range(TPB):
                    for b in range(2):
                        t = i * (2 * TPB) + (b * TPB + l)
                        nc.vector.tensor_tensor(core.X[:, t, :], core.X[:, t, :], lc.b[:], ALU.add).then_inc(xb_done, 1)
                for l in range(TPB):
                    for b in range(2):
                        t = i * (2 * TPB) + (b * TPB + l)
                        n = 2 * l + b + 1
                        dve.wait_ge(xb_done, i * (2 * TPB) + n)
                        dve.wait_ge(o_ps, i * TPB + (l + 1))
                        nc.vector.tensor_tensor(core.X[:, t, :], psO[:, b * D:(b + 1) * D], core.X[:, t, :],
                                                ALU.add).then_inc(x_done, 1)
                        dve.wait_ge(x_done, i * (2 * TPB) + n)
                        core.apart(dve)
                        nc.vector.bn_stats(core.bn[:, t, :], core.X[:, t, :])


def conv_constants():
    import numpy as np

    l = np.arange(S)[:, None]
    f = np.arange(S)[None, :]
    turn = 2 * np.pi * ((l * f) % (2 * S)) / (2 * S)
    fwd = np.concatenate([np.cos(turn), -np.sin(turn)], 1)
    fwd[:, S] = (-1.0) ** np.arange(S)
    inv = fwd.T / S
    inv[0] /= 2
    inv[S] /= 2
    index = np.concatenate([np.arange(P), P * np.arange(TPB)])
    chan = np.arange(P)[:, None] // NMODE == np.arange(CPT)[None, :]
    return [np.ascontiguousarray(a.astype(np.float32)) for a in (fwd, inv, index, chan)]
NH = 16
HD = D // NH
PAD = 32
HPT = P // PAD
NG_H = NH // HPT
BF16 = mybir.dt.bfloat16
Q_PART = (0, 0, 0, 1, 1, 2)
K_PART = (0, 1, 2, 0, 1, 0)
NSLOT = len(Q_PART)
NROW = NSLOT * HD + 6
NLOAD = 2 * NSLOT + 2


def distance_attention_stage(nc, core, tag, wq, wk, bq, bk, wv, bv, wo, bo, sel):
    with ExitStack() as ctx:
        sbf = lambda n, s: core.sbuf(f"{tag}_{n}", s, ctx)
        sb16 = lambda n, s: ctx.enter_context(nc.sbuf_tensor(f"{tag}_{n}", s, BF16))
        parts_d = nc.dram_tensor(f"{tag}_parts_dram", [B * 2 * KD * 3, P, S], BF16).ap()
        lens_d = nc.dram_tensor(f"{tag}_lens_dram", [B, 3, 2 * NH, S], BF16).ap()
        wqk = sbf("wqk", [P, 2, KD, D])
        bqk = sbf("bqk", [P, 2, KD])
        nbq = sbf("nbq", [P, KD])
        wv_sb, wo_sb = sbf("wv", [P, KD, D]), sbf("wo", [P, KD, D])
        bv_sb, bo_sb = sbf("bv", [P, D]), sbf("bo", [P, D])
        sel_sb = sbf("sel", [P, 2 * KD, 2 * NH])
        sq = sbf("sq", [P, 2 * KD, S])
        xn = sq[:, 0:KD, :].rearrange("p k s -> p (k s)").rearrange("p (j d) -> p j d", d=D)
        xnT = sbf("xnT", [P, KD, S])
        raw = sbf("raw", [P, 2, S])
        parts = sb16("parts", [P, 2 * KD, 3, S])
        lens = sb16("lens", [2 * NH, 3, S])
        stack = sb16("stack", [P, 2, 2, HPT, S])
        va = sbf("va", [P, TPB, NH, PAD])
        dist = sbf("dist", [P, 2, HPT, TPB, S])
        fold = sbf("fold", [P, 2, S])
        rest = fold[:, 0, :]
        least = sbf("least", [P, 2, S])
        mq = sbf("mq", [P, 2, HPT, TPB])
        mb = sbf("mb", [P, HPT, S])
        oT = sbf("oT", [P, NG_H, S])
        rec = sbf("rec", [P, NH])
        on = sbf("on", [P, D])
        onT = sbf("onT", [P, KD, P])
        psS = core.psum(f"{tag}_psS", [P, TPB, 512], ctx)
        psM, psB, psO, psX = (core.psum(f"{tag}_{n}", [P, 512], ctx) for n in ("psM", "psB", "psO", "psX"))
        sem = lambda n: core.sem(f"{tag}_{n}", ctx)
        loaded, va_set, nbq_done = sem("loaded"), sem("va_set"), sem("nbq_done")
        xn_done, tr_done, xnT_done = sem("xn_done"), sem("tr_done"), sem("xnT_done")
        pr_ps, raw_done, split_step, split_done = sem("pr_ps"), sem("raw_done"), sem("split_step"), sem("split_done")
        len_ps, len_step, len_done, parts_out, stack_in = sem("len_ps"), sem("len_step"), sem("len_done"), sem("parts_out"), [sem("stack0"), sem("stack1")]
        v_ps, v_done = sem("v_ps"), sem("v_done")
        s_ps, clamp_done, fold_done, least_done = sem("s_ps"), sem("clamp_done"), sem("fold_done"), sem("least_done")
        m_ps, mq_done, root_done, mroot_done = sem("m_ps"), sem("mq_done"), sem("root_done"), sem("mroot_done")
        b_ps, mb_done, exp_done, sq_done = sem("b_ps"), sem("mb_done"), sem("exp_done"), sem("sq_done")
        sub0_done, sub_done = sem("sub0_done"), sem("sub_done")
        o_ps, oT_done = sem("o_ps"), sem("oT_done")
        q_ps, rec_done, on_done, onT_ps, onT_done = sem("q_ps"), sem("rec_done"), sem("on_done"), sem("onT_ps"), sem("onT_done")
        y_ps, xb_done, x_done = sem("y_ps"), sem("xb_done"), sem("x_done")
        block = ctx.enter_context(nc.Block())
        NPR = 2 * KD

        def at(b, per, c):
            v = b * per + c
            return max(v, 0) if type(b) is int else v

        def batches(eng, body):
            body(0, True, False)
            with eng.Fori(1, B - 1) as b:
                body(b, False, False)
            body(B - 1, False, True)

        def before(b, g):
            return (b - 1, NG_H - 1) if g == 0 else (b, g - 1)

        @block.sync
        def _(sp):
            for n, w in enumerate((wq, wk)):
                sp.dma_start(wqk[:, n], w.rearrange("(k p) n -> p k n", p=P)).then_inc(loaded, 16)
            for n, b in enumerate((bq, bk)):
                sp.dma_start(bqk[:, n], b).then_inc(loaded, 16)
            sp.dma_start(wv_sb[:], wv.rearrange("(k p) n -> p k n", p=P)).then_inc(loaded, 16)
            sp.dma_start(wo_sb[:], wo.rearrange("(k p) n -> p k n", p=P)).then_inc(loaded, 16)
            sp.dma_start(bv_sb[:], bv.unsqueeze(0).broadcast_to([P, D])).then_inc(loaded, 16)
            sp.dma_start(bo_sb[:], bo.unsqueeze(0).broadcast_to([P, D])).then_inc(loaded, 16)
            sp.dma_start(sel_sb[:], sel).then_inc(loaded, 16)
            sp.wait_ge(va_set, 3)

            def store(b):
                for p in range(NPR):
                    sp.wait_ge(split_done, at(b, NPR, p + 1))
                    sp.dma_start(parts_d[bass.ds((b * NPR + p) * 3, 3)].rearrange("k p s -> p k s"),
                                 parts[:, p]).then_inc(parts_out, 16)
                sp.wait_ge(len_done, at(b, 1, 1))
                sp.dma_start(lens_d[b].rearrange("k h s -> h k s"), lens[:]).then_inc(parts_out, 16)

            def load(b, g):
                u, half = g % 2, slice(g % 2 * P // 2, (g % 2 + 1) * P // 2)
                if type(b) is not int or b or g >= 2:
                    sp.wait_ge(s_ps, at(b, 2 * NH, 2 * HPT * (g - 1)))
                for n, part in ((0, Q_PART), (1, K_PART)):
                    for s in range(NSLOT):
                        src = parts_d[(b * NPR + (n * KD + g // 2)) * 3 + part[s]]
                        sp.dma_start(stack[s * HD:(s + 1) * HD, u, n],
                                     src[half, :].rearrange("(i d) s -> d i s", i=HPT)).then_inc(stack_in[u], 16)
                    r = NSLOT * HD + 3 * n
                    sp.dma_start(stack[r:r + 3, u, n],
                                 lens_d[b][:, n * NH + g * HPT:n * NH + (g + 1) * HPT, :]).then_inc(stack_in[u], 16)

            def body(b, first, last):
                for g in range(NG_H):
                    if g == 0:
                        sp.wait_ge(parts_out, at(b, 16 * (NPR + 1), 16 * (NPR + 1)))
                    load(b, g)
                if not last:
                    store(b + 1)

            store(0)
            batches(sp, body)

        @block.tensor
        def _(pe):
            mm, turn = nc.tensor.matmul, nc.tensor.transpose
            pe.wait_ge(loaded, 144)

            def scores(b, g, i):
                h, u = g * HPT + i, g % 2
                if i == 0:
                    pe.wait_ge(stack_in[u], at(b, 2 * 16 * NLOAD, (g // 2 + 1) * 16 * NLOAD))
                for kb in range(TPB):
                    if kb % 2 == 0:
                        pe.wait_ge(clamp_done, at(b, 2 * NH, 2 * h - 1 + kb // 2))
                    last = mm(psS[:, kb, :], stack[0:NROW, u, 1, i, kb * P:(kb + 1) * P],
                              stack[0:NROW, u, 0, i, :], start=True, stop=True)
                    if kb % 2:
                        last.then_inc(s_ps, 1)

            def turn_least(b, g, i):
                h = g * HPT + i
                pe.wait_ge(least_done, at(b, NH, h + 1))
                pe.wait_ge(mq_done, at(b, NH, h))
                if i == 0:
                    pe.wait_ge(mb_done, at(b, NH, h))
                for q in range(TPB):
                    last = turn(psM[:, q * P:(q + 1) * P], least[:, h % 2, q * P:(q + 1) * P], core.ident[:])
                last.then_inc(m_ps, 1)

            def spread_least(b, g, i, last_batch):
                h, bank = g * HPT + i, (psB, psM)[i % 2]
                if i == 0:
                    pe.wait_ge(mroot_done, at(b, NG_H, g + 1))
                    if g == 1:
                        pe.wait_ge(onT_done, at(b, TPB, 0))
                    if g == 2:
                        pe.wait_ge(x_done, at(b, TPB, 0))
                        if not last_batch:
                            pe.wait_ge(raw_done, at(b, NPR, 2 * NPR))
                if i >= 2:
                    pe.wait_ge(mb_done, at(b, NH, h - 1))
                for q in range(TPB):
                    last = turn(bank[:, q * P:(q + 1) * P], mq[:, g % 2, i, q:q + 1].broadcast_to([P, P]), core.ident[:])
                last.then_inc(b_ps, 1)

            def weigh_v(b, g, i):
                h = g * HPT + i
                if i == 0:
                    pe.wait_ge(oT_done, at(b, NG_H, g))
                    if g == 0:
                        pe.wait_ge(v_done, at(b, 2, 2))
                pe.wait_ge(exp_done, at(b, NH, h + 1))
                for kb in range(TPB):
                    last = mm(psO[i * PAD:(i + 1) * PAD, :], va[:, kb, h, :], dist[:, g % 2, i, kb, :],
                              start=(kb == 0), stop=(kb == TPB - 1))
                last.then_inc(o_ps, 1)

            def project_v(b, half):
                if half == 0:
                    pe.wait_ge(len_done, at(b, 1, 1))
                else:
                    pe.wait_ge(v_done, at(b, 2, 1))
                for j in (2 * half, 2 * half + 1):
                    for k in range(KD):
                        last = mm(psX[:, (j % 2) * D:(j % 2 + 1) * D], xnT[:, k, j * P:(j + 1) * P], wv_sb[:, k, :],
                                  start=(k == 0), stop=(k == KD - 1))
                last.then_inc(v_ps, 1)

            def turn_rows(b, k, first):
                if k == 0:
                    pe.wait_ge(xn_done, at(b, TPB, TPB))
                    if not first:
                        pe.wait_ge(v_done, at(b, 2, 0))
                        pe.wait_ge(on_done, at(b, TPB, -TPB))
                elif not first:
                    pe.wait_ge(mb_done, at(b, NH, -NH + 2 * HPT))
                    pe.wait_ge(x_done, at(b, TPB, -TPB))
                for j in range(TPB):
                    last = turn((psX, psB)[k][:, j * P:(j + 1) * P], xn[:, j, k * P:(k + 1) * P], core.ident[:])
                last.then_inc(tr_done, 1)

            def project(b, p):
                pe.wait_ge(xnT_done, at(b, KD, KD))
                if p >= 2:
                    pe.wait_ge(raw_done, at(b, NPR, p - 1))
                for k in range(KD):
                    last = mm((psX, psB)[p % 2][:], wqk[:, p // KD, k, (p % KD) * P:(p % KD + 1) * P], xnT[:, k, :],
                              start=(k == 0), stop=(k == KD - 1))
                last.then_inc(pr_ps, 1)

            def lengths(b):
                pe.wait_ge(sq_done, at(b, NPR, NPR))
                pe.wait_ge(raw_done, at(b, NPR, NPR))
                for p in range(NPR):
                    last = mm(psX[0:2 * NH, :], sel_sb[:, p, :], sq[:, p, :], start=(p == 0), stop=(p == NPR - 1))
                last.then_inc(len_ps, 1)

            def out_turn(b, j):
                if j == 0:
                    pe.wait_ge(oT_done, at(b, NG_H, NG_H))
                pe.wait_ge(on_done, at(b, TPB, j))
                for g in range(NG_H):
                    last = turn(psX[:, g * P:(g + 1) * P], oT[:, g, j * P:(j + 1) * P], core.ident[:])
                last.then_inc(q_ps, 1)

            def out_turn_back(b, j):
                pe.wait_ge(on_done, at(b, TPB, j + 1))
                pe.wait_ge(x_done, at(b, TPB, j))
                for k in range(KD):
                    last = turn(psB[:, k * P:(k + 1) * P], on[:, k * P:(k + 1) * P], core.ident[:])
                last.then_inc(onT_ps, 1)

            def out_project(b, j):
                pe.wait_ge(onT_done, at(b, TPB, j + 1))
                for k in range(KD):
                    last = mm(psB[:, 0:D], onT[:, k, :], wo_sb[:, k, :], start=(k == 0), stop=(k == KD - 1))
                last.then_inc(y_ps, 1)

            def body(b, first, last):
                for g in range(NG_H):
                    for i in range(HPT):
                        if g == 1 and not first:
                            if i == 0:
                                pe.wait_ge(v_done, at(b, 2, 2))
                            out_turn(b - 1, i)
                            if i:
                                out_project(b - 1, i - 1)
                        if g == 2:
                            if i == 0 and not first:
                                pe.wait_ge(mb_done, at(b, NH, 2 * HPT))
                                out_project(b - 1, TPB - 1)
                            if not last:
                                if i == 1:
                                    turn_rows(b + 1, 1, False)
                                elif i:
                                    project(b + 1, 2 * i - 3)
                        if i < HPT - 1:
                            scores(b, g, i + 1)
                        if g == 1 and not first:
                            if i == 0:
                                pe.wait_ge(mb_done, at(b, NH, HPT))
                            out_turn_back(b - 1, i)
                        if g == 2 and not last:
                            if i == 0:
                                turn_rows(b + 1, 0, False)
                            elif i < HPT - 1:
                                project(b + 1, 2 * i - 2)
                        if g == 3 and i == 0 and not last:
                            lengths(b + 1)
                        turn_least(b, g, i)
                        if g or not first:
                            weigh_v(*before(b, g), i)
                        if g == 0 and i == HPT - 1:
                            project_v(b, 0)
                    if g < NG_H - 1:
                        scores(b, g + 1, 0)
                    elif not last:
                        scores(b + 1, 0, 0)
                    if g == 0:
                        project_v(b, 1)
                    for i in range(HPT):
                        spread_least(b, g, i, last)

            for k in range(KD):
                turn_rows(0, k, True)
            for p in range(NPR):
                project(0, p)
            lengths(0)
            scores(0, 0, 0)
            batches(pe, body)
            for i in range(HPT):
                weigh_v(B - 1, NG_H - 1, i)
            pe.wait_ge(mb_done, B * NH)
            for j in range(TPB):
                out_turn(B - 1, j)
                out_turn_back(B - 1, j)
                out_project(B - 1, j)

        @block.scalar
        def _(act):
            a = nc.scalar.activation
            act.wait_ge(loaded, 144)
            act.wait_ge(nbq_done, 1)

            def normalise(b):
                act.wait_ge(len_ps, at(b, 1, 0))
                core.apart(act)
                for j in range(TPB):
                    t = b * TPB + j
                    a(xn[:, j, :], core.X[:, t, :], ACT.Identity, bias=core.shift[:, bass.ds(t, 1)],
                      scale=core.rstd[:, bass.ds(t, 1)]).then_inc(xn_done, 1)

            def take_rows(b):
                for k in range(KD):
                    act.wait_ge(tr_done, at(b, KD, k + 1))
                    a(xnT[:, k, :], (psX, psB)[k][:], ACT.Identity).then_inc(xnT_done, 1)

            def take_projection(b, p):
                act.wait_ge(pr_ps, at(b, NPR, p + 1))
                act.wait_ge(split_done, at(b, NPR, p - 1))
                act.wait_ge(sq_done, at(b, NPR, p - 1))
                scale, bias = (-2.0, nbq[:, p:p + 1]) if p < KD else (1.0, bqk[:, 1, p - KD:p - KD + 1])
                a(raw[:, p % 2, :], (psX, psB)[p % 2][:], ACT.Identity, scale=scale, bias=bias).then_inc(raw_done, 1)

            def root(b, g, i):
                h = g * HPT + i
                act.wait_ge(clamp_done, at(b, 2 * NH, 2 * h + 2))
                act.wait_ge(least_done, at(b, NH, h + 1))
                a(dist[:, g % 2, i], dist[:, g % 2, i], ACT.Sqrt).then_inc(root_done, 1)

            def weights(b, g, i):
                if i == 0:
                    act.wait_ge(sub0_done, at(b, NG_H, g + 1))
                else:
                    act.wait_ge(sub_done, at(b, NG_H * (HPT - 1), g * (HPT - 1) + i))
                a(dist[:, g % 2, i], dist[:, g % 2, i], ACT.Exp, scale=-1.0).then_inc(exp_done, 1)

            def take_sums(b, g):
                act.wait_ge(o_ps, at(b, NH, (g + 1) * HPT))
                act.wait_ge(q_ps, at(b, TPB, 0))
                a(oT[:, g, :], psO[:], ACT.Identity).then_inc(oT_done, 1)

            def take_turned(b, j):
                act.wait_ge(onT_ps, at(b, TPB, j + 1))
                act.wait_ge(y_ps, at(b, TPB, j))
                a(onT[:], psB[:, 0:D].rearrange("p (k q) -> p k q", k=KD), ACT.Identity).then_inc(onT_done, 1)

            def body(b, first, last):
                for g in range(NG_H):
                    prev = g or not first
                    out, prep = g == 1 and not first, g == 2 and not last
                    if prep:
                        normalise(b + 1)
                    for two in range(2):
                        for i in (2 * two, 2 * two + 1):
                            if prev:
                                weights(*before(b, g), i)
                        if prep:
                            if two == 0:
                                take_rows(b + 1)
                            else:
                                take_projection(b + 1, 2)
                        if out:
                            take_turned(b - 1, 2 * two)
                        root(b, g, 2 * two)
                        if prep and two:
                            take_projection(b + 1, 3)
                        root(b, g, 2 * two + 1)
                        if prep and two == 0:
                            take_projection(b + 1, 0)
                            take_projection(b + 1, 1)
                        if out:
                            take_turned(b - 1, 2 * two + 1)
                    if prev:
                        take_sums(*before(b, g))
                    act.wait_ge(mq_done, at(b, NH, (g + 1) * HPT))
                    a(mq[:, g % 2], mq[:, g % 2], ACT.Sqrt).then_inc(mroot_done, 1)
                    for i in range(HPT):
                        act.wait_ge(b_ps, at(b, NH, g * HPT + i + 1))
                        if i == 0:
                            act.wait_ge(sub0_done, at(b, NG_H, g))
                            act.wait_ge(sub_done, at(b, NG_H * (HPT - 1), g * (HPT - 1)))
                        a(mb[:, i, :], (psB, psM)[i % 2][:], ACT.Identity).then_inc(mb_done, 1)

            normalise(0)
            take_rows(0)
            for p in range(NPR):
                take_projection(0, p)
            batches(act, body)
            for i in range(HPT):
                weights(B - 1, NG_H - 1, i)
            take_sums(B - 1, NG_H - 1)
            for j in range(TPB):
                take_turned(B - 1, j)

        @block.gpsimd
        def _(pool):
            nc.gpsimd.memset(va[:], 0.0).then_inc(va_set, 1)
            pool.wait_ge(va_set, 1)
            nc.gpsimd.memset(va[:, :, :, HD:HD + 1], 1.0).then_inc(va_set, 1)
            pool.wait_ge(va_set, 2)
            nc.gpsimd.memset(stack[NSLOT * HD:], 1.0).then_inc(va_set, 1)

            def squares(b):
                for p in range(NPR):
                    pool.wait_ge(raw_done, at(b, NPR, p + 1))
                    r = raw[:, p % 2, :]
                    nc.gpsimd.tensor_tensor(sq[:, p, :], r, r, ALU.mult).then_inc(sq_done, 1)

            def body(b, first, last):
                for h in range(NH):
                    g, i = h // HPT, h % HPT
                    if i == 0:
                        continue
                    pool.wait_ge(root_done, at(b, NH, h + 1))
                    pool.wait_ge(mb_done, at(b, NH, h + 1))
                    d = dist[:, g % 2, i]
                    nc.gpsimd.tensor_tensor(d, d, spread(mb[:, i, :], [P, TPB, S], 1),
                                            ALU.subtract).then_inc(sub_done, 1)
                    if g == 1 and i == HPT - 1 and not last:
                        squares(b + 1)

            pool.wait_ge(va_set, 3)
            squares(0)
            batches(pool, body)

        @block.vector
        def _(dve):
            tt, copy = nc.vector.tensor_tensor, nc.vector.tensor_copy
            dve.wait_ge(loaded, 144)
            nc.vector.tensor_scalar(nbq[:], bqk[:, 0], -2.0, None, ALU.mult).then_inc(nbq_done, 1)
            dve.wait_ge(va_set, 2)

            def split(b, p):
                r = raw[:, p % 2, :]
                dve.wait_ge(raw_done, at(b, NPR, p + 1))
                dve.wait_ge(parts_out, at(b, 16 * (NPR + 1), 0))
                copy(parts[:, p, 0, :], r).then_inc(split_step, 1)
                dve.wait_ge(split_step, at(b, 3 * NPR, 3 * p + 1))
                tt(rest, r, parts[:, p, 0, :], ALU.subtract).then_inc(split_step, 1)
                dve.wait_ge(split_step, at(b, 3 * NPR, 3 * p + 2))
                copy(parts[:, p, 1, :], rest).then_inc(split_step, 1)
                dve.wait_ge(split_step, at(b, 3 * NPR, 3 * p + 3))
                tt(parts[:, p, 2, :], rest, parts[:, p, 1, :], ALU.subtract).then_inc(split_done, 1)

            def split_lengths(b):
                ps, r = psX[0:2 * NH, :], fold[0:2 * NH, 0, :]
                dve.wait_ge(len_ps, at(b, 1, 1))
                dve.wait_ge(parts_out, at(b, 16 * (NPR + 1), 0))
                dve.wait_ge(split_done, at(b, NPR, NPR))
                copy(lens[:, 0, :], ps).then_inc(len_step, 1)
                dve.wait_ge(len_step, at(b, 3, 1))
                tt(r, ps, lens[:, 0, :], ALU.subtract).then_inc(len_step, 1)
                dve.wait_ge(len_step, at(b, 3, 2))
                copy(lens[:, 1, :], r).then_inc(len_step, 1)
                dve.wait_ge(len_step, at(b, 3, 3))
                tt(lens[:, 2, :], r, lens[:, 1, :], ALU.subtract).then_inc(len_done, 1)

            def take_v(b, half):
                dve.wait_ge(v_ps, at(b, 2, half + 1))
                dve.wait_ge(o_ps, at(b, NH, 0))
                tt(va[:, 2 * half:2 * half + 2, :, 0:HD], psX[:].rearrange("p (j h d) -> p j h d", j=2, h=NH),
                   spread(bv_sb[:].rearrange("p (h d) -> p h d", h=NH), [P, 2, NH, HD], 1), ALU.add).then_inc(v_done, 1)

            def reduce_least(b, h):
                dve.wait_ge(m_ps, at(b, NH, h + 1))
                nc.vector.tensor_reduce(mq[:, h // HPT % 2, h % HPT, :], psM[:].rearrange("p (q k) -> p q k", k=P),
                                        AX.X, ALU.min).then_inc(mq_done, 1)

            def norm_rows(b, j):
                t = b * TPB + j
                heads = psX[:].rearrange("p (h c) -> p h c", c=PAD)
                dve.wait_ge(q_ps, at(b, TPB, j + 1))
                nc.vector.reciprocal(rec[:], heads[:, :, HD]).then_inc(rec_done, 1)
                tt(core.X[:, t, :], core.X[:, t, :], bo_sb[:], ALU.add).then_inc(xb_done, 1)
                dve.wait_ge(rec_done, at(b, TPB, j + 1))
                dve.wait_ge(onT_ps, at(b, TPB, j))
                tt(on[:].rearrange("p (h d) -> p h d", h=NH), heads[:, :, 0:HD],
                   spread(rec[:], [P, NH, HD], 2), ALU.mult).then_inc(on_done, 1)

            def add_rows(b, j):
                t = b * TPB + j
                dve.wait_ge(xb_done, at(b, TPB, j + 1))
                dve.wait_ge(y_ps, at(b, TPB, j + 1))
                tt(core.X[:, t, :], psB[:, 0:D], core.X[:, t, :], ALU.add).then_inc(x_done, 1)
                dve.wait_ge(x_done, at(b, TPB, j + 1))
                core.apart(dve)
                nc.vector.bn_stats(core.bn[:, t, :], core.X[:, t, :])

            def shift_first(b, g):
                d = dist[:, g % 2, 0]
                dve.wait_ge(root_done, at(b, NH, g * HPT + 1))
                dve.wait_ge(mb_done, at(b, NH, g * HPT + 1))
                tt(d, d, spread(mb[:, 0, :], [P, TPB, S], 1), ALU.subtract).then_inc(sub0_done, 1)

            def body(b, first, last):
                for g in range(NG_H):
                    out, prep = g == 1 and not first, g == 2 and not last
                    for i in range(HPT):
                        h = g * HPT + i
                        d = dist[:, g % 2, i]
                        dve.wait_ge(o_ps, at(b, NH, h - 2 * HPT + 1))
                        for c in range(2):
                            dve.wait_ge(s_ps, at(b, 2 * NH, 2 * h + c + 1))
                            nc.vector.tensor_scalar(d[:, 2 * c:2 * c + 2, :], psS[:, 2 * c:2 * c + 2, :], 1e-12, None,
                                                    ALU.max).then_inc(clamp_done, 1)
                        if i == 0 and (g or not first):
                            shift_first(*before(b, g))
                        dve.wait_ge(clamp_done, at(b, 2 * NH, 2 * h + 2))
                        tt(fold[:], d[:, 0:2, :], d[:, 2:4, :], ALU.min).then_inc(fold_done, 1)
                        if i:
                            reduce_least(b, h - 1)
                        dve.wait_ge(fold_done, at(b, NH, h + 1))
                        dve.wait_ge(m_ps, at(b, NH, h - 1))
                        tt(least[:, h % 2, :], fold[:, 0, :], fold[:, 1, :], ALU.min).then_inc(least_done, 1)
                        if out:
                            norm_rows(b - 1, i)
                        if out and i:
                            add_rows(b - 1, i - 1)
                        if g == 2 and i == 0 and not first:
                            add_rows(b - 1, TPB - 1)
                        if prep and i == 2:
                            split(b + 1, 0)
                            split(b + 1, 1)
                        if prep and i == 3:
                            split(b + 1, 2)
                        if g == 3 and i == 1 and not last:
                            split_lengths(b + 1)
                    if g == 0:
                        take_v(b, 0)
                    reduce_least(b, (g + 1) * HPT - 1)
                    if g == 0:
                        take_v(b, 1)
                    if prep:
                        split(b + 1, 3)

            for p in range(NPR):
                split(0, p)
            split_lengths(0)
            batches(dve, body)
            shift_first(B - 1, NG_H - 1)
            for j in range(TPB):
                norm_rows(B - 1, j)
                add_rows(B - 1, j)


def attention_constants():
    import numpy as np

    sel = np.zeros((P, 2 * KD, 2 * NH), np.float32)
    for p in range(2 * KD):
        sel[np.arange(P), p, (p // KD) * NH + (p % KD) * (P // HD) + np.arange(P) // HD] = (0.25, 1.0)[p // KD]
    return sel
DI = 512
HM, PM = 8, 64
NST = 128
TAPS = 4
NCT = (DI + 2 * NST) // P
KI = DI // P


def state_space_stage(nc, core, tag, w_in, conv_w, conv_b, dt_bias, a_log, norm_w, w_out, upto):
    with ExitStack() as ctx:
        WIN = 2 * DI + 2 * NST + HM
        sbf = lambda n, s: core.sbuf(f"{tag}_{n}", s, ctx)
        win = sbf("win", [P, KD, WIN])
        wout = sbf("wout", [P, KI, D])
        cw = sbf("cw", [P, NCT, TAPS])
        cb = sbf("cb", [P, NCT])
        nw = sbf("nw", [P, KI])
        dtb = sbf("dtb", [P, HM])
        neg_a = sbf("neg_a", [P, HM])
        tri = sbf("tri", [P, P])
        xn = sbf("xn", [P, TPB, D])
        xnT = sbf("xnT", [P, KD, S])
        padded = sbf("padded", [P, NCT, TAPS - 1 + S])
        xbc2 = sbf("xbc", [P, 2, NCT, S])
        z2 = sbf("z", [P, 2, TPB, DI])
        dtT = sbf("dtT", [P, S])
        dv2 = sbf("dv", [P, 2, 12, TPB, HM])
        xdt = sbf("xdt", [P, 2, DI])
        xdec = sbf("xdec", [P, 2, DI])
        b_tok = sbf("b_tok", [P, 2, NST])
        gm = sbf("gm", [P, 2, P])
        lt = sbf("lt", [P, 2, HM, P])
        st = sbf("st", [P, DI])
        st2 = sbf("st2", [P, DI])
        yo = sbf("yo", [P, DI])
        y = sbf("y", [P, TPB, DI])
        ybn = sbf("ybn", [P, TPB, 6])
        ymv = sbf("ymv", [P, TPB, 2])
        yr = sbf("yr", [P, TPB])
        yT = sbf("yT", [P, 2, KI, P])
        psP = core.psum(f"{tag}_psP", [P, 2, 512], ctx)
        psX = core.psum(f"{tag}_psX", [P, 512], ctx)
        psG = core.psum(f"{tag}_psG", [P, 512], ctx)
        psC = core.psum(f"{tag}_psC", [P, 2, 512], ctx)
        psY = core.psum(f"{tag}_psY", [P, 512], ctx)
        psO = core.psum(f"{tag}_psO", [P, 512], ctx)
        sem = lambda n: core.sem(f"{tag}_{n}", ctx)
        loaded, prep = sem("loaded"), sem("prep")
        a_exp = sem("a_exp")
        xn_done, tr_done, xnT_done = sem("xn_done"), sem("tr_done"), sem("xnT_done")
        p_ps, p_done, tap, conv_done, silu_done = sem("p_ps"), sem("p_done"), sem("tap"), sem("conv_done"), sem("silu_done")
        dt_ps, dt_step, dt_act, cs_ps = sem("dt_ps"), sem("dt_step"), sem("dt_act"), sem("cs_ps")
        x_ps, g_ps, c_ps = sem("x_ps"), sem("g_ps"), sem("c_ps")
        xdt_done, xdec_done, g_done, l_done, lexp_done, m_done = (
            sem("xdt_done"), sem("xdec_done"), sem("g_done"), sem("l_done"), sem("lexp_done"), sem("m_done"))
        yo_ps, yd_ps, st_ps, yo_done, y_done, st_done, st_step = (
            sem("yo_ps"), sem("yd_ps"), sem("st_ps"), sem("yo_done"), sem("y_done"), sem("st_done"), sem("st_step"))
        ybn_done, ymv_done, yroot_done, yr_done, yn_done, yz_done = (
            sem("ybn_done"), sem("ymv_done"), sem("yroot_done"), sem("yr_done"), sem("yn_done"), sem("yz_done"))
        yT_ps, yT_done, o_ps, x_done = sem("yT_ps"), sem("yT_done"), sem("o_ps"), sem("x_done")
        block = ctx.enter_context(nc.Block())
        NP_ = NCT + TPB + 1
        (XD, AB, RL, DT, A, CS, NCS, TOT, DIF, EOUT, DEC, ETOT) = range(12)

        @block.sync
        def _(sp):
            for dst, src in ((win[:], w_in.rearrange("(k p) n -> p k n", p=P)),
                             (wout[:], w_out.rearrange("(k p) n -> p k n", p=P)),
                             (cw[:], conv_w), (cb[:], conv_b), (nw[:], norm_w),
                             (dtb[:], dt_bias.unsqueeze(0).broadcast_to([P, HM])),
                             (neg_a[:], a_log.unsqueeze(0).broadcast_to([P, HM])), (tri[:], upto)):
                sp.dma_start(dst, src).then_inc(loaded, 16)

        def batches(eng, front, back):
            front(0)
            with eng.Fori(0, B // 2 - 1) as b2:
                for u in range(2):
                    back(b2 * 2 + u, u, True)
            back(B - 2, 0, True)
            back(B - 1, 1, False)

        @block.tensor
        def _(pe):
            pe.wait_ge(loaded, 128)
            pe.wait_ge(prep, 1 + KI)

            def turn_rows(b, k):
                pe.wait_ge(p_done, b * NP_)
                if k == 0:
                    pe.wait_ge(xn_done, b * TPB + TPB)
                for j in range(TPB):
                    last = nc.tensor.transpose(psP[:, k, j * P:(j + 1) * P], xn[:, j, k * P:(k + 1) * P],
                                               core.ident[:])
                last.then_inc(tr_done, 1)

            def project(b, v, p):
                if p < 2:
                    pe.wait_ge(xnT_done, b * KD + KD)
                else:
                    pe.wait_ge(p_done, b * NP_ + (p - 1))
                for k in range(KD):
                    if p < NCT:
                        lhsT, rhs = win[:, k, DI + p * P:DI + (p + 1) * P], xnT[:, k, :]
                        out = psP[:, p % 2, :]
                    elif p > NCT:
                        j = p - NCT - 1
                        lhsT, rhs = xnT[:, k, j * P:(j + 1) * P], win[:, k, 0:DI]
                        out = psP[:, p % 2, :]
                    else:
                        lhsT, rhs = win[:, k, WIN - HM:WIN], xnT[:, k, :]
                        out = psP[0:HM, p % 2, :]
                    last = nc.tensor.matmul(out, lhsT, rhs, start=(k == 0), stop=(k == KD - 1))
                last.then_inc(p_ps, 1)

            def turn_dt(b):
                pe.wait_ge(p_done, b * NP_ + (NCT + 1))
                core.behind(pe)
                for j in range(TPB):
                    last = nc.tensor.transpose(psO[:, j * HM:(j + 1) * HM], dtT[0:HM, j * P:(j + 1) * P],
                                               core.ident[0:HM, 0:HM])
                last.then_inc(dt_ps, 1)

            def sum_dt(b, v):
                steps = dv2[:, v, A].rearrange("p c h -> p (c h)")
                pe.wait_ge(dt_step, b * 8 + 4)
                nc.tensor.matmul(psO[:, 64:64 + TPB * HM], tri[:], steps, start=True, stop=True)
                nc.tensor.matmul(psO[:, 128:128 + TPB * HM], core.ones[:], steps,
                                 start=True, stop=True).then_inc(cs_ps, 1)

            def front(b):
                for k in range(KD):
                    turn_rows(b, k)
                for p in range(NP_):
                    project(b, 0, p)
                turn_dt(b)
                sum_dt(b, 0)

            def back(b, u, more):
                at = lambda per, c: b * per + c
                xbc, dv = xbc2[:, u], dv2[:, u]
                pe.wait_ge(silu_done, at(NCT, NCT))
                pe.wait_ge(dt_step, at(8, 8))

                def chunk_inputs(c):
                    q = slice(c * P, (c + 1) * P)
                    pe.wait_ge(xdt_done, at(TPB, c))
                    if c == 0:
                        pe.wait_ge(yT_done, at(TPB, 0))
                    for k in range(KI):
                        last = nc.tensor.transpose(psX[:, k * P:(k + 1) * P], xbc[:, k, q], core.ident[:])
                    last.then_inc(x_ps, 1)
                    pe.wait_ge(g_done, at(TPB, c))
                    if c == 0:
                        pe.wait_ge(x_done, at(TPB, 0))
                    nc.tensor.transpose(psG[:, 0:NST], xbc[:, KI, q], core.ident[:])
                    nc.tensor.matmul(psG[:, NST:2 * NST], xbc[:, KI, q], xbc[:, KI + 1, q],
                                     start=True, stop=True).then_inc(g_ps, 1)
                    pe.wait_ge(l_done, at(TPB, c))
                    for h in range(HM):
                        last = nc.tensor.transpose(psC[:, h // 4, (h % 4) * P:(h % 4 + 1) * P],
                                                   dv[:, CS, c, h:h + 1].broadcast_to([P, P]), core.ident[:])
                    last.then_inc(c_ps, 1)

                chunk_inputs(0)
                if more:
                    for k in range(KD):
                        turn_rows(b + 1, k)
                for c in range(TPB):
                    q = slice(c * P, (c + 1) * P)
                    if c + 1 < TPB:
                        chunk_inputs(c + 1)
                    if c:
                        pe.wait_ge(st_done, at(TPB - 1, c))
                        nc.tensor.matmul(psO[:], xbc[:, KI + 1, q], st[:], start=True, stop=True).then_inc(yo_ps, 1)
                    else:
                        pe.wait_ge(yo_done, at(TPB - 1, 0))
                    if more and c < 2:
                        project(b + 1, 1 - u, 2 * c)
                    if more and c >= 2:
                        project(b + 1, 1 - u, 2 + c)
                    if c + 1 < TPB:
                        pe.wait_ge(xdec_done, at(TPB - 1, c + 1))
                        pe.wait_ge(yo_done, at(TPB - 1, c))
                        nc.tensor.matmul(psO[:], b_tok[:, c % 2, :], xdec[:, c % 2, :],
                                         start=True, stop=True).then_inc(st_ps, 1)
                    if more and c < 2:
                        project(b + 1, 1 - u, 2 * c + 1)
                    pe.wait_ge(m_done, at(TPB, c + 1))
                    pe.wait_ge(y_done, at(TPB, c))
                    for h in range(HM):
                        last = nc.tensor.matmul(psY[:, h * PM:(h + 1) * PM], lt[:, c % 2, h, :],
                                                xdt[:, c % 2, h * PM:(h + 1) * PM], start=True, stop=True)
                    last.then_inc(yd_ps, 1)
                for j in range(TPB):
                    pe.wait_ge(yz_done, at(TPB, j + 1))
                    pe.wait_ge(yT_done, at(TPB, j))
                    for k in range(KI):
                        last = nc.tensor.transpose(psX[:, k * P:(k + 1) * P], y[:, j, k * P:(k + 1) * P], core.ident[:])
                    last.then_inc(yT_ps, 1)
                    if more:
                        if j == 0:
                            project(b + 1, 1 - u, NCT)
                        if j == 1:
                            pe.wait_ge(yo_done, at(TPB - 1, TPB - 1))
                            turn_dt(b + 1)
                        project(b + 1, 1 - u, NCT + 1 + j)
                        if j == 2:
                            sum_dt(b + 1, 1 - u)
                    pe.wait_ge(yT_done, at(TPB, j + 1))
                    pe.wait_ge(x_done, at(TPB, j))
                    for k in range(KI):
                        last = nc.tensor.matmul(psG[:, 0:D], yT[:, j % 2, k, :], wout[:, k, :],
                                                start=(k == 0), stop=(k == KI - 1))
                    last.then_inc(o_ps, 1)

            batches(pe, front, back)

        @block.scalar
        def _(act):
            a = nc.scalar.activation
            act.wait_ge(loaded, 128)
            a(neg_a[:], neg_a[:], ACT.Exp).then_inc(a_exp, 1)
            act.wait_ge(prep, 1 + KI)

            def normalise(b):
                act.wait_ge(tr_done, b * KD)
                core.apart(act)
                for j in range(TPB):
                    t = b * TPB + j
                    a(xn[:, j, :], core.X[:, t, :], ACT.Identity, bias=core.shift[:, bass.ds(t, 1)],
                      scale=core.rstd[:, bass.ds(t, 1)]).then_inc(xn_done, 1)

            def take_rows(b):
                for k in range(KD):
                    act.wait_ge(tr_done, b * KD + (k + 1))
                    a(xnT[:, k, :], psP[:, k, :], ACT.Identity).then_inc(xnT_done, 1)

            def take_projection(b, v, p):
                act.wait_ge(p_ps, b * NP_ + (p + 1))
                if p < NCT:
                    act.wait_ge(conv_done, b * NCT)
                    a(padded[:, p, TAPS - 1:], psP[:, p % 2, :], ACT.Identity).then_inc(p_done, 1)
                elif p > NCT:
                    a(z2[:, v, p - NCT - 1, :], psP[:, p % 2, :], ACT.Silu).then_inc(p_done, 1)
                else:
                    a(dtT[0:HM, :], psP[0:HM, p % 2, :], ACT.Identity).then_inc(p_done, 1)

            def silu(b, v, c):
                act.wait_ge(conv_done, b * NCT + (c + 1))
                a(xbc2[:, v, c, :], xbc2[:, v, c, :], ACT.Silu, bias=cb[:, c:c + 1]).then_inc(silu_done, 1)

            def softplus(b, v):
                dv = dv2[:, v]
                act.wait_ge(dt_step, b * 8 + 1)
                a(dv[:, AB], dv[:, XD], ACT.Abs).then_inc(dt_act, 1)
                act.wait_ge(dt_act, b * 6 + 1)
                a(dv[:, AB], dv[:, AB], ACT.Exp, scale=-1.0).then_inc(dt_act, 1)
                act.wait_ge(dt_act, b * 6 + 2)
                a(dv[:, AB], dv[:, AB], ACT.Ln, bias=core.ones[:, 0:1]).then_inc(dt_act, 1)

            def front(b):
                normalise(b)
                take_rows(b)
                for p in range(NCT):
                    take_projection(b, 0, p)
                for c in range(NCT):
                    silu(b, 0, c)
                for p in range(NCT, NP_):
                    take_projection(b, 0, p)
                softplus(b, 0)

            def back(b, u, more):
                at = lambda per, c: b * per + c
                dv = dv2[:, u]
                act.wait_ge(dt_step, at(8, 8))
                for o, i in ((EOUT, CS), (DEC, DIF), (ETOT, TOT)):
                    a(dv[:, o], dv[:, i], ACT.Exp).then_inc(dt_act, 1)
                if more:
                    normalise(b + 1)
                if more:
                    take_rows(b + 1)
                for c in range(TPB):
                    for n in (range(2) if c == 0 else range(c + 1, min(c + 2, TPB))):
                        act.wait_ge(l_done, at(TPB, n + 1))
                        a(lt[:, n % 2], lt[:, n % 2], ACT.Exp).then_inc(lexp_done, 1)
                    if more and c < 2:
                        take_projection(b + 1, 1 - u, 2 * c)
                        take_projection(b + 1, 1 - u, 2 * c + 1)
                    if more and c >= 2:
                        take_projection(b + 1, 1 - u, 2 + c)
                act.wait_ge(ymv_done, at(1, 1))
                a(yr[:], ymv[:, :, 1], ACT.Sqrt, bias=core.eps[:]).then_inc(yroot_done, 1)
                for j in range(TPB):
                    act.wait_ge(yT_ps, at(TPB, j + 1))
                    act.wait_ge(o_ps, at(TPB, max(j - 1, 0)))
                    a(yT[:, j % 2], psX[:].rearrange("p (k q) -> p k q", k=KI), ACT.Identity).then_inc(yT_done, 1)
                    if more:
                        if j == 0:
                            take_projection(b + 1, 1 - u, NCT)
                        if j == 1:
                            softplus(b + 1, 1 - u)
                        take_projection(b + 1, 1 - u, NCT + 1 + j)
                        if j == 0:
                            silu(b + 1, 1 - u, 0)
                            silu(b + 1, 1 - u, 1)
                        silu(b + 1, 1 - u, 2 + j)

            batches(act, front, back)

        @block.gpsimd
        def _(pool):
            tt = nc.gpsimd.tensor_tensor
            nc.gpsimd.memset(padded[:, :, 0:TAPS - 1], 0.0).then_inc(prep, 1)

            def back(b, u, more):
                at = lambda per, c: b * per + c
                dv = dv2[:, u]
                for c in range(TPB):
                    if c == 0:
                        pool.wait_ge(dt_act, at(6, 6))
                    if c + 1 < TPB:
                        pool.wait_ge(xdt_done, at(TPB, c + 1))
                        pool.wait_ge(st_ps, at(TPB - 1, max(c - 1, 0)))
                        tt(xdec[:, c % 2, :].rearrange("p (h q) -> p h q", h=HM),
                           xdt[:, c % 2, :].rearrange("p (h q) -> p h q", h=HM),
                           spread(dv[:, DEC, c, :], [P, HM, PM], 2), ALU.mult).then_inc(xdec_done, 1)
                    pool.wait_ge(lexp_done, at(TPB, c + 1))
                    pool.wait_ge(g_done, at(TPB, c + 1))
                    tt(lt[:, c % 2], lt[:, c % 2], spread(gm[:, c % 2, :], [P, HM, P], 1), ALU.mult).then_inc(m_done, 1)
                for j in range(TPB):
                    pool.wait_ge(yn_done, at(TPB, j + 1))
                    tt(y[:, j, :], y[:, j, :], z2[:, u, j, :], ALU.mult).then_inc(yz_done, 1)

            batches(pool, lambda b: None, back)

        @block.vector
        def _(dve):
            tt, ts, stt = nc.vector.tensor_tensor, nc.vector.tensor_scalar, nc.vector.scalar_tensor_tensor
            dve.wait_ge(loaded, 128)
            for k in range(KI):
                ts(wout[:, k, :], wout[:, k, :], nw[:, k:k + 1], None, ALU.mult).then_inc(prep, 1)
            dve.wait_ge(prep, 1 + KI)
            dve.wait_ge(a_exp, 1)

            def convolve(b, v, c):
                dve.wait_ge(p_done, b * NP_ + (c + 1))
                src, o = padded[:, c], xbc2[:, v, c, :]
                ts(o, src[:, 0:S], cw[:, c, 0:1], None, ALU.mult).then_inc(tap, 1)
                for j in range(1, TAPS):
                    dve.wait_ge(tap, b * (NCT * (TAPS - 1)) + (c * (TAPS - 1) + j))
                    last = stt(o, src[:, j:j + S], cw[:, c, j:j + 1], o, ALU.mult, ALU.add)
                    last.then_inc(tap if j < TAPS - 1 else conv_done, 1)

            def dt_biased(b, v):
                dv = dv2[:, v]
                dve.wait_ge(dt_ps, b + 1)
                raw = psO[:, 0:TPB * HM].rearrange("p (c h) -> p c h", h=HM)
                tt(dv[:, XD], raw, spread(dtb[:], [P, TPB, HM], 1), ALU.add).then_inc(dt_step, 1)
                dve.wait_ge(dt_step, b * 8 + 1)
                ts(dv[:, RL], dv[:, XD], 0.0, None, ALU.max).then_inc(dt_step, 1)

            def dt_decay(b, v):
                dv = dv2[:, v]
                dve.wait_ge(dt_step, b * 8 + 2)
                dve.wait_ge(dt_act, b * 6 + 3)
                tt(dv[:, DT], dv[:, RL], dv[:, AB], ALU.add).then_inc(dt_step, 1)
                dve.wait_ge(dt_step, b * 8 + 3)
                stt(dv[:, A], dv[:, DT], -1.0, spread(neg_a[:], [P, TPB, HM], 1), ALU.mult, ALU.mult).then_inc(dt_step, 1)

            def dt_sums(b, v):
                dv = dv2[:, v]
                dve.wait_ge(cs_ps, b + 1)
                cs = psO[:, 64:64 + TPB * HM].rearrange("p (c h) -> p c h", h=HM)
                tot = psO[:, 128:128 + TPB * HM].rearrange("p (c h) -> p c h", h=HM)
                nc.vector.tensor_copy(dv[:, CS], cs).then_inc(dt_step, 1)
                ts(dv[:, NCS], cs, -1.0, None, ALU.mult).then_inc(dt_step, 1)
                nc.vector.tensor_copy(dv[:, TOT], tot).then_inc(dt_step, 1)
                dve.wait_ge(dt_step, b * 8 + 7)
                tt(dv[:, DIF], dv[:, TOT], dv[:, CS], ALU.subtract).then_inc(dt_step, 1)

            def front(b):
                for c in range(NCT):
                    convolve(b, 0, c)
                dt_biased(b, 0)
                dt_decay(b, 0)
                dt_sums(b, 0)

            def back(b, u, more):
                at = lambda per, c: b * per + c
                dv = dv2[:, u]

                def chunk_inputs(c):
                    dve.wait_ge(x_ps, at(TPB, c + 1))
                    if c >= 2:
                        dve.wait_ge(yd_ps, at(TPB, c - 1))
                    else:
                        dve.wait_ge(yd_ps, at(TPB, 0))
                    if c >= 2:
                        dve.wait_ge(xdec_done, at(TPB - 1, c - 1))
                    tt(xdt[:, c % 2, :].rearrange("p (h q) -> p h q", h=HM), psX[:].rearrange("p (h q) -> p h q", h=HM),
                       spread(dv[:, DT, c, :], [P, HM, PM], 2), ALU.mult).then_inc(xdt_done, 1)
                    dve.wait_ge(g_ps, at(TPB, c + 1))
                    if c >= 2:
                        dve.wait_ge(st_ps, at(TPB - 1, c - 1))
                    nc.vector.tensor_copy(b_tok[:, c % 2, :], psG[:, 0:NST])
                    tt(gm[:, c % 2, :], psG[:, NST:2 * NST], tri[:], ALU.mult).then_inc(g_done, 1)

                def chunk_decays(c):
                    dve.wait_ge(c_ps, at(TPB, c + 1))
                    for h in range(HM):
                        last = ts(lt[:, c % 2, h, :], psC[:, h // 4, (h % 4) * P:(h % 4 + 1) * P],
                                  dv[:, NCS, c, h:h + 1], 0.0, ALU.add, ALU.min)
                    last.then_inc(l_done, 1)

                chunk_inputs(0)
                chunk_decays(0)
                for c in range(TPB):
                    if c + 1 < TPB:
                        chunk_inputs(c + 1)
                    if c:
                        dve.wait_ge(yo_ps, at(TPB - 1, c))
                        dve.wait_ge(dt_act, at(6, 6))
                        tt(yo[:].rearrange("p (h q) -> p h q", h=HM), psO[:].rearrange("p (h q) -> p h q", h=HM),
                           spread(dv[:, EOUT, c, :], [P, HM, PM], 2), ALU.mult).then_inc(yo_done, 1)
                    if 0 < c < TPB - 1:
                        dve.wait_ge(st_done, at(TPB - 1, c))
                        tt(st2[:].rearrange("p (h q) -> p h q", h=HM), st[:].rearrange("p (h q) -> p h q", h=HM),
                           spread(dv[:, ETOT, c, :], [P, HM, PM], 2), ALU.mult).then_inc(st_step, 1)
                        dve.wait_ge(st_step, at(TPB - 2, c))
                    if c + 1 < TPB:
                        chunk_decays(c + 1)
                    if c < TPB - 1:
                        dve.wait_ge(st_ps, at(TPB - 1, c + 1))
                        if c:
                            tt(st[:], psO[:], st2[:], ALU.add).then_inc(st_done, 1)
                        else:
                            nc.vector.tensor_copy(st[:], psO[:]).then_inc(st_done, 1)
                    if more and 0 < c < TPB - 1:
                        convolve(b + 1, 1 - u, c - 1)
                    dve.wait_ge(yd_ps, at(TPB, c + 1))
                    if c:
                        dve.wait_ge(yo_done, at(TPB - 1, c))
                        tt(y[:, c, :], psY[:], yo[:], ALU.add).then_inc(y_done, 1)
                    else:
                        dve.wait_ge(yT_ps, at(TPB, 0))
                        nc.vector.tensor_copy(y[:, c, :], psY[:]).then_inc(y_done, 1)
                    dve.wait_ge(y_done, at(TPB, c + 1))
                    nc.vector.bn_stats(ybn[:, c, :], y[:, c, :]).then_inc(ybn_done, 1)
                dve.wait_ge(ybn_done, at(TPB, TPB))
                core.behind(dve)
                for c in range(TPB):
                    last = nc.vector.bn_aggr(ymv[:, c, :], ybn[:, c, :])
                last.then_inc(ymv_done, 1)
                dve.wait_ge(yroot_done, at(1, 1))
                nc.vector.reciprocal(yr[:], yr[:]).then_inc(yr_done, 1)
                dve.wait_ge(yr_done, at(1, 1))
                for j in range(TPB):
                    ts(y[:, j, :], y[:, j, :], ymv[:, j, 0:1], yr[:, j:j + 1], ALU.subtract, ALU.mult).then_inc(yn_done, 1)
                for j in range(TPB):
                    t = at(TPB, j)
                    if more:
                        if j == 1:
                            dt_biased(b + 1, 1 - u)
                        convolve(b + 1, 1 - u, 2 + j)
                        if j == 1:
                            dt_decay(b + 1, 1 - u)
                        if j == 2:
                            dt_sums(b + 1, 1 - u)
                    dve.wait_ge(o_ps, at(TPB, j + 1))
                    tt(core.X[:, t, :], psG[:, 0:D], core.X[:, t, :], ALU.add).then_inc(x_done, 1)
                    dve.wait_ge(x_done, at(TPB, j + 1))
                    core.apart(dve)
                    nc.vector.bn_stats(core.bn[:, t, :], core.X[:, t, :])

            batches(dve, front, back)
GRP_T = 8
EPS_D = 1e-6


def delta_inputs(nc, core, tag, beta, w_qk, w_vb, tok_qk, seq_k, seq_nbk, seq_v):
    with ExitStack() as ctx:
        sbf = lambda n, s: core.sbuf(f"{tag}_{n}", s, ctx)
        wqk = sbf("wqk", [P, KD, 2 * D])
        wvb = sbf("wvb", [P, KD, D + NH])
        xn = sbf("xn", [P, TPB, D])
        xnT = sbf("xnT", [P, KD, S])
        qk = sbf("qk", [P, 2, TPB, 2 * D])
        v = sbf("v", [P, 2, TPB, D])
        sqr = sbf("sqr", [P, 2, 2 * D])
        ss = sbf("ss", [P, TPB * 2 * NH])
        nbk = sbf("nbk", [P, 2, TPB, D])
        psT = core.psum(f"{tag}_psT", [P, 2, 512], ctx)
        psA = core.psum(f"{tag}_psA", [P, 2, 512], ctx)
        psV = core.psum(f"{tag}_psV", [P, 2, 512], ctx)
        psB = core.psum(f"{tag}_psB", [P, 512], ctx)
        sem = lambda n: core.sem(f"{tag}_{n}", ctx)
        loaded = sem("loaded")
        xn_done, tr_done, xnT_done = sem("xn_done"), sem("tr_done"), sem("xnT_done")
        a_ps, silu_done, b_ps, beta_done = sem("a_ps"), sem("silu_done"), sem("b_ps"), sem("beta_done")
        sq_done, ss_done, root_done, inv_step, norm_done, nbk_done = (
            sem("sq_done"), sem("ss_done"), sem("root_done"), sem("inv_step"), sem("norm_done"), sem("nbk_done"))
        stored = [sem(f"stored{u}") for u in range(2)]
        block = ctx.enter_context(nc.Block())
        NOUT = 1 + 3 * TPB

        @block.sync
        def _(sp):
            sp.dma_start(wqk[:], w_qk.rearrange("(k p) n -> p k n", p=P)).then_inc(loaded, 16)
            sp.dma_start(wvb[:], w_vb.rearrange("(k p) n -> p k n", p=P)).then_inc(loaded, 16)
            with sp.Fori(0, B // 2) as b2:
                for u in range(2):
                    at = at_batch(b2, u)
                    b = b2 * 2 + u

                    def by_sequence(dst, src):
                        rows = dst.rearrange("(b h) (j p) d -> b j p h d", b=B, p=P)
                        for j in range(TPB):
                            sp.dma_start(rows[b, j], src[:, u, j, :].rearrange("p (h d) -> p h d", h=NH)).then_inc(stored[u], 16)

                    sp.wait_ge(silu_done, at(2 * TPB, 2 * TPB))
                    by_sequence(seq_v, v)
                    sp.wait_ge(norm_done, at(TPB, TPB))
                    sp.dma_start(tok_qk.rearrange("(b j p) n -> b p j n", b=B, p=P)[b], qk[:, u]).then_inc(stored[u], 16)
                    by_sequence(seq_k, qk[:, :, :, D:])
                    sp.wait_ge(nbk_done, at(1, 1))
                    by_sequence(seq_nbk, nbk)
            for u in range(2):
                sp.wait_ge(stored[u], 16 * NOUT * (B // 2))

        @block.tensor
        def _(pe):
            pe.wait_ge(loaded, 32)
            with pe.Fori(0, B // 2) as b2:
                for u in range(2):
                    at = at_batch(b2, u)
                    for k in range(KD):
                        for j in range(TPB):
                            if k == 0:
                                pe.wait_ge(xn_done, at(TPB, j + 1))
                            last = nc.tensor.transpose(psT[:, k, j * P:(j + 1) * P], xn[:, j, k * P:(k + 1) * P],
                                                       core.ident[:])
                        last.then_inc(tr_done, 1)
                    pe.wait_ge(xnT_done, at(KD, KD))
                    pe.wait_ge(beta_done, at(1, 0))
                    for j in range(TPB):
                        pe.wait_ge(silu_done, at(2 * TPB, max(2 * j - 2, 0)))
                        for k in range(KD):
                            nc.tensor.matmul(psA[:, j % 2, :], xnT[:, k, j * P:(j + 1) * P], wqk[:, k, :],
                                             start=(k == 0), stop=(k == KD - 1))
                        for k in range(KD):
                            last = nc.tensor.matmul(psV[:, j % 2, 0:D], xnT[:, k, j * P:(j + 1) * P], wvb[:, k, 0:D],
                                                    start=(k == 0), stop=(k == KD - 1))
                        last.then_inc(a_ps, 1)
                        for k in range(KD):
                            last = nc.tensor.matmul(psB[:, j * NH:(j + 1) * NH], xnT[:, k, j * P:(j + 1) * P],
                                                    wvb[:, k, D:], start=(k == 0), stop=(k == KD - 1))
                    last.then_inc(b_ps, 1)

        @block.scalar
        def _(act):
            a = nc.scalar.activation

            def root(at):
                act.wait_ge(ss_done, at(TPB, 0))
                a(ss[:], ss[:], ACT.Sqrt).then_inc(root_done, 1)

            def body(b2, u, first):
                at = at_batch(b2, u)
                act.wait_ge(tr_done, at(KD, 0))
                core.apart(act)
                for j in range(TPB):
                    t = at(TPB, j)
                    a(xn[:, j, :], core.X[:, t, :], ACT.Identity, bias=core.shift[:, bass.ds(t, 1)],
                      scale=core.rstd[:, bass.ds(t, 1)]).then_inc(xn_done, 1)
                for k in range(KD):
                    act.wait_ge(tr_done, at(KD, k + 1))
                    a(xnT[:, k, :], psT[:, k, :], ACT.Identity).then_inc(xnT_done, 1)
                if not first:
                    root(at)
                act.wait_ge(stored[u], b2 * (16 * NOUT))
                for j in range(TPB):
                    act.wait_ge(a_ps, at(TPB, j + 1))
                    a(qk[:, u, j, :], psA[:, j % 2, :], ACT.Silu).then_inc(silu_done, 1)
                    a(v[:, u, j, :], psV[:, j % 2, 0:D], ACT.Silu).then_inc(silu_done, 1)
                act.wait_ge(b_ps, at(1, 1))
                core.apart(act)
                a(beta[:, bass.ds(at(TPB, 0), TPB), :], psB[:, 0:TPB * NH].rearrange("p (j h) -> p j h", h=NH),
                  ACT.Sigmoid).then_inc(beta_done, 1)

            for u in range(2):
                body(0, u, u == 0)
            with act.Fori(1, B // 2) as b2:
                for u in range(2):
                    body(b2, u, False)
            root(at_batch(B // 2, 0))

        @block.gpsimd
        def _(pool):
            with pool.Fori(0, B // 2) as b2:
                for u in range(2):
                    at = at_batch(b2, u)
                    for j in range(TPB):
                        pool.wait_ge(silu_done, at(2 * TPB, 2 * j + 1))
                        pool.wait_ge(ss_done, at(TPB, max(j - 1, 0)))
                        nc.gpsimd.tensor_tensor(sqr[:, j % 2, :], qk[:, u, j, :], qk[:, u, j, :], ALU.mult).then_inc(sq_done, 1)

        @block.vector
        def _(dve):
            tt = nc.vector.tensor_tensor
            with dve.Fori(0, B // 2) as b2:
                for u in range(2):
                    at = at_batch(b2, u)
                    ss3 = ss[:].rearrange("p (j h) -> p j h", j=TPB)
                    for j in range(TPB):
                        dve.wait_ge(sq_done, at(TPB, j + 1))
                        nc.vector.tensor_reduce(ss3[:, j, :], sqr[:, j % 2, :].rearrange("p (h d) -> p h d", d=HD),
                                                AX.X, ALU.add).then_inc(ss_done, 1)
                    dve.wait_ge(root_done, at(1, 1))
                    nc.vector.tensor_scalar(ss[:], ss[:], EPS_D, None, ALU.add).then_inc(inv_step, 1)
                    dve.wait_ge(inv_step, at(2, 1))
                    nc.vector.reciprocal(ss[:], ss[:]).then_inc(inv_step, 1)
                    dve.wait_ge(inv_step, at(2, 2))
                    for j in range(TPB):
                        q3 = qk[:, u, j, :].rearrange("p (h d) -> p h d", d=HD)
                        tt(q3, q3, spread(ss3[:, j, :], [P, 2 * NH, HD], 2), ALU.mult).then_inc(norm_done, 1)
                    dve.wait_ge(norm_done, at(TPB, TPB))
                    dve.wait_ge(beta_done, at(1, 1))
                    for j in range(TPB):
                        last = nc.vector.scalar_tensor_tensor(
                            nbk[:, u, j, :].rearrange("p (h d) -> p h d", d=HD),
                            qk[:, u, j, D:].rearrange("p (h d) -> p h d", d=HD), -1.0,
                            beta[:, at(TPB, j), :].unsqueeze(2).broadcast_to([P, NH, HD]), ALU.mult, ALU.mult)
                    last.then_inc(nbk_done, 1)


def delta_scan(nc, core, tag, beta, tok_qk, seq_k, seq_nbk, seq_v, tok_d, wo, rms_w, masks, beside):
    with ExitStack() as ctx:
        sbf = lambda n, s: core.sbuf(f"{tag}_{n}", s, ctx)
        CH = P // 2
        NCH = S // CH
        NGT = CH // GRP_T
        H2 = HD // 2
        k_sb = sbf("k", [P, 2, CH, HD])
        bk_sb = sbf("bk", [P, 2, CH, HD])
        v_sb = sbf("v", [P, 2, CH, HD])
        d_sb = sbf("d", [P, 2, CH, HD])
        m = sbf("m", [P, HD, HD])
        prod = sbf("prod", [P, 2, GRP_T, HD, HD + 1])
        outer = sbf("outer", [P, 2, HD, HD])
        ndm = sbf("ndm", [P, HD])
        dots, dot = sbf("dots", [P, HD]), sbf("dot", [P, 1])
        nd = sbf("nd", [P, 2, GRP_T, HD])
        wo_sb = sbf("wo", [P, KD, D])
        rw = sbf("rw", [P, KD])
        par = sbf("par", [P, 2])
        before = sbf("before", [P, P])
        own = sbf("own", [P, P])
        eps6 = sbf("eps6", [P, 1])
        qk = sbf("qk", [P, 2 * D])
        dt = sbf("dt", [P, D])
        bd = sbf("bd", [P, D])
        kT = sbf("kT", [P, KD, P])
        qT = sbf("qT", [P, KD, P])
        q2 = sbf("q2", [P, KD, 2, P])
        aT = sbf("aT", [P, NH, P])
        states = sbf("states", [P, B, KD, P])
        m0 = sbf("m0", [P, KD, P])
        mt = sbf("mt", [P, KD, P])
        o1 = sbf("o1", [P, KD, P])
        oT = sbf("oT", [P, KD, P])
        osq = sbf("osq", [P, KD, P])
        r = sbf("r", [P, 1])
        psT = core.psum(f"{tag}_psT", [P, 512], ctx)
        psA = core.psum(f"{tag}_psA", [P, 4, 512], ctx)
        psE = core.psum(f"{tag}_psE", [P, KD, 2, P], ctx)
        psM = core.psum(f"{tag}_psM", [P, 512], ctx)
        psY = core.psum(f"{tag}_psY", [P, 512], ctx)
        sem = lambda n: core.sem(f"{tag}_{n}", ctx)
        in_k = [sem(f"in{u}") for u in range(2)]
        m_zero, v_set, nd_out = sem("m_zero"), sem("v_set"), sem("nd_out")
        mul_n, red_n, dot_n, d_n, out_n, add_n = (
            sem("mul_n"), sem("red_n"), sem("dot_n"), sem("d_n"), sem("out_n"), sem("add_n"))
        stored = [sem(f"stored{u}") for u in range(2)]
        loaded, wo_done, tile_in = sem("loaded"), sem("wo_done"), sem("tile_in")
        t_ps, qk_done, a_ps, a_done, bd_done = sem("t_ps"), sem("qk_done"), sem("a_ps"), sem("a_done"), sem("bd_done")
        e_ps, e1_done, e2_done, osq_done, m_ps, mt_done, st_done, m0_done = (
            sem("e_ps"), sem("e1_done"), sem("e2_done"), sem("osq_done"), sem("m_ps"), sem("mt_done"),
            sem("st_done"), sem("m0_done"))
        y_ps, root_done, r_done, x_done = sem("y_ps"), sem("root_done"), sem("r_done"), sem("x_done")
        beside.allocate(core, ctx)
        block = ctx.enter_context(nc.Block())

        def at(c, b, per, n):
            return b * per + (c * B * per + n)

        @block.sync
        def _(sp):
            rows = tok_d.rearrange("(b t) (h d) -> b h t d", b=B, h=NH)

            def load_steps(hc):
                for dst, src in ((k_sb, seq_k), (bk_sb, seq_nbk), (v_sb, seq_v)):
                    sp.dma_start(dst[:, hc % 2], src[:, hc * CH:(hc + 1) * CH, :]).then_inc(in_k[hc % 2], 16)

            def load_tile(c, b):
                sp.wait_ge(t_ps if c == TPB - 1 else m_ps, at(c, b, 1, 0))
                if c == TPB - 1:
                    sp.wait_ge(m_ps, B * (TPB - 1))
                sp.wait_ge(bd_done, at(c, b, 1, 0))
                t = b * TPB + c
                sp.dma_start(qk[:], tok_qk.rearrange("(t p) n -> t p n", p=P)[t]).then_inc(tile_in, 16)
                sp.dma_start(dt[:], tok_d.rearrange("(t p) n -> t p n", p=P)[t]).then_inc(tile_in, 16)

            load_steps(0)
            load_steps(1)
            sp.dma_start(wo_sb[:], wo.rearrange("(k p) n -> p k n", p=P)).then_inc(loaded, 16)
            sp.dma_start(rw[:], rms_w).then_inc(loaded, 16)
            for dst, src in ((par, masks[0]), (before, masks[1]), (own, masks[2])):
                sp.dma_start(dst[:], src).then_inc(loaded, 16)
            for hc in range(1, NCH + 1):
                if hc + 1 < NCH:
                    sp.wait_ge(add_n, 3 * CH // 2 * hc)
                    sp.wait_ge(v_set, hc * NGT)
                    load_steps(hc + 1)
                sp.wait_ge(nd_out, hc * NGT)
                for b in range(B):
                    sp.dma_start(rows[b, :, (hc - 1) * CH:hc * CH, :],
                                 d_sb[b * NH:(b + 1) * NH, (hc - 1) % 2]).then_inc(stored[(hc - 1) % 2], 16)
                if hc >= 2:
                    if hc % 2 == 0:
                        for u in range(2):
                            sp.wait_ge(stored[u], 16 * B * (hc // 2))
                    with sp.Fori(0, B if hc == NCH else B // 2) as g:
                        load_tile(hc // 2 - 1, g + hc % 2 * (B // 2))

        @block.gpsimd
        def _(pool):
            nc.gpsimd.memset(m[:], 0.0).then_inc(m_zero, 1)
            nc.gpsimd.memset(eps6[:], EPS_D).then_inc(m_zero, 1)
            beside.run(nc, pool)

        @block.tensor
        def _(pe):
            pe.wait_ge(loaded, 80)
            pe.wait_ge(wo_done, KD)

            def tile(c, b):
                pe.wait_ge(tile_in, at(c, b, 32, 32))
                pe.wait_ge(qk_done, at(c, b, 4, 0))
                for k in range(2 * KD):
                    last = nc.tensor.transpose(psT[:, k * P:(k + 1) * P], qk[:, k * P:(k + 1) * P], core.ident[:])
                last.then_inc(t_ps, 1)
                pe.wait_ge(qk_done, at(c, b, 4, 4))
                for k in range(KD):
                    for i in range(4):
                        rr = slice(i * PAD, (i + 1) * PAD)
                        if k == 0:
                            pe.wait_ge(a_done, at(c, b, 4, 0))
                        last = nc.tensor.matmul(psA[:, i, k * 2 * P:(k + 1) * 2 * P], kT[rr, k, :],
                                                q2[rr, k].rearrange("p e t -> p (e t)"), start=True, stop=True)
                        if k:
                            last.then_inc(a_ps, 1)
                pe.wait_ge(e2_done, at(c, b, 1, 0))
                pe.wait_ge(bd_done, at(c, b, 1, 1))
                if c:
                    pe.wait_ge(m0_done, at(c - 1, b, 1, 1))
                for k in range(KD):
                    if c:
                        nc.tensor.matmul(psE[:, k].rearrange("p e t -> p (e t)"), m0[:, k, :],
                                         qT[:, k, :].unsqueeze(1).broadcast_to([P, 2, P]), start=True, stop=False,
                                         skip_group_check=True)
                    for i in range(4):
                        n = k * 4 + i
                        pe.wait_ge(a_done, at(c, b, 4, i + 1))
                        last = nc.tensor.matmul(psE[i * PAD:(i + 1) * PAD, k].rearrange("p e t -> p (e t)"),
                                                bd[:, k * P + i * PAD:k * P + (i + 1) * PAD],
                                                aT[:, 2 * n:2 * n + 2, :].rearrange("p h t -> p (h t)"),
                                                start=(c == 0), stop=True, skip_group_check=True)
                last.then_inc(e_ps, 1)
                if c < TPB - 1:
                    pe.wait_ge(mt_done, at(c, b, 1, 0))
                    for k in range(KD):
                        last = nc.tensor.matmul(psM[:, k * P:(k + 1) * P], qk[:, D + k * P:D + (k + 1) * P],
                                                bd[:, k * P:(k + 1) * P], start=True, stop=True)
                    last.then_inc(m_ps, 1)
                pe.wait_ge(osq_done, at(c, b, 1, 1))
                pe.wait_ge(x_done, at(c, b, 1, 0))
                for k in range(KD):
                    nc.tensor.matmul(psY[:, 0:D], oT[:, k, :], wo_sb[:, k, :], start=(k == 0), stop=(k == KD - 1))
                for k in range(KD):
                    last = nc.tensor.matmul(psY[:, D:D + 1], osq[:, k, :], core.ones[:, 0:1],
                                            start=(k == 0), stop=(k == KD - 1))
                last.then_inc(y_ps, 1)

            for c in range(TPB):
                with pe.Fori(0, B) as b:
                    tile(c, b)

        @block.scalar
        def _(act):
            a = nc.scalar.activation

            def put_v(hc, g, w):
                a(prod[:, w, :, :, HD], v_sb[:, hc % 2, bass.ds(g * GRP_T, GRP_T), :], ACT.Copy,
                  scale=-1.0).then_inc(v_set, 1)

            def take_d(hc, g, w, n):
                act.wait_ge(d_n, n)
                core.apart(act)
                a(d_sb[:, hc % 2, bass.ds(g * GRP_T, GRP_T), :], nd[:, w], ACT.Copy, scale=-1.0).then_inc(nd_out, 1)

            def turned(c, b):
                act.wait_ge(t_ps, at(c, b, 1, 1))
                act.wait_ge(e_ps, at(c, b, 1, 0))
                q = psT[:, 0:KD * P].rearrange("p (k t) -> p k t", k=KD)
                for e in range(2):
                    a(q2[:, :, e, :], q, ACT.Identity, scale=par[:, e:e + 1]).then_inc(qk_done, 1)
                a(kT[:], psT[:, KD * P:].rearrange("p (k t) -> p k t", k=KD), ACT.Identity).then_inc(qk_done, 1)
                a(qT[:], q, ACT.Identity).then_inc(qk_done, 1)
                if c:
                    act.wait_ge(st_done, at(c - 1, b, 1, 1))
                    core.apart(act)
                    a(m0[:], states[:, b, :, :], ACT.Identity).then_inc(m0_done, 1)

            def even_heads(c, b):
                act.wait_ge(e_ps, at(c, b, 1, 1))
                a(o1[:], psE[:, :, 0, :], ACT.Identity, scale=par[:, 0:1]).then_inc(e1_done, 1)

            def squares(c, b):
                act.wait_ge(e2_done, at(c, b, 1, 1))
                a(osq[:], oT[:], ACT.Square).then_inc(osq_done, 1)
                act.wait_ge(y_ps, at(c, b, 1, 1))
                a(r[:], psY[:, D:D + 1], ACT.Sqrt, scale=1.0 / D, bias=eps6[:]).then_inc(root_done, 1)

            act.wait_ge(in_k[0], 48)
            put_v(0, 0, 0)
            put_v(0, 1, 1)
            act.wait_ge(m_zero, 2)
            for hc in range(NCH):
                if hc == 1:
                    act.wait_ge(loaded, 80)
                c = hc // 2 - 1
                base, per = CH // 2 * hc, GRP_T // 2
                if hc >= 2:
                    act.wait_ge(stored[hc % 2], 16 * B * (hc // 2))
                with act.Fori(0, NGT // 2 - 1) as g2:
                    b = g2 + hc % 2 * (B // 2)
                    for w in range(2):
                        if c >= 0 and w == 0:
                            turned(c, b)
                        if c >= 0 and w == 1:
                            even_heads(c, b)
                            squares(c, b)
                        take_d(hc, g2 * 2 + w, w, g2 * (2 * per) + (base + per * (w + 1)))
                        put_v(hc, g2 * 2 + (w + 2), w)
                b = NGT // 2 - 1 + hc % 2 * (B // 2)
                for w in range(2):
                    if c >= 0 and w == 0:
                        turned(c, b)
                    if c >= 0 and w == 1:
                        even_heads(c, b)
                        squares(c, b)
                    take_d(hc, NGT - 2 + w, w, base + per * (NGT - 1 + w))
                    if hc + 1 < NCH:
                        act.wait_ge(in_k[(hc + 1) % 2], 48 * ((hc + 1) // 2 + 1))
                        a(prod[:, w, :, :, HD], v_sb[:, (hc + 1) % 2, w * GRP_T:(w + 1) * GRP_T, :],
                          ACT.Copy, scale=-1.0).then_inc(v_set, 1)
            with act.Fori(0, B) as b:
                turned(TPB - 1, b)
                even_heads(TPB - 1, b)
                squares(TPB - 1, b)

        @block.vector
        def _(dve):
            tt, stt, red = nc.vector.tensor_tensor, nc.vector.scalar_tensor_tensor, nc.vector.tensor_reduce
            halves = [slice(0, H2), slice(H2, HD)]
            dve.wait_ge(m_zero, 2)

            def outer_half(i, bk, nd_t, which):
                r = halves[i]
                tt(outer[:, which, r, :], bk[:, r].unsqueeze(2).broadcast_to([P, H2, HD]),
                   spread(nd_t, [P, H2, HD], 1), ALU.mult).then_inc(out_n, 1)

            def two_steps(hc, g2, w, s):
                u = hc % 2
                at = lambda per, n: g2 * (per * GRP_T) + (per * (hc * CH + w * GRP_T + s) // 2 + n)
                t = g2 * (2 * GRP_T) + (w * GRP_T + s)
                k0, k1 = k_sb[:, u, t, :], k_sb[:, u, t + 1, :]
                bk0, bk1 = bk_sb[:, u, t, :], bk_sb[:, u, t + 1, :]
                nd0, nd1 = nd[:, w, s, :], nd[:, w, s + 1, :]
                for i, r in enumerate(halves):
                    if hc or w or s:
                        dve.wait_ge(add_n, at(3, i - 1))
                    else:
                        dve.wait_ge(add_n, at(3, 0))
                    tt(prod[:, w, s, r, 0:HD], m[:, r, :], k0.unsqueeze(1).broadcast_to([P, H2, HD]),
                       ALU.mult).then_inc(mul_n, 1)
                tt(prod[:, w, s + 1, :, 0:HD], m[:], k1.unsqueeze(1).broadcast_to([P, HD, HD]),
                   ALU.mult).then_inc(mul_n, 1)
                if s == 0:
                    dve.wait_ge(v_set, g2 * 2 + (hc * NGT + w + 1))
                dve.wait_ge(mul_n, at(3, 2))
                red(nd0, prod[:, w, s], AX.X, ALU.add).then_inc(red_n, 1)
                dve.wait_ge(mul_n, at(3, 3))
                red(ndm[:], prod[:, w, s + 1], AX.X, ALU.add).then_inc(red_n, 1)
                dve.wait_ge(red_n, at(2, 1))
                tt(dots[:], nd0, k1, ALU.mult).then_inc(dot_n, 1)
                outer_half(0, bk0, nd0, 0)
                dve.wait_ge(dot_n, at(2, 1))
                red(dot[:], dots[:], AX.X, ALU.add).then_inc(dot_n, 1)
                outer_half(1, bk0, nd0, 0)
                dve.wait_ge(dot_n, at(2, 2))
                dve.wait_ge(red_n, at(2, 2))
                stt(nd1, bk0, dot[:], ndm[:], ALU.mult, ALU.add).then_inc(d_n, 1)
                dve.wait_ge(out_n, at(4, 2))
                tt(m[:], m[:], outer[:, 0], ALU.add).then_inc(add_n, 1)
                dve.wait_ge(d_n, at(1, 1))
                for i in range(2):
                    outer_half(i, bk1, nd1, 1)
                dve.wait_ge(add_n, at(3, 1))
                for i, r in enumerate(halves):
                    dve.wait_ge(out_n, at(4, 3 + i))
                    tt(m[:, r, :], m[:, r, :], outer[:, 1, r, :], ALU.add).then_inc(add_n, 1)

            def scale_d(c, b):
                dve.wait_ge(tile_in, at(c, b, 32, 32))
                dve.wait_ge(y_ps, at(c, b, 1, 0))
                tt(bd[:].rearrange("p (h d) -> p h d", d=HD), dt[:].rearrange("p (h d) -> p h d", d=HD),
                   beta[:, b * TPB + c, :].unsqueeze(2).broadcast_to([P, NH, HD]), ALU.mult).then_inc(bd_done, 1)

            def mask(c, b, g):
                dve.wait_ge(a_ps, at(c, b, 4, g + 1))
                if g == 0:
                    dve.wait_ge(e_ps, at(c, b, 1, 0))
                tt(aT[:].rearrange("p (k i e) t -> p k i e t", k=KD, e=2)[:, :, g],
                   psA[:, g, :].rearrange("p (k e t) -> p k e t", k=KD, e=2),
                   spread(before[:], [P, 2 * KD, P], 1).rearrange("p (k e) t -> p k e t", k=KD),
                   ALU.mult).then_inc(a_done, 1)

            def odd_heads(c, b):
                dve.wait_ge(e1_done, at(c, b, 1, 1))
                dve.wait_ge(y_ps, at(c, b, 1, 0))
                stt(oT[:], psE[:, :, 1, :], par[:, 1:2], o1[:], ALU.mult, ALU.add).then_inc(e2_done, 1)

            def own_heads(c, b):
                dve.wait_ge(m_ps, at(c, b, 1, 1))
                dve.wait_ge(st_done, at(c, b, 1, 0))
                tt(mt[:], psM[:, 0:KD * P].rearrange("p (k t) -> p k t", k=KD), spread(own[:], [P, KD, P], 1),
                   ALU.mult).then_inc(mt_done, 1)

            def advance_state(c, b):
                new = states[:, b, :, :]
                dve.wait_ge(mt_done, at(c, b, 1, 1))
                if c == 0:
                    core.apart(dve)
                    nc.vector.tensor_copy(new, mt[:]).then_inc(st_done, 1)
                else:
                    dve.wait_ge(m0_done, at(c - 1, b, 1, 1))
                    tt(new, new, mt[:], ALU.add).then_inc(st_done, 1)

            def invert_root(c, b):
                dve.wait_ge(root_done, at(c, b, 1, 1))
                nc.vector.reciprocal(r[:], r[:]).then_inc(r_done, 1)

            def add_rows(c, b):
                t = b * TPB + c
                dve.wait_ge(r_done, at(c, b, 1, 1))
                stt(core.X[:, t, :], psY[:, 0:D], r[:], core.X[:, t, :], ALU.mult, ALU.add).then_inc(x_done, 1)

            def statistics(c, b):
                t = b * TPB + c
                dve.wait_ge(x_done, at(c, b, 1, 1))
                core.apart(dve)
                nc.vector.bn_stats(core.bn[:, t, :], core.X[:, t, :])

            for hc in range(NCH):
                c = hc // 2 - 1
                dve.wait_ge(in_k[hc % 2], 48 * (hc // 2 + 1))
                if hc == 1:
                    dve.wait_ge(loaded, 80)
                    for k in range(KD):
                        nc.vector.tensor_scalar(wo_sb[:, k, :], wo_sb[:, k, :], rw[:, k:k + 1], None,
                                                ALU.mult).then_inc(wo_done, 1)
                with dve.Fori(0, NGT // 2) as g2:
                    b = g2 + hc % 2 * (B // 2)
                    for pair in range(GRP_T):
                        two_steps(hc, g2, pair // (GRP_T // 2), pair % (GRP_T // 2) * 2)
                        if c < 0:
                            continue
                        if pair == 1:
                            scale_d(c, b)
                        if pair in (2, 3):
                            mask(c, b, 2 * (pair - 2))
                            mask(c, b, 2 * (pair - 2) + 1)
                        if pair == 5:
                            odd_heads(c, b)
                            own_heads(c, b)
                        if pair == 6:
                            invert_root(c, b)
                            advance_state(c, b)
                            add_rows(c, b)
                        if pair == 7:
                            statistics(c, b)
            with dve.Fori(0, B) as b:
                scale_d(TPB - 1, b)
                for g in range(4):
                    mask(TPB - 1, b, g)
                odd_heads(TPB - 1, b)
                invert_root(TPB - 1, b)
                add_rows(TPB - 1, b)
                statistics(TPB - 1, b)


def delta_constants():
    import numpy as np

    p = np.arange(P)
    par = np.stack([(p // HD) % 2 == 0, (p // HD) % 2 == 1], 1)
    before = p[:, None] < p[None, :]
    own = p[:, None] // HD == p[None, :] // HD
    return [np.ascontiguousarray(a.astype(np.float32)) for a in (par, before, own)]


def hybrid_layers_program(nc, x, ident, w_qk, w_vb, d_wo, rms_w, par, before, own,
                          w_exp, b_exp, w_con_t, up_w, down_w, up_bias, b_con, down_bias,
                          wq, wk, bq, bk, wv, bv, a_wo, bo, sel,
                          fwd, inv, conv_wt, conv_bias, modes, index, chan,
                          weight_t, gate_t, u_t, v,
                          w_in, conv_w, conv_b, dt_bias, a_log, norm_w, w_out, upto, out):
    with ExitStack() as ctx:
        core = Core(nc, ctx)
        tok_qk = nc.dram_tensor("tok_qk", [B * S, 2 * D], F32).ap()
        tok_d = nc.dram_tensor("tok_d", [B * S, D], F32).ap()
        seq = [nc.dram_tensor(f"seq_{n}", [P, S, HD], F32).ap() for n in ("k", "nbk", "v")]

        start(nc, core, x, ident)
        row_scales(nc, core, "r0")
        with ExitStack() as ffn_ctx:
            core.ctx = ffn_ctx
            bf = Butterfly(nc, core, [w_exp, b_exp, w_con_t, up_w, down_w])
            core.ctx = ctx
            with ExitStack() as delta_ctx:
                bf.allocate_folding(core, delta_ctx)
                beta = core.sbuf("beta", [P, NT, NH], delta_ctx)
                delta_inputs(nc, core, "di", beta, w_qk, w_vb, tok_qk, *seq)
                delta_scan(nc, core, "ds", beta, tok_qk, *seq, tok_d, d_wo, rms_w, (par, before, own), bf)
                ffn_prepare(nc, core, bf, up_bias, b_con, down_bias)
            row_scales(nc, core, "r1")
            ffn_stage(nc, core, bf, "f1")
            row_scales(nc, core, "r2")
            distance_attention_stage(nc, core, "a1", wq, wk, bq, bk, wv, bv, a_wo, bo,
                                     sel)
            row_scales(nc, core, "r3")
            ffn_stage(nc, core, bf, "f2")
        with ExitStack() as conv_ctx:
            lc = LongConv(nc, core, conv_ctx)
            conv_kernel(nc, core, lc, (fwd, inv, conv_wt, conv_bias), modes, index, chan)
            row_scales(nc, core, "r4")
            conv_stage(nc, core, lc, "c1")
        core.clear_semaphores()
        mx = MixtureWeights(nc, core)
        with ExitStack() as load_ctx:
            block = load_ctx.enter_context(nc.Block())

            @block.sync
            def _(sp):
                mx.load(sp, weight_t, gate_t, u_t, v)
        row_scales(nc, core, "r5")
        mixture_stage(nc, core, mx, "m1")
        row_scales(nc, core, "r6")
        state_space_stage(nc, core, "s1", w_in, conv_w, conv_b, dt_bias, a_log, norm_w, w_out, upto)
        row_scales(nc, core, "r7")
        mixture_stage(nc, core, mx, "m2")
        finish(nc, core, out)


def kernel(**inputs):
    import numpy as np
    import concourse.bacc as _bacc
    from concourse import mybir as _mybir
    from concourse.bass_utils import run_bass_kernel_spmd as _run

    a = {n: np.asarray(v) for n, v in inputs.items()}
    q, f, g = (lambda n: a["L0_attn_a_" + n]), (lambda n: a["L0_ffn_" + n]), (lambda n: a["L0_attn_b_" + n])
    c, s, m = (lambda n: a["L1_attn_a_" + n]), (lambda n: a["L1_attn_b_" + n]), (lambda n: a["L1_ffn_" + n])
    stages = lambda w: w.reshape(10, 512, 4).transpose(0, 2, 1)
    lay = lambda t: t.reshape(64, 4, 32).transpose(1, 2, 0).reshape(128, 64)
    par, before, own = delta_constants()
    fwd, inv, index, chan = conv_constants()
    sel = attention_constants()
    laid = dict(
        x=q("x"), ident=np.eye(128, dtype=np.float32),
        w_qk=np.concatenate([q("Wq").T, q("Wk").T], 1), w_vb=np.concatenate([q("Wv").T, q("Wbeta").T], 1),
        d_wo=q("Wo").T, rms_w=q("rms_weight").reshape(2, 128).T, par=par, before=before, own=own,
        w_exp=f("W_exp"), b_exp=f("b_exp"), w_con_t=f("W_con").T, up_w=stages(f("up_weights")),
        down_w=stages(f("down_weights").transpose(0, 1, 3, 2))[::-1],
        up_bias=f("up_bias").reshape(8, 128).T, b_con=f("b_con"), down_bias=f("down_bias"),
        wq=g("wq").T, wk=g("wk").T, bq=g("bq").reshape(2, 128).T, bk=g("bk").reshape(2, 128).T, wv=g("wv").T, bv=g("bv"), a_wo=g("wo").T, bo=g("bo"),
        sel=sel, fwd=fwd, inv=inv, conv_wt=c("W").T, conv_bias=c("b"),
        modes=np.stack([lay(np.repeat(c("log_dt")[:, None], 32, 1)), lay(c("log_A_real")),
                        lay(c("A_imag")), lay(c("C_real")), lay(c("C_imag"))]),
        index=index, chan=chan,
        weight_t=m("weight").T, gate_t=m("gate_w").T, u_t=m("lora_U").reshape(128, 256).T,
        v=m("lora_V").transpose(0, 2, 1).reshape(128, 256),
        w_in=s("W_in"), conv_w=s("conv_w").reshape(6, 128, 4).transpose(1, 0, 2),
        conv_b=s("conv_b").reshape(6, 128).T, dt_bias=s("dt_bias"), a_log=s("A_log"),
        norm_w=s("norm_w").reshape(4, 128).T, w_out=s("W_out"),
        upto=np.triu(np.ones((128, 128), np.float32)))

    nc = _bacc.Bacc("TRN2", target_bir_lowering=False, num_devices=1)
    arrays, args = {}, {}
    for name, value in laid.items():
        arrays[f"in_{name}_dram"] = np.ascontiguousarray(value)
        args[name] = nc.dram_tensor(f"in_{name}_dram", value.shape, _mybir.dt.from_np(value.dtype),
                                    kind="ExternalInput").ap()
    args["out"] = nc.dram_tensor("out_0_dram", (8, 512, 256), _mybir.dt.from_np(np.dtype("float32")),
                                 kind="ExternalOutput").ap()
    hybrid_layers_program(nc, **args)
    r = _run(nc, [arrays], core_ids=[0])
    return r.results[0]["out_0_dram"]
```
